# Optimizing a Trainium2 kernel written in Bass

```python
import numpy as np
import jax
import jax.numpy as jnp

def _softmax(x, axis=-1):
    return jax.nn.softmax(x, axis=axis)

def _gelu(x):
    return jax.nn.gelu(x, approximate=True)

def _silu(x):
    return jax.nn.silu(x)

def _sigmoid(x):
    return jax.nn.sigmoid(x)

def _layernorm(x, axis=-1, eps=1e-05):
    m = jnp.mean(x, axis=axis, keepdims=True)
    v = jnp.var(x, axis=axis, keepdims=True)
    return (x - m) / jnp.sqrt(v + eps)

def _scatter_add(tgt, idx, src, axis=0):
    return tgt.at[idx].add(src)

def _segment_sum(src, seg, n):
    return jax.ops.segment_sum(src, seg, n)
kernel_name = 'mk_perceiver_d4_seqx_r8_d1c990'

def setup_inputs(seed: int=0):
    np.random.seed(seed)
    _w = jnp.asarray

    def _rec_inputs():
        import jax
        import jax.numpy as jnp
        _rk = jax.random.key(seed)
        x = -0.000125 + 0.9999 * jax.random.normal(jax.random.fold_in(_rk, 1), (1, 64, 256), jnp.float32)
        _lenS = 64 - jax.random.randint(jax.random.fold_in(_rk, 7), (1,), 0, max(1, 64 // 4) + 1, jnp.int32)
        _lenS2 = 6272 - jax.random.randint(jax.random.fold_in(_rk, 8), (1,), 0, max(1, 6272 // 4) + 1, jnp.int32)
        _ctx_2048P = jax.random.normal(jax.random.fold_in(_rk, 11), (1, 16, 256), jnp.float32)
        _ctx_2048c = jax.random.dirichlet(jax.random.fold_in(_rk, 511), 0.3 * jnp.ones((16,), jnp.float32), (1, 6272))
        _ctx_2048t = jnp.einsum('bsk,bkd->bsd', _ctx_2048c, _ctx_2048P)
        _ctx_2048t = _ctx_2048t * jax.lax.rsqrt(jnp.mean(jnp.square(_ctx_2048t)) + 1e-12) * 0.953939
        ctx_2048 = -1.52775e-05 + 0.999936 * (_ctx_2048t + 0.3 * jax.random.normal(jax.random.fold_in(_rk, 611), (1, 6272, 256), jnp.float32))
        _validS = jnp.arange(64)[None, :] < _lenS[:, None]
        _validS2 = jnp.arange(6272)[None, :] < _lenS2[:, None]
        _causal = jnp.tril(jnp.ones((64, 64), dtype=bool))
        mask_BxS2_ff1 = jnp.where(jnp.ones((1, 6272), dtype=bool), 1.0, 0.0).astype(jnp.float32)
        mask_BxSx4224_bf0 = jnp.logical_not(jnp.ones((1, 64, 528), dtype=bool))
        return (x, ctx_2048, mask_BxS2_ff1, mask_BxSx4224_bf0)
    x, ctx_2048, mask_BxS2_ff1, mask_BxSx4224_bf0 = _rec_inputs()

    def _L0_xattn_setup():
        import jax, jax.numpy as jnp
        import numpy as np
        H = 256
        NH = 16
        HD = H // NH
        FD = 64
        key = jax.random.key(seed)
        ks = jax.random.split(key, 12)
        B, S = (4, 512)
        s = 1.0 / np.sqrt(H)
        sf = 1.0 / np.sqrt(HD)
        return {'query': jax.random.normal(ks[0], (B, S, H), jnp.float32), 'key': jax.random.normal(ks[1], (B, S, H), jnp.float32), 'value': jax.random.normal(ks[2], (B, S, H), jnp.float32), 'attention_mask': jnp.ones((B, S), jnp.float32), 'Wq': jax.random.normal(ks[3], (H, H), jnp.float32) * s, 'bq': jnp.zeros((H,), jnp.float32), 'Wk': jax.random.normal(ks[4], (H, H), jnp.float32) * s, 'bk': jnp.zeros((H,), jnp.float32), 'Wv': jax.random.normal(ks[5], (H, H), jnp.float32) * s, 'bv': jnp.zeros((H,), jnp.float32), 'Wqf': jax.random.normal(ks[6], (FD, HD), jnp.float32) * sf, 'Wkf': jax.random.normal(ks[7], (FD, HD), jnp.float32) * sf, 'Wo': jax.random.normal(ks[8], (H, H), jnp.float32) * s, 'bo': jnp.zeros((H,), jnp.float32)}
    _L0_xattn_all = _L0_xattn_setup()
    _L0_xattn_in = {k: v for k, v in _L0_xattn_all.items() if k in ('Wq', 'bq', 'Wk', 'bk', 'Wv', 'bv', 'Wqf', 'Wkf', 'Wo', 'bo')}
    del _L0_xattn_all

    def _L0_attn_setup():
        import jax, jax.numpy as jnp
        import numpy as np
        import math
        HIDDEN = 256
        NUM_HEADS = 16
        HEAD_SIZE = HIDDEN // NUM_HEADS
        BATCH = 2
        SEQ = 256
        key = jax.random.key(seed)
        k_x, k_wq, k_bq, k_wo, k_bo = jax.random.split(key, 5)
        scale_in = 1.0 / math.sqrt(HIDDEN)
        return {'x': jax.random.normal(k_x, (BATCH, SEQ, HIDDEN), dtype=jnp.float32), 'Wqkv': jax.random.normal(k_wq, (HIDDEN, 3 * HIDDEN), dtype=jnp.float32) * scale_in, 'bqkv': jax.random.normal(k_bq, (3 * HIDDEN,), dtype=jnp.float32) * 0.01, 'Wo': jax.random.normal(k_wo, (HIDDEN, HIDDEN), dtype=jnp.float32) * scale_in, 'bo': jax.random.normal(k_bo, (HIDDEN,), dtype=jnp.float32) * 0.01}
    _L0_attn_all = _L0_attn_setup()
    _L0_attn_in = {k: v for k, v in _L0_attn_all.items() if k in ('Wqkv', 'bqkv', 'Wo', 'bo')}
    del _L0_attn_all

    def _L0_ffn_setup():
        import jax, jax.numpy as jnp
        import numpy as np
        HIDDEN = 256
        INTER = 1024
        MOE_INTER = 128
        N_ROUTED = 8
        NUM_LOCAL = 8
        TOP_K = 2
        B, S = (4, 256)

        def _mlp(x, gw, uw, dw):
            g = x @ gw.T
            u = x @ uw.T
            return g * jax.nn.sigmoid(g) * u @ dw.T
        key = jax.random.key(seed)
        ks = jax.random.split(key, 8)
        std = 0.02
        return {'hidden_states': jax.random.normal(ks[0], (B, S, HIDDEN), jnp.float32), 'router_weight': jax.random.normal(ks[1], (N_ROUTED, HIDDEN), jnp.float32) * std, 'sh_gate': jax.random.normal(ks[2], (INTER, HIDDEN), jnp.float32) * std, 'sh_up': jax.random.normal(ks[3], (INTER, HIDDEN), jnp.float32) * std, 'sh_down': jax.random.normal(ks[4], (HIDDEN, INTER), jnp.float32) * std, 'r_gate': jax.random.normal(ks[5], (MOE_INTER, HIDDEN), jnp.float32) * std, 'r_up': jax.random.normal(ks[6], (MOE_INTER, HIDDEN), jnp.float32) * std, 'r_down': jax.random.normal(ks[7], (HIDDEN, MOE_INTER), jnp.float32) * std}
    _L0_ffn_all = _L0_ffn_setup()
    _L0_ffn_in = {k: v for k, v in _L0_ffn_all.items() if k in ('router_weight', 'sh_gate', 'sh_up', 'sh_down', 'r_gate', 'r_up', 'r_down')}
    del _L0_ffn_all

    def _L1_xattn_setup():
        import jax, jax.numpy as jnp
        import numpy as np
        D_MODEL = 256
        NUM_HEADS = 16
        HEAD_DIM = D_MODEL // NUM_HEADS

        def _fq_sym(x, axis):
            s = jnp.max(jnp.abs(x), axis=axis, keepdims=True) / 127.0
            s = jnp.maximum(s, 1e-08)
            q = jnp.clip(jnp.round(x / s), -127.0, 127.0) * s
            return x + jax.lax.stop_gradient(q - x)

        def _fq_unsigned(x, axis):
            s = jnp.max(x, axis=axis, keepdims=True) / 255.0
            s = jnp.maximum(s, 1e-08)
            q = jnp.clip(jnp.round(x / s), 0.0, 255.0) * s
            return x + jax.lax.stop_gradient(q - x)
        key = jax.random.key(seed)
        ks = jax.random.split(key, 8)
        B, N, M, C = (2, 256, 64, D_MODEL)
        return {'x': jax.random.normal(ks[0], (B, N, C), jnp.float32), 'cond': jax.random.normal(ks[1], (B, M, C), jnp.float32), 'Wq': jax.random.normal(ks[2], (C, C), jnp.float32) * 0.02, 'bq': jnp.zeros((C,), jnp.float32), 'Wkv': jax.random.normal(ks[3], (C, 2 * C), jnp.float32) * 0.02, 'bkv': jnp.zeros((2 * C,), jnp.float32), 'Wp': jax.random.normal(ks[4], (C, C), jnp.float32) * 0.02, 'bp': jnp.zeros((C,), jnp.float32)}
    _L1_xattn_all = _L1_xattn_setup()
    _L1_xattn_in = {k: v for k, v in _L1_xattn_all.items() if k in ('Wq', 'bq', 'Wkv', 'bkv', 'Wp', 'bp')}
    del _L1_xattn_all

    def _L1_attn_setup():
        import jax, jax.numpy as jnp
        import numpy as np
        NUM_HEADS = 16
        HIDDEN = 256
        HEAD_DIM = HIDDEN // NUM_HEADS
        ROTARY_DIM = HEAD_DIM // 4
        ROPE_BASE = 10000.0

        def _rope_angles(seq_len, dtype=jnp.float32):
            inv_freq = 1.0 / ROPE_BASE ** (jnp.arange(0, ROTARY_DIM, 2, dtype=dtype) / ROTARY_DIM)
            t = jnp.arange(seq_len, dtype=dtype)
            freqs = jnp.einsum('s,d->sd', t, inv_freq)
            emb = jnp.concatenate([freqs, freqs], axis=-1)
            return (jnp.cos(emb), jnp.sin(emb))

        def _rotate_half(x):
            x1, x2 = jnp.split(x, 2, axis=-1)
            return jnp.concatenate([-x2, x1], axis=-1)
        key = jax.random.key(seed)
        k1, k2, k3 = jax.random.split(key, 3)
        B, S = (2, 256)
        scale_qkv = 1.0 / np.sqrt(HIDDEN)
        return {'hidden_states': jax.random.normal(k1, (B, S, HIDDEN), dtype=jnp.float32), 'w_qkv': jax.random.normal(k2, (HIDDEN, 3 * HIDDEN), dtype=jnp.float32) * scale_qkv, 'b_qkv': jnp.zeros((3 * HIDDEN,), dtype=jnp.float32), 'w_out': jax.random.normal(k3, (HIDDEN, HIDDEN), dtype=jnp.float32) * scale_qkv, 'b_out': jnp.zeros((HIDDEN,), dtype=jnp.float32)}
    _L1_attn_all = _L1_attn_setup()
    _L1_attn_in = {k: v for k, v in _L1_attn_all.items() if k in ('w_qkv', 'b_qkv', 'w_out', 'b_out')}
    del _L1_attn_all

    def _L1_ffn_setup():
        import jax, jax.numpy as jnp
        import numpy as np
        TOP_K = 2
        SCALING = 2.0
        key = jax.random.key(seed)
        ks = jax.random.split(key, 10)
        B, S, H, I, E, R = (1, 64, 256, 128, 8, 16)
        w = 1.0 / np.sqrt(H)
        inp = {'x': jax.random.normal(ks[0], (B, S, H), jnp.float32), 'gate_weight': jax.random.normal(ks[1], (E, H), jnp.float32) * w, 'gate_lora_A': jax.random.normal(ks[2], (R, H), jnp.float32) * 0.02, 'gate_lora_B': jax.random.normal(ks[3], (E, R), jnp.float32) * 0.02, 'gate_up_proj': jax.random.normal(ks[4], (E, H, 2 * I), jnp.float32) * w, 'down_proj': jax.random.normal(ks[5], (E, I, H), jnp.float32) * (1.0 / np.sqrt(I)), 'gup_lora_A': jax.random.normal(ks[6], (E, R, H), jnp.float32) * 0.02, 'gup_lora_B': jax.random.normal(ks[7], (E, 2 * I, R), jnp.float32) * 0.02, 'down_lora_A': jax.random.normal(ks[8], (E, R, I), jnp.float32) * 0.02, 'down_lora_B': jax.random.normal(ks[9], (E, H, R), jnp.float32) * 0.02}
        return inp
    _L1_ffn_all = _L1_ffn_setup()
    _L1_ffn_in = {k: v for k, v in _L1_ffn_all.items() if k in ('gate_weight', 'gate_lora_A', 'gate_lora_B', 'gate_up_proj', 'down_proj', 'gup_lora_A', 'gup_lora_B', 'down_lora_A', 'down_lora_B')}
    del _L1_ffn_all

    def _L2_xattn_setup():
        import jax, jax.numpy as jnp
        import numpy as np
        FP8_MAX = 448.0
        EPS = 1e-05

        def _fp8_roundtrip(x):
            return x.astype(jnp.float8_e4m3fn).astype(jnp.float32)

        def _div_clamp_fp8(x, scale):
            y = jnp.clip(x.astype(jnp.float32) / scale, -FP8_MAX, FP8_MAX)
            y = y.astype(jnp.bfloat16).astype(jnp.float32)
            return _fp8_roundtrip(y)

        def _ln(x, w, b):
            mu = jnp.mean(x, axis=-1, keepdims=True)
            var = jnp.mean(jnp.square(x - mu), axis=-1, keepdims=True)
            return (x - mu) * jax.lax.rsqrt(var + EPS) * w + b

        def _fp8_linear_pertensor(x, wq, w_scale, in_scale):
            xq = _div_clamp_fp8(x, in_scale)
            return jnp.einsum('bsi,oi->bso', xq * in_scale, wq) * w_scale

        def _gqa(q, k, v):
            scale = 1.0 / np.sqrt(q.shape[-1])
            scores = jnp.einsum('bsghd,btgd->bghst', q, k) * scale
            p = jax.nn.softmax(scores, axis=-1)
            return jnp.einsum('bghst,btgd->bsghd', p, v)
        key = jax.random.key(seed)
        ks = jax.random.split(key, 8)
        B, S, SC, H, NH, G, D = (2, 256, 64, 256, 16, 8, 128)

        def qw(k, out_f, in_f):
            w = jax.random.normal(k, (out_f, in_f), jnp.float32) * 0.02
            sc = jnp.max(jnp.abs(w)) / FP8_MAX
            return (_fp8_roundtrip(w / sc), sc.astype(jnp.float32))
        wq, wq_s = qw(ks[0], NH * D, H)
        wqx, wqx_s = qw(ks[1], NH * D, H)
        wk, wk_s = qw(ks[2], G * D, H)
        wv, wv_s = qw(ks[3], G * D, H)
        wproj, wp_s = qw(ks[4], H, 2 * NH * D)
        return {'hidden_states': jax.random.normal(ks[5], (B, S, H), jnp.float32), 'cond': jax.random.normal(ks[6], (B, SC, H), jnp.float32), 'ln_w': jnp.ones((H,), jnp.float32), 'ln_b': jnp.zeros((H,), jnp.float32), 'wq': wq, 'wq_scale': wq_s, 'q_in_scale': jnp.full((H,), 0.05, jnp.float32), 'wqx': wqx, 'wqx_scale': wqx_s, 'qx_in_scale': jnp.full((H,), 0.05, jnp.float32), 'wk': wk, 'wk_scale': wk_s, 'k_in_scale': jnp.full((H,), 0.05, jnp.float32), 'wv': wv, 'wv_scale': wv_s, 'v_in_scale': jnp.full((H,), 0.05, jnp.float32), 'w_kv_x': jax.random.normal(ks[7], (2 * G * D, H), jnp.float32) * 0.02, 'qln_w': jnp.ones((D,), jnp.float32), 'qln_b': jnp.zeros((D,), jnp.float32), 'kln_w': jnp.ones((D,), jnp.float32), 'kln_b': jnp.zeros((D,), jnp.float32), 'qxln_w': jnp.ones((D,), jnp.float32), 'qxln_b': jnp.zeros((D,), jnp.float32), 'kxln_w': jnp.ones((D,), jnp.float32), 'kxln_b': jnp.zeros((D,), jnp.float32), 'wproj': wproj, 'proj_w_scale': wp_s, 'proj_in_scale': jnp.asarray(0.05, jnp.float32), 'proj_smooth': jnp.full((2 * NH * D,), 0.05, jnp.float32)}
    _L2_xattn_all = _L2_xattn_setup()
    _L2_xattn_in = {k: v for k, v in _L2_xattn_all.items() if k in ('ln_w', 'ln_b', 'wq', 'wq_scale', 'q_in_scale', 'wqx', 'wqx_scale', 'qx_in_scale', 'wk', 'wk_scale', 'k_in_scale', 'wv', 'wv_scale', 'v_in_scale', 'w_kv_x', 'qln_w', 'qln_b', 'kln_w', 'kln_b', 'qxln_w', 'qxln_b', 'kxln_w', 'kxln_b', 'wproj', 'proj_w_scale', 'proj_in_scale', 'proj_smooth')}
    del _L2_xattn_all

    def _L2_attn_setup():
        import jax, jax.numpy as jnp
        import numpy as np
        N_KV_HEAD = 8
        GROUP_SIZE = 4
        ROPE_BASE = 10000.0

        def _rope(x):
            t, d = (x.shape[-2], x.shape[-1])
            j = jnp.arange(d // 2, dtype=jnp.float32)
            theta = jnp.asarray(ROPE_BASE, jnp.float32) ** (-2.0 * j / d)
            pos = (jnp.arange(t, dtype=jnp.float32) + 1.0)[:, None]
            ang = pos * theta[None, :]
            C = jnp.concatenate([ang, ang], axis=-1)
            x2 = jnp.concatenate([-x[..., d // 2:], x[..., :d // 2]], axis=-1)
            return x * jnp.cos(C) + x2 * jnp.sin(C)
        key = jax.random.key(seed)
        ks = jax.random.split(key, 9)
        b, t, e = (2, 256, 256)
        kv = e // GROUP_SIZE
        s_in = 1.0 / np.sqrt(e)
        return {'x': jax.random.normal(ks[0], (b, t, e), jnp.float32), 'Wq': jax.random.normal(ks[1], (e, e), jnp.float32) * s_in, 'bq': jax.random.normal(ks[2], (e,), jnp.float32) * 0.01, 'Wk': jax.random.normal(ks[3], (kv, e), jnp.float32) * s_in, 'bk': jax.random.normal(ks[4], (kv,), jnp.float32) * 0.01, 'Wv': jax.random.normal(ks[5], (kv, e), jnp.float32) * s_in, 'bv': jax.random.normal(ks[6], (kv,), jnp.float32) * 0.01, 'Wo': jax.random.normal(ks[7], (e, e), jnp.float32) * s_in, 'bo': jax.random.normal(ks[8], (e,), jnp.float32) * 0.01}
    _L2_attn_all = _L2_attn_setup()
    _L2_attn_in = {k: v for k, v in _L2_attn_all.items() if k in ('Wq', 'bq', 'Wk', 'bk', 'Wv', 'bv', 'Wo', 'bo')}
    del _L2_attn_all

    def _L2_ffn_setup():
        import jax, jax.numpy as jnp
        import numpy as np
        B_, S, D = (2, 256, 256)
        F_ = 1024
        R = 16
        H = 16
        HD = D // H
        MOD_SCALE = 0.1
        EPS = 1e-06

        def _rmsnorm(x, w):
            v = jnp.mean(x * x, axis=-1, keepdims=True)
            return x * jax.lax.rsqrt(v + EPS) * w

        def _attention(x, Wq, Wk, Wv, Wo):
            b, s, d = x.shape
            q = (x @ Wq.T).reshape(b, s, H, HD)
            k = (x @ Wk.T).reshape(b, s, H, HD)
            v = (x @ Wv.T).reshape(b, s, H, HD)
            scores = jnp.einsum('bqhd,bkhd->bhqk', q, k) / np.sqrt(HD).astype(np.float32)
            causal = jnp.tril(jnp.ones((s, s), bool))
            scores = jnp.where(causal, scores, jnp.finfo(scores.dtype).min)
            probs = jax.nn.softmax(scores, axis=-1)
            out = jnp.einsum('bhqk,bkhd->bqhd', probs, v).reshape(b, s, d)
            return out @ Wo.T
        key = jax.random.key(seed)
        ks = jax.random.split(key, 12)
        sd = 0.02
        return {'hidden_states': jax.random.normal(ks[0], (B_, S, D), jnp.float32), 'ln1_w': jnp.ones((D,), jnp.float32), 'ln2_w': jnp.ones((D,), jnp.float32), 'Wq': jax.random.normal(ks[1], (D, D), jnp.float32) * sd, 'Wk': jax.random.normal(ks[2], (D, D), jnp.float32) * sd, 'Wv': jax.random.normal(ks[3], (D, D), jnp.float32) * sd, 'Wo': jax.random.normal(ks[4], (D, D), jnp.float32) * sd, 'A': jax.random.normal(ks[5], (D, R), jnp.float32) * (0.01 / np.sqrt(D)), 'B': jax.random.normal(ks[6], (R, F_), jnp.float32) * (0.01 / np.sqrt(R)), 'W_in_base': jax.random.normal(ks[7], (F_, D), jnp.float32) * sd, 'W_up_base': jax.random.normal(ks[8], (F_, D), jnp.float32) * sd, 'W_down': jax.random.normal(ks[9], (D, F_), jnp.float32) * sd}
    _L2_ffn_all = _L2_ffn_setup()
    _L2_ffn_in = {k: v for k, v in _L2_ffn_all.items() if k in ('ln1_w', 'ln2_w', 'Wq', 'Wk', 'Wv', 'Wo', 'A', 'B', 'W_in_base', 'W_up_base', 'W_down')}
    del _L2_ffn_all

    def _L3_xattn_setup():
        import jax, jax.numpy as jnp
        import numpy as np
        import math
        DIM = 256
        B, Q_LEN, KV_LEN = (8, 128, 512)
        key = jax.random.key(seed)
        ks = jax.random.split(key, 8)
        x = jax.random.normal(ks[0], (B, Q_LEN, DIM), dtype=jnp.float32)
        mask = jnp.zeros((B, Q_LEN, KV_LEN + Q_LEN), dtype=bool)
        k_cache = jax.random.normal(ks[1], (B, KV_LEN, DIM), dtype=jnp.float32)
        v_cache = jax.random.normal(ks[2], (B, KV_LEN, DIM), dtype=jnp.float32)
        scale = 1.0 / math.sqrt(DIM)
        wq = jax.random.normal(ks[3], (DIM, DIM), dtype=jnp.float32) * scale
        wk = jax.random.normal(ks[4], (DIM, DIM), dtype=jnp.float32) * scale
        wv = jax.random.normal(ks[5], (DIM, DIM), dtype=jnp.float32) * scale
        wo = jax.random.normal(ks[6], (DIM, DIM), dtype=jnp.float32) * scale
        return {'x': x, 'mask': mask, 'k_cache': k_cache, 'v_cache': v_cache, 'wq': wq, 'wk': wk, 'wv': wv, 'wo': wo}
    _L3_xattn_all = _L3_xattn_setup()
    _L3_xattn_in = {k: v for k, v in _L3_xattn_all.items() if k in ('wq', 'wk', 'wv', 'wo')}
    del _L3_xattn_all

    def _L3_attn_setup():
        import jax, jax.numpy as jnp
        import numpy as np
        D_MODEL = 256
        B, L = (4, 256)

        def _dwconv(x, w, b):
            y = jax.lax.conv_general_dilated(x, w, window_strides=(1,), padding=[(2, 0)], feature_group_count=x.shape[1], dimension_numbers=('NCH', 'OIH', 'NCH'))
            return y + b[None, :, None]
        key = jax.random.key(seed)
        ks = jax.random.split(key, 12)
        D = D_MODEL
        s = 0.02
        inp = {'u': jax.random.normal(ks[0], (B, L, D), jnp.float32), 'Wq': jax.random.normal(ks[1], (D, D), jnp.float32) * s, 'bq': jnp.zeros((D,), jnp.float32), 'Wk': jax.random.normal(ks[2], (D, D), jnp.float32) * s, 'bk': jnp.zeros((D,), jnp.float32), 'Wv': jax.random.normal(ks[3], (D, D), jnp.float32) * s, 'bv': jnp.zeros((D,), jnp.float32), 'convq_w': jax.random.normal(ks[4], (D, 1, 3), jnp.float32) * 0.5, 'convq_b': jnp.zeros((D,), jnp.float32), 'convk_w': jax.random.normal(ks[5], (D, 1, 3), jnp.float32) * 0.5, 'convk_b': jnp.zeros((D,), jnp.float32), 'ssm_kernel': jax.random.normal(ks[6], (D, L), jnp.float32) * 0.01, 'D_skip': jax.random.normal(ks[7], (D,), jnp.float32), 'Wo': jax.random.normal(ks[8], (D, D), jnp.float32) * s, 'bo': jnp.zeros((D,), jnp.float32)}
        return inp
    _L3_attn_all = _L3_attn_setup()
    _L3_attn_in = {k: v for k, v in _L3_attn_all.items() if k in ('Wq', 'bq', 'Wk', 'bk', 'Wv', 'bv', 'convq_w', 'convq_b', 'convk_w', 'convk_b', 'ssm_kernel', 'D_skip', 'Wo', 'bo')}
    del _L3_attn_all

    def _L3_ffn_setup():
        import jax, jax.numpy as jnp
        import numpy as np
        D_MODEL, D_FF, NS, NR, KR = (256, 176, 2, 16, 4)
        B, S = (4, 256)

        def _moe_forward(u, shared_w1, shared_b1, shared_w2, shared_b2, routed_w1, routed_b1, routed_w2, routed_b2, centroids, bias):
            b, s, d = u.shape
            flat = u.reshape(-1, d)
            T = flat.shape[0]
            h = jax.nn.relu(jnp.einsum('td,ndf->ntf', flat, shared_w1) + shared_b1[:, None, :])
            shared_out = jnp.einsum('ntf,nfd->td', h, shared_w2) + shared_b2.sum(0)
            out = flat + shared_out
            scores = jax.nn.sigmoid(flat @ centroids.T) + bias
            vals, idx = jax.lax.top_k(scores, KR)
            gating = jnp.zeros_like(scores).at[jnp.arange(T)[:, None], idx].set(vals)
            gating = gating / jnp.clip(gating.sum(-1, keepdims=True), 1e-08)

            def step(acc, ew):
                w1, b1, w2, b2, g = ew
                hj = jax.nn.relu(flat @ w1 + b1)
                yj = hj @ w2 + b2
                return (acc + yj * g[:, None], None)
            rout0 = jnp.zeros_like(flat)
            rout, _ = jax.lax.scan(step, rout0, (routed_w1, routed_b1, routed_w2, routed_b2, gating.T))
            return (out + rout).reshape(b, s, d)
        key = jax.random.key(seed)
        ks = jax.random.split(key, 10)
        s1 = 1.0 / np.sqrt(D_MODEL)
        s2 = 1.0 / np.sqrt(D_FF)
        return {'u': jax.random.normal(ks[0], (B, S, D_MODEL), dtype=jnp.float32), 'shared_w1': jax.random.normal(ks[1], (NS, D_MODEL, D_FF), dtype=jnp.float32) * s1, 'shared_b1': jnp.zeros((NS, D_FF), dtype=jnp.float32), 'shared_w2': jax.random.normal(ks[2], (NS, D_FF, D_MODEL), dtype=jnp.float32) * s2, 'shared_b2': jnp.zeros((NS, D_MODEL), dtype=jnp.float32), 'routed_w1': jax.random.normal(ks[3], (NR, D_MODEL, D_FF), dtype=jnp.float32) * s1, 'routed_b1': jnp.zeros((NR, D_FF), dtype=jnp.float32), 'routed_w2': jax.random.normal(ks[4], (NR, D_FF, D_MODEL), dtype=jnp.float32) * s2, 'routed_b2': jnp.zeros((NR, D_MODEL), dtype=jnp.float32), 'centroids': jax.random.normal(ks[5], (NR, D_MODEL), dtype=jnp.float32) * s1, 'bias': jnp.zeros((NR,), dtype=jnp.float32)}
    _L3_ffn_all = _L3_ffn_setup()
    _L3_ffn_in = {k: v for k, v in _L3_ffn_all.items() if k in ('shared_w1', 'shared_b1', 'shared_w2', 'shared_b2', 'routed_w1', 'routed_b1', 'routed_w2', 'routed_b2', 'centroids', 'bias')}
    del _L3_ffn_all
    return {'x': x, 'ctx_2048': ctx_2048, 'mask_BxS2_ff1': mask_BxS2_ff1, 'mask_BxSx4224_bf0': mask_BxSx4224_bf0, 'L0_xattn_Wq': _L0_xattn_in['Wq'], 'L0_xattn_bq': _L0_xattn_in['bq'], 'L0_xattn_Wk': _L0_xattn_in['Wk'], 'L0_xattn_bk': _L0_xattn_in['bk'], 'L0_xattn_Wv': _L0_xattn_in['Wv'], 'L0_xattn_bv': _L0_xattn_in['bv'], 'L0_xattn_Wqf': _L0_xattn_in['Wqf'], 'L0_xattn_Wkf': _L0_xattn_in['Wkf'], 'L0_xattn_Wo': _L0_xattn_in['Wo'], 'L0_xattn_bo': _L0_xattn_in['bo'], 'L0_attn_Wqkv': _L0_attn_in['Wqkv'], 'L0_attn_bqkv': _L0_attn_in['bqkv'], 'L0_attn_Wo': _L0_attn_in['Wo'], 'L0_attn_bo': _L0_attn_in['bo'], 'L0_ffn_router_weight': _L0_ffn_in['router_weight'], 'L0_ffn_sh_gate': _L0_ffn_in['sh_gate'], 'L0_ffn_sh_up': _L0_ffn_in['sh_up'], 'L0_ffn_sh_down': _L0_ffn_in['sh_down'], 'L0_ffn_r_gate': _L0_ffn_in['r_gate'], 'L0_ffn_r_up': _L0_ffn_in['r_up'], 'L0_ffn_r_down': _L0_ffn_in['r_down'], 'L1_xattn_Wq': _L1_xattn_in['Wq'], 'L1_xattn_bq': _L1_xattn_in['bq'], 'L1_xattn_Wkv': _L1_xattn_in['Wkv'], 'L1_xattn_bkv': _L1_xattn_in['bkv'], 'L1_xattn_Wp': _L1_xattn_in['Wp'], 'L1_xattn_bp': _L1_xattn_in['bp'], 'L1_attn_w_qkv': _L1_attn_in['w_qkv'], 'L1_attn_b_qkv': _L1_attn_in['b_qkv'], 'L1_attn_w_out': _L1_attn_in['w_out'], 'L1_attn_b_out': _L1_attn_in['b_out'], 'L1_ffn_gate_weight': _L1_ffn_in['gate_weight'], 'L1_ffn_gate_lora_A': _L1_ffn_in['gate_lora_A'], 'L1_ffn_gate_lora_B': _L1_ffn_in['gate_lora_B'], 'L1_ffn_gate_up_proj': _L1_ffn_in['gate_up_proj'], 'L1_ffn_down_proj': _L1_ffn_in['down_proj'], 'L1_ffn_gup_lora_A': _L1_ffn_in['gup_lora_A'], 'L1_ffn_gup_lora_B': _L1_ffn_in['gup_lora_B'], 'L1_ffn_down_lora_A': _L1_ffn_in['down_lora_A'], 'L1_ffn_down_lora_B': _L1_ffn_in['down_lora_B'], 'L2_xattn_ln_w': _L2_xattn_in['ln_w'], 'L2_xattn_ln_b': _L2_xattn_in['ln_b'], 'L2_xattn_wq': _L2_xattn_in['wq'], 'L2_xattn_wq_scale': _L2_xattn_in['wq_scale'], 'L2_xattn_q_in_scale': _L2_xattn_in['q_in_scale'], 'L2_xattn_wqx': _L2_xattn_in['wqx'], 'L2_xattn_wqx_scale': _L2_xattn_in['wqx_scale'], 'L2_xattn_qx_in_scale': _L2_xattn_in['qx_in_scale'], 'L2_xattn_wk': _L2_xattn_in['wk'], 'L2_xattn_wk_scale': _L2_xattn_in['wk_scale'], 'L2_xattn_k_in_scale': _L2_xattn_in['k_in_scale'], 'L2_xattn_wv': _L2_xattn_in['wv'], 'L2_xattn_wv_scale': _L2_xattn_in['wv_scale'], 'L2_xattn_v_in_scale': _L2_xattn_in['v_in_scale'], 'L2_xattn_w_kv_x': _L2_xattn_in['w_kv_x'], 'L2_xattn_qln_w': _L2_xattn_in['qln_w'], 'L2_xattn_qln_b': _L2_xattn_in['qln_b'], 'L2_xattn_kln_w': _L2_xattn_in['kln_w'], 'L2_xattn_kln_b': _L2_xattn_in['kln_b'], 'L2_xattn_qxln_w': _L2_xattn_in['qxln_w'], 'L2_xattn_qxln_b': _L2_xattn_in['qxln_b'], 'L2_xattn_kxln_w': _L2_xattn_in['kxln_w'], 'L2_xattn_kxln_b': _L2_xattn_in['kxln_b'], 'L2_xattn_wproj': _L2_xattn_in['wproj'], 'L2_xattn_proj_w_scale': _L2_xattn_in['proj_w_scale'], 'L2_xattn_proj_in_scale': _L2_xattn_in['proj_in_scale'], 'L2_xattn_proj_smooth': _L2_xattn_in['proj_smooth'], 'L2_attn_Wq': _L2_attn_in['Wq'], 'L2_attn_bq': _L2_attn_in['bq'], 'L2_attn_Wk': _L2_attn_in['Wk'], 'L2_attn_bk': _L2_attn_in['bk'], 'L2_attn_Wv': _L2_attn_in['Wv'], 'L2_attn_bv': _L2_attn_in['bv'], 'L2_attn_Wo': _L2_attn_in['Wo'], 'L2_attn_bo': _L2_attn_in['bo'], 'L2_ffn_ln1_w': _L2_ffn_in['ln1_w'], 'L2_ffn_ln2_w': _L2_ffn_in['ln2_w'], 'L2_ffn_Wq': _L2_ffn_in['Wq'], 'L2_ffn_Wk': _L2_ffn_in['Wk'], 'L2_ffn_Wv': _L2_ffn_in['Wv'], 'L2_ffn_Wo': _L2_ffn_in['Wo'], 'L2_ffn_A': _L2_ffn_in['A'], 'L2_ffn_B': _L2_ffn_in['B'], 'L2_ffn_W_in_base': _L2_ffn_in['W_in_base'], 'L2_ffn_W_up_base': _L2_ffn_in['W_up_base'], 'L2_ffn_W_down': _L2_ffn_in['W_down'], 'L3_xattn_wq': _L3_xattn_in['wq'], 'L3_xattn_wk': _L3_xattn_in['wk'], 'L3_xattn_wv': _L3_xattn_in['wv'], 'L3_xattn_wo': _L3_xattn_in['wo'], 'L3_attn_Wq': _L3_attn_in['Wq'], 'L3_attn_bq': _L3_attn_in['bq'], 'L3_attn_Wk': _L3_attn_in['Wk'], 'L3_attn_bk': _L3_attn_in['bk'], 'L3_attn_Wv': _L3_attn_in['Wv'], 'L3_attn_bv': _L3_attn_in['bv'], 'L3_attn_convq_w': _L3_attn_in['convq_w'], 'L3_attn_convq_b': _L3_attn_in['convq_b'], 'L3_attn_convk_w': _L3_attn_in['convk_w'], 'L3_attn_convk_b': _L3_attn_in['convk_b'], 'L3_attn_ssm_kernel': _L3_attn_in['ssm_kernel'], 'L3_attn_D_skip': _L3_attn_in['D_skip'], 'L3_attn_Wo': _L3_attn_in['Wo'], 'L3_attn_bo': _L3_attn_in['bo'], 'L3_ffn_shared_w1': _L3_ffn_in['shared_w1'], 'L3_ffn_shared_b1': _L3_ffn_in['shared_b1'], 'L3_ffn_shared_w2': _L3_ffn_in['shared_w2'], 'L3_ffn_shared_b2': _L3_ffn_in['shared_b2'], 'L3_ffn_routed_w1': _L3_ffn_in['routed_w1'], 'L3_ffn_routed_b1': _L3_ffn_in['routed_b1'], 'L3_ffn_routed_w2': _L3_ffn_in['routed_w2'], 'L3_ffn_routed_b2': _L3_ffn_in['routed_b2'], 'L3_ffn_centroids': _L3_ffn_in['centroids'], 'L3_ffn_bias': _L3_ffn_in['bias']}

def reference(x, ctx_2048, mask_BxS2_ff1, mask_BxSx4224_bf0, L0_xattn_Wq, L0_xattn_bq, L0_xattn_Wk, L0_xattn_bk, L0_xattn_Wv, L0_xattn_bv, L0_xattn_Wqf, L0_xattn_Wkf, L0_xattn_Wo, L0_xattn_bo, L0_attn_Wqkv, L0_attn_bqkv, L0_attn_Wo, L0_attn_bo, L0_ffn_router_weight, L0_ffn_sh_gate, L0_ffn_sh_up, L0_ffn_sh_down, L0_ffn_r_gate, L0_ffn_r_up, L0_ffn_r_down, L1_xattn_Wq, L1_xattn_bq, L1_xattn_Wkv, L1_xattn_bkv, L1_xattn_Wp, L1_xattn_bp, L1_attn_w_qkv, L1_attn_b_qkv, L1_attn_w_out, L1_attn_b_out, L1_ffn_gate_weight, L1_ffn_gate_lora_A, L1_ffn_gate_lora_B, L1_ffn_gate_up_proj, L1_ffn_down_proj, L1_ffn_gup_lora_A, L1_ffn_gup_lora_B, L1_ffn_down_lora_A, L1_ffn_down_lora_B, L2_xattn_ln_w, L2_xattn_ln_b, L2_xattn_wq, L2_xattn_wq_scale, L2_xattn_q_in_scale, L2_xattn_wqx, L2_xattn_wqx_scale, L2_xattn_qx_in_scale, L2_xattn_wk, L2_xattn_wk_scale, L2_xattn_k_in_scale, L2_xattn_wv, L2_xattn_wv_scale, L2_xattn_v_in_scale, L2_xattn_w_kv_x, L2_xattn_qln_w, L2_xattn_qln_b, L2_xattn_kln_w, L2_xattn_kln_b, L2_xattn_qxln_w, L2_xattn_qxln_b, L2_xattn_kxln_w, L2_xattn_kxln_b, L2_xattn_wproj, L2_xattn_proj_w_scale, L2_xattn_proj_in_scale, L2_xattn_proj_smooth, L2_attn_Wq, L2_attn_bq, L2_attn_Wk, L2_attn_bk, L2_attn_Wv, L2_attn_bv, L2_attn_Wo, L2_attn_bo, L2_ffn_ln1_w, L2_ffn_ln2_w, L2_ffn_Wq, L2_ffn_Wk, L2_ffn_Wv, L2_ffn_Wo, L2_ffn_A, L2_ffn_B, L2_ffn_W_in_base, L2_ffn_W_up_base, L2_ffn_W_down, L3_xattn_wq, L3_xattn_wk, L3_xattn_wv, L3_xattn_wo, L3_attn_Wq, L3_attn_bq, L3_attn_Wk, L3_attn_bk, L3_attn_Wv, L3_attn_bv, L3_attn_convq_w, L3_attn_convq_b, L3_attn_convk_w, L3_attn_convk_b, L3_attn_ssm_kernel, L3_attn_D_skip, L3_attn_Wo, L3_attn_bo, L3_ffn_shared_w1, L3_ffn_shared_b1, L3_ffn_shared_w2, L3_ffn_shared_b2, L3_ffn_routed_w1, L3_ffn_routed_b1, L3_ffn_routed_w2, L3_ffn_routed_b2, L3_ffn_centroids, L3_ffn_bias):
    import jax
    import jax.numpy as jnp

    def _L0_xattn_ref(query, key, value, attention_mask, Wq, bq, Wk, bk, Wv, bv, Wqf, Wkf, Wo, bo):
        import jax, jax.numpy as jnp
        import numpy as np
        H = 256
        NH = 16
        HD = H // NH
        FD = 64
        B, Sq, _ = query.shape
        Sk = key.shape[1]

        def heads(x, W, b, S):
            return (x @ W.T + b).reshape(B, S, NH, HD).transpose(0, 2, 1, 3)
        q = heads(query, Wq, bq, Sq)
        k = heads(key, Wk, bk, Sk)
        v = heads(value, Wv, bv, Sk)
        q_prime = jax.nn.relu(jnp.einsum('bhnd,fd->bhnf', q, Wqf))
        k_prime = jax.nn.relu(jnp.einsum('bhnd,fd->bhnf', k, Wkf))
        k_prime = k_prime * attention_mask[:, None, :, None]
        kv = jnp.einsum('bhnf,bhne->bhfe', k_prime, v)
        qkv = jnp.einsum('bhmf,bhfe->bhme', q_prime, kv)
        k_sum = jnp.sum(k_prime, axis=2)
        qk_sum = jnp.einsum('bhmf,bhf->bhm', q_prime, k_sum)[..., None]
        out = qkv / (qk_sum + 1e-08)
        out = out.transpose(0, 2, 1, 3).reshape(B, Sq, H)
        return out @ Wo.T + bo

    def _L0_attn_ref(x, Wqkv, bqkv, Wo, bo):
        import jax, jax.numpy as jnp
        import numpy as np
        import math
        HIDDEN = 256
        NUM_HEADS = 16
        HEAD_SIZE = HIDDEN // NUM_HEADS
        BATCH = 2
        SEQ = 256
        b, s, _ = x.shape
        kqv = x @ Wqkv + bqkv
        kqv = kqv.reshape(b, s, 3, NUM_HEADS, HEAD_SIZE)
        q = kqv[:, :, 0]
        k = kqv[:, :, 1]
        v = kqv[:, :, 2]
        scores = jnp.einsum('bsnh,btnh->bnst', k, q) / math.sqrt(HEAD_SIZE)
        ones = jnp.ones_like(scores)
        scores = jnp.triu(scores) + -10000.0 * jnp.tril(ones, k=-1)
        attn = jax.nn.softmax(scores, axis=2)
        out = jnp.einsum('bnkq,bknh->bqnh', attn, v)
        out = out.reshape(b, s, NUM_HEADS * HEAD_SIZE)
        return out @ Wo + bo

    def _L0_ffn_ref(hidden_states, router_weight, sh_gate, sh_up, sh_down, r_gate, r_up, r_down):
        import jax, jax.numpy as jnp
        import numpy as np
        HIDDEN = 256
        INTER = 1024
        MOE_INTER = 128
        N_ROUTED = 8
        NUM_LOCAL = 8
        TOP_K = 2
        B, S = (4, 256)

        def _mlp(x, gw, uw, dw):
            g = x @ gw.T
            u = x @ uw.T
            return g * jax.nn.sigmoid(g) * u @ dw.T
        Bsz, Seq, H = hidden_states.shape
        x = hidden_states.reshape(-1, H)
        logits = x.astype(jnp.float32) @ router_weight.astype(jnp.float32).T
        topk_vals, topk_idx = jax.lax.top_k(logits, TOP_K)
        topk_w = jax.nn.softmax(topk_vals, axis=-1)
        slot_mask = (topk_idx < NUM_LOCAL).astype(topk_w.dtype)
        comb_w = jnp.sum(topk_w * slot_mask, axis=-1).astype(x.dtype)
        shared = _mlp(x, sh_gate, sh_up, sh_down)
        routed = _mlp(x, r_gate, r_up, r_down) * comb_w[:, None]
        return (shared + routed).reshape(Bsz, Seq, H)

    def _L1_xattn_ref(x, cond, Wq, bq, Wkv, bkv, Wp, bp):
        import jax, jax.numpy as jnp
        import numpy as np
        D_MODEL = 256
        NUM_HEADS = 16
        HEAD_DIM = D_MODEL // NUM_HEADS

        def _fq_sym(x, axis):
            s = jnp.max(jnp.abs(x), axis=axis, keepdims=True) / 127.0
            s = jnp.maximum(s, 1e-08)
            q = jnp.clip(jnp.round(x / s), -127.0, 127.0) * s
            return x + jax.lax.stop_gradient(q - x)

        def _fq_unsigned(x, axis):
            s = jnp.max(x, axis=axis, keepdims=True) / 255.0
            s = jnp.maximum(s, 1e-08)
            q = jnp.clip(jnp.round(x / s), 0.0, 255.0) * s
            return x + jax.lax.stop_gradient(q - x)
        B, N, C = x.shape
        H, hd = (NUM_HEADS, HEAD_DIM)
        q = (x @ Wq + bq).reshape(1, B * N, H, hd)
        kv = (cond @ Wkv + bkv).reshape(1, -1, 2, H, hd)
        k, v = (kv[:, :, 0], kv[:, :, 1])
        scale = 1.0 / np.sqrt(hd).astype(np.float32)
        q = jnp.transpose(q * scale, (0, 2, 1, 3))
        k = jnp.transpose(k, (0, 2, 1, 3))
        v = jnp.transpose(v, (0, 2, 1, 3))
        q = _fq_sym(q, axis=-1)
        k = _fq_sym(k, axis=-1)
        v = _fq_sym(v, axis=2)
        attn = jnp.einsum('bhqd,bhkd->bhqk', q, k)
        attn = jax.nn.softmax(attn.astype(jnp.float32), axis=-1)
        attn = _fq_unsigned(attn, axis=-1)
        out = jnp.einsum('bhqk,bhkd->bhqd', attn, v)
        out = jnp.transpose(out, (0, 2, 1, 3)).reshape(B, N, C)
        return out @ Wp + bp

    def _L1_attn_ref(hidden_states, w_qkv, b_qkv, w_out, b_out):
        import jax, jax.numpy as jnp
        import numpy as np
        NUM_HEADS = 16
        HIDDEN = 256
        HEAD_DIM = HIDDEN // NUM_HEADS
        ROTARY_DIM = HEAD_DIM // 4
        ROPE_BASE = 10000.0

        def _rope_angles(seq_len, dtype=jnp.float32):
            inv_freq = 1.0 / ROPE_BASE ** (jnp.arange(0, ROTARY_DIM, 2, dtype=dtype) / ROTARY_DIM)
            t = jnp.arange(seq_len, dtype=dtype)
            freqs = jnp.einsum('s,d->sd', t, inv_freq)
            emb = jnp.concatenate([freqs, freqs], axis=-1)
            return (jnp.cos(emb), jnp.sin(emb))

        def _rotate_half(x):
            x1, x2 = jnp.split(x, 2, axis=-1)
            return jnp.concatenate([-x2, x1], axis=-1)
        B, S, H = hidden_states.shape
        qkv = jnp.einsum('bsh,hf->bsf', hidden_states, w_qkv) + b_qkv
        qkv = qkv.reshape(B, S, NUM_HEADS, 3 * HEAD_DIM)
        q = jnp.transpose(qkv[..., :HEAD_DIM], (0, 2, 1, 3))
        k = jnp.transpose(qkv[..., HEAD_DIM:2 * HEAD_DIM], (0, 2, 1, 3))
        v = jnp.transpose(qkv[..., 2 * HEAD_DIM:], (0, 2, 1, 3))
        cos, sin = _rope_angles(S, q.dtype)
        q_rot, q_pass = (q[..., :ROTARY_DIM], q[..., ROTARY_DIM:])
        k_rot, k_pass = (k[..., :ROTARY_DIM], k[..., ROTARY_DIM:])
        q_rot = q_rot * cos + _rotate_half(q_rot) * sin
        k_rot = k_rot * cos + _rotate_half(k_rot) * sin
        q = jnp.concatenate([q_rot, q_pass], axis=-1)
        k = jnp.concatenate([k_rot, k_pass], axis=-1)
        scores = jnp.einsum('bhqd,bhkd->bhqk', q, k)
        causal = jnp.tril(jnp.ones((S, S), dtype=bool))
        scores = jnp.where(causal, scores, jnp.float32(-jnp.inf).astype(scores.dtype))
        probs = jax.nn.softmax(scores, axis=-1)
        attn = jnp.einsum('bhqk,bhkd->bhqd', probs, v)
        attn = jnp.transpose(attn, (0, 2, 1, 3)).reshape(B, S, H)
        return jnp.einsum('bsh,hf->bsf', attn, w_out) + b_out

    def _L1_ffn_ref(x, gate_weight, gate_lora_A, gate_lora_B, gate_up_proj, down_proj, gup_lora_A, gup_lora_B, down_lora_A, down_lora_B):
        import jax, jax.numpy as jnp
        import numpy as np
        TOP_K = 2
        SCALING = 2.0
        B, S, H = x.shape
        xf = x.reshape(-1, H)
        gate_delta = SCALING * (gate_lora_B @ gate_lora_A)
        router_logits = xf @ gate_weight.T + xf @ gate_delta.T
        probs = jax.nn.softmax(router_logits.astype(jnp.float32), axis=-1)
        routing_weights, selected = jax.lax.top_k(probs, TOP_K)
        routing_weights = routing_weights / routing_weights.sum(-1, keepdims=True)
        routing_weights = routing_weights.astype(xf.dtype)
        gup = jnp.einsum('th,eho->teo', xf, gate_up_proj)
        gup = gup + SCALING * jnp.einsum('ter,eor->teo', jnp.einsum('th,erh->ter', xf, gup_lora_A), gup_lora_B)
        gates, h = jnp.split(gup, 2, axis=-1)
        h = jax.nn.silu(gates) * h
        out = jnp.einsum('tei,eih->teh', h, down_proj)
        out = out + SCALING * jnp.einsum('ter,ehr->teh', jnp.einsum('tei,eri->ter', h, down_lora_A), down_lora_B)
        out_sel = jnp.take_along_axis(out, selected[:, :, None], axis=1)
        y = jnp.einsum('tkh,tk->th', out_sel, routing_weights)
        return y.reshape(B, S, H)

    def _L2_xattn_ref(hidden_states, cond, ln_w, ln_b, wq, wq_scale, q_in_scale, wqx, wqx_scale, qx_in_scale, wk, wk_scale, k_in_scale, wv, wv_scale, v_in_scale, w_kv_x, qln_w, qln_b, kln_w, kln_b, qxln_w, qxln_b, kxln_w, kxln_b, wproj, proj_w_scale, proj_in_scale, proj_smooth):
        import jax, jax.numpy as jnp
        import numpy as np
        FP8_MAX = 448.0
        EPS = 1e-05

        def _fp8_roundtrip(x):
            return x.astype(jnp.float8_e4m3fn).astype(jnp.float32)

        def _div_clamp_fp8(x, scale):
            y = jnp.clip(x.astype(jnp.float32) / scale, -FP8_MAX, FP8_MAX)
            y = y.astype(jnp.bfloat16).astype(jnp.float32)
            return _fp8_roundtrip(y)

        def _ln(x, w, b):
            mu = jnp.mean(x, axis=-1, keepdims=True)
            var = jnp.mean(jnp.square(x - mu), axis=-1, keepdims=True)
            return (x - mu) * jax.lax.rsqrt(var + EPS) * w + b

        def _fp8_linear_pertensor(x, wq, w_scale, in_scale):
            xq = _div_clamp_fp8(x, in_scale)
            return jnp.einsum('bsi,oi->bso', xq * in_scale, wq) * w_scale

        def _gqa(q, k, v):
            scale = 1.0 / np.sqrt(q.shape[-1])
            scores = jnp.einsum('bsghd,btgd->bghst', q, k) * scale
            p = jax.nn.softmax(scores, axis=-1)
            return jnp.einsum('bghst,btgd->bsghd', p, v)
        b, s, _ = hidden_states.shape
        sc = cond.shape[1]
        d = qln_w.shape[0]
        nh = wq.shape[0] // d
        g = wk.shape[0] // d
        hpg = nh // g
        ln_out = _ln(hidden_states, ln_w, ln_b)
        q = _fp8_linear_pertensor(ln_out, wq, wq_scale, q_in_scale).reshape(b, s, g, hpg, d)
        q = _ln(q, qln_w, qln_b)
        k = _fp8_linear_pertensor(ln_out, wk, wk_scale, k_in_scale).reshape(b, s, g, d)
        k = _ln(k, kln_w, kln_b)
        v = _fp8_linear_pertensor(ln_out, wv, wv_scale, v_in_scale).reshape(b, s, g, d)
        core = _gqa(q, k, v).reshape(b, s, nh * d)
        qx = _fp8_linear_pertensor(ln_out, wqx, wqx_scale, qx_in_scale).reshape(b, s, g, hpg, d)
        qx = _ln(qx, qxln_w, qxln_b)
        kvx = jnp.einsum('bsi,oi->bso', cond, w_kv_x)
        kx, vx = jnp.split(kvx, 2, axis=-1)
        kx = _ln(kx.reshape(b, sc, g, d), kxln_w, kxln_b)
        vx = vx.reshape(b, sc, g, d)
        xout = _gqa(qx, kx, vx).reshape(b, s, nh * d)
        cat = jnp.concatenate([core, xout], axis=-1)
        catq = _div_clamp_fp8(cat, proj_smooth)
        return jnp.einsum('bsi,oi->bso', catq, wproj) * (proj_in_scale * proj_w_scale)

    def _L2_attn_ref(x, Wq, bq, Wk, bk, Wv, bv, Wo, bo):
        import jax, jax.numpy as jnp
        import numpy as np
        N_KV_HEAD = 8
        GROUP_SIZE = 4
        ROPE_BASE = 10000.0

        def _rope(x):
            t, d = (x.shape[-2], x.shape[-1])
            j = jnp.arange(d // 2, dtype=jnp.float32)
            theta = jnp.asarray(ROPE_BASE, jnp.float32) ** (-2.0 * j / d)
            pos = (jnp.arange(t, dtype=jnp.float32) + 1.0)[:, None]
            ang = pos * theta[None, :]
            C = jnp.concatenate([ang, ang], axis=-1)
            x2 = jnp.concatenate([-x[..., d // 2:], x[..., :d // 2]], axis=-1)
            return x * jnp.cos(C) + x2 * jnp.sin(C)
        b, t, e = x.shape
        h, g = (N_KV_HEAD, GROUP_SIZE)
        d = e // (h * g)
        q = x @ Wq.T + bq
        k = x @ Wk.T + bk
        v = x @ Wv.T + bv
        q = q.reshape(b, t, h, g, d).transpose(0, 3, 2, 1, 4)
        k = k.reshape(b, t, h, d).transpose(0, 2, 1, 3)
        v = v.reshape(b, t, h, d).transpose(0, 2, 1, 3)
        q = _rope(q)
        k = _rope(k)
        scale = jnp.asarray(np.sqrt(d), x.dtype)
        att = jnp.einsum('bghqd,bhkd->bghqk', q, k) / scale
        causal = jnp.tril(jnp.ones((t, t), bool))
        att = jnp.where(causal, att, -jnp.inf)
        att = jax.nn.softmax(att, axis=-1)
        y = jnp.einsum('bghqk,bhkd->bghqd', att, v)
        y = y.transpose(0, 3, 2, 1, 4).reshape(b, t, e)
        return y @ Wo.T + bo

    def _L2_ffn_ref(hidden_states, ln1_w, ln2_w, Wq, Wk, Wv, Wo, A, B, W_in_base, W_up_base, W_down):
        import jax, jax.numpy as jnp
        import numpy as np
        B_, S, D = (2, 256, 256)
        F_ = 1024
        R = 16
        H = 16
        HD = D // H
        MOD_SCALE = 0.1
        EPS = 1e-06

        def _rmsnorm(x, w):
            v = jnp.mean(x * x, axis=-1, keepdims=True)
            return x * jax.lax.rsqrt(v + EPS) * w

        def _attention(x, Wq, Wk, Wv, Wo):
            b, s, d = x.shape
            q = (x @ Wq.T).reshape(b, s, H, HD)
            k = (x @ Wk.T).reshape(b, s, H, HD)
            v = (x @ Wv.T).reshape(b, s, H, HD)
            scores = jnp.einsum('bqhd,bkhd->bhqk', q, k) / np.sqrt(HD).astype(np.float32)
            causal = jnp.tril(jnp.ones((s, s), bool))
            scores = jnp.where(causal, scores, jnp.finfo(scores.dtype).min)
            probs = jax.nn.softmax(scores, axis=-1)
            out = jnp.einsum('bhqk,bkhd->bqhd', probs, v).reshape(b, s, d)
            return out @ Wo.T
        residual = hidden_states
        x = _rmsnorm(hidden_states, ln1_w)
        attn = _attention(x, Wq, Wk, Wv, Wo)
        mod = MOD_SCALE * jnp.tanh(attn @ A)
        h = _rmsnorm(residual, ln2_w)
        gate_pre = h @ W_in_base.T + mod * (h @ A) @ B
        gate = jax.nn.silu(gate_pre)
        up = h @ W_up_base.T
        mlp_out = gate * up @ W_down.T
        return residual + mlp_out

    def _L3_xattn_ref(x, mask, k_cache, v_cache, wq, wk, wv, wo):
        import jax, jax.numpy as jnp
        import numpy as np
        import math
        DIM = 256
        B, Q_LEN, KV_LEN = (8, 128, 512)
        q = jnp.einsum('bsd,ed->bse', x, wq)
        k_new = jnp.einsum('bsd,ed->bse', x, wk)
        v_new = jnp.einsum('bsd,ed->bse', x, wv)
        k = jnp.concatenate([k_cache, k_new], axis=1)
        v = jnp.concatenate([v_cache, v_new], axis=1)
        scale = 1.0 / math.sqrt(q.shape[-1])
        scores = jnp.einsum('bqd,bkd->bqk', q, k) * scale
        attn = jax.nn.softmax(scores, axis=-1)
        out = jnp.einsum('bqk,bkd->bqd', attn, v)
        return jnp.einsum('bqd,ed->bqe', out, wo)

    def _L3_attn_ref(u, Wq, bq, Wk, bk, Wv, bv, convq_w, convq_b, convk_w, convk_b, ssm_kernel, D_skip, Wo, bo):
        import jax, jax.numpy as jnp
        import numpy as np
        D_MODEL = 256
        B, L = (4, 256)

        def _dwconv(x, w, b):
            y = jax.lax.conv_general_dilated(x, w, window_strides=(1,), padding=[(2, 0)], feature_group_count=x.shape[1], dimension_numbers=('NCH', 'OIH', 'NCH'))
            return y + b[None, :, None]
        Lq = u.shape[1]
        fft_size = 2 * Lq
        q = jnp.einsum('blh,eh->ble', u, Wq) + bq
        k = jnp.einsum('blh,eh->ble', u, Wk) + bk
        v = jnp.einsum('blh,eh->ble', u, Wv) + bv
        q = jnp.transpose(q, (0, 2, 1))
        k = jnp.transpose(k, (0, 2, 1))
        v = jnp.transpose(v, (0, 2, 1))
        q = _dwconv(q, convq_w, convq_b)
        k = _dwconv(k, convk_w, convk_b)
        kv = k * v
        kv_f = jnp.fft.rfft(kv, n=fft_size)
        kernel_f = jnp.fft.rfft(ssm_kernel, n=fft_size)
        y = jnp.fft.irfft(kv_f * kernel_f, n=fft_size)[..., :Lq]
        y = (y + kv * D_skip[None, :, None]) * q
        y = jnp.transpose(y, (0, 2, 1))
        return jnp.einsum('blh,eh->ble', y, Wo) + bo

    def _L3_ffn_ref(u, shared_w1, shared_b1, shared_w2, shared_b2, routed_w1, routed_b1, routed_w2, routed_b2, centroids, bias):
        import jax, jax.numpy as jnp
        import numpy as np
        D_MODEL, D_FF, NS, NR, KR = (256, 176, 2, 16, 4)
        B, S = (4, 256)

        def _moe_forward(u, shared_w1, shared_b1, shared_w2, shared_b2, routed_w1, routed_b1, routed_w2, routed_b2, centroids, bias):
            b, s, d = u.shape
            flat = u.reshape(-1, d)
            T = flat.shape[0]
            h = jax.nn.relu(jnp.einsum('td,ndf->ntf', flat, shared_w1) + shared_b1[:, None, :])
            shared_out = jnp.einsum('ntf,nfd->td', h, shared_w2) + shared_b2.sum(0)
            out = flat + shared_out
            scores = jax.nn.sigmoid(flat @ centroids.T) + bias
            vals, idx = jax.lax.top_k(scores, KR)
            gating = jnp.zeros_like(scores).at[jnp.arange(T)[:, None], idx].set(vals)
            gating = gating / jnp.clip(gating.sum(-1, keepdims=True), 1e-08)

            def step(acc, ew):
                w1, b1, w2, b2, g = ew
                hj = jax.nn.relu(flat @ w1 + b1)
                yj = hj @ w2 + b2
                return (acc + yj * g[:, None], None)
            rout0 = jnp.zeros_like(flat)
            rout, _ = jax.lax.scan(step, rout0, (routed_w1, routed_b1, routed_w2, routed_b2, gating.T))
            return (out + rout).reshape(b, s, d)
        return _moe_forward(u, shared_w1, shared_b1, shared_w2, shared_b2, routed_w1, routed_b1, routed_w2, routed_b2, centroids, bias)
    x = x + _L0_xattn_ref(_layernorm(x, axis=-1), ctx_2048, ctx_2048, mask_BxS2_ff1, L0_xattn_Wq, L0_xattn_bq, L0_xattn_Wk, L0_xattn_bk, L0_xattn_Wv, L0_xattn_bv, L0_xattn_Wqf, L0_xattn_Wkf, L0_xattn_Wo, L0_xattn_bo)
    x = x + _L0_attn_ref(_layernorm(x, axis=-1), L0_attn_Wqkv, L0_attn_bqkv, L0_attn_Wo, L0_attn_bo)
    x = x + _L0_ffn_ref(_layernorm(x, axis=-1), L0_ffn_router_weight, L0_ffn_sh_gate, L0_ffn_sh_up, L0_ffn_sh_down, L0_ffn_r_gate, L0_ffn_r_up, L0_ffn_r_down)
    x = x + _L1_xattn_ref(_layernorm(x, axis=-1), ctx_2048, L1_xattn_Wq, L1_xattn_bq, L1_xattn_Wkv, L1_xattn_bkv, L1_xattn_Wp, L1_xattn_bp)
    x = x + _L1_attn_ref(_layernorm(x, axis=-1), L1_attn_w_qkv, L1_attn_b_qkv, L1_attn_w_out, L1_attn_b_out)
    x = x + _L1_ffn_ref(_layernorm(x, axis=-1), L1_ffn_gate_weight, L1_ffn_gate_lora_A, L1_ffn_gate_lora_B, L1_ffn_gate_up_proj, L1_ffn_down_proj, L1_ffn_gup_lora_A, L1_ffn_gup_lora_B, L1_ffn_down_lora_A, L1_ffn_down_lora_B)
    x = x + _L2_xattn_ref(_layernorm(x, axis=-1), ctx_2048, L2_xattn_ln_w, L2_xattn_ln_b, L2_xattn_wq, L2_xattn_wq_scale, L2_xattn_q_in_scale, L2_xattn_wqx, L2_xattn_wqx_scale, L2_xattn_qx_in_scale, L2_xattn_wk, L2_xattn_wk_scale, L2_xattn_k_in_scale, L2_xattn_wv, L2_xattn_wv_scale, L2_xattn_v_in_scale, L2_xattn_w_kv_x, L2_xattn_qln_w, L2_xattn_qln_b, L2_xattn_kln_w, L2_xattn_kln_b, L2_xattn_qxln_w, L2_xattn_qxln_b, L2_xattn_kxln_w, L2_xattn_kxln_b, L2_xattn_wproj, L2_xattn_proj_w_scale, L2_xattn_proj_in_scale, L2_xattn_proj_smooth)
    x = x + _L2_attn_ref(_layernorm(x, axis=-1), L2_attn_Wq, L2_attn_bq, L2_attn_Wk, L2_attn_bk, L2_attn_Wv, L2_attn_bv, L2_attn_Wo, L2_attn_bo)
    x = x + _L2_ffn_ref(_layernorm(x, axis=-1), L2_ffn_ln1_w, L2_ffn_ln2_w, L2_ffn_Wq, L2_ffn_Wk, L2_ffn_Wv, L2_ffn_Wo, L2_ffn_A, L2_ffn_B, L2_ffn_W_in_base, L2_ffn_W_up_base, L2_ffn_W_down)
    x = x + _L3_xattn_ref(_layernorm(x, axis=-1), mask_BxSx4224_bf0, ctx_2048, ctx_2048, L3_xattn_wq, L3_xattn_wk, L3_xattn_wv, L3_xattn_wo)
    x = x + _L3_attn_ref(_layernorm(x, axis=-1), L3_attn_Wq, L3_attn_bq, L3_attn_Wk, L3_attn_bk, L3_attn_Wv, L3_attn_bv, L3_attn_convq_w, L3_attn_convq_b, L3_attn_convk_w, L3_attn_convk_b, L3_attn_ssm_kernel, L3_attn_D_skip, L3_attn_Wo, L3_attn_bo)
    x = x + _L3_ffn_ref(_layernorm(x, axis=-1), L3_ffn_shared_w1, L3_ffn_shared_b1, L3_ffn_shared_w2, L3_ffn_shared_b2, L3_ffn_routed_w1, L3_ffn_routed_b1, L3_ffn_routed_w2, L3_ffn_routed_b2, L3_ffn_centroids, L3_ffn_bias)
    return x

_drawn_inputs = setup_inputs


def setup_inputs(seed=0):
    import zlib

    import numpy as np

    out = dict(_drawn_inputs(seed))
    spreads = {'L0_xattn_bq': (0.0, 0.1),
     'L0_xattn_bk': (0.0, 0.1),
     'L0_xattn_bv': (0.0, 0.1),
     'L0_xattn_bo': (0.0, 0.1),
     'L1_xattn_bq': (0.0, 0.1),
     'L1_xattn_bkv': (0.0, 0.1),
     'L1_xattn_bp': (0.0, 0.1),
     'L1_attn_b_qkv': (0.0, 0.1),
     'L1_attn_b_out': (0.0, 0.1),
     'L2_xattn_ln_w': (1.0, 0.2),
     'L2_xattn_ln_b': (0.0, 0.1),
     'L2_xattn_q_in_scale': (0.05000000074505806, 0.2),
     'L2_xattn_qx_in_scale': (0.05000000074505806, 0.2),
     'L2_xattn_k_in_scale': (0.05000000074505806, 0.2),
     'L2_xattn_v_in_scale': (0.05000000074505806, 0.2),
     'L2_xattn_qln_w': (1.0, 0.2),
     'L2_xattn_qln_b': (0.0, 0.1),
     'L2_xattn_kln_w': (1.0, 0.2),
     'L2_xattn_kln_b': (0.0, 0.1),
     'L2_xattn_qxln_w': (1.0, 0.2),
     'L2_xattn_qxln_b': (0.0, 0.1),
     'L2_xattn_kxln_w': (1.0, 0.2),
     'L2_xattn_kxln_b': (0.0, 0.1),
     'L2_xattn_proj_smooth': (0.05000000074505806, 0.2),
     'L2_ffn_ln1_w': (1.0, 0.2),
     'L2_ffn_ln2_w': (1.0, 0.2),
     'L3_attn_bq': (0.0, 0.1),
     'L3_attn_bk': (0.0, 0.1),
     'L3_attn_bv': (0.0, 0.1),
     'L3_attn_convq_b': (0.0, 0.1),
     'L3_attn_convk_b': (0.0, 0.1),
     'L3_attn_bo': (0.0, 0.1),
     'L3_ffn_shared_b1': (0.0, 0.1),
     'L3_ffn_shared_b2': (0.0, 0.1),
     'L3_ffn_routed_b1': (0.0, 0.1),
     'L3_ffn_routed_b2': (0.0, 0.1),
     'L3_ffn_bias': (0.0, 0.1)}
    factors = {}
    for name, (base, spread) in spreads.items():
        noise = np.random.default_rng([zlib.crc32(name.encode()), seed]).standard_normal(out[name].shape)
        drawn = base * np.exp(spread * noise) if base else spread * noise
        out[name] = jnp.asarray(drawn.astype(out[name].dtype))
    for name, factor in factors.items():
        out[name] = (out[name] * factor).astype(out[name].dtype)
    return out
```

```python
from contextlib import ExitStack

import numpy as np

import concourse.bass as bass
from concourse import mybir

ALU = mybir.AluOpType
ACT = mybir.ActivationFunctionType
AX = mybir.AxisListType.X
F32 = mybir.dt.float32
BF16 = mybir.dt.bfloat16
U32 = mybir.dt.uint32

T = 64
D = 256
KT = D // 128
SK = 6272
TILE = 112
NT = SK // TILE
SUB = 4
CHUNK = SUB * TILE
NC = SK // CHUNK
NH = 16
HD = 16
PAIRS = NH // 2
FD = 64
GROUPS = 8
GD = 128
NQ = 2 * GROUPS
NE = 18
FF = 176
FH = FF // 2
LN_EPS = 1e-5
RMS_EPS = 1e-6
NEG = -3.0e38
MAGIC = 12582912.0
LN255 = float(np.log(255.0))

SLOT = 2048
NSLOT = 4



def k_major(m):
    k, n = m.shape
    return m.reshape(k // 128, 128, n).transpose(1, 0, 2).reshape(128, -1)


def rows(m):
    out = np.zeros((128, m.shape[1]), np.float32)
    out[:m.shape[0]] = m
    return out


def head_diagonal(w):
    d, f = w.shape
    out = np.zeros((128, 128 // d * f), np.float32)
    for h in range(128 // d):
        out[h * d:(h + 1) * d, h * f:(h + 1) * f] = w
    return out


def expert_columns(a):
    e, r, i = a.shape
    out = np.zeros((i, e, e, r), np.float32)
    for n in range(e):
        out[:, n, n, :] = a[n].T
    return out.reshape(i, -1)


def column(v):
    return v.reshape(-1, 128).T


def by_head(w):
    return w.reshape(-1, NH, 3, HD).transpose(0, 2, 1, 3).reshape(-1, 3 * D)


def for_query_groups(w):
    return np.repeat(w.reshape(8, 1, 8, -1), 4, axis=1).reshape(D, -1)


PIECES = (
    [(-1, "pre", 2048), (-1, "pre_features", 512)]
    + [(0, "x0", 1536), (1, "a0", 2048)]
    + [(2, "f0_gate", 2048), (2, "f0_up", 2048), (2, "f0_routed", 784), (2, "f0_down", 2048)]
    + [(3, "x1", 1024), (4, "a1", 2048)]
    + [(5, "f1_gate", 280), (5, "f1_lora", 1792)] + [(5, f"f1_experts{n}", 1536) for n in range(4)]
    + [(6, "x2_q0", 2048), (6, "x2_q1", 2048), (6, "x2_k", 2048), (6, "x2_qx0", 2048), (6, "x2_qx1", 2048),
       (6, "x2_v", 2048), (6, "x2_kx", 2048), (6, "x2_vx", 2048)]
    + [(6, f"x2_proj{n}", 2048) for n in range(4)]
    + [(7, "a2", 2048), (8, "f2_attn", 2048), (8, "f2_mod", 1056), (8, "f2_gate", 2048), (8, "f2_up", 2048),
       (8, "f2_down", 2048)]
    + [(9, "x3", 2048), (10, "a3", 2048)]
    + [(11, "f3_gate", 288)] + [(11, f"f3_experts{n}", 1728) for n in range(9)]
)


def pack_piece(name, a):
    tr = lambda n: k_major(np.ascontiguousarray(a[n].T))
    cat = lambda *p: np.concatenate(p, 1)
    last = int(name[-1]) if name[-1].isdigit() else 0
    half = lambda n, i: k_major(np.ascontiguousarray(a[n][1024 * i:1024 * (i + 1)].T))
    if name == "pre":
        return cat(tr("L0_xattn_Wk"), k_major(cat(a["L0_xattn_Wv"].T, a["L1_xattn_Wkv"])))
    if name == "pre_features":
        return head_diagonal(a["L0_xattn_Wkf"].T)
    if name == "x0":
        return cat(tr("L0_xattn_Wq"), head_diagonal(a["L0_xattn_Wqf"].T), tr("L0_xattn_Wo"))
    if name == "a0":
        return cat(k_major(a["L0_attn_Wqkv"]), k_major(a["L0_attn_Wo"]))
    if name == "f0_gate":
        return tr("L0_ffn_sh_gate")
    if name == "f0_up":
        return tr("L0_ffn_sh_up")
    if name == "f0_down":
        return tr("L0_ffn_sh_down")
    if name == "f0_routed":
        return cat(tr("L0_ffn_r_gate"), tr("L0_ffn_r_up"), tr("L0_ffn_r_down"), tr("L0_ffn_router_weight"))
    if name == "x1":
        return cat(k_major(a["L1_xattn_Wq"]), k_major(a["L1_xattn_Wp"]))
    if name == "a1":
        return cat(k_major(by_head(a["L1_attn_w_qkv"])), k_major(a["L1_attn_w_out"]))
    if name == "f1_gate":
        return cat(tr("L1_ffn_gate_weight"), rows(a["L1_ffn_gate_lora_A"]), rows(a["L1_ffn_gate_lora_B"].T))
    if name == "f1_lora":
        gup_b = a["L1_ffn_gup_lora_B"].transpose(0, 2, 1).reshape(128, D)
        down_b = a["L1_ffn_down_lora_B"].transpose(0, 2, 1).reshape(128, D)
        return cat(k_major(a["L1_ffn_gup_lora_A"].reshape(128, D).T), gup_b, down_b,
                   expert_columns(a["L1_ffn_down_lora_A"]))
    if name.startswith("f1_experts"):
        two = [cat(k_major(a["L1_ffn_gate_up_proj"][e]), a["L1_ffn_down_proj"][e]) for e in (2 * last, 2 * last + 1)]
        return cat(*two)
    if name in ("x2_q0", "x2_q1"):
        return half("L2_xattn_wq", last)
    if name in ("x2_qx0", "x2_qx1"):
        return half("L2_xattn_wqx", last)
    if name == "x2_k":
        return tr("L2_xattn_wk")
    if name == "x2_v":
        return tr("L2_xattn_wv")
    if name == "x2_kx":
        return half("L2_xattn_w_kv_x", 0)
    if name == "x2_vx":
        return half("L2_xattn_w_kv_x", 1)
    if name.startswith("x2_proj"):
        return k_major(np.ascontiguousarray(a["L2_xattn_wproj"].T[1024 * last:1024 * (last + 1)]))
    if name == "a2":
        w = cat(a["L2_attn_Wq"].T, for_query_groups(a["L2_attn_Wk"]).T, for_query_groups(a["L2_attn_Wv"]).T)
        return cat(k_major(w), tr("L2_attn_Wo"))
    if name == "f2_attn":
        return cat(k_major(cat(a["L2_ffn_Wq"].T, a["L2_ffn_Wk"].T, a["L2_ffn_Wv"].T)), tr("L2_ffn_Wo"))
    if name == "f2_mod":
        return cat(k_major(a["L2_ffn_A"]), rows(a["L2_ffn_B"]))
    if name == "f2_gate":
        return tr("L2_ffn_W_in_base")
    if name == "f2_up":
        return tr("L2_ffn_W_up_base")
    if name == "f2_down":
        return tr("L2_ffn_W_down")
    if name == "x3":
        return cat(*(tr(f"L3_xattn_{w}") for w in ("wq", "wk", "wv", "wo")))
    if name == "a3":
        return cat(*(tr(f"L3_attn_{w}") for w in ("Wq", "Wk", "Wv", "Wo")))
    if name == "f3_gate":
        return cat(tr("L3_ffn_centroids"), rows(np.concatenate([a["L3_ffn_routed_b2"], a["L3_ffn_shared_b2"]], 0)))
    w1 = np.concatenate([a["L3_ffn_routed_w1"], a["L3_ffn_shared_w1"]], 0)
    w2 = np.concatenate([a["L3_ffn_routed_w2"], a["L3_ffn_shared_w2"]], 0)
    two = [cat(k_major(w1[e]), rows(w2[e].reshape(2, FH, D).transpose(1, 0, 2).reshape(FH, 2 * D)))
           for e in (2 * last, 2 * last + 1)]
    return cat(*two)


ROW_BIASES = (("bv0", D), ("bo0", D), ("a0_qkv", 3 * D), ("a0_out", D), ("kv1", 2 * D), ("q1", D), ("out1", D),
              ("a1_qkv", 3 * D), ("a1_out", D), ("a2_qkv", 3 * D), ("a2_out", D), ("a3_out", D), ("f3_bias", 16))


def pack_row_biases(a):
    r = {"bv0": a["L0_xattn_bv"], "bo0": a["L0_xattn_bo"], "a0_qkv": a["L0_attn_bqkv"], "a0_out": a["L0_attn_bo"],
         "kv1": a["L1_xattn_bkv"], "q1": a["L1_xattn_bq"], "out1": a["L1_xattn_bp"],
         "a1_qkv": by_head(a["L1_attn_b_qkv"][None])[0], "a1_out": a["L1_attn_b_out"],
         "a2_qkv": np.concatenate([a["L2_attn_bq"], for_query_groups(a["L2_attn_bk"]).ravel(),
                                   for_query_groups(a["L2_attn_bv"]).ravel()]),
         "a2_out": a["L2_attn_bo"], "a3_out": a["L3_attn_bo"], "f3_bias": a["L3_ffn_bias"]}
    row = np.concatenate([r[n] for n, _ in ROW_BIASES])
    return np.ascontiguousarray(np.broadcast_to(row, (128, row.size)))


COLUMNS = (("bk0", 2), ("bq0", 2), ("ln_w", 2), ("ln_b", 2), ("in_scale", 8), ("head_ln", 8), ("smooth", 32),
           ("scales", 6), ("ln1_w", 2), ("ln2_w", 2), ("a3_b", 6), ("conv_w", 12), ("conv_b", 4), ("d_skip", 2),
           ("f3_b1", 36))


def pack_columns(a):
    x2 = lambda n: a["L2_xattn_" + n]
    scalars = [x2(n) for n in ("wq_scale", "wk_scale", "wqx_scale", "wv_scale", "proj_in_scale", "proj_w_scale")]
    b1 = np.concatenate([a["L3_ffn_routed_b1"], a["L3_ffn_shared_b1"]], 0)
    c = {"bk0": column(a["L0_xattn_bk"]), "bq0": column(a["L0_xattn_bq"]),
         "ln_w": column(x2("ln_w")), "ln_b": column(x2("ln_b")),
         "in_scale": np.concatenate([column(x2(n + "_in_scale")) for n in ("q", "k", "qx", "v")], 1),
         "head_ln": np.stack([x2(n) for n in ("qln_w", "qln_b", "kln_w", "kln_b", "qxln_w", "qxln_b",
                                              "kxln_w", "kxln_b")], 1),
         "smooth": column(x2("proj_smooth")),
         "scales": np.broadcast_to(np.array([np.asarray(s).reshape(()) for s in scalars], np.float32), (128, 6)),
         "ln1_w": column(a["L2_ffn_ln1_w"]), "ln2_w": column(a["L2_ffn_ln2_w"]),
         "a3_b": np.concatenate([column(a["L3_attn_" + n]) for n in ("bq", "bk", "bv")], 1),
         "conv_w": np.concatenate([a[f"L3_attn_conv{n}_w"].reshape(2, 128, 3).transpose(1, 0, 2).reshape(128, 6)
                                   for n in "qk"], 1),
         "conv_b": np.concatenate([column(a[f"L3_attn_conv{n}_b"]) for n in "qk"], 1),
         "d_skip": column(a["L3_attn_D_skip"]),
         "f3_b1": rows(b1.reshape(18, 2, FH).transpose(2, 0, 1).reshape(FH, 36))}
    return np.ascontiguousarray(np.concatenate([c[n] for n, _ in COLUMNS], 1).astype(np.float32))


FREQ = T + 1
CONSTANTS = (("ident", 128), ("ones", 128), ("mean128", 128), ("tri", T), ("tri_10000", T), ("tri_neg", T),
             ("heads16", 8), ("heads8", 16), ("neg_half", 1), ("earlier8", 64), ("earlier16", 256),
             ("rope1", 8), ("rope2", 16), ("dft", 2 * FREQ), ("idft", 2 * T))


def rope_table(angle):
    cos, sin = np.cos(angle), np.sin(angle)
    return np.concatenate([cos, cos, -sin, sin], 1)


def constants():
    p, t = np.arange(128), np.arange(T)
    lower = (t[None, :] <= t[:, None]).astype(np.float32)
    f32 = np.float32
    inv1 = f32(1.0) / f32(10000.0) ** (np.arange(0, 4, 2, dtype=f32) / f32(4))
    inv2 = f32(10000.0) ** (f32(-2.0) * np.arange(4, dtype=f32) / f32(8))
    angle = 2 * np.pi * np.outer(p, np.arange(FREQ)) / (2 * T)
    weight = np.where((np.arange(FREQ) % T) == 0, 1.0, 2.0)[:, None] / (2 * T)
    back = 2 * np.pi * np.outer(np.arange(FREQ), t) / (2 * T)
    c = {"ident": np.eye(128), "ones": np.ones((128, 128)), "mean128": np.full((128, 128), 1 / 128),
         "tri": lower, "tri_10000": -10000.0 * (1 - lower), "tri_neg": NEG * (1 - lower),
         "heads16": (p[:, None] // 16 == np.arange(8)), "heads8": (p[:, None] // 8 == np.arange(16)),
         "neg_half": np.full((128, 1), -0.5),
         "earlier8": np.tile((np.arange(8)[None, :] < np.arange(8)[:, None]).reshape(1, -1), (T, 1)),
         "earlier16": np.tile((np.arange(16)[None, :] < np.arange(16)[:, None]).reshape(1, -1), (T, 1)),
         "rope1": rope_table((t[:, None].astype(f32) * inv1[None]).astype(f32)),
         "rope2": rope_table(((t[:, None].astype(f32) + 1) * inv2[None]).astype(f32)),
         "dft": np.concatenate([np.cos(angle), -np.sin(angle)], 1),
         "idft": np.concatenate([weight * np.cos(back), -weight * np.sin(back)], 1)}
    return np.concatenate([rows(np.asarray(c[n], np.float32)) for n, _ in CONSTANTS], 1)


def offsets(table):
    at, out = 0, {}
    for n, w in table:
        out[n] = (at, w)
        at += w
    return out, at


def laid_out(a):
    ctx = a["ctx_2048"][0]
    out = {
        "x": a["x"][0],
        "ctxT": ctx.T.reshape(KT, 128, SK).transpose(1, 0, 2),
        "ctxN": ctx.reshape(NT, TILE, D).transpose(1, 0, 2),
        "mask": a["mask_BxS2_ff1"][0].reshape(NT, TILE).T,
        "row_biases": pack_row_biases(a),
        "columns": pack_columns(a),
        "constants": constants(),
        "filterT": a["L3_attn_ssm_kernel"][:, :2 * T].T,
        "weights": np.concatenate([pack_piece(n, a) for _, n, _ in PIECES], 1),
    }
    return {n: np.ascontiguousarray(v, np.float32) for n, v in out.items()}



def perceiver(nc, io, first=0, last=11):
    constant_at, n_constants = offsets(CONSTANTS)
    column_at, n_columns = offsets(COLUMNS)
    row_bias_at, n_row_biases = offsets(ROW_BIASES)
    runs = lambda s: first <= s <= last
    sweep = runs(0) or runs(3)
    pieces = [p for p in PIECES if runs(p[0]) or (p[0] == -1 and sweep)]
    piece_no = {n: k for k, (_, n, _) in enumerate(pieces)}
    piece_from, at = {}, 0
    for s, n, w in PIECES:
        piece_from[n] = at
        at += w

    with ExitStack() as stack:
        def sb(name, shape, dt=F32):
            return stack.enter_context(nc.sbuf_tensor(name, shape, dt))

        sems = {}

        shared = {
            "queries_psum": (("x0_qT_psum", 0, 1), ("x1_q_psum", 3, 1), ("x2_heads_psum", 6, 1),
                             ("x3_qkv_psum", 9, 1), ("a3_qkv_psum", 10, 1)),
            "scores_psum": (("x1_scores_psum", 3, PAIRS * NC), ("x2_scores_psum", 6, GROUPS * NC),
                            ("x3_scores_psum", 9, NC + 1)),
            "scores": (("x1_scores", 3, PAIRS * NC), ("x2_scores", 6, GROUPS * NC), ("x3_scores", 9, NC + 1)),
            "exp_bias_ready": (("x1_bias_ready", 3, PAIRS), ("x2_bias_ready", 6, GROUPS), ("x3_bias_ready", 9, 1)),
            "exp": (("x1_exp", 3, PAIRS * NC), ("x2_exp", 6, GROUPS * NC), ("x3_exp", 9, NC + 1)),
            "probsT_psum": (("x1_probsT_psum", 3, PAIRS * NC), ("x2_probsT_psum", 6, GROUPS * NC),
                            ("x3_probsT_psum", 9, NC + 1)),
            "probsT_ready": (("x2_probsT_ready", 6, GROUPS * NC), ("x3_probsT", 9, NC + 1)),
            "weighed": (("x1_weighed", 3, PAIRS * NC), ("x2_weighed", 6, GROUPS * NC), ("x3_weighed", 9, NC + 1)),
            "tile_ready": (("x1_tile_ready", 3, PAIRS), ("x2_tile_ready", 6, GROUPS)),
            "logits_psum": (("f0_logits_psum", 2, 1), ("f1_logits_psum", 5, 1), ("f3_logits_psum", 11, 1)),
            "logits_shifted": (("f0_shifted", 2, 1), ("f1_shifted", 5, 1)),
            "logits_exp": (("f0_router_exp", 2, 1), ("f1_router_exp", 5, 1), ("f3_exp", 11, 1)),
            "hidden_psum": (("f0_hidden_psum", 2, 1), ("f1_gates_psum", 5, 4), ("f2_hidden_psum", 8, 1),
                            ("f3_hidden_psum", 11, NE)),
            "gates_exp": (("f0_exp", 2, 1), ("f1_exp", 5, 4), ("f2_exp", 8, 1)),
            "hidden": (("f0_hidden", 2, 1), ("f1_hidden", 5, 4), ("f2_hidden", 8, 1)),
            "expert_psum": (("f1_expert_psum", 5, 4), ("f3_expert_psum", 11, NE)),
            "expert_added": (("f1_added", 5, 4), ("f3_added", 11, NE)),
            "out_psum": (("f0_out_psum", 2, 1), ("f1_lora_psum", 5, 1), ("x2_out_psum", 6, 1), ("f2_out_psum", 8, 1),
                         ("a3_out_psum", 10, 1), ("f3_bias_psum", 11, 1)),
            "low_psum": (("f1_low_psum", 5, 1), ("f2_low_psum", 8, 1)),
            "narrowT_psum": (("f1_down_lowT_psum", 5, 1), ("f2_modT_psum", 8, 1), ("f3_gatesT_psum", 11, 1)),
            "narrowT_ready": (("f1_down_lowT_ready", 5, 1), ("f2_modT_ready", 8, 1), ("f3_gatesT_ready", 11, 1)),
            "x2_head_sums_psum": (("x2_mean_psum", 6, 1), ("x2_var_psum", 6, 1), ("x2_core_psum", 6, 1),
                                  ("x2_const_psum", 6, 1), ("x2_coreT_psum", 6, 1), ("x2_core_out_psum", 6, 1)),
            "x2_heads_step": (("x2_raw", 6, 3), ("x2_square", 6, 1), ("x2_std", 6, 1), ("x2_v_ready", 6, 1),
                              ("x2_core_exp", 6, 1), ("x2_coreT", 6, 1), ("x2_core_done", 6, 1)),
        }
        shared_by = {name: by for by, signals in shared.items() for name, _, _ in signals}

        def sem(name):
            name = shared_by.get(name, name)
            if name not in sems:
                sems[name] = stack.enter_context(nc.semaphore(name))
            return sems[name]

        def since(name, n):
            for other, s, times in shared[shared_by[name]]:
                if other == name:
                    return n
                if runs(s):
                    n = n + times

        consts = sb("consts", [128, n_constants])
        cols = sb("cols", [128, n_columns])
        row_biases = sb("row_biases_sb", [128, n_row_biases])
        filter_sb = sb("filter_sb", [128, D])
        ring = sb("ring", [128, NSLOT, SLOT])
        x = sb("x_sb", [T, D])
        xn = sb("xn", [T, D])
        xnT = sb("xnT", [128, KT, 2, T])
        stats = sb("stats", [T, 6])
        moments = sb("moments", [T, 2])
        var_eps = sb("var_eps", [T, 1])
        rstd = sb("rstd", [T, 1])
        keysT = sb("keysT", [128, KT, TILE + SK])
        vals = sb("vals", [128, NT, D])
        S = sb("S", [128, SK])
        mask_sb = sb("mask_sb", [TILE, NT])
        sweep_sums = sb("sweep_sums", [128, PAIRS, 34])
        value_step = sb("value_step", [128, D])
        ps = stack.enter_context(nc.psum_tensor("ps", [128, 8, 512], F32))
        psf = ps[:, :, :].rearrange("p b n -> p (b n)")

        def bank(b, n=512, p=128):
            return ps[0:p, b, 0:n]

        def C(name):
            a, w = constant_at[name]
            return consts[:, a:a + w]

        def V(name):
            a, w = column_at[name]
            return cols[:, a:a + w]

        def R(name, p=T):
            a, w = row_bias_at[name]
            return row_biases[0:p, a:a + w]

        def scratch(a, n, p=128):
            return S[0:p, a:a + n]

        def cut(ap, *dims):
            if len(dims) == 2:
                return ap.rearrange("p (a b) -> p a b", a=dims[0])
            return ap.rearrange("p (a b c) -> p a b c", a=dims[0], b=dims[1])

        def spread(ap, axis, n):
            shape = list(ap.shape)
            return ap.unsqueeze(axis).broadcast_to(shape[:axis] + [n] + shape[axis:])

        def W(name):
            n = piece_no[name]
            return ring[:, n % NSLOT, 0:pieces[n][2]]

        def weights_here(eng, name):
            n = piece_no[name]
            eng.wait_ge(sem(f"weights_in{n % NSLOT}"), 16 * (n // NSLOT + 1))

        weights_used = sem("weights_used")

        steps = {"dve": 0, "act": 0, "pool": 0}

        def link(eng, name, ins):
            steps[name] += 1
            ins.then_inc(sem(name + "_step"), 1)
            eng.wait_ge(sem(name + "_step"), steps[name])

        norms = [n for s in range(12) if runs(s) for n in ([s] if s not in (6, 8) else [s, s + 0.5])]
        norm_no = {n: k for k, n in enumerate(norms)}
        transposed = [n for n in norms if n not in (6, 8)]
        transposed_no = {n: k for k, n in enumerate(transposed)}

        def norm_vector(dve, n, src=x, out=xn, eps=LN_EPS, rms=False):
            k = norm_no[n]
            if rms:
                link(dve, "dve", dve.tensor_tensor_reduce(out[:, :], src[:, :], src[:, :], 1.0 / D, 0.0, ALU.mult,
                                                          ALU.add, moments[:, 1:2]))
            else:
                link(dve, "dve", dve.bn_stats(stats[:, :], src[:, :]))
                link(dve, "dve", dve.bn_aggr(moments[:, :], stats[:, :]))
            dve.tensor_scalar(var_eps[:, :], moments[:, 1:2], eps, None, ALU.add).then_inc(sem("var_ready"), 1)
            dve.wait_ge(sem("rstd_ready"), k + 1)
            if rms:
                ins = dve.tensor_scalar(out[:, :], src[:, :], rstd[:, 0:1], None, ALU.mult)
            else:
                ins = dve.tensor_scalar(out[:, :], src[:, :], moments[:, 0:1], rstd[:, 0:1], ALU.subtract, ALU.mult)
            ins.then_inc(sem("norm_ready"), 1)
            dve.wait_ge(sem("norm_ready"), k + 1)

        def norm_pool(pool, n):
            k = norm_no[n]
            if k == 0:
                pool.wait_ge(sem("constants_in"), 16)
            pool.wait_ge(sem("var_ready"), k + 1)
            pool.tensor_tensor(rstd[:, :], var_eps[:, :], C("neg_half")[0:T, :], ALU.pow).then_inc(sem("rstd_ready"), 1)

        def norm_tensor(pe, n, src=xn):
            if transposed_no[n] == 0:
                pe.wait_ge(sem("constants_in"), 16)
            pe.wait_ge(sem("norm_ready"), norm_no[n] + 1)
            for k in range(KT):
                ins = pe.transpose(ps[:, 7, k * T:(k + 1) * T], src[:, k * 128:(k + 1) * 128], C("ident")[0:T, 0:T])
            ins.then_inc(sem("normT_psum"), 1)

        def norm_scalar(act, n):
            act.wait_ge(sem("normT_psum"), transposed_no[n] + 1)
            act.copy(xnT[:, :, :, :], spread(cut(bank(7, KT * T), KT, T), 2, 2)).then_inc(sem("normT_ready"), 1)

        def normT_here(eng, n):
            eng.wait_ge(sem("normT_ready"), transposed_no[n] + 1)

        biased = [s for s in (0, 1, 3, 4, 7, 10) if runs(s)]

        def bias_pool(pool, s, name):
            pool.wait_ge(sem("norm_ready"), norm_no[s] + 1)
            pool.tensor_tensor(x[:, :], x[:, :], R(name), ALU.add).then_inc(sem("x_biased"), 1)

        def residual_vector(dve, s, product, ready):
            dve.wait_ge(*ready)
            if s in biased:
                dve.wait_ge(sem("x_biased"), biased.index(s) + 1)
            link(dve, "dve", dve.tensor_tensor(x[:, :], x[:, :], product, ALU.add))

        outs = [s for s in (0, 1, 3, 4, 7, 8, 9) if runs(s)]

        def out_tensor(pe, s, src, w, piece=None):
            k = outs.index(s)
            pe.wait_ge(sem("attended"), k + 1)
            for n in range(KT):
                ins = pe.transpose(ps[:, 7, n * T:(n + 1) * T], src[:, n * 128:(n + 1) * 128], C("ident")[0:T, 0:T])
            ins.then_inc(sem("attendedT_psum"), 1)
            pe.wait_ge(sem("attendedT_ready"), k + 1)
            for n in range(KT):
                ins = pe.matmul(bank(6, D, T), attendedT[:, n, :], w[:, n * D:(n + 1) * D], start=n == 0, stop=n == KT - 1)
            ins.then_inc(sem("projected"), 1)
            if piece:
                pe.wait_ge(sem("projected"), k + 1)
                pe.sem_inc(weights_used, 1)

        def out_scalar(act, s):
            k = outs.index(s)
            act.wait_ge(sem("attendedT_psum"), k + 1)
            act.copy(attendedT[:, :, :], cut(bank(7, KT * T), KT, T)).then_inc(sem("attendedT_ready"), 1)

        attendedT = sb("attendedT", [128, KT, T])
        attended = sb("attended", [T, D])

        MHA = {1: dict(piece="a0", bias="a0_qkv", heads=16, scale=0.25, rope=None, mask="tri_10000"),
               4: dict(piece="a1", bias="a1_qkv", heads=16, scale=1.0, rope=("rope1", 2), mask="tri_neg"),
               7: dict(piece="a2", bias="a2_qkv", heads=32, scale=float(1 / np.sqrt(8)), rope=("rope2", 4), mask="tri_neg"),
               8: dict(piece="f2_attn", bias=None, heads=16, scale=0.25, rope=None, mask="tri_neg")}
        mha_order = [s for s in MHA if runs(s)]
        m_qkv, m_tmp = scratch(0, 768), scratch(768, 512, T)
        m_qT = cut(scratch(1280, 2 * T), KT, T)
        m_v = scratch(5504, 256)
        m_max, m_den = scratch(5760, 32, T), scratch(5792, 32, T)

        def mha_views(s):
            h = MHA[s]["heads"]
            d = D // h
            g = h // KT
            keys = S[:, 1408:1408 + h * T].rearrange("p (k h t) -> p k h t", k=KT, h=g)
            scores = cut(scratch(3456, h * T, T), h, T)
            probsT = cut(scratch(1408, h // 2 * T), h // 2, T)
            values = cut(m_v, h // 2, 2 * d)
            return h, d, g, keys, scores, probsT, values

        def mha_tensor(pe, s, n):
            u = mha_order.index(s)
            h, d, g, keys, scores, probsT, values = mha_views(s)
            w = W(MHA[s]["piece"])
            weights_here(pe, MHA[s]["piece"])
            normT_here(pe, n)
            for a, b in ((0, 512), (512, 768)):
                for k in range(KT):
                    ins = pe.matmul(psf[:, a:b], xnT[:, k, :, :].rearrange("p a t -> p (a t)"),
                                    w[:, 768 * k + a:768 * k + b], start=k == 0, stop=k == KT - 1)
            ins.then_inc(sem("mha_qkv_psum"), 1)
            pe.wait_ge(sem("mha_qk_ready"), u + 1)
            for k in range(2 * KT):
                ins = pe.transpose(ps[:, 2, k * T:(k + 1) * T], m_qkv[0:T, k * 128:(k + 1) * 128], C("ident")[0:T, 0:T])
            ins.then_inc(sem("mha_qkT_psum"), 1)
            pe.wait_ge(sem("mha_keys_ready"), u + 1)
            for k in range(KT):
                flat = keys[:, k, :, :].rearrange("p h t -> p (h t)")
                for c in range(g * T // 512):
                    ins = pe.matmul(ps[0:T, 3 + k * (g * T // 512) + c, :], m_qT[:, k, :], flat[:, 512 * c:512 * c + 512],
                                    start=True, stop=True)
            ins.then_inc(sem("mha_scores_psum"), 1)
            pe.wait_ge(sem("mha_exp_ready"), u + 1)
            for j in range(h // 2):
                ins = pe.transpose(psf[:, j * T:(j + 1) * T], scores[:, 2 * j:2 * j + 2, :].rearrange("p h t -> p (h t)"),
                                   C("ident")[0:T, 0:T])
            ins.then_inc(sem("mha_probsT_psum"), 1)
            pe.wait_ge(sem("mha_probsT_ready"), u + 1)
            pe.wait_ge(sem("mha_values_ready"), u + 1)
            for j in range(h // 2):
                ins = pe.matmul(ps[0:T, 2, 2 * d * j:2 * d * (j + 1)], probsT[:, j, :], values[:, j, :], start=True, stop=True)
            ins.then_inc(sem("mha_out_psum"), 1)
            out_tensor(pe, s, attended, w[:, 1536:2048], MHA[s]["piece"])

        def mha_vector(dve, s):
            u = mha_order.index(s)
            m = MHA[s]
            h, d, g, keys, scores, probsT, values = mha_views(s)
            dve.wait_ge(sem("mha_qkv_psum"), u + 1)
            if m["bias"]:
                ins = dve.tensor_tensor(m_qkv, psf[:, 0:768], R(m["bias"], 128), ALU.add)
            else:
                ins = dve.tensor_copy(m_qkv, psf[:, 0:768])
            if m["rope"]:
                link(dve, "dve", ins)
                table, half = C(m["rope"][0])[0:T, :], m["rope"][1]
                r, n = 2 * half, 512 // d
                qk, tmp = cut(m_qkv[0:T, 0:512], n, d), cut(m_tmp[:, 0:n * r], n, r)
                cos, sin = spread(table[:, 0:r], 1, n), spread(table[:, r:2 * r], 1, n)
                link(dve, "dve", dve.tensor_tensor(tmp[:, :, 0:half], qk[:, :, half:r], sin[:, :, 0:half], ALU.mult))
                link(dve, "dve", dve.tensor_tensor(tmp[:, :, half:r], qk[:, :, 0:half], sin[:, :, half:r], ALU.mult))
                link(dve, "dve", dve.tensor_tensor(qk[:, :, 0:r], qk[:, :, 0:r], cos, ALU.mult))
                ins = dve.tensor_tensor(qk[:, :, 0:r], qk[:, :, 0:r], tmp, ALU.add)
            ins.then_inc(sem("mha_qk_ready"), 1)
            dve.wait_ge(sem("mha_qk_ready"), u + 1)
            dve.wait_ge(sem("mha_zeros"), u + 1)
            v = m_qkv[:, 512:768].rearrange("p (j e d) -> p j e d", e=2, d=d)
            dve.tensor_copy(values[0:T, :, 0:d], v[0:T, :, 0, :]).then_inc(sem("mha_half"), 1)
            dve.tensor_copy(values[T:128, :, d:2 * d], v[T:128, :, 1, :]).then_inc(sem("mha_values_ready"), 1)
            dve.wait_ge(sem("mha_qkT_psum"), u + 1)
            dve.tensor_scalar(m_qT, cut(bank(2, KT * T), KT, T), m["scale"], None, ALU.mult).then_inc(sem("mha_half"), 1)
            kT = cut(ps[:, 2, KT * T:2 * KT * T], KT, T)
            dve.tensor_tensor(keys, spread(kT, 2, g), spread(spread(C("heads%d" % d), 1, KT), 3, T), ALU.mult)\
               .then_inc(sem("mha_keys_ready"), 1)
            dve.wait_ge(sem("mha_scores_psum"), u + 1)
            raw = cut(psf[0:T, 3 * 512:3 * 512 + h * T], h, T)
            if m["mask"] == "tri_10000":
                link(dve, "dve", dve.tensor_tensor(scores, raw, spread(C("tri")[0:T, :], 1, h), ALU.mult))
                raw = scores
            link(dve, "dve", dve.tensor_tensor(scores, raw, spread(C(m["mask"])[0:T, :], 1, h), ALU.add))
            link(dve, "dve", dve.tensor_reduce(m_max[:, 0:h], scores, AX, ALU.max))
            dve.tensor_tensor(scores, scores, spread(m_max[:, 0:h], 2, T), ALU.subtract).then_inc(sem("mha_shifted"), 1)
            dve.wait_ge(sem("mha_exp_ready"), u + 1)
            link(dve, "dve", dve.tensor_reduce(m_den[:, 0:h], scores, AX, ALU.add))
            link(dve, "dve", dve.reciprocal(m_den[:, 0:h], m_den[:, 0:h]))
            dve.wait_ge(sem("mha_out_psum"), u + 1)
            dve.tensor_tensor(cut(attended[:, :], h, d), cut(bank(2, D, T), h, d), spread(m_den[:, 0:h], 2, d), ALU.mult)\
               .then_inc(sem("attended"), 1)

        def mha_scalar(act, s):
            u = mha_order.index(s)
            h, d, g, keys, scores, probsT, values = mha_views(s)
            act.wait_ge(sem("mha_shifted"), u + 1)
            act.activation(scores, scores, ACT.Exp).then_inc(sem("mha_exp_ready"), 1)
            act.wait_ge(sem("mha_probsT_psum"), u + 1)
            act.copy(probsT, cut(psf[:, 0:h // 2 * T], h // 2, T)).then_inc(sem("mha_probsT_ready"), 1)
            out_scalar(act, s)

        def mha_pool(pool, s):
            pool.wait_ge(sem("norm_ready"), norm_no[s if s != 8 else 8] + 1)
            pool.memset(m_v, 0.0).then_inc(sem("mha_zeros"), 1)

        def self_attention(s, bias):
            def pe_(pe):
                norm_tensor(pe, s)
                mha_tensor(pe, s, s)

            def dve_(dve):
                norm_vector(dve, s)
                mha_vector(dve, s)
                residual_vector(dve, s, bank(6, D, T), (sem("projected"), outs.index(s) + 1))

            def act_(act):
                norm_scalar(act, s)
                mha_scalar(act, s)

            def pool_(pool):
                norm_pool(pool, s)
                mha_pool(pool, s)
                bias_pool(pool, s, bias)
            return pe_, dve_, act_, pool_

        STAGES = {1: self_attention(1, "a0_out"), 4: self_attention(4, "a1_out"), 7: self_attention(7, "a2_out")}

        def rank_vector(dve, s, n, top, earlier, greater, equal, chosen):
            other, own = spread(s, 1, n), spread(s, 2, n)
            link(dve, "dve", dve.tensor_tensor(greater, other, own, ALU.is_gt))
            link(dve, "dve", dve.tensor_tensor(equal, other, own, ALU.is_equal))
            link(dve, "dve", dve.tensor_tensor(equal, equal, cut(earlier[0:T, :], n, n), ALU.mult))
            link(dve, "dve", dve.tensor_tensor(greater, greater, equal, ALU.add))
            link(dve, "dve", dve.tensor_reduce(chosen, greater, AX, ALU.add))
            link(dve, "dve", dve.tensor_scalar(chosen, chosen, top - 0.5, None, ALU.is_lt))

        f0_e = scratch(0, 9 * T)
        f0_h = cut(scratch(576, 9 * T), 9, T)
        f0_l = scratch(1152, 8, T)
        f0_max, f0_sum, f0_weight = scratch(1160, 1, T), scratch(1161, 1, T), scratch(1162, 1, T)
        f0_exp, f0_chosen = scratch(1168, 8, T), scratch(1176, 8, T)
        f0_greater, f0_equal = cut(scratch(1184, 64, T), 8, 8), cut(scratch(1248, 64, T), 8, 8)
        f0_g, f0_u = psf[:, 0:9 * T], psf[:, 1024:1024 + 9 * T]

        def f0_tensor(pe):
            norm_tensor(pe, 2)
            normT_here(pe, 2)
            for name, at in (("f0_gate", 0), ("f0_up", 1024)):
                weights_here(pe, name)
                for m in range(8):
                    for k in range(KT):
                        ins = pe.matmul(psf[:, at + m * T:at + (m + 1) * T], W(name)[:, k * 1024 + m * 128:k * 1024 + (m + 1) * 128],
                                        xnT[:, k, 0, :], start=k == 0, stop=k == KT - 1)
                ins.then_inc(weights_used, 1)
            weights_here(pe, "f0_routed")
            w = W("f0_routed")
            for i, at in ((0, 512), (1, 1024 + 512)):
                for k in range(KT):
                    ins = pe.matmul(psf[:, at:at + T], w[:, 256 * i + 128 * k:256 * i + 128 * k + 128], xnT[:, k, 0, :],
                                    start=k == 0, stop=k == KT - 1)
            ins.then_inc(sem("f0_hidden_psum"), 1)
            for k in range(KT):
                ins = pe.matmul(ps[0:T, 4, 0:8], xnT[:, k, 0, :], w[:, 768 + 8 * k:776 + 8 * k], start=k == 0, stop=k == KT - 1)
            ins.then_inc(sem("f0_logits_psum"), 1)
            pe.wait_ge(sem("f0_hidden"), since("f0_hidden", 1))
            pe.matmul(bank(5, D, T), f0_h[:, 8, :], w[:, 512:768], start=True, stop=True).then_inc(weights_used, 1)
            weights_here(pe, "f0_down")
            for m in range(8):
                ins = pe.matmul(bank(6, D, T), f0_h[:, m, :], W("f0_down")[:, m * D:(m + 1) * D], start=m == 0, stop=m == 7)
            ins.then_inc(sem("f0_out_psum"), 1)
            pe.wait_ge(sem("f0_out_psum"), since("f0_out_psum", 1))
            pe.sem_inc(weights_used, 1)

        def silu_vector(dve, e, g, u, h, done):
            link(dve, "dve", dve.tensor_scalar(e, e, 1.0, None, ALU.add))
            link(dve, "dve", dve.reciprocal(e, e))
            link(dve, "dve", dve.tensor_tensor(h, e, g, ALU.mult))
            dve.tensor_tensor(h, h, u, ALU.mult).then_inc(done, 1)

        def f0_vector(dve):
            norm_vector(dve, 2)
            dve.wait_ge(sem("f0_exp"), since("f0_exp", 1))
            silu_vector(dve, f0_e, f0_g, f0_u, f0_h.rearrange("p m t -> p (m t)"), sem("f0_hidden"))
            dve.wait_ge(sem("f0_logits_psum"), since("f0_logits_psum", 1))
            link(dve, "dve", dve.tensor_copy(f0_l, ps[0:T, 4, 0:8]))
            link(dve, "dve", dve.tensor_reduce(f0_max, f0_l, AX, ALU.max))
            dve.tensor_scalar(f0_exp, f0_l, f0_max, None, ALU.subtract).then_inc(sem("f0_shifted"), 1)
            rank_vector(dve, f0_l, 8, 2, C("earlier8"), f0_greater, f0_equal, f0_chosen)
            dve.wait_ge(sem("f0_router_exp"), since("f0_router_exp", 1))
            link(dve, "dve", dve.tensor_tensor(f0_exp, f0_exp, f0_chosen, ALU.mult))
            link(dve, "dve", dve.tensor_reduce(f0_sum, f0_exp, AX, ALU.add))
            link(dve, "dve", dve.reciprocal(f0_sum, f0_sum))
            link(dve, "dve", dve.tensor_scalar(f0_exp, f0_exp, f0_sum, None, ALU.mult))
            link(dve, "dve", dve.tensor_reduce(f0_weight, f0_exp, AX, ALU.add))
            dve.wait_ge(sem("f0_out_psum"), since("f0_out_psum", 1))
            link(dve, "dve", dve.tensor_tensor(x[:, :], x[:, :], bank(6, D, T), ALU.add))
            link(dve, "dve", dve.scalar_tensor_tensor(x[:, :], bank(5, D, T), f0_weight, x[:, :], ALU.mult, ALU.add))

        def f0_scalar(act):
            norm_scalar(act, 2)
            act.wait_ge(sem("f0_hidden_psum"), since("f0_hidden_psum", 1))
            act.activation(f0_e, f0_g, ACT.Exp, scale=-1.0).then_inc(sem("f0_exp"), 1)
            act.wait_ge(sem("f0_shifted"), since("f0_shifted", 1))
            act.activation(f0_exp, f0_exp, ACT.Exp).then_inc(sem("f0_router_exp"), 1)

        STAGES[2] = (f0_tensor, f0_vector, f0_scalar, lambda pool: norm_pool(pool, 2))

        f1_lora = scratch(0, 1792)
        f1_up_a, f1_up_b, f1_down_b, f1_down_a = f1_lora[:, 0:256], f1_lora[:, 256:512], f1_lora[:, 512:768], f1_lora[:, 768:1792]
        f1_low = cut(scratch(1792, 8 * T), 8, T)
        f1_e = cut(scratch(2304, 4 * T), 4, T)
        f1_h = cut(scratch(2560, 8 * T), 8, T)
        f1_router = cut(scratch(3072, 16), KT, 8)
        f1_p, f1_chosen = scratch(3088, 8, T), scratch(3096, 8, T)
        f1_max, f1_sum = scratch(3104, 1, T), scratch(3105, 1, T)
        f1_greater, f1_equal = cut(scratch(3112, 64, T), 8, 8), cut(scratch(3176, 64, T), 8, 8)
        f1_down_low = scratch(3240, 128, T)
        f1_down_lowT = scratch(3368, T)

        def f1_tensor(pe):
            weights_here(pe, "f1_gate")
            gate = W("f1_gate")
            for k in range(KT):
                ins = pe.matmul(ps[:, 0, 8 * k:8 * k + 8], gate[0:16, 16 + 128 * k:144 + 128 * k], gate[0:16, 272:280],
                                start=True, stop=True)
            ins.then_inc(sem("f1_delta_psum"), 1)
            norm_tensor(pe, 5)
            normT_here(pe, 5)
            pe.wait_ge(sem("f1_router_ready"), 1)
            pe.sem_inc(weights_used, 1)
            for k in range(KT):
                ins = pe.matmul(ps[0:T, 0, 32:40], xnT[:, k, 0, :], f1_router[:, k, :], start=k == 0, stop=k == KT - 1)
            ins.then_inc(sem("f1_logits_psum"), 1)
            pe.wait_ge(sem("f1_lora_copied"), 1)
            pe.sem_inc(weights_used, 1)
            for k in range(KT):
                ins = pe.matmul(ps[:, 1, 0:T], f1_up_a[:, 128 * k:128 * k + 128], xnT[:, k, 0, :], start=k == 0, stop=k == KT - 1)
            ins.then_inc(sem("f1_low_psum"), 1)
            pe.wait_ge(sem("f1_low_ready"), 1)

            def up(n):
                weights_here(pe, f"f1_experts{n}")
                if n >= 2:
                    pe.wait_ge(sem("f1_hidden"), since("f1_hidden", n - 1))
                for i in range(2):
                    for o in range(2):
                        out = ps[:, 2 + n % 2, (2 * o + i) * T:(2 * o + i + 1) * T]
                        for k in range(KT):
                            a = 768 * i + 256 * k + 128 * o
                            pe.matmul(out, W(f"f1_experts{n}")[:, a:a + 128], xnT[:, k, 0, :], start=k == 0, stop=False)
                        ins = pe.matmul(out, f1_up_b[:, 128 * o:128 * o + 128], f1_low[:, 2 * n + i, :], start=False, stop=True)
                ins.then_inc(sem("f1_gates_psum"), 1)

            def down(n):
                pe.wait_ge(sem("f1_hidden"), since("f1_hidden", n + 1))
                for i in range(2):
                    e = 2 * n + i
                    pe.matmul(ps[0:T, 1, 128:256], f1_h[:, e, :], f1_down_a[:, 128 * e:128 * e + 128], start=e == 0, stop=e == 7,
                              skip_group_check=True)
                if n >= 2:
                    pe.wait_ge(sem("f1_added"), since("f1_added", n - 1))
                for i in range(2):
                    a = 768 * i + 512
                    ins = pe.matmul(ps[0:T, 4 + n % 2, D * i:D * i + D], f1_h[:, 2 * n + i, :], W(f"f1_experts{n}")[:, a:a + D],
                                    start=True, stop=True)
                ins.then_inc(sem("f1_expert_psum"), 1)
                pe.wait_ge(sem("f1_expert_psum"), since("f1_expert_psum", n + 1))
                pe.sem_inc(weights_used, 1)

            up(0)
            for n in range(1, 4):
                up(n)
                down(n - 1)
            down(3)
            pe.wait_ge(sem("f1_down_low_ready"), 1)
            pe.transpose(ps[:, 0, 64:64 + T], f1_down_low, C("ident")[0:T, 0:T]).then_inc(sem("f1_down_lowT_psum"), 1)
            pe.wait_ge(sem("f1_down_lowT_ready"), since("f1_down_lowT_ready", 1))
            pe.matmul(bank(6, D, T), f1_down_lowT, f1_down_b, start=True, stop=True).then_inc(sem("f1_lora_psum"), 1)

        def f1_vector(dve):
            weights_here(dve, "f1_gate")
            dve.wait_ge(sem("f1_delta_psum"), 1)
            dve.scalar_tensor_tensor(f1_router, cut(ps[:, 0, 0:16], KT, 8), 2.0, cut(W("f1_gate")[:, 0:16], KT, 8),
                                     ALU.mult, ALU.add).then_inc(sem("f1_router_ready"), 1)
            norm_vector(dve, 5)
            dve.wait_ge(sem("f1_low_psum"), since("f1_low_psum", 1))
            dve.scalar_tensor_tensor(f1_low, spread(ps[:, 1, 0:T], 1, 8), 2.0, spread(C("heads16"), 2, T), ALU.mult, ALU.mult)\
               .then_inc(sem("f1_low_ready"), 1)
            dve.wait_ge(sem("f1_logits_psum"), since("f1_logits_psum", 1))
            link(dve, "dve", dve.tensor_reduce(f1_max, ps[0:T, 0, 32:40], AX, ALU.max))
            dve.tensor_scalar(f1_p, ps[0:T, 0, 32:40], f1_max, None, ALU.subtract).then_inc(sem("f1_shifted"), 1)
            dve.wait_ge(sem("f1_router_exp"), since("f1_router_exp", 1))
            link(dve, "dve", dve.tensor_reduce(f1_sum, f1_p, AX, ALU.add))
            link(dve, "dve", dve.reciprocal(f1_sum, f1_sum))
            link(dve, "dve", dve.tensor_scalar(f1_p, f1_p, f1_sum, None, ALU.mult))
            rank_vector(dve, f1_p, 8, 2, C("earlier8"), f1_greater, f1_equal, f1_chosen)
            link(dve, "dve", dve.tensor_tensor(f1_p, f1_p, f1_chosen, ALU.mult))
            link(dve, "dve", dve.tensor_reduce(f1_sum, f1_p, AX, ALU.add))
            link(dve, "dve", dve.reciprocal(f1_sum, f1_sum))
            link(dve, "dve", dve.tensor_scalar(f1_p, f1_p, f1_sum, None, ALU.mult))

            def add(n):
                dve.wait_ge(sem("f1_expert_psum"), since("f1_expert_psum", n + 1))
                for i in range(2):
                    ins = dve.scalar_tensor_tensor(x[:, :], ps[0:T, 4 + n % 2, D * i:D * i + D], f1_p[:, 2 * n + i:2 * n + i + 1],
                                                   x[:, :], ALU.mult, ALU.add)
                    if i == 0:
                        link(dve, "dve", ins)
                ins.then_inc(sem("f1_added"), 1)
                dve.wait_ge(sem("f1_added"), since("f1_added", n + 1))

            for n in range(4):
                dve.wait_ge(sem("f1_exp"), since("f1_exp", n + 1))
                b = ps[:, 2 + n % 2, :]
                silu_vector(dve, f1_e[:, 2 * (n % 2):2 * (n % 2) + 2, :], cut(b[:, 0:2 * T], 2, T), cut(b[:, 2 * T:4 * T], 2, T),
                            f1_h[:, 2 * n:2 * n + 2, :], sem("f1_hidden"))
                if n >= 1:
                    add(n - 1)
            dve.wait_ge(sem("f1_expert_psum"), since("f1_expert_psum", 4))
            dve.scalar_tensor_tensor(cut(f1_down_low, 8, 16), cut(ps[0:T, 1, 128:256], 8, 16), 2.0, spread(f1_p, 2, 16),
                                     ALU.mult, ALU.mult).then_inc(sem("f1_down_low_ready"), 1)
            add(3)
            residual_vector(dve, 5, bank(6, D, T), (sem("f1_lora_psum"), since("f1_lora_psum", 1)))

        def f1_scalar(act):
            norm_scalar(act, 5)
            act.wait_ge(sem("f1_shifted"), since("f1_shifted", 1))
            act.activation(f1_p, f1_p, ACT.Exp).then_inc(sem("f1_router_exp"), 1)
            for n in range(4):
                act.wait_ge(sem("f1_gates_psum"), since("f1_gates_psum", n + 1))
                act.activation(f1_e[:, 2 * (n % 2):2 * (n % 2) + 2, :], cut(ps[:, 2 + n % 2, 0:2 * T], 2, T), ACT.Exp, scale=-1.0)\
                   .then_inc(sem("f1_exp"), 1)
            act.wait_ge(sem("f1_down_lowT_psum"), since("f1_down_lowT_psum", 1))
            act.copy(f1_down_lowT, ps[:, 0, 64:64 + T]).then_inc(sem("f1_down_lowT_ready"), 1)

        def f1_pool(pool):
            norm_pool(pool, 5)
            weights_here(pool, "f1_lora")
            pool.tensor_copy(f1_lora, W("f1_lora")).then_inc(sem("f1_lora_copied"), 1)

        STAGES[5] = (f1_tensor, f1_vector, f1_scalar, f1_pool)

        xr = sb("xr", [T, D])
        f2_attn = scratch(0, D, T)
        f2_attnT = cut(scratch(256, KT * T), KT, T)
        f2_hT = cut(scratch(6016, KT * T), KT, T)
        f2_mod, f2_modT = scratch(384, 16, T), scratch(400, T, 16)
        f2_e, f2_h = scratch(512, 512), cut(scratch(1024, 512), 8, T)
        f2_g, f2_u = bank(3), bank(4)

        def f2_tensor(pe):
            norm_tensor(pe, 8.5, xr)
            mha_tensor(pe, 8, 8.5)
            pe.wait_ge(sem("f2_attn_ready"), 1)
            for n in range(KT):
                ins = pe.transpose(ps[:, 7, n * T:(n + 1) * T], f2_attn[:, n * 128:(n + 1) * 128], C("ident")[0:T, 0:T])
            ins.then_inc(sem("f2_attnT_psum"), 1)
            weights_here(pe, "f2_mod")
            w = W("f2_mod")
            pe.wait_ge(sem("f2_attnT_ready"), 1)
            for at, src in ((0, f2_attnT), (16, f2_hT)):
                for k in range(KT):
                    ins = pe.matmul(ps[0:T, 0, at:at + 16], src[:, k, :], w[:, 16 * k:16 * k + 16], start=k == 0, stop=k == KT - 1)
            ins.then_inc(sem("f2_low_psum"), 1)
            pe.wait_ge(sem("f2_mod_ready"), 1)
            pe.transpose(ps[0:16, 1, 0:T], f2_mod, C("ident")[0:T, 0:T]).then_inc(sem("f2_modT_psum"), 1)
            pe.wait_ge(sem("f2_modT_ready"), since("f2_modT_ready", 1))
            weights_here(pe, "f2_gate")
            for m in range(8):
                out = ps[:, 3, m * T:(m + 1) * T]
                ins = pe.matmul(out, w[0:16, 32 + m * 128:32 + (m + 1) * 128], f2_modT, start=True, stop=False)
                if m == 7:
                    ins.then_inc(weights_used, 1)
                for k in range(KT):
                    ins = pe.matmul(out, W("f2_gate")[:, k * 1024 + m * 128:k * 1024 + (m + 1) * 128], f2_hT[:, k, :],
                                    start=False, stop=k == KT - 1)
            ins.then_inc(weights_used, 1)
            weights_here(pe, "f2_up")
            for m in range(8):
                for k in range(KT):
                    ins = pe.matmul(ps[:, 4, m * T:(m + 1) * T], W("f2_up")[:, k * 1024 + m * 128:k * 1024 + (m + 1) * 128],
                                    f2_hT[:, k, :], start=k == 0, stop=k == KT - 1)
            ins.then_inc(sem("f2_hidden_psum"), 1)
            pe.wait_ge(sem("f2_hidden_psum"), since("f2_hidden_psum", 1))
            pe.sem_inc(weights_used, 1)
            pe.wait_ge(sem("f2_hidden"), since("f2_hidden", 1))
            weights_here(pe, "f2_down")
            for m in range(8):
                ins = pe.matmul(bank(6, D, T), f2_h[:, m, :], W("f2_down")[:, m * D:(m + 1) * D], start=m == 0, stop=m == 7)
            ins.then_inc(sem("f2_out_psum"), 1)
            pe.wait_ge(sem("f2_out_psum"), since("f2_out_psum", 1))
            pe.sem_inc(weights_used, 1)

        def f2_vector(dve):
            norm_vector(dve, 8)
            norm_vector(dve, 8.5, xn, xr, RMS_EPS, rms=True)
            mha_vector(dve, 8)
            dve.wait_ge(sem("projected"), outs.index(8) + 1)
            dve.tensor_copy(f2_attn, bank(6, D, T)).then_inc(sem("f2_attn_ready"), 1)
            dve.wait_ge(sem("f2_tanh"), 1)
            dve.scalar_tensor_tensor(f2_mod, f2_mod, 0.1, ps[0:T, 0, 16:32], ALU.mult, ALU.mult).then_inc(sem("f2_mod_ready"), 1)
            dve.wait_ge(sem("f2_exp"), since("f2_exp", 1))
            silu_vector(dve, f2_e, f2_g, f2_u, f2_h.rearrange("p m t -> p (m t)"), sem("f2_hidden"))
            link(dve, "dve", dve.tensor_tensor(x[:, :], x[:, :], xn[:, :], ALU.add))
            residual_vector(dve, 8, bank(6, D, T), (sem("f2_out_psum"), since("f2_out_psum", 1)))

        def f2_scalar(act):
            act.wait_ge(sem("normT_psum"), transposed_no[8.5] + 1)
            src = cut(bank(7, KT * T), KT, T)
            for k in range(KT):
                act.activation(f2_hT[:, k, :], src[:, k, :], ACT.Copy, scale=V("ln2_w")[:, k:k + 1]).then_inc(sem("f2_hT_half"), 1)
            for k in range(KT):
                ins = act.activation(xnT[:, k, :, :], spread(src[:, k, :], 1, 2), ACT.Copy, scale=V("ln1_w")[:, k:k + 1])
            ins.then_inc(sem("normT_ready"), 1)
            mha_scalar(act, 8)
            act.wait_ge(sem("f2_attnT_psum"), 1)
            act.copy(f2_attnT, src).then_inc(sem("f2_attnT_ready"), 1)
            act.wait_ge(sem("f2_low_psum"), since("f2_low_psum", 1))
            act.activation(f2_mod, ps[0:T, 0, 0:16], ACT.Tanh).then_inc(sem("f2_tanh"), 1)
            act.wait_ge(sem("f2_modT_psum"), since("f2_modT_psum", 1))
            act.copy(f2_modT, ps[0:16, 1, 0:T]).then_inc(sem("f2_modT_ready"), 1)
            act.wait_ge(sem("f2_hidden_psum"), since("f2_hidden_psum", 1))
            act.activation(f2_e, f2_g, ACT.Exp, scale=-1.0).then_inc(sem("f2_exp"), 1)

        def f2_pool(pool):
            norm_pool(pool, 8)
            norm_pool(pool, 8.5)
            mha_pool(pool, 8)

        STAGES[8] = (f2_tensor, f2_vector, f2_scalar, f2_pool)

        a3_padded = scratch(0, 4 * (T + 2)).rearrange("p (w k t) -> p w k t", w=2, k=KT)
        a3_v = cut(scratch(264, KT * T), KT, T)
        a3_conv = scratch(392, 4 * T).rearrange("p (w k t) -> p w k t", w=2, k=KT)
        a3_kv, a3_y = cut(scratch(648, KT * T), KT, T), cut(scratch(776, KT * T), KT, T)
        a3_kvN = scratch(904, D, T)
        a3_filter = cut(scratch(1160, 2 * D, FREQ), 2, D)
        a3_left, a3_right = cut(scratch(1672, 2 * D, FREQ), 2, D), cut(scratch(2184, 2 * D, FREQ), 2, D)

        def a3_tensor(pe):
            for i in range(2):
                ins = pe.matmul(ps[0:FREQ, 2, D * i:D * i + D], C("dft")[:, FREQ * i:FREQ * i + FREQ], filter_sb[:, :], start=True, stop=True)
            ins.then_inc(sem("a3_filter_psum"), 1)
            norm_tensor(pe, 10)
            normT_here(pe, 10)
            weights_here(pe, "a3")
            w = W("a3")
            for i in range(3):
                for o in range(KT):
                    for k in range(KT):
                        a = 512 * i + 256 * k + 128 * o
                        ins = pe.matmul(ps[:, 0, (2 * i + o) * T:(2 * i + o + 1) * T], w[:, a:a + 128], xnT[:, k, 0, :],
                                        start=k == 0, stop=k == KT - 1)
            ins.then_inc(sem("a3_qkv_psum"), 1)
            pe.wait_ge(sem("a3_kv_ready"), 1)
            for k in range(KT):
                ins = pe.transpose(ps[0:T, 1, 128 * k:128 * k + 128], a3_kv[:, k, :], C("ident"))
            ins.then_inc(sem("a3_kvN_psum"), 1)
            pe.wait_ge(sem("a3_kvN_ready"), 1)
            for i in range(2):
                ins = pe.matmul(ps[0:FREQ, 3, D * i:D * i + D], C("dft")[0:T, FREQ * i:FREQ * i + FREQ], a3_kvN, start=True, stop=True)
            ins.then_inc(sem("a3_spectrum_psum"), 1)
            pe.wait_ge(sem("a3_product_ready"), 1)
            for o in range(KT):
                for i in range(2):
                    ins = pe.matmul(ps[:, 4, o * T:(o + 1) * T], a3_left[:, i, 128 * o:128 * o + 128],
                                    C("idft")[0:FREQ, T * i:T * i + T], start=i == 0, stop=i == 1)
            ins.then_inc(sem("a3_long_psum"), 1)
            pe.wait_ge(sem("a3_y_ready"), 1)
            for k in range(KT):
                ins = pe.matmul(bank(6, D, T), a3_y[:, k, :], w[:, 1536 + D * k:1536 + D * k + D], start=k == 0, stop=k == KT - 1)
            ins.then_inc(sem("a3_out_psum"), 1)
            pe.wait_ge(sem("a3_out_psum"), since("a3_out_psum", 1))
            pe.sem_inc(weights_used, 1)

        def a3_vector(dve):
            norm_vector(dve, 10)
            dve.wait_ge(sem("a3_filter_psum"), 1)
            link(dve, "dve", dve.tensor_copy(a3_filter, cut(ps[0:FREQ, 2, :], 2, D)))
            dve.wait_ge(sem("a3_padding"), 1)
            dve.wait_ge(sem("a3_qkv_psum"), since("a3_qkv_psum", 1))
            for i in (1, 2, 0):
                for k in range(KT):
                    out = a3_padded[:, i, k, 2:] if i < 2 else a3_v[:, k, :]
                    ins = dve.tensor_scalar(out, ps[:, 0, (2 * i + k) * T:(2 * i + k + 1) * T], V("a3_b")[:, 2 * i + k:2 * i + k + 1],
                                            None, ALU.add)
            link(dve, "dve", ins)
            for i in (1, 0):
                for tap in range(3):
                    for k in range(KT):
                        src, out = a3_padded[:, i, k, tap:tap + T], a3_conv[:, i, k, :]
                        weight = V("conv_w")[:, 6 * i + 3 * k + tap:6 * i + 3 * k + tap + 1]
                        if tap == 0:
                            ins = dve.tensor_scalar(out, src, weight, V("conv_b")[:, 2 * i + k:2 * i + k + 1], ALU.mult, ALU.add)
                        else:
                            ins = dve.scalar_tensor_tensor(out, src, weight, out, ALU.mult, ALU.add)
                    link(dve, "dve", ins)
                if i == 1:
                    dve.tensor_tensor(a3_kv, a3_conv[:, 1, :, :], a3_v, ALU.mult).then_inc(sem("a3_kv_ready"), 1)
            dve.wait_ge(sem("a3_spectrum_psum"), 1)
            spectrum = cut(ps[0:FREQ, 3, :], 2, D)
            dve.tensor_tensor(a3_left, spectrum, spread(a3_filter[:, 0, :], 1, 2), ALU.mult).then_inc(sem("a3_part"), 1)
            dve.tensor_tensor(a3_right[:, 0, :], spectrum[:, 1, :], a3_filter[:, 1, :], ALU.mult).then_inc(sem("a3_part"), 1)
            dve.tensor_tensor(a3_right[:, 1, :], spectrum[:, 0, :], a3_filter[:, 1, :], ALU.mult).then_inc(sem("a3_part"), 1)
            dve.wait_ge(sem("a3_part"), 3)
            link(dve, "dve", dve.tensor_tensor(a3_left[:, 0, :], a3_left[:, 0, :], a3_right[:, 0, :], ALU.subtract))
            dve.tensor_tensor(a3_left[:, 1, :], a3_left[:, 1, :], a3_right[:, 1, :], ALU.add).then_inc(sem("a3_product_ready"), 1)
            dve.wait_ge(sem("a3_kv_ready"), 1)
            dve.wait_ge(sem("a3_long_psum"), 1)
            for k in range(KT):
                ins = dve.scalar_tensor_tensor(a3_y[:, k, :], a3_kv[:, k, :], V("d_skip")[:, k:k + 1], ps[:, 4, k * T:(k + 1) * T],
                                               ALU.mult, ALU.add)
            link(dve, "dve", ins)
            dve.tensor_tensor(a3_y, a3_y, a3_conv[:, 0, :, :], ALU.mult).then_inc(sem("a3_y_ready"), 1)
            residual_vector(dve, 10, bank(6, D, T), (sem("a3_out_psum"), since("a3_out_psum", 1)))

        def a3_scalar(act):
            norm_scalar(act, 10)
            act.wait_ge(sem("a3_kvN_psum"), 1)
            act.copy(a3_kvN, ps[0:T, 1, 0:D]).then_inc(sem("a3_kvN_ready"), 1)

        def a3_pool(pool):
            norm_pool(pool, 10)
            pool.wait_ge(sem("norm_ready"), norm_no[10] + 1)
            pool.memset(a3_padded[:, :, :, 0:2], 0.0).then_inc(sem("a3_padding"), 1)
            bias_pool(pool, 10, "a3_out")

        STAGES[10] = (a3_tensor, a3_vector, a3_scalar, a3_pool)

        f3_s, f3_chosen = scratch(0, 16, T), scratch(16, 16, T)
        f3_sum = scratch(32, 1, T)
        f3_gates, f3_gatesT = scratch(36, NE, T), scratch(64, T, NE)
        f3_greater, f3_equal = cut(scratch(128, 256, T), 16, 16), cut(scratch(384, 256, T), 16, 16)
        f3_h = [cut(scratch(640 + 128 * i, 2 * T, FH), 2, T) for i in range(2)]

        def f3_tensor(pe):
            norm_tensor(pe, 11)
            normT_here(pe, 11)
            weights_here(pe, "f3_gate")
            w = W("f3_gate")
            for k in range(KT):
                ins = pe.matmul(ps[0:T, 0, 0:16], xnT[:, k, 0, :], w[:, 16 * k:16 * k + 16], start=k == 0, stop=k == KT - 1)
            ins.then_inc(sem("f3_logits_psum"), 1)

            def hidden(e):
                weights_here(pe, f"f3_experts{e // 2}")
                if e >= 2:
                    pe.wait_ge(sem("f3_hidden"), e - 1)
                for i in range(2):
                    for k in range(KT):
                        a = 864 * (e % 2) + FF * k + FH * i
                        ins = pe.matmul(ps[0:FH, 1 + e % 2, T * i:T * i + T], W(f"f3_experts{e // 2}")[:, a:a + FH], xnT[:, k, 0, :],
                                        start=k == 0, stop=k == KT - 1)
                ins.then_inc(sem("f3_hidden_psum"), 1)

            def output(e):
                pe.wait_ge(sem("f3_hidden"), e + 1)
                if e >= 2:
                    pe.wait_ge(sem("f3_added"), since("f3_added", e - 1))
                for i in range(2):
                    a = 864 * (e % 2) + 2 * FF + D * i
                    ins = pe.matmul(ps[0:T, 3 + e % 2, 0:D], f3_h[e % 2][:, i, :], W(f"f3_experts{e // 2}")[0:FH, a:a + D],
                                    start=i == 0, stop=i == 1)
                ins.then_inc(sem("f3_expert_psum"), 1)
                if e % 2:
                    pe.wait_ge(sem("f3_expert_psum"), since("f3_expert_psum", e + 1))
                    pe.sem_inc(weights_used, 1)

            hidden(0)
            hidden(1)
            pe.wait_ge(sem("f3_gates_ready"), 1)
            pe.transpose(ps[0:NE, 0, 32:32 + T], f3_gates, C("ident")[0:T, 0:T]).then_inc(sem("f3_gatesT_psum"), 1)
            pe.wait_ge(sem("f3_gatesT_ready"), since("f3_gatesT_ready", 1))
            pe.matmul(bank(6, D, T), f3_gatesT, w[0:NE, 32:288], start=True, stop=True).then_inc(sem("f3_bias_psum"), 1)
            pe.wait_ge(sem("f3_bias_psum"), since("f3_bias_psum", 1))
            pe.sem_inc(weights_used, 1)
            for e in range(NE):
                output(e)
                if e + 2 < NE:
                    hidden(e + 2)

        def f3_vector(dve):
            norm_vector(dve, 11)
            dve.memset(f3_gates[:, 16:NE], 1.0).then_inc(sem("f3_ones"), 1)
            dve.wait_ge(sem("f3_exp"), since("f3_exp", 1))
            link(dve, "dve", dve.tensor_scalar(f3_s, f3_s, 1.0, None, ALU.add))
            link(dve, "dve", dve.reciprocal(f3_s, f3_s))
            link(dve, "dve", dve.tensor_tensor(f3_s, f3_s, R("f3_bias"), ALU.add))
            rank_vector(dve, f3_s, 16, 4, C("earlier16"), f3_greater, f3_equal, f3_chosen)
            link(dve, "dve", dve.tensor_tensor(f3_s, f3_s, f3_chosen, ALU.mult))
            link(dve, "dve", dve.tensor_reduce(f3_sum, f3_s, AX, ALU.add))
            link(dve, "dve", dve.tensor_scalar(f3_sum, f3_sum, 1e-8, None, ALU.max))
            link(dve, "dve", dve.reciprocal(f3_sum, f3_sum))
            dve.wait_ge(sem("f3_ones"), 1)
            dve.tensor_scalar(f3_gates[:, 0:16], f3_s, f3_sum, None, ALU.mult).then_inc(sem("f3_gates_ready"), 1)
            dve.wait_ge(sem("f3_gates_ready"), 1)
            link(dve, "dve", dve.tensor_tensor(x[:, :], x[:, :], xn[:, :], ALU.add))
            residual_vector(dve, 11, bank(6, D, T), (sem("f3_bias_psum"), since("f3_bias_psum", 1)))
            for e in range(NE):
                dve.wait_ge(sem("f3_expert_psum"), since("f3_expert_psum", e + 1))
                dve.scalar_tensor_tensor(x[:, :], ps[0:T, 3 + e % 2, 0:D], f3_gates[:, e:e + 1], x[:, :], ALU.mult, ALU.add)\
                   .then_inc(sem("f3_added"), 1)
                dve.wait_ge(sem("f3_added"), since("f3_added", e + 1))

        def f3_scalar(act):
            norm_scalar(act, 11)
            act.wait_ge(sem("f3_logits_psum"), since("f3_logits_psum", 1))
            act.activation(f3_s, ps[0:T, 0, 0:16], ACT.Exp, scale=-1.0).then_inc(sem("f3_exp"), 1)

            def relu(e):
                act.wait_ge(sem("f3_hidden_psum"), since("f3_hidden_psum", e + 1))
                if e >= 2:
                    act.wait_ge(sem("f3_expert_psum"), since("f3_expert_psum", e - 1))
                for i in range(2):
                    ins = act.activation(f3_h[e % 2][:, i, :], ps[0:FH, 1 + e % 2, T * i:T * i + T], ACT.Relu,
                                         bias=V("f3_b1")[0:FH, 2 * e + i:2 * e + i + 1])
                ins.then_inc(sem("f3_hidden"), 1)

            relu(0)
            relu(1)
            act.wait_ge(sem("f3_gatesT_psum"), since("f3_gatesT_psum", 1))
            act.copy(f3_gatesT, ps[0:NE, 0, 32:32 + T]).then_inc(sem("f3_gatesT_ready"), 1)
            for e in range(2, NE):
                relu(e)

        STAGES[11] = (f3_tensor, f3_vector, f3_scalar, lambda pool: norm_pool(pool, 11))

        ds = bass.ds

        sw_ctxT = [cut(scratch(896 * i, 896), KT, CHUNK) for i in range(2)]
        sw_kT = cut(scratch(1792, 896), KT, CHUNK)
        sw_features = [scratch(2688 + 1024 * i, 1024, TILE) for i in range(2)]
        sw_values = [cut(scratch(4736 + 264 * i, 264, TILE), PAIRS, 33) for i in range(2)]
        sw_key = scratch(5264, D, TILE)
        sw_key_out = [scratch(5520 + D * i, D, TILE) for i in range(2)]
        sw_absmax, sw_step, sw_inv = scratch(6032, 16, TILE), scratch(6048, 16, TILE), scratch(6064, 16, TILE)
        key_views = lambda: cut(sw_key, NH, HD)
        absmax_all = scratch(0, D)
        value_inv = scratch(256, D, TILE)
        value_tmp = [scratch(512 + 2048 * i, 2048, TILE) for i in range(2)]
        vals_flat = vals[:, :, :].rearrange("p n d -> p (n d)")
        vals_int = cut(vals_flat[0:TILE, 0:NT * D // 2].bitcast(BF16), NT, D)
        back = vals_flat[:, NT * D // 2:]

        def sweep_first_loads(sp):
            for i in range(2):
                sp.dma_start(sw_ctxT[i], io["ctxT"][:, :, CHUNK * i:CHUNK * i + CHUNK]).then_inc(sem(f"ctx_in{i}"), 16)
            sp.dma_start(mask_sb[:, :], io["mask"]).then_inc(sem("mask_in"), 16)

        def sweep_loads(sp):
            with sp.Fori(0, NC // 2 - 1) as i:
                for ph in range(2):
                    sp.wait_ge(sem("sw_proj_psum"), SUB * (i * 2 + ph + 1))
                    sp.dma_start(sw_ctxT[ph], io["ctxT"][:, :, ds((i * 2 + ph + 2) * CHUNK, CHUNK)]).then_inc(sem(f"ctx_in{ph}"), 16)

        def sweep_tensor(pe):
            weights_here(pe, "pre")
            weights_here(pe, "pre_features")
            w, wf = W("pre"), W("pre_features")
            sums = ps[:, 6, :]

            def add_sums(buf, start, stop):
                for j in range(PAIRS):
                    ins = pe.matmul(sums[:, 33 * j:33 * j + 33], sw_features[buf][:, 128 * j:128 * j + 128], sw_values[buf][:, j, :],
                                    start=start, stop=stop, skip_group_check=True)
                return ins

            def turn_keys(buf):
                for k in range(KT):
                    ins = pe.transpose(ps[:, 7, TILE * k:TILE * k + TILE], sw_key_out[buf][:, 128 * k:128 * k + 128],
                                       C("ident")[0:TILE, 0:TILE])
                ins.then_inc(sem("sw_keysT_psum"), 1)

            for free in ("sw_features_psum0", "sw_features_psum1", "sw_added", "sw_keysT_psum"):
                pe.sem_inc(sem(free), 1)
            pe.wait_ge(sem("sw_zeros"), 3)
            add_sums(1, True, False)
            with pe.Fori(0, NC // 2) as i:
                for ph in range(2):
                    it = i * 2 + ph
                    pe.wait_ge(sem(f"ctx_in{ph}"), (i + 1) * 16)
                    for o in range(KT):
                        pe.wait_ge(sem(f"sw_kT{o}"), it + 1)
                        for k in range(KT):
                            ins = pe.matmul(ps[:, o, 0:CHUNK], w[:, 256 * k + 128 * o:256 * k + 128 * o + 128], sw_ctxT[ph][:, k, :],
                                            start=k == 0, stop=k == KT - 1)
                        ins.then_inc(sem(f"sw_kT_psum{o}"), 1)
                    for s in range(SUB):
                        u = it * SUB + s
                        pe.wait_ge(sem("sw_proj_used"), u + 1)
                        for b, a, n in ((2, 0, 512), (3, 512, 256)):
                            for k in range(KT):
                                ins = pe.matmul(ps[0:TILE, b, 0:n], sw_ctxT[ph][:, k, TILE * s:TILE * s + TILE],
                                                w[:, 512 + 768 * k + a:512 + 768 * k + a + n], start=k == 0, stop=k == KT - 1)
                        ins.then_inc(sem("sw_proj_psum"), 1)
                        for g in range(KT):
                            if s == 0:
                                pe.wait_ge(sem(f"sw_kT{g}"), it + 2)
                            pe.wait_ge(sem(f"sw_features{g}"), u + 1)
                            pe.matmul(ps[0:TILE, 4 + g, :], sw_kT[:, g, TILE * s:TILE * s + TILE], wf, start=True, stop=True)\
                              .then_inc(sem(f"sw_features_psum{g}"), 1)
                        pe.wait_ge(sem("sw_values_ready"), u + 1)
                        add_sums((s + 1) % 2, False, False).then_inc(sem("sw_added"), 1)
                        pe.wait_ge(sem("sw_key_ready"), u + 1)
                        pe.wait_ge(sem("sw_keysT"), u + 1)
                        turn_keys((s + 1) % 2)
            for g in range(KT):
                pe.wait_ge(sem(f"sw_features{g}"), NT + 1)
            pe.wait_ge(sem("sw_values_ready"), NT + 1)
            add_sums(1, False, True).then_inc(sem("sw_added"), 1)
            pe.wait_ge(sem("sw_key_ready"), NT + 1)
            pe.wait_ge(sem("sw_keysT"), NT + 1)
            turn_keys(1)
            pe.wait_ge(sem("sw_features_psum1"), NT + 1)
            pe.sem_inc(weights_used, 2)
            pe.wait_ge(sem("sw_keysT"), NT + 2)

        def sweep_scalar(act):
            for free in ("sw_kT0", "sw_kT1", "sw_features0", "sw_features1", "sw_keysT"):
                act.sem_inc(sem(free), 1)
            with act.Fori(0, NC // 2) as i:
                for ph in range(2):
                    it = i * 2 + ph
                    for o in range(KT):
                        act.wait_ge(sem(f"sw_kT_psum{o}"), it + 1)
                        act.wait_ge(sem(f"sw_features_psum{o}"), it * SUB + 1)
                        act.activation(sw_kT[:, o, :], ps[:, o, 0:CHUNK], ACT.Identity, bias=V("bk0")[:, o:o + 1])\
                           .then_inc(sem(f"sw_kT{o}"), 1)
                    for s in range(SUB):
                        u = it * SUB + s
                        act.wait_ge(sem("sw_added"), u + 1)
                        for g in range(KT):
                            act.wait_ge(sem(f"sw_features_psum{g}"), u + 2)
                            act.activation(sw_features[s % 2][:, 512 * g:512 * g + 512], ps[0:TILE, 4 + g, :], ACT.Relu)\
                               .then_inc(sem(f"sw_features{g}"), 1)
                        act.wait_ge(sem("sw_keysT_psum"), u + 2)
                        act.copy(keysT[:, :, ds(u * TILE, TILE)], cut(ps[:, 7, 0:KT * TILE], KT, TILE)).then_inc(sem("sw_keysT"), 1)
            act.wait_ge(sem("sw_keysT_psum"), NT + 2)
            act.copy(keysT[:, :, NT * TILE:], cut(ps[:, 7, 0:KT * TILE], KT, TILE)).then_inc(sem("sw_keysT"), 1)

        def sweep_vector(dve):
            for free in ("sw_proj_used", "sw_values_ready", "sw_key_ready"):
                dve.sem_inc(sem(free), 1)
            dve.wait_ge(sem("mask_in"), 16)
            key = cut(sw_key, NH, HD)
            with dve.Fori(0, NC // 2) as i:
                for ph in range(2):
                    for s in range(SUB):
                        u = (i * 2 + ph) * SUB + s
                        at = [0]

                        def step(ins):
                            at[0] += 1
                            ins.then_inc(sem("sw_step"), 1)
                            dve.wait_ge(sem("sw_step"), u * 5 + at[0])

                        m = mask_sb[:, ds(u, 1)]
                        dve.wait_ge(sem("sw_proj_psum"), u + 1)
                        dve.wait_ge(sem("sw_added"), u + 1)
                        dve.tensor_scalar(sw_values[s % 2][:, :, 0:32], cut(ps[0:TILE, 2, 0:D], PAIRS, 32), m, None, ALU.mult)\
                           .then_inc(sem("sw_part"), 1)
                        dve.tensor_copy(sw_values[s % 2][:, :, 32:33], m.unsqueeze(1).broadcast_to([TILE, PAIRS, 1]))\
                           .then_inc(sem("sw_values_ready"), 1)
                        dve.wait_ge(sem("sw_key_ready"), u + 1)
                        dve.tensor_tensor(sw_key, ps[0:TILE, 2, D:2 * D], R("kv1", TILE)[:, 0:D], ALU.add).then_inc(sem("sw_part"), 1)
                        dve.tensor_tensor(vals[0:TILE, ds(u, 1), :].rearrange("p a d -> p (a d)"), ps[0:TILE, 3, 0:D],
                                          R("kv1", TILE)[:, D:2 * D], ALU.add).then_inc(sem("sw_proj_used"), 1)
                        dve.wait_ge(sem("sw_proj_used"), u + 2)
                        step(dve.tensor_reduce(sw_absmax, key, AX, ALU.max, apply_absolute_value=True))
                        step(dve.tensor_scalar(sw_step, sw_absmax, 1.0 / 127.0, 1e-8, ALU.mult, ALU.max))
                        step(dve.reciprocal(sw_inv, sw_step))
                        step(dve.tensor_tensor(key, key, spread(sw_inv, 2, HD), ALU.mult))
                        step(dve.tensor_scalar(sw_key, sw_key, MAGIC, MAGIC, ALU.add, ALU.subtract))
                        dve.wait_ge(sem("sw_keysT_psum"), u + 1)
                        dve.tensor_tensor(cut(sw_key_out[s % 2], NH, HD), key, spread(sw_step, 2, HD), ALU.mult)\
                           .then_inc(sem("sw_key_ready"), 1)
            dve.wait_ge(sem("sw_key_ready"), NT + 1)
            dve.wait_ge(sem("sw_sums_zeros"), 1)
            dve.wait_ge(sem("sw_added"), NT + 2)
            total = cut(ps[:, 6, 0:33 * PAIRS], PAIRS, 33)
            for e in range(2):
                half = slice(T * e, T * e + T)
                dve.tensor_copy(sweep_sums[half, :, HD * e:HD * e + HD], total[half, :, HD * e:HD * e + HD]).then_inc(sem("sw_sums"), 1)
                dve.tensor_copy(sweep_sums[half, :, 32 + e:33 + e], total[half, :, 32:33]).then_inc(sem("sw_sums"), 1)
            if not runs(3):
                return
            dve.wait_ge(sem("sw_sums"), 4)
            dve.wait_ge(sem("sw_keysT_psum"), NT + 2)
            dve.wait_ge(sem("sw_keysT"), NT + 2)
            link(dve, "dve", dve.memset(absmax_all, 0.0))
            dve.tensor_reduce(absmax_all[0:TILE, :], vals[0:TILE, :, :].rearrange("p n d -> p d n"), AX, ALU.max,
                              apply_absolute_value=True).then_inc(sem("sw_value_absmax"), 1)
            dve.wait_ge(sem("sw_value_max"), 1)
            link(dve, "dve", dve.tensor_scalar(value_step[:, :], value_step[:, :], 1.0 / 127.0, 1e-8, ALU.mult, ALU.max))
            link(dve, "dve", dve.reciprocal(value_inv, value_step[0:TILE, :]))
            for c in range(7):
                tmp = value_tmp[c % 2]
                link(dve, "dve", dve.tensor_tensor(cut(tmp, 8, D), vals[0:TILE, 8 * c:8 * c + 8, :], spread(value_inv, 1, 8), ALU.mult))
                link(dve, "dve", dve.tensor_scalar(vals_int[:, 8 * c:8 * c + 8, :].rearrange("p n d -> p (n d)"), tmp, MAGIC, MAGIC,
                                                   ALU.add, ALU.subtract))

        def sweep_pool(pool):
            pool.memset(sw_features[1], 0.0).then_inc(sem("sw_zeros"), 1)
            pool.memset(sw_values[1], 0.0).then_inc(sem("sw_zeros"), 1)
            pool.memset(sw_key_out[1], 0.0).then_inc(sem("sw_zeros"), 1)
            pool.memset(sweep_sums[:, :, :], 0.0).then_inc(sem("sw_sums_zeros"), 1)
            if runs(3):
                pool.wait_ge(sem("sw_value_absmax"), 1)
                pool.partition_all_reduce(value_step[:, :], absmax_all, 128, bass.bass_isa.ReduceOp.max).then_inc(sem("sw_value_max"), 1)

        SWEEP = (sweep_tensor, sweep_vector, sweep_scalar, sweep_pool)
        SWEEP_LOADS = (sweep_first_loads, sweep_loads)

        x0_qT = cut(scratch(0, KT * T), KT, T)
        x0_features = cut(scratch(128, PAIRS * T), PAIRS, T)
        x0_part = scratch(640, D, T).rearrange("p (j e d) -> p j e d", e=2, d=HD)
        x0_den = cut(scratch(896, NH, T), PAIRS, 2)

        def x0_tensor(pe):
            norm_tensor(pe, 0)
            normT_here(pe, 0)
            weights_here(pe, "x0")
            w = W("x0")
            for o in range(KT):
                for k in range(KT):
                    ins = pe.matmul(ps[:, 0, o * T:(o + 1) * T], w[:, 256 * k + 128 * o:256 * k + 128 * o + 128], xnT[:, k, 0, :],
                                    start=k == 0, stop=k == KT - 1)
            ins.then_inc(sem("x0_qT_psum"), 1)
            pe.wait_ge(sem("x0_qT"), 2)
            for j in range(PAIRS):
                ins = pe.matmul(ps[:, 1, j * T:(j + 1) * T], w[:, 512 + 128 * (j % 4):640 + 128 * (j % 4)], x0_qT[:, j // 4, :],
                                start=True, stop=True)
            ins.then_inc(sem("x0_features_psum"), 1)
            pe.wait_ge(sem("x0_features"), 1)
            pe.wait_ge(sem("sw_sums"), 4)
            for j in range(PAIRS):
                ins = pe.matmul(ps[0:T, 2, 34 * j:34 * j + 34], x0_features[:, j, :], sweep_sums[:, j, :], start=True, stop=True)
            ins.then_inc(sem("x0_sums_psum"), 1)
            out_tensor(pe, 0, attended, w[:, 1024:1536], "x0")

        def x0_vector(dve):
            norm_vector(dve, 0)
            dve.wait_ge(sem("x0_sums_psum"), 1)
            sums = cut(ps[0:T, 2, 0:34 * PAIRS], PAIRS, 34)
            link(dve, "dve", dve.tensor_copy(x0_den, sums[:, :, 32:34]))
            link(dve, "dve", dve.tensor_tensor(x0_part, R("bv0").rearrange("p (j e d) -> p j e d", e=2, d=HD), spread(x0_den, 3, HD), ALU.mult))
            link(dve, "dve", dve.tensor_tensor(x0_part, x0_part, sums[:, :, 0:32].rearrange("p j (e d) -> p j e d", e=2), ALU.add))
            link(dve, "dve", dve.tensor_scalar(x0_den, x0_den, 1e-8, None, ALU.add))
            link(dve, "dve", dve.reciprocal(x0_den, x0_den))
            dve.tensor_tensor(attended[:, :].rearrange("p (j e d) -> p j e d", e=2, d=HD), x0_part, spread(x0_den, 3, HD), ALU.mult)\
               .then_inc(sem("attended"), 1)
            residual_vector(dve, 0, bank(6, D, T), (sem("projected"), outs.index(0) + 1))

        def x0_scalar(act):
            norm_scalar(act, 0)
            act.wait_ge(sem("x0_qT_psum"), since("x0_qT_psum", 1))
            for o in range(KT):
                act.activation(x0_qT[:, o, :], ps[:, 0, o * T:(o + 1) * T], ACT.Identity, bias=V("bq0")[:, o:o + 1])\
                   .then_inc(sem("x0_qT"), 1)
            act.wait_ge(sem("x0_features_psum"), 1)
            act.activation(x0_features, cut(bank(1), PAIRS, T), ACT.Relu).then_inc(sem("x0_features"), 1)
            out_scalar(act, 0)

        def x0_pool(pool):
            norm_pool(pool, 0)
            bias_pool(pool, 0, "bo0")

        STAGES[0] = (x0_tensor, x0_vector, x0_scalar, x0_pool)

        x1_q = back[0:T, 0:D]
        x1_absmax, x1_step, x1_inv = back[0:T, 256:272], back[0:T, 272:288], back[0:T, 288:304]
        x1_row_step = back[:, 304:312]
        x1_queries = back[:, 320:1344]
        x1_tile_q, x1_tile_step = back[:, 1344:1472], back[:, 1472:1473]
        x1_max, x1_top, x1_bias = back[:, 1480:1494], back[:, 1494:1495], back[:, 1495:1496]
        x1_sum, x1_total = back[:, 1500:1514], back[:, 1514:1515]
        x1_ident = back[:, 1520:1584].bitcast(BF16)
        x1_probs = [back[:, 1600 + 224 * i:1824 + 224 * i].bitcast(BF16) for i in range(2)]
        x1_probsT = [cut(back[0:TILE, 2048 + 256 * i:2304 + 256 * i].bitcast(BF16), SUB, 128) for i in range(2)]
        x1_out = back[:, 2560:2816]
        keys_flat = keysT[:, :, :].rearrange("p k n -> p (k n)")

        def x1_tensor(pe):
            norm_tensor(pe, 3)
            normT_here(pe, 3)
            weights_here(pe, "x1")
            w = W("x1")
            for k in range(KT):
                ins = pe.matmul(bank(0, D, T), xnT[:, k, 0, :], w[:, D * k:D * k + D], start=k == 0, stop=k == KT - 1)
            ins.then_inc(sem("x1_q_psum"), 1)
            pe.wait_ge(sem("x1_q_ready"), 1)
            for k in range(KT):
                ins = pe.transpose(ps[:, 1, k * T:(k + 1) * T], x1_q[:, 128 * k:128 * k + 128], C("ident")[0:T, 0:T])
            ins.then_inc(sem("x1_qT_psum"), 1)
            pe.wait_ge(sem("x1_ident_ready"), 1)
            with pe.Fori(0, PAIRS) as j:
                j = pe.snap(j, max_val=PAIRS - 1)
                n0 = j * NC
                pe.wait_ge(sem("x1_tile_ready"), since("x1_tile_ready", j + 1))
                for c in range(NC):
                    if c >= 2:
                        pe.wait_ge(sem("x1_scores"), since("x1_scores", n0 + (c - 1)))
                    pe.matmul(ps[:, c % 2, 0:CHUNK], x1_tile_q, keys_flat[:, ds((j & 4) * ((TILE + SK) // 4) + (TILE + c * CHUNK), CHUNK)],
                              start=True, stop=True).then_inc(sem("x1_scores_psum"), 1)

                def turn(c):
                    pe.wait_ge(sem("x1_probs_ready"), n0 + (c + 1))
                    if c >= 2:
                        pe.wait_ge(sem("x1_probsT_ready"), n0 + (c - 1))
                    out = ps[0:TILE, 2 + c % 2, 0:256].bitcast(BF16)
                    for s in range(SUB):
                        ins = pe.transpose(out[:, 128 * s:128 * s + 128], x1_probs[c % 2][:, TILE * s:TILE * s + TILE], x1_ident)
                    ins.then_inc(sem("x1_probsT_psum"), 1)

                def weigh(c):
                    pe.wait_ge(sem("x1_probsT_ready"), n0 + (c + 1))
                    for s in range(SUB):
                        ins = pe.matmul(ps[:, 4, 0:32], x1_probsT[c % 2][:, s, :],
                                        vals_int[:, SUB * c + s, ds(j * 32, 32)], start=c == 0 and s == 0,
                                        stop=c == NC - 1 and s == SUB - 1)
                    ins.then_inc(sem("x1_weighed"), 1)

                turn(0)
                for c in range(1, NC):
                    turn(c)
                    weigh(c - 1)
                weigh(NC - 1)
            out_tensor(pe, 3, attended, w[:, 512:1024], "x1")

        def x1_vector(dve):
            norm_vector(dve, 3)
            q = cut(x1_q, NH, HD)
            dve.wait_ge(sem("x1_q_psum"), since("x1_q_psum", 1))
            link(dve, "dve", dve.tensor_tensor(x1_q, bank(0, D, T), R("q1"), ALU.add))
            link(dve, "dve", dve.tensor_scalar(x1_q, x1_q, 0.25, None, ALU.mult))
            link(dve, "dve", dve.tensor_reduce(x1_absmax, q, AX, ALU.max, apply_absolute_value=True))
            link(dve, "dve", dve.tensor_scalar(x1_step, x1_absmax, 1.0 / 127.0, 1e-8, ALU.mult, ALU.max))
            link(dve, "dve", dve.reciprocal(x1_inv, x1_step))
            link(dve, "dve", dve.tensor_tensor(q, q, spread(x1_inv, 2, HD), ALU.mult))
            dve.tensor_scalar(x1_q, x1_q, MAGIC, MAGIC, ALU.add, ALU.subtract).then_inc(sem("x1_q_ready"), 1)
            by_pair = cut(x1_step, PAIRS, 2)
            for e in range(2):
                link(dve, "dve", dve.tensor_copy(x1_row_step[T * e:T * e + T, :], by_pair[:, :, e]))
            dve.wait_ge(sem("x1_qT_psum"), 1)
            link(dve, "dve", dve.tensor_tensor(x1_queries.rearrange("p (k h t) -> p k h t", k=KT, h=8),
                                               spread(cut(bank(1, KT * T), KT, T), 2, 8),
                                               spread(spread(C("heads16"), 1, KT), 3, T), ALU.mult))
            with dve.Fori(0, PAIRS) as j:
                n0 = j * NC
                dve.tensor_copy(x1_tile_step, x1_row_step[:, ds(j, 1)]).then_inc(sem("x1_part"), 1)
                dve.tensor_copy(x1_tile_q, x1_queries[:, ds(j * 128, 128)]).then_inc(sem("x1_tile_ready"), 1)
                for c in range(NC):
                    dve.wait_ge(sem("x1_scores_psum"), since("x1_scores_psum", n0 + (c + 1)))
                    dve.tensor_scalar(S[:, CHUNK * c:CHUNK * c + CHUNK], ps[:, c % 2, 0:CHUNK], 1.0, NEG, ALU.mult, ALU.max,
                                      accum_out=x1_max[:, c:c + 1]).then_inc(sem("x1_scores"), 1)
                dve.wait_ge(sem("x1_scores"), since("x1_scores", n0 + NC))
                dve.tensor_reduce(x1_top, x1_max, AX, ALU.max).then_inc(sem("x1_small"), 1)
                dve.wait_ge(sem("x1_small"), j * 4 + 1)
                dve.tensor_tensor(x1_bias, x1_top, x1_tile_step, ALU.mult).then_inc(sem("x1_small"), 1)
                dve.wait_ge(sem("x1_small"), j * 4 + 2)
                dve.tensor_scalar(x1_bias, x1_bias, -1.0, LN255, ALU.mult, ALU.add).then_inc(sem("x1_bias_ready"), 1)
                for c in range(NC):
                    dve.wait_ge(sem("x1_exp"), since("x1_exp", n0 + (c + 1)))
                    if c >= 2:
                        dve.wait_ge(sem("x1_probsT_psum"), since("x1_probsT_psum", n0 + (c - 1)))
                    dve.tensor_scalar(x1_probs[c % 2], S[:, CHUNK * c:CHUNK * c + CHUNK], MAGIC, MAGIC, ALU.add, ALU.subtract)\
                       .then_inc(sem("x1_probs_ready"), 1)
                dve.tensor_reduce(x1_total, x1_sum, AX, ALU.add).then_inc(sem("x1_small"), 1)
                dve.wait_ge(sem("x1_small"), j * 4 + 3)
                dve.reciprocal(x1_total, x1_total).then_inc(sem("x1_small"), 1)
                dve.wait_ge(sem("x1_small"), j * 4 + 4)
                dve.wait_ge(sem("x1_weighed"), since("x1_weighed", n0 + NC))
                dve.tensor_scalar(x1_out[:, ds(j * 32, 32)], ps[:, 4, 0:32], x1_total, None, ALU.mult).then_inc(sem("x1_tile_done"), 1)
            dve.wait_ge(sem("x1_tile_done"), PAIRS)
            out, step = cut(attended[:, :], PAIRS, 32), cut(value_step[:, :], PAIRS, 32)
            by_tile = cut(x1_out, PAIRS, 32)
            for e in range(2):
                rows_, cols_ = slice(T * e, T * e + T), slice(HD * e, HD * e + HD)
                ins = dve.tensor_tensor(out[:, :, cols_], by_tile[rows_, :, cols_], step[rows_, :, cols_], ALU.mult)
            ins.then_inc(sem("attended"), 1)
            residual_vector(dve, 3, bank(6, D, T), (sem("projected"), outs.index(3) + 1))

        def x1_scalar(act):
            norm_scalar(act, 3)
            act.wait_ge(sem("x1_q_psum"), since("x1_q_psum", 1))
            act.copy(x1_ident, C("ident")).then_inc(sem("x1_ident_ready"), 1)
            with act.Fori(0, PAIRS) as j:
                act.wait_ge(sem("x1_bias_ready"), since("x1_bias_ready", j + 1))
                n0 = j * NC

                def copy(c):
                    act.wait_ge(sem("x1_probsT_psum"), since("x1_probsT_psum", n0 + (c + 1)))
                    if c >= 2:
                        act.wait_ge(sem("x1_weighed"), since("x1_weighed", n0 + (c - 1)))
                    act.copy(x1_probsT[c % 2], cut(ps[0:TILE, 2 + c % 2, 0:256].bitcast(BF16), SUB, 128))\
                       .then_inc(sem("x1_probsT_ready"), 1)

                for c in range(NC):
                    part = S[:, CHUNK * c:CHUNK * c + CHUNK]
                    act.activation(part, part, ACT.Exp, scale=x1_tile_step, bias=x1_bias, accum_out=x1_sum[:, c:c + 1])\
                       .then_inc(sem("x1_exp"), 1)
                    if c >= 2:
                        copy(c - 2)
                copy(NC - 2)
                copy(NC - 1)
            out_scalar(act, 3)

        def x1_pool(pool):
            norm_pool(pool, 3)
            bias_pool(pool, 3, "out1")

        STAGES[3] = (x1_tensor, x1_vector, x1_scalar, x1_pool)

        x2_cat = cut(row_biases[:, 0:2 * NQ * T], 2 * NQ, T)
        x2_queries = row_biases[:, 2048:3072]
        x2_wk = cut(row_biases[:, 3072:3328], KT, GD)
        x2_wv = cut(row_biases[:, 3328:3584], KT, GD)
        x2_keys = sb("x2_keys", [128, 2, CHUNK])
        x2_dev = sb("x2_dev", [128, 2, CHUNK])
        x2_probsT = sb("x2_probsT", [TILE, 2, 512])
        x2_mix = x2_dev[:, 0, 0:D]
        x2_mixT = cut(x2_dev[:, 1, 0:D], KT, 128)
        x2_q = sb("x2_q", [128, 128])
        x2_const, x2_tile_const = sb("x2_const", [128, GROUPS]), sb("x2_tile_const", [128, 1])
        x2_max, x2_sum, x2_small = sb("x2_max", [128, NC + 1]), sb("x2_sum", [128, NC + 1]), sb("x2_small", [128, 4])
        x2_eps = sb("x2_eps", [128, 1])
        SCALE2 = float(1 / np.sqrt(GD))
        x2_lnT = cut(scratch(5120, KT * T), KT, T)
        x2_in = scratch(5248, 512).rearrange("p (w k t) -> p w k t", w=4, k=KT)
        x2_inv_scale = scratch(5760, 8)
        x2_raw = scratch(0, 2560)
        x2_square = scratch(2560, 2560)
        x2_v = scratch(2560, 1024, T)
        x2_s, x2_stat = cut(scratch(3584, 512), GROUPS, T), scratch(5776, 16)
        x2_coreT = scratch(4096, 1024, T)
        x2_sq_cols = ((0, 1024, 0), (1024, 1536, 1), (1536, 2560, 2))
        x2_mean_w = scratch(5800, 16)
        ctxT = keysT[:, :, TILE:]
        ctxN = vals[0:TILE, :, :]

        def x2_tensor(pe):
            norm_tensor(pe, 6.5, xr)
            pe.wait_ge(sem("x2_in_ready"), 1)

            def heads(name, n0, at, which):
                weights_here(pe, name)
                for n in range(8):
                    for k in range(KT):
                        ins = pe.matmul(psf[:, at + (n0 + n) * T:at + (n0 + n + 1) * T], W(name)[:, 1024 * k + GD * n:1024 * k + GD * n + GD],
                                        x2_in[:, which, k, :], start=k == 0, stop=k == KT - 1)
                ins.then_inc(weights_used, 1)

            heads("x2_q0", 0, 0, 0)
            heads("x2_q1", 8, 0, 0)
            heads("x2_k", 0, 1024, 1)
            heads("x2_qx0", 0, 1536, 2)
            heads("x2_qx1", 8, 1536, 2)
            weights_here(pe, "x2_v")
            for c in range(2):
                for k in range(KT):
                    ins = pe.matmul(ps[0:T, 5 + c, :], x2_in[:, 3, k, :], W("x2_v")[:, 1024 * k + 512 * c:1024 * k + 512 * c + 512],
                                    start=k == 0, stop=k == KT - 1)
            ins.then_inc(sem("x2_heads_psum"), 1)
            pe.wait_ge(sem("x2_heads_psum"), since("x2_heads_psum", 1))
            pe.sem_inc(weights_used, 1)
            pe.wait_ge(sem("x2_raw"), since("x2_raw", 3))
            for c in range(5):
                ins = pe.matmul(bank(c), C("mean128"), x2_raw[:, 512 * c:512 * c + 512], start=True, stop=True)
            ins.then_inc(sem("x2_mean_psum"), 1)
            pe.wait_ge(sem("x2_square"), since("x2_square", 1))
            for c in range(5):
                ins = pe.matmul(bank(c), C("mean128"), x2_square[:, 512 * c:512 * c + 512], start=True, stop=True)
            ins.then_inc(sem("x2_var_psum"), 1)
            pe.wait_ge(sem("x2_normed"), 1)
            for g in range(GROUPS):
                ins = pe.matmul(ps[:, 7, T * g:T * g + T], x2_raw[:, 128 * g:128 * g + 128], x2_raw[:, 1024 + T * g:1024 + T * g + T],
                                start=True, stop=True)
            ins.then_inc(sem("x2_core_psum"), 1)
            for g in range(GROUPS):
                ins = pe.matmul(ps[:, 4, g:g + 1], x2_raw[:, 1536 + 128 * g:1536 + 128 * g + 128], V("head_ln")[:, 7:8], start=True, stop=True)
            ins.then_inc(sem("x2_const_psum"), 1)
            pe.wait_ge(sem("x2_core_probs"), 1)
            for g in range(GROUPS):
                ins = pe.transpose(psf[0:T, 128 * g:128 * g + 128], x2_s[:, g, :], C("ident"))
            ins.then_inc(sem("x2_coreT_psum"), 1)
            pe.wait_ge(sem("x2_coreT"), since("x2_coreT", 1))
            for g in range(GROUPS):
                ins = pe.matmul(psf[:, 1024 + 128 * g:1024 + 128 * g + 128], x2_v[:, GD * g:GD * g + GD], x2_coreT[:, 128 * g:128 * g + 128],
                                start=True, stop=True)
            ins.then_inc(sem("x2_core_out_psum"), 1)
            pe.wait_ge(sem("x2_core_done"), since("x2_core_done", 1))
            pe.wait_ge(sem("ctx_reloaded"), 32)
            with pe.Fori(0, GROUPS) as g:
                n0 = g * NC
                pe.wait_ge(sem("x2_tile_ready"), since("x2_tile_ready", g + 1))

                def keys(c):
                    if c >= 3:
                        pe.wait_ge(sem("x2_keys_ready"), n0 + (c - 2))
                    for k in range(KT):
                        ins = pe.matmul(ps[:, c % 3, 0:CHUNK], x2_wk[:, k, :], ctxT[:, k, CHUNK * c:CHUNK * c + CHUNK],
                                        start=k == 0, stop=k == KT - 1)
                    ins.then_inc(sem("x2_keys_psum"), 1)

                def variance(c):
                    pe.wait_ge(sem("x2_squared"), n0 + (c + 1))
                    if c >= 1:
                        pe.wait_ge(sem("x2_deviation"), n0 + c)
                    pe.matmul(ps[:, 3, 0:CHUNK], C("mean128"), x2_dev[:, c % 2, :], start=True, stop=True).then_inc(sem("x2_keys_var"), 1)

                def scores(c):
                    pe.wait_ge(sem("x2_keys_ready"), n0 + (c + 1))
                    if c >= 1:
                        pe.wait_ge(sem("x2_scores"), since("x2_scores", n0 + c))
                    pe.matmul(ps[:, 4, 0:CHUNK], x2_q[:, :], x2_keys[:, c % 2, :], start=True, stop=True).then_inc(sem("x2_scores_psum"), 1)

                for c in range(NC + 2):
                    if c < NC:
                        keys(c)
                    if 1 <= c <= NC:
                        variance(c - 1)
                    if c >= 2:
                        scores(c - 2)

                def turn(c):
                    pe.wait_ge(sem("x2_exp"), since("x2_exp", n0 + (c + 1)))
                    if c >= 2:
                        pe.wait_ge(sem("x2_probsT_ready"), since("x2_probsT_ready", n0 + (c - 1)))
                    for s in range(SUB):
                        a = CHUNK * c + TILE * s
                        ins = pe.transpose(ps[0:TILE, 5 + c % 2, 128 * s:128 * s + 128], S[:, a:a + TILE], C("ident"))
                    ins.then_inc(sem("x2_probsT_psum"), 1)

                def weigh(c):
                    pe.wait_ge(sem("x2_probsT_ready"), since("x2_probsT_ready", n0 + (c + 1)))
                    for s in range(SUB):
                        ins = pe.matmul(bank(7, D), x2_probsT[:, c % 2, 128 * s:128 * s + 128], ctxN[:, SUB * c + s, :],
                                        start=c == 0 and s == 0, stop=c == NC - 1 and s == SUB - 1)
                    ins.then_inc(sem("x2_weighed"), 1)

                turn(0)
                for c in range(1, NC):
                    turn(c)
                    weigh(c - 1)
                weigh(NC - 1)
                pe.wait_ge(sem("x2_mix"), g + 1)
                for k in range(KT):
                    ins = pe.transpose(ps[:, 5, 128 * k:128 * k + 128], x2_mix[:, 128 * k:128 * k + 128], C("ident"))
                ins.then_inc(sem("x2_mixT_psum"), 1)
                pe.wait_ge(sem("x2_mixT"), g + 1)
                for k in range(KT):
                    ins = pe.matmul(ps[:, 6, 0:128], x2_wv[:, k, :], x2_mixT[:, k, :], start=k == 0, stop=k == KT - 1)
                ins.then_inc(sem("x2_cross_psum"), 1)
            pe.wait_ge(sem("x2_cross_done"), GROUPS)
            pe.sem_inc(weights_used, 2)
            pe.wait_ge(sem("x2_cat_ready"), 1)
            for n in range(2 * NQ):
                name = f"x2_proj{n // 8}"
                if n % 8 == 0:
                    weights_here(pe, name)
                ins = pe.matmul(bank(0, D, T), x2_cat[:, n, :], W(name)[:, D * (n % 8):D * (n % 8) + D], start=n == 0, stop=n == 2 * NQ - 1)
                if n % 8 == 7 and n < 2 * NQ - 1:
                    ins.then_inc(weights_used, 1)
            ins.then_inc(sem("x2_out_psum"), 1)
            pe.wait_ge(sem("x2_out_psum"), since("x2_out_psum", 1))
            pe.sem_inc(weights_used, 1)

        def x2_vector(dve):
            norm_vector(dve, 6)
            norm_vector(dve, 6.5, xn, xr)
            link(dve, "dve", dve.memset(x2_eps[:, :], LN_EPS))
            link(dve, "dve", dve.reciprocal(x2_inv_scale, V("in_scale")))
            normT_here(dve, 6.5)
            by_use = lambda v: cut(v, 4, KT)
            flat_in = scratch(5248, 512)
            y = spread(x2_lnT, 1, 4)
            wide = scratch(0, 512).rearrange("p (w k t) -> p w k t", w=4, k=KT)
            link(dve, "dve", dve.tensor_tensor(wide, y, spread(by_use(x2_inv_scale), 3, T), ALU.mult))
            round_vector(dve, 512, 0, flat_in)
            dve.tensor_tensor(x2_in, x2_in, spread(by_use(V("in_scale")), 3, T), ALU.mult).then_inc(sem("x2_in_ready"), 1)
            dve.wait_ge(sem("x2_mean_psum"), since("x2_mean_psum", 1))
            dve.tensor_tensor(x2_raw, x2_raw, psf[:, 0:2560], ALU.subtract).then_inc(sem("x2_centred"), 1)
            weights_here(dve, "x2_kx")
            wk = cut(W("x2_kx"), KT * GROUPS, GD)
            link(dve, "dve", dve.tensor_reduce(x2_mean_w, wk, AX, ALU.add))
            link(dve, "dve", dve.tensor_scalar(x2_mean_w, x2_mean_w, 1.0 / GD, None, ALU.mult))
            link(dve, "dve", dve.tensor_tensor(wk, wk, spread(x2_mean_w, 2, GD), ALU.subtract))
            dve.wait_ge(sem("x2_std"), since("x2_std", 1))
            link(dve, "dve", dve.reciprocal(x2_square, x2_square))
            link(dve, "dve", dve.tensor_tensor(x2_raw, x2_raw, x2_square, ALU.mult))
            for a, b, i in x2_sq_cols:
                ins = dve.tensor_scalar(x2_raw[:, a:b], x2_raw[:, a:b], V("head_ln")[:, 2 * i:2 * i + 1], V("head_ln")[:, 2 * i + 1:2 * i + 2],
                                        ALU.mult, ALU.add)
            ins.then_inc(sem("x2_normed"), 1)
            dve.wait_ge(sem("x2_normed"), 1)
            link(dve, "dve", dve.tensor_scalar(x2_queries, x2_raw[:, 1536:2560], V("head_ln")[:, 6:7], None, ALU.mult))
            dve.wait_ge(sem("x2_const_psum"), since("x2_const_psum", 1))
            link(dve, "dve", dve.tensor_copy(x2_const[:, :], ps[:, 4, 0:GROUPS]))
            dve.wait_ge(sem("x2_core_psum"), since("x2_core_psum", 1))
            raw = cut(bank(7), GROUPS, T)
            link(dve, "dve", dve.tensor_reduce(x2_stat[:, 0:8], raw, AX, ALU.max))
            dve.tensor_tensor(x2_s, raw, spread(x2_stat[:, 0:8], 2, T), ALU.subtract).then_inc(sem("x2_core_shifted"), 1)
            dve.wait_ge(sem("x2_core_exp"), since("x2_core_exp", 1))
            link(dve, "dve", dve.tensor_reduce(x2_stat[:, 8:16], x2_s, AX, ALU.add))
            link(dve, "dve", dve.reciprocal(x2_stat[:, 8:16], x2_stat[:, 8:16]))
            dve.tensor_tensor(x2_s, x2_s, spread(x2_stat[:, 8:16], 2, T), ALU.mult).then_inc(sem("x2_core_probs"), 1)
            weights_here(dve, "x2_vx")
            dve.wait_ge(sem("x2_core_done"), since("x2_core_done", 1))
            wks, wvs = cut(W("x2_kx"), KT, 1024), cut(W("x2_vx"), KT, 1024)
            with dve.Fori(0, GROUPS) as g:
                g = dve.snap(g, max_val=GROUPS - 1)
                n0 = g * NC
                dve.tensor_copy(x2_wk, wks[:, :, ds(g * GD, GD)]).then_inc(sem("x2_part"), 1)
                dve.tensor_copy(x2_wv, wvs[:, :, ds(g * GD, GD)]).then_inc(sem("x2_part"), 1)
                dve.tensor_copy(x2_tile_const[:, :], x2_const[:, ds(g, 1)]).then_inc(sem("x2_tile_const_ready"), 1)
                dve.tensor_copy(x2_q[:, :], x2_queries[:, ds(g * 128, 128)]).then_inc(sem("x2_tile_ready"), 1)
                dve.wait_ge(sem("x2_tile_ready"), since("x2_tile_ready", g + 1))

                def normalise(c):
                    dve.wait_ge(sem("x2_deviation"), n0 + (c + 1))
                    dve.reciprocal(x2_dev[:, c % 2, :], x2_dev[:, c % 2, :]).then_inc(sem("x2_inverse"), 1)
                    dve.wait_ge(sem("x2_inverse"), n0 + (c + 1))
                    if c >= 2:
                        dve.wait_ge(sem("x2_scores_psum"), since("x2_scores_psum", n0 + (c - 1)))
                    dve.tensor_tensor(x2_keys[:, c % 2, :], ps[:, c % 3, 0:CHUNK], x2_dev[:, c % 2, :], ALU.mult)\
                       .then_inc(sem("x2_keys_ready"), 1)

                def score(c):
                    dve.wait_ge(sem("x2_scores_psum"), since("x2_scores_psum", n0 + (c + 1)))
                    dve.tensor_scalar(S[:, CHUNK * c:CHUNK * c + CHUNK], ps[:, 4, 0:CHUNK], x2_tile_const[:, 0:1], NEG, ALU.add, ALU.max,
                                      accum_out=x2_max[:, c:c + 1]).then_inc(sem("x2_scores"), 1)

                for c in range(NC + 1):
                    if c < NC:
                        normalise(c)
                    if c >= 1:
                        score(c - 1)
                dve.wait_ge(sem("x2_scores"), since("x2_scores", n0 + NC))
                dve.tensor_reduce(x2_small[:, 0:1], x2_max[:, 0:NC], AX, ALU.max).then_inc(sem("x2_step"), 1)
                dve.wait_ge(sem("x2_step"), g * 3 + 1)
                dve.tensor_scalar(x2_small[:, 1:2], x2_small[:, 0:1], -SCALE2, None, ALU.mult).then_inc(sem("x2_bias_ready"), 1)
                for c in range(NC):
                    dve.wait_ge(sem("x2_probsT_psum"), since("x2_probsT_psum", n0 + (c + 1)))
                    if c >= 2:
                        dve.wait_ge(sem("x2_weighed"), since("x2_weighed", n0 + (c - 1)))
                    dve.tensor_copy(x2_probsT[:, c % 2, :], ps[0:TILE, 5 + c % 2, :]).then_inc(sem("x2_probsT_ready"), 1)
                dve.tensor_reduce(x2_small[:, 2:3], x2_sum[:, 0:NC], AX, ALU.add).then_inc(sem("x2_step"), 1)
                dve.wait_ge(sem("x2_step"), g * 3 + 2)
                dve.reciprocal(x2_small[:, 3:4], x2_small[:, 2:3]).then_inc(sem("x2_step"), 1)
                dve.wait_ge(sem("x2_step"), g * 3 + 3)
                dve.wait_ge(sem("x2_weighed"), since("x2_weighed", n0 + NC))
                dve.tensor_scalar(x2_mix, bank(7, D), x2_small[:, 3:4], None, ALU.mult).then_inc(sem("x2_mix"), 1)
                dve.wait_ge(sem("x2_cross_done"), g + 1)
            link(dve, "dve", dve.reciprocal(scratch(0, 32), V("smooth")))
            wide = cut(scratch(64, 2048), 32, T)
            link(dve, "dve", dve.tensor_tensor(wide, x2_cat, spread(scratch(0, 32), 2, T), ALU.mult))
            last = round_vector(dve, 2048, 64, row_biases[:, 0:2048], wait=False)
            last.then_inc(sem("x2_cat_ready"), 1)
            link(dve, "dve", dve.tensor_tensor(x2_small[0:T, 0:1], V("scales")[0:T, 4:5], V("scales")[0:T, 5:6], ALU.mult))
            dve.wait_ge(sem("x2_out_psum"), since("x2_out_psum", 1))
            link(dve, "dve", dve.scalar_tensor_tensor(x[:, :], bank(0, D, T), x2_small[0:T, 0:1], x[:, :], ALU.mult, ALU.add))

        def round_vector(dve, n, at, out, wait=True):
            wide, narrow = scratch(at, n), scratch(at + n, n // 2).bitcast(BF16)
            power = scratch(at + n + n // 2, n // 2).bitcast(BF16)
            u16 = mybir.dt.uint16
            link(dve, "dve", dve.tensor_scalar(narrow, wide, 448.0, -448.0, ALU.min, ALU.max))
            link(dve, "dve", dve.tensor_scalar(power.bitcast(u16), narrow.bitcast(u16), 0x7F80, None, ALU.bitwise_and))
            link(dve, "dve", dve.tensor_scalar(wide, power, 2.0 ** -6, 1.5 * 2.0 ** 20, ALU.max, ALU.mult))
            link(dve, "dve", dve.tensor_tensor(out, narrow, wide, ALU.add))
            last = dve.tensor_tensor(out, out, wide, ALU.subtract)
            if wait:
                link(dve, "dve", last)
            return last

        def x2_scalar(act):
            act.wait_ge(sem("normT_psum"), transposed_no[6.5] + 1)
            src = cut(bank(7, KT * T), KT, T)
            for k in range(KT):
                ins = act.activation(x2_lnT[:, k, :], src[:, k, :], ACT.Identity, scale=V("ln_w")[:, k:k + 1], bias=V("ln_b")[:, k:k + 1])
            ins.then_inc(sem("normT_ready"), 1)
            act.wait_ge(sem("x2_heads_psum"), since("x2_heads_psum", 1))
            for a, b, i in x2_sq_cols:
                act.activation(x2_raw[:, a:b], psf[:, a:b], ACT.Copy, scale=V("scales")[:, i:i + 1]).then_inc(sem("x2_raw"), 1)
            act.wait_ge(sem("x2_centred"), 1)
            act.activation(x2_square, x2_raw, ACT.Square).then_inc(sem("x2_square"), 1)
            act.wait_ge(sem("x2_var_psum"), since("x2_var_psum", 1))
            act.activation(x2_square, psf[:, 0:2560], ACT.Sqrt, bias=x2_eps[:, 0:1]).then_inc(sem("x2_std"), 1)
            act.wait_ge(sem("x2_normed"), 1)
            act.activation(x2_v, psf[0:T, 2560:3584], ACT.Copy, scale=V("scales")[0:T, 3:4]).then_inc(sem("x2_v_ready"), 1)
            act.wait_ge(sem("x2_core_shifted"), 1)
            act.activation(x2_s, x2_s, ACT.Exp, scale=SCALE2).then_inc(sem("x2_core_exp"), 1)
            act.wait_ge(sem("x2_coreT_psum"), since("x2_coreT_psum", 1))
            act.wait_ge(sem("x2_v_ready"), since("x2_v_ready", 1))
            act.copy(x2_coreT, psf[0:T, 0:1024]).then_inc(sem("x2_coreT"), 1)
            act.wait_ge(sem("x2_core_out_psum"), since("x2_core_out_psum", 1))
            act.copy(x2_cat[:, 0:NQ, :], cut(psf[:, 1024:2048], NQ, T)).then_inc(sem("x2_core_done"), 1)
            with act.Fori(0, GROUPS) as g:
                g = act.snap(g, max_val=GROUPS - 1)
                n0 = g * NC

                def square(c):
                    act.wait_ge(sem("x2_keys_psum"), n0 + (c + 1))
                    if c >= 2:
                        act.wait_ge(sem("x2_keys_ready"), n0 + (c - 1))
                    act.activation(x2_dev[:, c % 2, :], ps[:, c % 3, 0:CHUNK], ACT.Square).then_inc(sem("x2_squared"), 1)

                square(0)
                for c in range(NC):
                    if c + 1 < NC:
                        square(c + 1)
                    act.wait_ge(sem("x2_keys_var"), n0 + (c + 1))
                    act.activation(x2_dev[:, c % 2, :], ps[:, 3, 0:CHUNK], ACT.Sqrt, bias=x2_eps[:, 0:1]).then_inc(sem("x2_deviation"), 1)
                act.wait_ge(sem("x2_bias_ready"), since("x2_bias_ready", g + 1))
                for c in range(NC):
                    part = S[:, CHUNK * c:CHUNK * c + CHUNK]
                    act.activation(part, part, ACT.Exp, scale=SCALE2, bias=x2_small[:, 1:2], accum_out=x2_sum[:, c:c + 1])\
                       .then_inc(sem("x2_exp"), 1)
                act.wait_ge(sem("x2_mixT_psum"), g + 1)
                act.copy(x2_mixT, cut(bank(5, D), KT, 128)).then_inc(sem("x2_mixT"), 1)
                act.wait_ge(sem("x2_cross_psum"), g + 1)
                act.copy(x2_cat[:, ds(g * 2 + NQ, 2), :], cut(ps[:, 6, 0:128], 2, T)).then_inc(sem("x2_cross_done"), 1)

        def x2_pool(pool):
            norm_pool(pool, 6)
            norm_pool(pool, 6.5)

        STAGES[6] = (x2_tensor, x2_vector, x2_scalar, x2_pool)

        x3_qT, x3_kT = cut(x2_keys[:, 0, 0:128], KT, T), cut(x2_keys[:, 0, 128:256], KT, T)
        x3_v = x2_mix[0:T, :]
        x3_own, x3_ownT = x2_q[0:T, 0:T], x2_q[0:T, T:2 * T]
        x3_max, x3_sum, x3_small = x2_max[0:T, :], x2_sum[0:T, :], x2_small[0:T, :]
        x3_probsT = x2_probsT[:, :, 0:SUB * T]

        def x3_tensor(pe):
            norm_tensor(pe, 9)
            normT_here(pe, 9)
            weights_here(pe, "x3")
            w = W("x3")
            for i in range(2):
                for o in range(KT):
                    for k in range(KT):
                        a = 512 * i + 256 * k + 128 * o
                        pe.matmul(ps[:, 0, (2 * i + o) * T:(2 * i + o + 1) * T], w[:, a:a + 128], xnT[:, k, 0, :], start=k == 0, stop=k == KT - 1)
            for k in range(KT):
                ins = pe.matmul(bank(1, D, T), xnT[:, k, 0, :], w[:, 1024 + 256 * k:1280 + 256 * k], start=k == 0, stop=k == KT - 1)
            ins.then_inc(sem("x3_qkv_psum"), 1)
            pe.wait_ge(sem("x3_qkv"), 3)
            pe.wait_ge(sem("ctx_reloaded"), 32)
            for c in range(NC + 1):
                if c >= 2:
                    pe.wait_ge(sem("x3_scores"), since("x3_scores", c - 1))
                out = ps[0:T, 2 + c % 2, 0:CHUNK if c < NC else T]
                for k in range(KT):
                    keys = ctxT[:, k, CHUNK * c:CHUNK * c + CHUNK] if c < NC else x3_kT[:, k, :]
                    ins = pe.matmul(out, x3_qT[:, k, :], keys, start=k == 0, stop=k == KT - 1)
                ins.then_inc(sem("x3_scores_psum"), 1)

            def turn(c):
                pe.wait_ge(sem("x3_exp"), since("x3_exp", c + 1))
                if c >= 2:
                    pe.wait_ge(sem("x3_probsT"), since("x3_probsT", c - 1))
                if c == NC:
                    pe.transpose(ps[0:T, 4 + c % 2, 0:T], x3_own, C("ident")[0:T, 0:T]).then_inc(sem("x3_probsT_psum"), 1)
                    return
                for s in range(SUB):
                    a = CHUNK * c + TILE * s
                    ins = pe.transpose(ps[0:TILE, 4 + c % 2, T * s:T * s + T], S[0:T, a:a + TILE], C("ident")[0:T, 0:T])
                ins.then_inc(sem("x3_probsT_psum"), 1)

            def weigh(c):
                pe.wait_ge(sem("x3_probsT"), since("x3_probsT", c + 1))
                if c == NC:
                    ins = pe.matmul(bank(0, D, T), x3_ownT, x3_v, start=False, stop=True)
                else:
                    for s in range(SUB):
                        ins = pe.matmul(bank(0, D, T), x3_probsT[:, c % 2, T * s:T * s + T], ctxN[:, SUB * c + s, :],
                                        start=c == 0 and s == 0, stop=False)
                ins.then_inc(sem("x3_weighed"), 1)

            turn(0)
            for c in range(1, NC + 1):
                turn(c)
                weigh(c - 1)
            weigh(NC)
            out_tensor(pe, 9, attended, w[:, 1536:2048], "x3")

        def x3_vector(dve):
            norm_vector(dve, 9)
            for c in range(NC + 1):
                dve.wait_ge(sem("x3_scores_psum"), since("x3_scores_psum", c + 1))
                out = S[0:T, CHUNK * c:CHUNK * c + CHUNK] if c < NC else x3_own
                dve.tensor_scalar(out, ps[0:T, 2 + c % 2, 0:CHUNK if c < NC else T], 1.0, NEG, ALU.mult, ALU.max,
                                  accum_out=x3_max[:, c:c + 1]).then_inc(sem("x3_scores"), 1)
            dve.wait_ge(sem("x3_scores"), since("x3_scores", NC + 1))
            link(dve, "dve", dve.tensor_reduce(x3_small[:, 0:1], x3_max, AX, ALU.max))
            dve.tensor_scalar(x3_small[:, 1:2], x3_small[:, 0:1], -1.0 / 16, None, ALU.mult).then_inc(sem("x3_bias_ready"), 1)
            for c in range(NC + 1):
                dve.wait_ge(sem("x3_probsT_psum"), since("x3_probsT_psum", c + 1))
                if c >= 2:
                    dve.wait_ge(sem("x3_weighed"), since("x3_weighed", c - 1))
                if c < NC:
                    ins = dve.tensor_copy(x3_probsT[:, c % 2, :], ps[0:TILE, 4 + c % 2, 0:SUB * T])
                else:
                    ins = dve.tensor_copy(x3_ownT, ps[0:T, 4 + c % 2, 0:T])
                ins.then_inc(sem("x3_probsT"), 1)
            link(dve, "dve", dve.tensor_reduce(x3_small[:, 2:3], x3_sum, AX, ALU.add))
            link(dve, "dve", dve.reciprocal(x3_small[:, 3:4], x3_small[:, 2:3]))
            dve.wait_ge(sem("x3_weighed"), since("x3_weighed", NC + 1))
            dve.tensor_scalar(attended[:, :], bank(0, D, T), x3_small[:, 3:4], None, ALU.mult).then_inc(sem("attended"), 1)
            residual_vector(dve, 9, bank(6, D, T), (sem("projected"), outs.index(9) + 1))

        def x3_scalar(act):
            norm_scalar(act, 9)
            act.wait_ge(sem("x3_qkv_psum"), since("x3_qkv_psum", 1))
            act.copy(x3_qT, cut(ps[:, 0, 0:KT * T], KT, T)).then_inc(sem("x3_qkv"), 1)
            act.copy(x3_kT, cut(ps[:, 0, KT * T:2 * KT * T], KT, T)).then_inc(sem("x3_qkv"), 1)
            act.copy(x3_v, bank(1, D, T)).then_inc(sem("x3_qkv"), 1)
            act.wait_ge(sem("x3_bias_ready"), since("x3_bias_ready", 1))
            for c in range(NC + 1):
                part = S[0:T, CHUNK * c:CHUNK * c + CHUNK] if c < NC else x3_own
                act.activation(part, part, ACT.Exp, scale=1.0 / 16, bias=x3_small[:, 1:2], accum_out=x3_sum[:, c:c + 1])\
                   .then_inc(sem("x3_exp"), 1)
            out_scalar(act, 9)

        STAGES[9] = (x3_tensor, x3_vector, x3_scalar, lambda pool: norm_pool(pool, 9))

        def reload_scalar(act):
            if runs(3):
                act.wait_ge(sem("attended"), outs.index(3) + 1)
            act.dma_start(ctxT, io["ctxT"]).then_inc(sem("ctx_reloaded"), 16)
            act.dma_start(ctxN, io["ctxN"]).then_inc(sem("ctx_reloaded"), 16)

        block = stack.enter_context(nc.Block())

        @block.sync
        def _(sp):
            sp.dma_start(consts[:, :], io["constants"]).then_inc(sem("constants_in"), 16)
            sp.dma_start(x[:, :], io["x"]).then_inc(sem("x_in"), 16)
            if sweep:
                SWEEP_LOADS[0](sp)
            n_first = min(len(pieces), NSLOT)

            def load(n):
                _, name, w = pieces[n]
                a = piece_from[name]
                sp.dma_start(W(name), io["weights"][:, a:a + w]).then_inc(sem(f"weights_in{n % NSLOT}"), 16)

            for n in range(n_first):
                load(n)
            sp.dma_start(row_biases[:, :], io["row_biases"]).then_inc(sem("params_in"), 16)
            sp.dma_start(cols[:, :], io["columns"]).then_inc(sem("params_in"), 16)
            sp.dma_start(filter_sb[:, :], io["filterT"]).then_inc(sem("params_in"), 16)
            if sweep:
                SWEEP_LOADS[1](sp)
            for n in range(n_first, len(pieces)):
                sp.wait_ge(weights_used, n - NSLOT + 1)
                load(n)
            sp.wait_ge(sem("latent_done"), 1)
            sp.dma_start(io["out"], x[:, :]).then_inc(sem("stored"), 16)
            sp.wait_ge(sem("stored"), 16)

        @block.tensor
        def _(pe):
            pe.wait_ge(sem("constants_in"), 16)
            pe.wait_ge(sem("params_in"), 48)
            if sweep:
                SWEEP[0](pe)
            for s in range(12):
                if runs(s):
                    STAGES[s][0](pe)

        @block.vector
        def _(dve):
            dve.wait_ge(sem("constants_in"), 16)
            dve.wait_ge(sem("params_in"), 48)
            dve.wait_ge(sem("x_in"), 16)
            if sweep:
                SWEEP[1](dve)
            for s in range(12):
                if runs(s):
                    STAGES[s][1](dve)
            dve.sem_inc(sem("latent_done"), 1)

        @block.scalar
        def _(act):
            act.wait_ge(sem("constants_in"), 16)
            act.wait_ge(sem("params_in"), 48)
            if sweep:
                SWEEP[2](act)
            for s in range(12):
                if s == 4 and (runs(6) or runs(9)):
                    reload_scalar(act)
                if runs(s):
                    STAGES[s][2](act)

        @block.gpsimd
        def _(pool):
            pool.wait_ge(sem("constants_in"), 16)
            pool.wait_ge(sem("params_in"), 48)
            if sweep:
                SWEEP[3](pool)
            for s in range(12):
                if runs(s):
                    STAGES[s][3](pool)



def kernel(**inputs):
    import concourse.bacc as bacc
    from concourse.bass_utils import run_bass_kernel_spmd

    nc = bacc.Bacc("TRN2", target_bir_lowering=False, num_devices=1)
    arrays = laid_out({n: np.asarray(v) for n, v in inputs.items()})
    io = {n: nc.dram_tensor(n, v.shape, F32, kind="ExternalInput").ap() for n, v in arrays.items()}
    io["out"] = nc.dram_tensor("out", (T, D), F32, kind="ExternalOutput").ap()
    perceiver(nc, io)
    result = run_bass_kernel_spmd(nc, [arrays], core_ids=[0])
    return result.results[0]["out"].reshape(1, T, D)
```

```python
from contextlib import ExitStack

import numpy as np

import concourse.bass as bass
from concourse import mybir

ALU = mybir.AluOpType
ACT = mybir.ActivationFunctionType
AX = mybir.AxisListType.X
F32 = mybir.dt.float32
BF16 = mybir.dt.bfloat16
U32 = mybir.dt.uint32

T = 64
D = 256
KT = D // 128
SK = 6272
TILE = 128
NT = SK // TILE
SUB = 4
CHUNK = SUB * TILE
NC = -(-NT // SUB)
NH = 16
HD = 16
PAIRS = NH // 2
FD = 64
GROUPS = 8
GD = 128
NQ = 2 * GROUPS
NE = 18
FF = 176
FH = FF // 2
LN_EPS = 1e-5
RMS_EPS = 1e-6
NEG = -3.0e38
MAGIC = 12582912.0
LN255 = float(np.log(255.0))

SLOT = 2048
NSLOT = 4


def subs(c):
    return min(SUB, NT - SUB * c)


def width(c):
    return TILE * subs(c)


def span(c):
    return slice(CHUNK * c, CHUNK * c + width(c))



def k_major(m):
    k, n = m.shape
    return m.reshape(k // 128, 128, n).transpose(1, 0, 2).reshape(128, -1)


def rows(m):
    out = np.zeros((128, m.shape[1]), np.float32)
    out[:m.shape[0]] = m
    return out


def head_diagonal(w):
    d, f = w.shape
    out = np.zeros((128, 128 // d * f), np.float32)
    for h in range(128 // d):
        out[h * d:(h + 1) * d, h * f:(h + 1) * f] = w
    return out


def expert_columns(a):
    e, r, i = a.shape
    out = np.zeros((i, e, e, r), np.float32)
    for n in range(e):
        out[:, n, n, :] = a[n].T
    return out.reshape(i, -1)


def column(v):
    return v.reshape(-1, 128).T


def by_head(w):
    return w.reshape(-1, NH, 3, HD).transpose(0, 2, 1, 3).reshape(-1, 3 * D)


def for_query_groups(w):
    return np.repeat(w.reshape(8, 1, 8, -1), 4, axis=1).reshape(D, -1)


PIECES = (
    [(-1, "pre", 2048), (-1, "pre_features", 512)]
    + [(0, "x0", 1536), (1, "a0", 2048)]
    + [(2, "f0_gate", 2048), (2, "f0_up", 2048), (2, "f0_routed", 784), (2, "f0_down", 2048)]
    + [(3, "x1", 1024), (4, "a1", 2048)]
    + [(5, "f1_gate", 280), (5, "f1_lora", 1792)] + [(5, f"f1_experts{n}", 1536) for n in range(4)]
    + [(6, "x2_q0", 2048), (6, "x2_q1", 2048), (6, "x2_k", 2048), (6, "x2_qx0", 2048), (6, "x2_qx1", 2048),
       (6, "x2_v", 2048), (6, "x2_kx", 2048), (6, "x2_vx", 2048)]
    + [(6, f"x2_proj{n}", 2048) for n in range(4)]
    + [(7, "a2", 2048), (8, "f2_attn", 2048), (8, "f2_mod", 1056), (8, "f2_gate", 2048), (8, "f2_up", 2048),
       (8, "f2_down", 2048)]
    + [(9, "x3", 2048), (10, "a3", 2048)]
    + [(11, "f3_gate", 288)] + [(11, f"f3_experts{n}", 1728) for n in range(9)]
)


def pack_piece(name, a):
    tr = lambda n: k_major(np.ascontiguousarray(a[n].T))
    cat = lambda *p: np.concatenate(p, 1)
    last = int(name[-1]) if name[-1].isdigit() else 0
    half = lambda n, i: k_major(np.ascontiguousarray(a[n][1024 * i:1024 * (i + 1)].T))
    if name == "pre":
        return cat(tr("L0_xattn_Wk"), k_major(cat(a["L0_xattn_Wv"].T, a["L1_xattn_Wkv"])))
    if name == "pre_features":
        return head_diagonal(a["L0_xattn_Wkf"].T)
    if name == "x0":
        return cat(tr("L0_xattn_Wq"), head_diagonal(a["L0_xattn_Wqf"].T), tr("L0_xattn_Wo"))
    if name == "a0":
        return cat(k_major(a["L0_attn_Wqkv"]), k_major(a["L0_attn_Wo"]))
    if name == "f0_gate":
        return tr("L0_ffn_sh_gate")
    if name == "f0_up":
        return tr("L0_ffn_sh_up")
    if name == "f0_down":
        return tr("L0_ffn_sh_down")
    if name == "f0_routed":
        return cat(tr("L0_ffn_r_gate"), tr("L0_ffn_r_up"), tr("L0_ffn_r_down"), tr("L0_ffn_router_weight"))
    if name == "x1":
        return cat(k_major(a["L1_xattn_Wq"]), k_major(a["L1_xattn_Wp"]))
    if name == "a1":
        return cat(k_major(by_head(a["L1_attn_w_qkv"])), k_major(a["L1_attn_w_out"]))
    if name == "f1_gate":
        return cat(tr("L1_ffn_gate_weight"), rows(a["L1_ffn_gate_lora_A"]), rows(a["L1_ffn_gate_lora_B"].T))
    if name == "f1_lora":
        gup_b = a["L1_ffn_gup_lora_B"].transpose(0, 2, 1).reshape(128, D)
        down_b = a["L1_ffn_down_lora_B"].transpose(0, 2, 1).reshape(128, D)
        return cat(k_major(a["L1_ffn_gup_lora_A"].reshape(128, D).T), gup_b, down_b,
                   expert_columns(a["L1_ffn_down_lora_A"]))
    if name.startswith("f1_experts"):
        two = [cat(k_major(a["L1_ffn_gate_up_proj"][e]), a["L1_ffn_down_proj"][e]) for e in (2 * last, 2 * last + 1)]
        return cat(*two)
    if name in ("x2_q0", "x2_q1"):
        return half("L2_xattn_wq", last)
    if name in ("x2_qx0", "x2_qx1"):
        return half("L2_xattn_wqx", last)
    if name == "x2_k":
        return tr("L2_xattn_wk")
    if name == "x2_v":
        return tr("L2_xattn_wv")
    if name == "x2_kx":
        return half("L2_xattn_w_kv_x", 0)
    if name == "x2_vx":
        return half("L2_xattn_w_kv_x", 1)
    if name.startswith("x2_proj"):
        return k_major(np.ascontiguousarray(a["L2_xattn_wproj"].T[1024 * last:1024 * (last + 1)]))
    if name == "a2":
        w = cat(a["L2_attn_Wq"].T, for_query_groups(a["L2_attn_Wk"]).T, for_query_groups(a["L2_attn_Wv"]).T)
        return cat(k_major(w), tr("L2_attn_Wo"))
    if name == "f2_attn":
        return cat(k_major(cat(a["L2_ffn_Wq"].T, a["L2_ffn_Wk"].T, a["L2_ffn_Wv"].T)), tr("L2_ffn_Wo"))
    if name == "f2_mod":
        return cat(k_major(a["L2_ffn_A"]), rows(a["L2_ffn_B"]))
    if name == "f2_gate":
        return tr("L2_ffn_W_in_base")
    if name == "f2_up":
        return tr("L2_ffn_W_up_base")
    if name == "f2_down":
        return tr("L2_ffn_W_down")
    if name == "x3":
        return cat(*(tr(f"L3_xattn_{w}") for w in ("wq", "wk", "wv", "wo")))
    if name == "a3":
        return cat(*(tr(f"L3_attn_{w}") for w in ("Wq", "Wk", "Wv", "Wo")))
    if name == "f3_gate":
        return cat(tr("L3_ffn_centroids"), rows(np.concatenate([a["L3_ffn_routed_b2"], a["L3_ffn_shared_b2"]], 0)))
    w1 = np.concatenate([a["L3_ffn_routed_w1"], a["L3_ffn_shared_w1"]], 0)
    w2 = np.concatenate([a["L3_ffn_routed_w2"], a["L3_ffn_shared_w2"]], 0)
    two = [cat(k_major(w1[e]), rows(w2[e].reshape(2, FH, D).transpose(1, 0, 2).reshape(FH, 2 * D)))
           for e in (2 * last, 2 * last + 1)]
    return cat(*two)


ROW_BIASES = (("bv0", D), ("bo0", D), ("a0_qkv", 3 * D), ("a0_out", D), ("kv1", 2 * D), ("q1", D), ("out1", D),
              ("a1_qkv", 3 * D), ("a1_out", D), ("a2_qkv", 3 * D), ("a2_out", D), ("a3_out", D), ("f3_bias", 16))


def pack_row_biases(a):
    r = {"bv0": a["L0_xattn_bv"], "bo0": a["L0_xattn_bo"], "a0_qkv": a["L0_attn_bqkv"], "a0_out": a["L0_attn_bo"],
         "kv1": a["L1_xattn_bkv"], "q1": a["L1_xattn_bq"], "out1": a["L1_xattn_bp"],
         "a1_qkv": by_head(a["L1_attn_b_qkv"][None])[0], "a1_out": a["L1_attn_b_out"],
         "a2_qkv": np.concatenate([a["L2_attn_bq"], for_query_groups(a["L2_attn_bk"]).ravel(),
                                   for_query_groups(a["L2_attn_bv"]).ravel()]),
         "a2_out": a["L2_attn_bo"], "a3_out": a["L3_attn_bo"], "f3_bias": a["L3_ffn_bias"]}
    row = np.concatenate([r[n] for n, _ in ROW_BIASES])
    return np.ascontiguousarray(np.broadcast_to(row, (128, row.size)))


COLUMNS = (("bk0", 2), ("bq0", 2), ("ln_w", 2), ("ln_b", 2), ("in_scale", 8), ("head_ln", 8), ("smooth", 32),
           ("scales", 6), ("ln1_w", 2), ("ln2_w", 2), ("a3_b", 6), ("conv_w", 12), ("conv_b", 4), ("d_skip", 2),
           ("f3_b1", 36))


def pack_columns(a):
    x2 = lambda n: a["L2_xattn_" + n]
    scalars = [x2(n) for n in ("wq_scale", "wk_scale", "wqx_scale", "wv_scale", "proj_in_scale", "proj_w_scale")]
    b1 = np.concatenate([a["L3_ffn_routed_b1"], a["L3_ffn_shared_b1"]], 0)
    c = {"bk0": column(a["L0_xattn_bk"]), "bq0": column(a["L0_xattn_bq"]),
         "ln_w": column(x2("ln_w")), "ln_b": column(x2("ln_b")),
         "in_scale": np.concatenate([column(x2(n + "_in_scale")) for n in ("q", "k", "qx", "v")], 1),
         "head_ln": np.stack([x2(n) for n in ("qln_w", "qln_b", "kln_w", "kln_b", "qxln_w", "qxln_b",
                                              "kxln_w", "kxln_b")], 1),
         "smooth": column(x2("proj_smooth")),
         "scales": np.broadcast_to(np.array([np.asarray(s).reshape(()) for s in scalars], np.float32), (128, 6)),
         "ln1_w": column(a["L2_ffn_ln1_w"]), "ln2_w": column(a["L2_ffn_ln2_w"]),
         "a3_b": np.concatenate([column(a["L3_attn_" + n]) for n in ("bq", "bk", "bv")], 1),
         "conv_w": np.concatenate([a[f"L3_attn_conv{n}_w"].reshape(2, 128, 3).transpose(1, 0, 2).reshape(128, 6)
                                   for n in "qk"], 1),
         "conv_b": np.concatenate([column(a[f"L3_attn_conv{n}_b"]) for n in "qk"], 1),
         "d_skip": column(a["L3_attn_D_skip"]),
         "f3_b1": rows(b1.reshape(18, 2, FH).transpose(2, 0, 1).reshape(FH, 36))}
    return np.ascontiguousarray(np.concatenate([c[n] for n, _ in COLUMNS], 1).astype(np.float32))


FREQ = T + 1
CONSTANTS = (("ident", 128), ("centre128", 128), ("mean128", 128), ("mean_band", 19), ("tri", T), ("tri_10000", T), ("tri_neg", T),
             ("heads16", 8), ("heads8", 16), ("neg_half", 1), ("earlier8", 64), ("earlier16", 256),
             ("rope1", 8), ("rope2", 16), ("dft", 2 * FREQ), ("idft", 2 * T))


def rope_table(angle):
    cos, sin = np.cos(angle), np.sin(angle)
    return np.concatenate([cos, cos, -sin, sin], 1)


def constants():
    p, t = np.arange(128), np.arange(T)
    lower = (t[None, :] <= t[:, None]).astype(np.float32)
    f32 = np.float32
    inv1 = f32(1.0) / f32(10000.0) ** (np.arange(0, 4, 2, dtype=f32) / f32(4))
    inv2 = f32(10000.0) ** (f32(-2.0) * np.arange(4, dtype=f32) / f32(8))
    angle = 2 * np.pi * np.outer(p, np.arange(FREQ)) / (2 * T)
    weight = np.where((np.arange(FREQ) % T) == 0, 1.0, 2.0)[:, None] / (2 * T)
    back = 2 * np.pi * np.outer(np.arange(FREQ), t) / (2 * T)
    c = {"ident": np.eye(128), "centre128": np.eye(128) - 1 / 128, "mean128": np.full((128, 128), 1 / 128),
         "mean_band": np.broadcast_to((np.arange(19) == 9) / 128, (128, 19)),
         "tri": lower, "tri_10000": -10000.0 * (1 - lower), "tri_neg": NEG * (1 - lower),
         "heads16": (p[:, None] // 16 == np.arange(8)), "heads8": (p[:, None] // 8 == np.arange(16)),
         "neg_half": np.full((128, 1), -0.5),
         "earlier8": np.tile((np.arange(8)[None, :] < np.arange(8)[:, None]).reshape(1, -1), (T, 1)),
         "earlier16": np.tile((np.arange(16)[None, :] < np.arange(16)[:, None]).reshape(1, -1), (T, 1)),
         "rope1": rope_table((t[:, None].astype(f32) * inv1[None]).astype(f32)),
         "rope2": rope_table(((t[:, None].astype(f32) + 1) * inv2[None]).astype(f32)),
         "dft": np.concatenate([np.cos(angle), -np.sin(angle)], 1),
         "idft": np.concatenate([weight * np.cos(back), -weight * np.sin(back)], 1)}
    return np.concatenate([rows(np.asarray(c[n], np.float32)) for n, _ in CONSTANTS], 1)


def offsets(table):
    at, out = 0, {}
    for n, w in table:
        out[n] = (at, w)
        at += w
    return out, at


def laid_out(a):
    ctx = a["ctx_2048"][0]
    out = {
        "x": a["x"][0],
        "ctxT": ctx.T.reshape(KT, 128, SK).transpose(1, 0, 2),
        "ctxN": ctx.reshape(NT, TILE, D).transpose(1, 0, 2),
        "mask": a["mask_BxS2_ff1"][0].reshape(NT, TILE).T,
        "row_biases": pack_row_biases(a),
        "columns": pack_columns(a),
        "constants": constants(),
        "filterT": a["L3_attn_ssm_kernel"][:, :2 * T].T,
        "weights": np.concatenate([pack_piece(n, a) for _, n, _ in PIECES], 1),
    }
    return {n: np.ascontiguousarray(v, np.float32) for n, v in out.items()}



def perceiver(nc, io, first=0, last=11):
    constant_at, n_constants = offsets(CONSTANTS)
    column_at, n_columns = offsets(COLUMNS)
    row_bias_at, n_row_biases = offsets(ROW_BIASES)
    runs = lambda s: first <= s <= last
    sweep = runs(0) or runs(3)
    pieces = [p for p in PIECES if runs(p[0]) or (p[0] == -1 and sweep)]
    piece_no = {n: k for k, (_, n, _) in enumerate(pieces)}
    piece_from, at = {}, 0
    for s, n, w in PIECES:
        piece_from[n] = at
        at += w

    with ExitStack() as stack:
        def sb(name, shape, dt=F32):
            return stack.enter_context(nc.sbuf_tensor(name, shape, dt))

        sems = {}

        shared = {
            "queries_psum": (("x0_qT_psum", 0, 1), ("x1_q_psum", 3, 1), ("x2_heads_psum", 6, 1),
                             ("x3_qkv_psum", 9, 1), ("a3_qkv_psum", 10, 1)),
            "scores_psum": (("x1_scores_psum", 3, PAIRS * NC), ("x2_scores_psum", 6, GROUPS * NC),
                            ("x3_scores_psum", 9, NC + 1)),
            "scores": (("x1_scores", 3, PAIRS * NC), ("x2_scores", 6, GROUPS * NC), ("x3_scores", 9, NC + 1)),
            "exp_bias_ready": (("x1_bias_ready", 3, PAIRS), ("x2_bias_ready", 6, GROUPS), ("x3_bias_ready", 9, 1)),
            "exp": (("x1_exp", 3, PAIRS * NC), ("x2_exp", 6, GROUPS * NC), ("x3_exp", 9, NC + 1)),
            "probsT_psum": (("x1_probsT_psum", 3, PAIRS * NC), ("x2_probsT_psum", 6, GROUPS * NC),
                            ("x3_probsT_psum", 9, NC + 1)),
            "probsT_ready": (("x2_probsT_ready", 6, GROUPS * NC), ("x3_probsT", 9, NC + 1)),
            "weighed": (("x1_weighed", 3, PAIRS * NC), ("x2_weighed", 6, GROUPS * NC), ("x3_weighed", 9, NC + 1)),
            "tile_ready": (("x1_tile_ready", 3, PAIRS), ("x2_tile_ready", 6, GROUPS)),
            "logits_psum": (("f0_logits_psum", 2, 1), ("f1_logits_psum", 5, 1), ("f3_logits_psum", 11, 1)),
            "logits_shifted": (("f0_shifted", 2, 1), ("f1_shifted", 5, 1)),
            "logits_exp": (("f0_router_exp", 2, 1), ("f1_router_exp", 5, 1), ("f3_exp", 11, 1)),
            "hidden_psum": (("f0_hidden_psum", 2, 1), ("f1_gates_psum", 5, 4), ("f2_hidden_psum", 8, 1),
                            ("f3_hidden_psum", 11, NE)),
            "gates_exp": (("f0_exp", 2, 1), ("f1_exp", 5, 4), ("f2_exp", 8, 1)),
            "hidden": (("f0_hidden", 2, 1), ("f1_hidden", 5, 4), ("f2_hidden", 8, 1)),
            "expert_psum": (("f1_expert_psum", 5, 4), ("f3_expert_psum", 11, NE)),
            "expert_added": (("f1_added", 5, 4), ("f3_added", 11, NE)),
            "out_psum": (("f0_out_psum", 2, 1), ("f1_lora_psum", 5, 1), ("x2_out_psum", 6, 1), ("f2_out_psum", 8, 1),
                         ("a3_out_psum", 10, 1), ("f3_bias_psum", 11, 1)),
            "low_psum": (("f1_low_psum", 5, 1), ("f2_low_psum", 8, 1)),
            "narrowT_psum": (("f1_down_lowT_psum", 5, 1), ("f2_modT_psum", 8, 1), ("f3_gatesT_psum", 11, 1)),
            "narrowT_ready": (("f1_down_lowT_ready", 5, 1), ("f2_modT_ready", 8, 1), ("f3_gatesT_ready", 11, 1)),
            "x2_head_sums_psum": (("x2_centre_psum", 6, 5), ("x2_var_psum", 6, 1), ("x2_inv_psum", 6, 1), ("x2_core_psum", 6, 1),
                                  ("x2_const_psum", 6, 1), ("x2_coreT_psum", 6, 1), ("x2_core_out_psum", 6, 1)),
            "x2_heads_step": (("x2_raw", 6, 3), ("x2_square", 6, 5), ("x2_std", 6, 1), ("x2_v_ready", 6, 1),
                              ("x2_core_exp", 6, 1), ("x2_coreT", 6, 1), ("x2_core_done", 6, 1)),
        }
        shared_by = {name: by for by, signals in shared.items() for name, _, _ in signals}

        def sem(name):
            name = shared_by.get(name, name)
            if name not in sems:
                sems[name] = stack.enter_context(nc.semaphore(name))
            return sems[name]

        def since(name, n):
            for other, s, times in shared[shared_by[name]]:
                if other == name:
                    return n
                if runs(s):
                    n = n + times

        consts = sb("consts", [128, n_constants])
        cols = sb("cols", [128, n_columns])
        row_biases = sb("row_biases_sb", [128, n_row_biases])
        filter_sb = sb("filter_sb", [128, D])
        ring = sb("ring", [128, NSLOT, SLOT])
        x = sb("x_sb", [T, D])
        xn = sb("xn", [T, D])
        xnT = sb("xnT", [128, KT, 2, T])
        stats = sb("stats", [T, 6])
        moments = sb("moments", [T, 2])
        var_eps = sb("var_eps", [T, 1])
        rstd = sb("rstd", [T, 1])
        keysT = sb("keysT", [128, KT, TILE + SK])
        vals = sb("vals", [128, NT, D])
        S = sb("S", [128, SK])
        mask_sb = sb("mask_sb", [TILE, NT])
        sweep_sums = sb("sweep_sums", [128, PAIRS, 34])
        value_step = sb("value_step", [128, D])
        wide = sb("wide", [128, 3, CHUNK])
        ps = stack.enter_context(nc.psum_tensor("ps", [128, 8, 512], F32))
        psf = ps[:, :, :].rearrange("p b n -> p (b n)")

        def bank(b, n=512, p=128):
            return ps[0:p, b, 0:n]

        def C(name):
            a, w = constant_at[name]
            return consts[:, a:a + w]

        def V(name):
            a, w = column_at[name]
            return cols[:, a:a + w]

        def R(name, p=T):
            a, w = row_bias_at[name]
            return row_biases[0:p, a:a + w]

        def scratch(a, n, p=128):
            return S[0:p, a:a + n]

        def cut(ap, *dims):
            if len(dims) == 2:
                return ap.rearrange("p (a b) -> p a b", a=dims[0])
            return ap.rearrange("p (a b c) -> p a b c", a=dims[0], b=dims[1])

        def spread(ap, axis, n):
            shape = list(ap.shape)
            return ap.unsqueeze(axis).broadcast_to(shape[:axis] + [n] + shape[axis:])

        def W(name):
            n = piece_no[name]
            return ring[:, n % NSLOT, 0:pieces[n][2]]

        def weights_here(eng, name):
            n = piece_no[name]
            eng.wait_ge(sem(f"weights_in{n % NSLOT}"), 16 * (n // NSLOT + 1))

        weights_used = sem("weights_used")

        steps = {"dve": 0, "act": 0, "pool": 0}

        def link(eng, name, ins):
            steps[name] += 1
            ins.then_inc(sem(name + "_step"), 1)
            eng.wait_ge(sem(name + "_step"), steps[name])

        norms = [n for s in range(12) if runs(s) for n in ([s] if s not in (6, 8) else [s, s + 0.5])]
        norm_no = {n: k for k, n in enumerate(norms)}
        transposed = [n for n in norms if n not in (6, 8)]
        transposed_no = {n: k for k, n in enumerate(transposed)}

        def norm_vector(dve, n, src=x, out=xn, eps=LN_EPS, rms=False):
            k = norm_no[n]
            if rms:
                link(dve, "dve", dve.tensor_tensor_reduce(out[:, :], src[:, :], src[:, :], 1.0 / D, 0.0, ALU.mult,
                                                          ALU.add, moments[:, 1:2]))
            else:
                link(dve, "dve", dve.bn_stats(stats[:, :], src[:, :]))
                link(dve, "dve", dve.bn_aggr(moments[:, :], stats[:, :]))
            dve.tensor_scalar(var_eps[:, :], moments[:, 1:2], eps, None, ALU.add).then_inc(sem("var_ready"), 1)
            dve.wait_ge(sem("rstd_ready"), k + 1)
            if rms:
                ins = dve.tensor_scalar(out[:, :], src[:, :], rstd[:, 0:1], None, ALU.mult)
            else:
                ins = dve.tensor_scalar(out[:, :], src[:, :], moments[:, 0:1], rstd[:, 0:1], ALU.subtract, ALU.mult)
            ins.then_inc(sem("norm_ready"), 1)
            dve.wait_ge(sem("norm_ready"), k + 1)

        def norm_pool(pool, n):
            k = norm_no[n]
            if k == 0:
                pool.wait_ge(sem("constants_in"), 16)
            pool.wait_ge(sem("var_ready"), k + 1)
            pool.tensor_tensor(rstd[:, :], var_eps[:, :], C("neg_half")[0:T, :], ALU.pow).then_inc(sem("rstd_ready"), 1)

        def norm_tensor(pe, n, src=xn):
            if transposed_no[n] == 0:
                pe.wait_ge(sem("constants_in"), 16)
            pe.wait_ge(sem("norm_ready"), norm_no[n] + 1)
            for k in range(KT):
                ins = pe.transpose(ps[:, 7, k * T:(k + 1) * T], src[:, k * 128:(k + 1) * 128], C("ident")[0:T, 0:T])
            ins.then_inc(sem("normT_psum"), 1)

        def norm_scalar(act, n):
            act.wait_ge(sem("normT_psum"), transposed_no[n] + 1)
            act.copy(xnT[:, :, :, :], spread(cut(bank(7, KT * T), KT, T), 2, 2)).then_inc(sem("normT_ready"), 1)

        def normT_here(eng, n):
            eng.wait_ge(sem("normT_ready"), transposed_no[n] + 1)

        biased = [s for s in (0, 1, 3, 4, 7, 10) if runs(s)]

        def bias_pool(pool, s, name):
            pool.wait_ge(sem("norm_ready"), norm_no[s] + 1)
            pool.tensor_tensor(x[:, :], x[:, :], R(name), ALU.add).then_inc(sem("x_biased"), 1)

        def residual_vector(dve, s, product, ready):
            dve.wait_ge(*ready)
            if s in biased:
                dve.wait_ge(sem("x_biased"), biased.index(s) + 1)
            link(dve, "dve", dve.tensor_tensor(x[:, :], x[:, :], product, ALU.add))

        outs = [s for s in (0, 1, 3, 4, 7, 8, 9) if runs(s)]

        def out_tensor(pe, s, src, w, piece=None):
            k = outs.index(s)
            pe.wait_ge(sem("attended"), k + 1)
            for n in range(KT):
                ins = pe.transpose(ps[:, 7, n * T:(n + 1) * T], src[:, n * 128:(n + 1) * 128], C("ident")[0:T, 0:T])
            ins.then_inc(sem("attendedT_psum"), 1)
            pe.wait_ge(sem("attendedT_ready"), k + 1)
            for n in range(KT):
                ins = pe.matmul(bank(6, D, T), attendedT[:, n, :], w[:, n * D:(n + 1) * D], start=n == 0, stop=n == KT - 1)
            ins.then_inc(sem("projected"), 1)
            if piece:
                pe.wait_ge(sem("projected"), k + 1)
                pe.sem_inc(weights_used, 1)

        def out_scalar(act, s):
            k = outs.index(s)
            act.wait_ge(sem("attendedT_psum"), k + 1)
            act.copy(attendedT[:, :, :], cut(bank(7, KT * T), KT, T)).then_inc(sem("attendedT_ready"), 1)

        attendedT = sb("attendedT", [128, KT, T])
        attended = sb("attended", [T, D])

        MHA = {1: dict(piece="a0", bias="a0_qkv", heads=16, scale=0.25, rope=None, mask="tri_10000"),
               4: dict(piece="a1", bias="a1_qkv", heads=16, scale=1.0, rope=("rope1", 2), mask="tri_neg"),
               7: dict(piece="a2", bias="a2_qkv", heads=32, scale=float(1 / np.sqrt(8)), rope=("rope2", 4), mask="tri_neg"),
               8: dict(piece="f2_attn", bias=None, heads=16, scale=0.25, rope=None, mask="tri_neg")}
        mha_order = [s for s in MHA if runs(s)]
        m_qkv, m_tmp = scratch(0, 768), scratch(768, 512, T)
        m_qT = cut(scratch(1280, 2 * T), KT, T)
        m_v = scratch(5504, 256)
        m_max, m_den = scratch(5760, 32, T), scratch(5792, 32, T)

        def mha_views(s):
            h = MHA[s]["heads"]
            d = D // h
            g = h // KT
            keys = S[:, 1408:1408 + h * T].rearrange("p (k h t) -> p k h t", k=KT, h=g)
            scores = cut(scratch(3456, h * T, T), h, T)
            probsT = cut(scratch(1408, h // 2 * T), h // 2, T)
            values = cut(m_v, h // 2, 2 * d)
            return h, d, g, keys, scores, probsT, values

        def mha_tensor(pe, s, n):
            u = mha_order.index(s)
            h, d, g, keys, scores, probsT, values = mha_views(s)
            w = W(MHA[s]["piece"])
            weights_here(pe, MHA[s]["piece"])
            normT_here(pe, n)
            for a, b in ((0, 512), (512, 768)):
                for k in range(KT):
                    ins = pe.matmul(psf[:, a:b], xnT[:, k, :, :].rearrange("p a t -> p (a t)"),
                                    w[:, 768 * k + a:768 * k + b], start=k == 0, stop=k == KT - 1)
            ins.then_inc(sem("mha_qkv_psum"), 1)
            pe.wait_ge(sem("mha_qk_ready"), u + 1)
            for k in range(2 * KT):
                ins = pe.transpose(ps[:, 2, k * T:(k + 1) * T], m_qkv[0:T, k * 128:(k + 1) * 128], C("ident")[0:T, 0:T])
            ins.then_inc(sem("mha_qkT_psum"), 1)
            pe.wait_ge(sem("mha_keys_ready"), u + 1)
            for k in range(KT):
                flat = keys[:, k, :, :].rearrange("p h t -> p (h t)")
                for c in range(g * T // 512):
                    ins = pe.matmul(ps[0:T, 3 + k * (g * T // 512) + c, :], m_qT[:, k, :], flat[:, 512 * c:512 * c + 512],
                                    start=True, stop=True)
            ins.then_inc(sem("mha_scores_psum"), 1)
            pe.wait_ge(sem("mha_exp_ready"), u + 1)
            for j in range(h // 2):
                ins = pe.transpose(psf[:, j * T:(j + 1) * T], scores[:, 2 * j:2 * j + 2, :].rearrange("p h t -> p (h t)"),
                                   C("ident")[0:T, 0:T])
            ins.then_inc(sem("mha_probsT_psum"), 1)
            pe.wait_ge(sem("mha_probsT_ready"), u + 1)
            pe.wait_ge(sem("mha_values_ready"), u + 1)
            for j in range(h // 2):
                ins = pe.matmul(ps[0:T, 2, 2 * d * j:2 * d * (j + 1)], probsT[:, j, :], values[:, j, :], start=True, stop=True)
            ins.then_inc(sem("mha_out_psum"), 1)
            out_tensor(pe, s, attended, w[:, 1536:2048], MHA[s]["piece"])

        def mha_vector(dve, s):
            u = mha_order.index(s)
            m = MHA[s]
            h, d, g, keys, scores, probsT, values = mha_views(s)
            dve.wait_ge(sem("mha_qkv_psum"), u + 1)
            if m["bias"]:
                ins = dve.tensor_tensor(m_qkv, psf[:, 0:768], R(m["bias"], 128), ALU.add)
            else:
                ins = dve.tensor_copy(m_qkv, psf[:, 0:768])
            if m["rope"]:
                link(dve, "dve", ins)
                table, half = C(m["rope"][0])[0:T, :], m["rope"][1]
                r, n = 2 * half, 512 // d
                qk, tmp = cut(m_qkv[0:T, 0:512], n, d), cut(m_tmp[:, 0:n * r], n, r)
                cos, sin = spread(table[:, 0:r], 1, n), spread(table[:, r:2 * r], 1, n)
                link(dve, "dve", dve.tensor_tensor(tmp[:, :, 0:half], qk[:, :, half:r], sin[:, :, 0:half], ALU.mult))
                link(dve, "dve", dve.tensor_tensor(tmp[:, :, half:r], qk[:, :, 0:half], sin[:, :, half:r], ALU.mult))
                link(dve, "dve", dve.tensor_tensor(qk[:, :, 0:r], qk[:, :, 0:r], cos, ALU.mult))
                ins = dve.tensor_tensor(qk[:, :, 0:r], qk[:, :, 0:r], tmp, ALU.add)
            ins.then_inc(sem("mha_qk_ready"), 1)
            dve.wait_ge(sem("mha_qk_ready"), u + 1)
            dve.wait_ge(sem("mha_zeros"), u + 1)
            v = m_qkv[:, 512:768].rearrange("p (j e d) -> p j e d", e=2, d=d)
            dve.tensor_copy(values[0:T, :, 0:d], v[0:T, :, 0, :]).then_inc(sem("mha_half"), 1)
            dve.tensor_copy(values[T:128, :, d:2 * d], v[T:128, :, 1, :]).then_inc(sem("mha_values_ready"), 1)
            dve.wait_ge(sem("mha_qkT_psum"), u + 1)
            dve.tensor_scalar(m_qT, cut(bank(2, KT * T), KT, T), m["scale"], None, ALU.mult).then_inc(sem("mha_half"), 1)
            kT = cut(ps[:, 2, KT * T:2 * KT * T], KT, T)
            dve.tensor_tensor(keys, spread(kT, 2, g), spread(spread(C("heads%d" % d), 1, KT), 3, T), ALU.mult)\
               .then_inc(sem("mha_keys_ready"), 1)
            dve.wait_ge(sem("mha_scores_psum"), u + 1)
            raw = cut(psf[0:T, 3 * 512:3 * 512 + h * T], h, T)
            if m["mask"] == "tri_10000":
                link(dve, "dve", dve.tensor_tensor(scores, raw, spread(C("tri")[0:T, :], 1, h), ALU.mult))
                raw = scores
            link(dve, "dve", dve.tensor_tensor(scores, raw, spread(C(m["mask"])[0:T, :], 1, h), ALU.add))
            link(dve, "dve", dve.tensor_reduce(m_max[:, 0:h], scores, AX, ALU.max))
            dve.tensor_tensor(scores, scores, spread(m_max[:, 0:h], 2, T), ALU.subtract).then_inc(sem("mha_shifted"), 1)
            dve.wait_ge(sem("mha_exp_ready"), u + 1)
            link(dve, "dve", dve.tensor_reduce(m_den[:, 0:h], scores, AX, ALU.add))
            link(dve, "dve", dve.reciprocal(m_den[:, 0:h], m_den[:, 0:h]))
            dve.wait_ge(sem("mha_out_psum"), u + 1)
            dve.tensor_tensor(cut(attended[:, :], h, d), cut(bank(2, D, T), h, d), spread(m_den[:, 0:h], 2, d), ALU.mult)\
               .then_inc(sem("attended"), 1)

        def mha_scalar(act, s):
            u = mha_order.index(s)
            h, d, g, keys, scores, probsT, values = mha_views(s)
            act.wait_ge(sem("mha_shifted"), u + 1)
            act.activation(scores, scores, ACT.Exp).then_inc(sem("mha_exp_ready"), 1)
            act.wait_ge(sem("mha_probsT_psum"), u + 1)
            act.copy(probsT, cut(psf[:, 0:h // 2 * T], h // 2, T)).then_inc(sem("mha_probsT_ready"), 1)
            out_scalar(act, s)

        def mha_pool(pool, s):
            pool.wait_ge(sem("norm_ready"), norm_no[s if s != 8 else 8] + 1)
            pool.memset(m_v, 0.0).then_inc(sem("mha_zeros"), 1)

        def self_attention(s, bias):
            def pe_(pe):
                norm_tensor(pe, s)
                mha_tensor(pe, s, s)

            def dve_(dve):
                norm_vector(dve, s)
                if s == 1:
                    quantise(dve, 2, 3)
                mha_vector(dve, s)
                residual_vector(dve, s, bank(6, D, T), (sem("projected"), outs.index(s) + 1))

            def act_(act):
                norm_scalar(act, s)
                mha_scalar(act, s)

            def pool_(pool):
                norm_pool(pool, s)
                mha_pool(pool, s)
                bias_pool(pool, s, bias)
            return pe_, dve_, act_, pool_

        STAGES = {1: self_attention(1, "a0_out"), 4: self_attention(4, "a1_out"), 7: self_attention(7, "a2_out")}

        def rank_vector(dve, s, n, top, earlier, greater, equal, chosen):
            other, own = spread(s, 1, n), spread(s, 2, n)
            link(dve, "dve", dve.tensor_tensor(greater, other, own, ALU.is_gt))
            link(dve, "dve", dve.tensor_tensor(equal, other, own, ALU.is_equal))
            link(dve, "dve", dve.tensor_tensor(equal, equal, cut(earlier[0:T, :], n, n), ALU.mult))
            link(dve, "dve", dve.tensor_tensor(greater, greater, equal, ALU.add))
            link(dve, "dve", dve.tensor_reduce(chosen, greater, AX, ALU.add))
            link(dve, "dve", dve.tensor_scalar(chosen, chosen, top - 0.5, None, ALU.is_lt))

        f0_e = scratch(0, 9 * T)
        f0_h = cut(scratch(576, 9 * T), 9, T)
        f0_l = scratch(1152, 8, T)
        f0_max, f0_sum, f0_weight = scratch(1160, 1, T), scratch(1161, 1, T), scratch(1162, 1, T)
        f0_exp, f0_chosen = scratch(1168, 8, T), scratch(1176, 8, T)
        f0_greater, f0_equal = cut(scratch(1184, 64, T), 8, 8), cut(scratch(1248, 64, T), 8, 8)
        f0_g, f0_u = psf[:, 0:9 * T], psf[:, 1024:1024 + 9 * T]

        def f0_tensor(pe):
            norm_tensor(pe, 2)
            normT_here(pe, 2)
            for name, at in (("f0_gate", 0), ("f0_up", 1024)):
                weights_here(pe, name)
                for m in range(8):
                    for k in range(KT):
                        ins = pe.matmul(psf[:, at + m * T:at + (m + 1) * T], W(name)[:, k * 1024 + m * 128:k * 1024 + (m + 1) * 128],
                                        xnT[:, k, 0, :], start=k == 0, stop=k == KT - 1)
                ins.then_inc(weights_used, 1)
            weights_here(pe, "f0_routed")
            w = W("f0_routed")
            for i, at in ((0, 512), (1, 1024 + 512)):
                for k in range(KT):
                    ins = pe.matmul(psf[:, at:at + T], w[:, 256 * i + 128 * k:256 * i + 128 * k + 128], xnT[:, k, 0, :],
                                    start=k == 0, stop=k == KT - 1)
            ins.then_inc(sem("f0_hidden_psum"), 1)
            for k in range(KT):
                ins = pe.matmul(ps[0:T, 4, 0:8], xnT[:, k, 0, :], w[:, 768 + 8 * k:776 + 8 * k], start=k == 0, stop=k == KT - 1)
            ins.then_inc(sem("f0_logits_psum"), 1)
            pe.wait_ge(sem("f0_hidden"), since("f0_hidden", 1))
            pe.matmul(bank(5, D, T), f0_h[:, 8, :], w[:, 512:768], start=True, stop=True).then_inc(weights_used, 1)
            weights_here(pe, "f0_down")
            for m in range(8):
                ins = pe.matmul(bank(6, D, T), f0_h[:, m, :], W("f0_down")[:, m * D:(m + 1) * D], start=m == 0, stop=m == 7)
            ins.then_inc(sem("f0_out_psum"), 1)
            pe.wait_ge(sem("f0_out_psum"), since("f0_out_psum", 1))
            pe.sem_inc(weights_used, 1)

        def silu_vector(dve, e, g, u, h, done):
            link(dve, "dve", dve.tensor_scalar(e, e, 1.0, None, ALU.add))
            link(dve, "dve", dve.reciprocal(e, e))
            link(dve, "dve", dve.tensor_tensor(h, e, g, ALU.mult))
            dve.tensor_tensor(h, h, u, ALU.mult).then_inc(done, 1)

        def f0_vector(dve):
            norm_vector(dve, 2)
            quantise(dve, 4, 5, 6, 7, 8)
            dve.wait_ge(sem("f0_exp"), since("f0_exp", 1))
            silu_vector(dve, f0_e, f0_g, f0_u, f0_h.rearrange("p m t -> p (m t)"), sem("f0_hidden"))
            dve.wait_ge(sem("f0_logits_psum"), since("f0_logits_psum", 1))
            link(dve, "dve", dve.tensor_copy(f0_l, ps[0:T, 4, 0:8]))
            link(dve, "dve", dve.tensor_reduce(f0_max, f0_l, AX, ALU.max))
            dve.tensor_scalar(f0_exp, f0_l, f0_max, None, ALU.subtract).then_inc(sem("f0_shifted"), 1)
            rank_vector(dve, f0_l, 8, 2, C("earlier8"), f0_greater, f0_equal, f0_chosen)
            dve.wait_ge(sem("f0_router_exp"), since("f0_router_exp", 1))
            link(dve, "dve", dve.tensor_tensor(f0_exp, f0_exp, f0_chosen, ALU.mult))
            link(dve, "dve", dve.tensor_reduce(f0_sum, f0_exp, AX, ALU.add))
            link(dve, "dve", dve.reciprocal(f0_sum, f0_sum))
            link(dve, "dve", dve.tensor_scalar(f0_exp, f0_exp, f0_sum, None, ALU.mult))
            link(dve, "dve", dve.tensor_reduce(f0_weight, f0_exp, AX, ALU.add))
            dve.wait_ge(sem("f0_out_psum"), since("f0_out_psum", 1))
            link(dve, "dve", dve.tensor_tensor(x[:, :], x[:, :], bank(6, D, T), ALU.add))
            link(dve, "dve", dve.scalar_tensor_tensor(x[:, :], bank(5, D, T), f0_weight, x[:, :], ALU.mult, ALU.add))

        def f0_scalar(act):
            norm_scalar(act, 2)
            act.wait_ge(sem("f0_hidden_psum"), since("f0_hidden_psum", 1))
            act.activation(f0_e, f0_g, ACT.Exp, scale=-1.0).then_inc(sem("f0_exp"), 1)
            act.wait_ge(sem("f0_shifted"), since("f0_shifted", 1))
            act.activation(f0_exp, f0_exp, ACT.Exp).then_inc(sem("f0_router_exp"), 1)

        STAGES[2] = (f0_tensor, f0_vector, f0_scalar, lambda pool: norm_pool(pool, 2))

        f1_lora = scratch(0, 1792)
        f1_up_a, f1_up_b, f1_down_b, f1_down_a = f1_lora[:, 0:256], f1_lora[:, 256:512], f1_lora[:, 512:768], f1_lora[:, 768:1792]
        f1_low = cut(scratch(1792, 8 * T), 8, T)
        f1_e = cut(scratch(2304, 4 * T), 4, T)
        f1_h = cut(scratch(2560, 8 * T), 8, T)
        f1_router = cut(scratch(3072, 16), KT, 8)
        f1_p, f1_chosen = scratch(3088, 8, T), scratch(3096, 8, T)
        f1_max, f1_sum = scratch(3104, 1, T), scratch(3105, 1, T)
        f1_greater, f1_equal = cut(scratch(3112, 64, T), 8, 8), cut(scratch(3176, 64, T), 8, 8)
        f1_down_low = scratch(3240, 128, T)
        f1_down_lowT = scratch(3368, T)

        def f1_tensor(pe):
            weights_here(pe, "f1_gate")
            gate = W("f1_gate")
            for k in range(KT):
                ins = pe.matmul(ps[:, 0, 8 * k:8 * k + 8], gate[0:16, 16 + 128 * k:144 + 128 * k], gate[0:16, 272:280],
                                start=True, stop=True)
            ins.then_inc(sem("f1_delta_psum"), 1)
            norm_tensor(pe, 5)
            normT_here(pe, 5)
            pe.wait_ge(sem("f1_router_ready"), 1)
            pe.sem_inc(weights_used, 1)
            for k in range(KT):
                ins = pe.matmul(ps[0:T, 0, 32:40], xnT[:, k, 0, :], f1_router[:, k, :], start=k == 0, stop=k == KT - 1)
            ins.then_inc(sem("f1_logits_psum"), 1)
            pe.wait_ge(sem("f1_lora_copied"), 1)
            pe.sem_inc(weights_used, 1)
            for k in range(KT):
                ins = pe.matmul(ps[:, 1, 0:T], f1_up_a[:, 128 * k:128 * k + 128], xnT[:, k, 0, :], start=k == 0, stop=k == KT - 1)
            ins.then_inc(sem("f1_low_psum"), 1)
            pe.wait_ge(sem("f1_low_ready"), 1)

            def up(n):
                weights_here(pe, f"f1_experts{n}")
                if n >= 2:
                    pe.wait_ge(sem("f1_hidden"), since("f1_hidden", n - 1))
                for i in range(2):
                    for o in range(2):
                        out = ps[:, 2 + n % 2, (2 * o + i) * T:(2 * o + i + 1) * T]
                        for k in range(KT):
                            a = 768 * i + 256 * k + 128 * o
                            pe.matmul(out, W(f"f1_experts{n}")[:, a:a + 128], xnT[:, k, 0, :], start=k == 0, stop=False)
                        ins = pe.matmul(out, f1_up_b[:, 128 * o:128 * o + 128], f1_low[:, 2 * n + i, :], start=False, stop=True)
                ins.then_inc(sem("f1_gates_psum"), 1)

            def down(n):
                pe.wait_ge(sem("f1_hidden"), since("f1_hidden", n + 1))
                for i in range(2):
                    e = 2 * n + i
                    pe.matmul(ps[0:T, 1, 128:256], f1_h[:, e, :], f1_down_a[:, 128 * e:128 * e + 128], start=e == 0, stop=e == 7,
                              skip_group_check=True)
                if n >= 2:
                    pe.wait_ge(sem("f1_added"), since("f1_added", n - 1))
                for i in range(2):
                    a = 768 * i + 512
                    ins = pe.matmul(ps[0:T, 4 + n % 2, D * i:D * i + D], f1_h[:, 2 * n + i, :], W(f"f1_experts{n}")[:, a:a + D],
                                    start=True, stop=True)
                ins.then_inc(sem("f1_expert_psum"), 1)
                pe.wait_ge(sem("f1_expert_psum"), since("f1_expert_psum", n + 1))
                pe.sem_inc(weights_used, 1)

            up(0)
            for n in range(1, 4):
                up(n)
                down(n - 1)
            down(3)
            pe.wait_ge(sem("f1_down_low_ready"), 1)
            pe.transpose(ps[:, 0, 64:64 + T], f1_down_low, C("ident")[0:T, 0:T]).then_inc(sem("f1_down_lowT_psum"), 1)
            pe.wait_ge(sem("f1_down_lowT_ready"), since("f1_down_lowT_ready", 1))
            pe.matmul(bank(6, D, T), f1_down_lowT, f1_down_b, start=True, stop=True).then_inc(sem("f1_lora_psum"), 1)

        def f1_vector(dve):
            weights_here(dve, "f1_gate")
            dve.wait_ge(sem("f1_delta_psum"), 1)
            dve.scalar_tensor_tensor(f1_router, cut(ps[:, 0, 0:16], KT, 8), 2.0, cut(W("f1_gate")[:, 0:16], KT, 8),
                                     ALU.mult, ALU.add).then_inc(sem("f1_router_ready"), 1)
            norm_vector(dve, 5)
            dve.wait_ge(sem("f1_low_psum"), since("f1_low_psum", 1))
            dve.scalar_tensor_tensor(f1_low, spread(ps[:, 1, 0:T], 1, 8), 2.0, spread(C("heads16"), 2, T), ALU.mult, ALU.mult)\
               .then_inc(sem("f1_low_ready"), 1)
            dve.wait_ge(sem("f1_logits_psum"), since("f1_logits_psum", 1))
            link(dve, "dve", dve.tensor_reduce(f1_max, ps[0:T, 0, 32:40], AX, ALU.max))
            dve.tensor_scalar(f1_p, ps[0:T, 0, 32:40], f1_max, None, ALU.subtract).then_inc(sem("f1_shifted"), 1)
            dve.wait_ge(sem("f1_router_exp"), since("f1_router_exp", 1))
            link(dve, "dve", dve.tensor_reduce(f1_sum, f1_p, AX, ALU.add))
            link(dve, "dve", dve.reciprocal(f1_sum, f1_sum))
            link(dve, "dve", dve.tensor_scalar(f1_p, f1_p, f1_sum, None, ALU.mult))
            rank_vector(dve, f1_p, 8, 2, C("earlier8"), f1_greater, f1_equal, f1_chosen)
            link(dve, "dve", dve.tensor_tensor(f1_p, f1_p, f1_chosen, ALU.mult))
            link(dve, "dve", dve.tensor_reduce(f1_sum, f1_p, AX, ALU.add))
            link(dve, "dve", dve.reciprocal(f1_sum, f1_sum))
            link(dve, "dve", dve.tensor_scalar(f1_p, f1_p, f1_sum, None, ALU.mult))

            def add(n):
                dve.wait_ge(sem("f1_expert_psum"), since("f1_expert_psum", n + 1))
                for i in range(2):
                    ins = dve.scalar_tensor_tensor(x[:, :], ps[0:T, 4 + n % 2, D * i:D * i + D], f1_p[:, 2 * n + i:2 * n + i + 1],
                                                   x[:, :], ALU.mult, ALU.add)
                    if i == 0:
                        link(dve, "dve", ins)
                ins.then_inc(sem("f1_added"), 1)
                dve.wait_ge(sem("f1_added"), since("f1_added", n + 1))

            for n in range(4):
                dve.wait_ge(sem("f1_exp"), since("f1_exp", n + 1))
                b = ps[:, 2 + n % 2, :]
                silu_vector(dve, f1_e[:, 2 * (n % 2):2 * (n % 2) + 2, :], cut(b[:, 0:2 * T], 2, T), cut(b[:, 2 * T:4 * T], 2, T),
                            f1_h[:, 2 * n:2 * n + 2, :], sem("f1_hidden"))
                if n >= 1:
                    add(n - 1)
            dve.wait_ge(sem("f1_expert_psum"), since("f1_expert_psum", 4))
            dve.scalar_tensor_tensor(cut(f1_down_low, 8, 16), cut(ps[0:T, 1, 128:256], 8, 16), 2.0, spread(f1_p, 2, 16),
                                     ALU.mult, ALU.mult).then_inc(sem("f1_down_low_ready"), 1)
            add(3)
            residual_vector(dve, 5, bank(6, D, T), (sem("f1_lora_psum"), since("f1_lora_psum", 1)))

        def f1_scalar(act):
            norm_scalar(act, 5)
            act.wait_ge(sem("f1_shifted"), since("f1_shifted", 1))
            act.activation(f1_p, f1_p, ACT.Exp).then_inc(sem("f1_router_exp"), 1)
            for n in range(4):
                act.wait_ge(sem("f1_gates_psum"), since("f1_gates_psum", n + 1))
                act.activation(f1_e[:, 2 * (n % 2):2 * (n % 2) + 2, :], cut(ps[:, 2 + n % 2, 0:2 * T], 2, T), ACT.Exp, scale=-1.0)\
                   .then_inc(sem("f1_exp"), 1)
            act.wait_ge(sem("f1_down_lowT_psum"), since("f1_down_lowT_psum", 1))
            act.copy(f1_down_lowT, ps[:, 0, 64:64 + T]).then_inc(sem("f1_down_lowT_ready"), 1)

        def f1_pool(pool):
            norm_pool(pool, 5)
            weights_here(pool, "f1_lora")
            pool.tensor_copy(f1_lora, W("f1_lora")).then_inc(sem("f1_lora_copied"), 1)

        STAGES[5] = (f1_tensor, f1_vector, f1_scalar, f1_pool)

        xr = sb("xr", [T, D])
        f2_attn = scratch(0, D, T)
        f2_attnT = cut(scratch(256, KT * T), KT, T)
        f2_hT = cut(scratch(6016, KT * T), KT, T)
        f2_mod, f2_modT = scratch(384, 16, T), scratch(400, T, 16)
        f2_e, f2_h = scratch(512, 512), cut(scratch(1024, 512), 8, T)
        f2_g, f2_u = bank(3), bank(4)

        def f2_tensor(pe):
            norm_tensor(pe, 8.5, xr)
            mha_tensor(pe, 8, 8.5)
            pe.wait_ge(sem("f2_attn_ready"), 1)
            for n in range(KT):
                ins = pe.transpose(ps[:, 7, n * T:(n + 1) * T], f2_attn[:, n * 128:(n + 1) * 128], C("ident")[0:T, 0:T])
            ins.then_inc(sem("f2_attnT_psum"), 1)
            weights_here(pe, "f2_mod")
            w = W("f2_mod")
            pe.wait_ge(sem("f2_attnT_ready"), 1)
            for at, src in ((0, f2_attnT), (16, f2_hT)):
                for k in range(KT):
                    ins = pe.matmul(ps[0:T, 0, at:at + 16], src[:, k, :], w[:, 16 * k:16 * k + 16], start=k == 0, stop=k == KT - 1)
            ins.then_inc(sem("f2_low_psum"), 1)
            pe.wait_ge(sem("f2_mod_ready"), 1)
            pe.transpose(ps[0:16, 1, 0:T], f2_mod, C("ident")[0:T, 0:T]).then_inc(sem("f2_modT_psum"), 1)
            pe.wait_ge(sem("f2_modT_ready"), since("f2_modT_ready", 1))
            weights_here(pe, "f2_gate")
            for m in range(8):
                out = ps[:, 3, m * T:(m + 1) * T]
                ins = pe.matmul(out, w[0:16, 32 + m * 128:32 + (m + 1) * 128], f2_modT, start=True, stop=False)
                if m == 7:
                    ins.then_inc(weights_used, 1)
                for k in range(KT):
                    ins = pe.matmul(out, W("f2_gate")[:, k * 1024 + m * 128:k * 1024 + (m + 1) * 128], f2_hT[:, k, :],
                                    start=False, stop=k == KT - 1)
            ins.then_inc(weights_used, 1)
            weights_here(pe, "f2_up")
            for m in range(8):
                for k in range(KT):
                    ins = pe.matmul(ps[:, 4, m * T:(m + 1) * T], W("f2_up")[:, k * 1024 + m * 128:k * 1024 + (m + 1) * 128],
                                    f2_hT[:, k, :], start=k == 0, stop=k == KT - 1)
            ins.then_inc(sem("f2_hidden_psum"), 1)
            pe.wait_ge(sem("f2_hidden_psum"), since("f2_hidden_psum", 1))
            pe.sem_inc(weights_used, 1)
            pe.wait_ge(sem("f2_hidden"), since("f2_hidden", 1))
            weights_here(pe, "f2_down")
            for m in range(8):
                ins = pe.matmul(bank(6, D, T), f2_h[:, m, :], W("f2_down")[:, m * D:(m + 1) * D], start=m == 0, stop=m == 7)
            ins.then_inc(sem("f2_out_psum"), 1)
            pe.wait_ge(sem("f2_out_psum"), since("f2_out_psum", 1))
            pe.sem_inc(weights_used, 1)

        def f2_vector(dve):
            norm_vector(dve, 8)
            norm_vector(dve, 8.5, xn, xr, RMS_EPS, rms=True)
            mha_vector(dve, 8)
            dve.wait_ge(sem("projected"), outs.index(8) + 1)
            dve.tensor_copy(f2_attn, bank(6, D, T)).then_inc(sem("f2_attn_ready"), 1)
            dve.wait_ge(sem("f2_tanh"), 1)
            dve.scalar_tensor_tensor(f2_mod, f2_mod, 0.1, ps[0:T, 0, 16:32], ALU.mult, ALU.mult).then_inc(sem("f2_mod_ready"), 1)
            dve.wait_ge(sem("f2_exp"), since("f2_exp", 1))
            silu_vector(dve, f2_e, f2_g, f2_u, f2_h.rearrange("p m t -> p (m t)"), sem("f2_hidden"))
            link(dve, "dve", dve.tensor_tensor(x[:, :], x[:, :], xn[:, :], ALU.add))
            residual_vector(dve, 8, bank(6, D, T), (sem("f2_out_psum"), since("f2_out_psum", 1)))

        def f2_scalar(act):
            act.wait_ge(sem("normT_psum"), transposed_no[8.5] + 1)
            src = cut(bank(7, KT * T), KT, T)
            for k in range(KT):
                act.activation(f2_hT[:, k, :], src[:, k, :], ACT.Copy, scale=V("ln2_w")[:, k:k + 1]).then_inc(sem("f2_hT_half"), 1)
            for k in range(KT):
                ins = act.activation(xnT[:, k, :, :], spread(src[:, k, :], 1, 2), ACT.Copy, scale=V("ln1_w")[:, k:k + 1])
            ins.then_inc(sem("normT_ready"), 1)
            mha_scalar(act, 8)
            act.wait_ge(sem("f2_attnT_psum"), 1)
            act.copy(f2_attnT, src).then_inc(sem("f2_attnT_ready"), 1)
            act.wait_ge(sem("f2_low_psum"), since("f2_low_psum", 1))
            act.activation(f2_mod, ps[0:T, 0, 0:16], ACT.Tanh).then_inc(sem("f2_tanh"), 1)
            act.wait_ge(sem("f2_modT_psum"), since("f2_modT_psum", 1))
            act.copy(f2_modT, ps[0:16, 1, 0:T]).then_inc(sem("f2_modT_ready"), 1)
            act.wait_ge(sem("f2_hidden_psum"), since("f2_hidden_psum", 1))
            act.activation(f2_e, f2_g, ACT.Exp, scale=-1.0).then_inc(sem("f2_exp"), 1)

        def f2_pool(pool):
            norm_pool(pool, 8)
            norm_pool(pool, 8.5)
            mha_pool(pool, 8)

        STAGES[8] = (f2_tensor, f2_vector, f2_scalar, f2_pool)

        a3_padded = scratch(0, 4 * (T + 2)).rearrange("p (w k t) -> p w k t", w=2, k=KT)
        a3_v = cut(scratch(264, KT * T), KT, T)
        a3_conv = scratch(392, 4 * T).rearrange("p (w k t) -> p w k t", w=2, k=KT)
        a3_kv, a3_y = cut(scratch(648, KT * T), KT, T), cut(scratch(776, KT * T), KT, T)
        a3_kvN = scratch(904, D, T)
        a3_filter = cut(scratch(1160, 2 * D, FREQ), 2, D)
        a3_left, a3_right = cut(scratch(1672, 2 * D, FREQ), 2, D), cut(scratch(2184, 2 * D, FREQ), 2, D)

        def a3_tensor(pe):
            for i in range(2):
                ins = pe.matmul(ps[0:FREQ, 2, D * i:D * i + D], C("dft")[:, FREQ * i:FREQ * i + FREQ], filter_sb[:, :], start=True, stop=True)
            ins.then_inc(sem("a3_filter_psum"), 1)
            norm_tensor(pe, 10)
            normT_here(pe, 10)
            weights_here(pe, "a3")
            w = W("a3")
            for i in range(3):
                for o in range(KT):
                    for k in range(KT):
                        a = 512 * i + 256 * k + 128 * o
                        ins = pe.matmul(ps[:, 0, (2 * i + o) * T:(2 * i + o + 1) * T], w[:, a:a + 128], xnT[:, k, 0, :],
                                        start=k == 0, stop=k == KT - 1)
            ins.then_inc(sem("a3_qkv_psum"), 1)
            pe.wait_ge(sem("a3_kv_ready"), 1)
            for k in range(KT):
                ins = pe.transpose(ps[0:T, 1, 128 * k:128 * k + 128], a3_kv[:, k, :], C("ident"))
            ins.then_inc(sem("a3_kvN_psum"), 1)
            pe.wait_ge(sem("a3_kvN_ready"), 1)
            for i in range(2):
                ins = pe.matmul(ps[0:FREQ, 3, D * i:D * i + D], C("dft")[0:T, FREQ * i:FREQ * i + FREQ], a3_kvN, start=True, stop=True)
            ins.then_inc(sem("a3_spectrum_psum"), 1)
            pe.wait_ge(sem("a3_product_ready"), 1)
            for o in range(KT):
                for i in range(2):
                    ins = pe.matmul(ps[:, 4, o * T:(o + 1) * T], a3_left[:, i, 128 * o:128 * o + 128],
                                    C("idft")[0:FREQ, T * i:T * i + T], start=i == 0, stop=i == 1)
            ins.then_inc(sem("a3_long_psum"), 1)
            pe.wait_ge(sem("a3_y_ready"), 1)
            for k in range(KT):
                ins = pe.matmul(bank(6, D, T), a3_y[:, k, :], w[:, 1536 + D * k:1536 + D * k + D], start=k == 0, stop=k == KT - 1)
            ins.then_inc(sem("a3_out_psum"), 1)
            pe.wait_ge(sem("a3_out_psum"), since("a3_out_psum", 1))
            pe.sem_inc(weights_used, 1)

        def a3_vector(dve):
            norm_vector(dve, 10)
            dve.wait_ge(sem("a3_filter_psum"), 1)
            link(dve, "dve", dve.tensor_copy(a3_filter, cut(ps[0:FREQ, 2, :], 2, D)))
            dve.wait_ge(sem("a3_padding"), 1)
            dve.wait_ge(sem("a3_qkv_psum"), since("a3_qkv_psum", 1))
            for i in (1, 2, 0):
                for k in range(KT):
                    out = a3_padded[:, i, k, 2:] if i < 2 else a3_v[:, k, :]
                    ins = dve.tensor_scalar(out, ps[:, 0, (2 * i + k) * T:(2 * i + k + 1) * T], V("a3_b")[:, 2 * i + k:2 * i + k + 1],
                                            None, ALU.add)
            link(dve, "dve", ins)
            for i in (1, 0):
                for tap in range(3):
                    for k in range(KT):
                        src, out = a3_padded[:, i, k, tap:tap + T], a3_conv[:, i, k, :]
                        weight = V("conv_w")[:, 6 * i + 3 * k + tap:6 * i + 3 * k + tap + 1]
                        if tap == 0:
                            ins = dve.tensor_scalar(out, src, weight, V("conv_b")[:, 2 * i + k:2 * i + k + 1], ALU.mult, ALU.add)
                        else:
                            ins = dve.scalar_tensor_tensor(out, src, weight, out, ALU.mult, ALU.add)
                    link(dve, "dve", ins)
                if i == 1:
                    dve.tensor_tensor(a3_kv, a3_conv[:, 1, :, :], a3_v, ALU.mult).then_inc(sem("a3_kv_ready"), 1)
            dve.wait_ge(sem("a3_spectrum_psum"), 1)
            spectrum = cut(ps[0:FREQ, 3, :], 2, D)
            dve.tensor_tensor(a3_left, spectrum, spread(a3_filter[:, 0, :], 1, 2), ALU.mult).then_inc(sem("a3_part"), 1)
            dve.tensor_tensor(a3_right[:, 0, :], spectrum[:, 1, :], a3_filter[:, 1, :], ALU.mult).then_inc(sem("a3_part"), 1)
            dve.tensor_tensor(a3_right[:, 1, :], spectrum[:, 0, :], a3_filter[:, 1, :], ALU.mult).then_inc(sem("a3_part"), 1)
            dve.wait_ge(sem("a3_part"), 3)
            link(dve, "dve", dve.tensor_tensor(a3_left[:, 0, :], a3_left[:, 0, :], a3_right[:, 0, :], ALU.subtract))
            dve.tensor_tensor(a3_left[:, 1, :], a3_left[:, 1, :], a3_right[:, 1, :], ALU.add).then_inc(sem("a3_product_ready"), 1)
            dve.wait_ge(sem("a3_kv_ready"), 1)
            dve.wait_ge(sem("a3_long_psum"), 1)
            for k in range(KT):
                ins = dve.scalar_tensor_tensor(a3_y[:, k, :], a3_kv[:, k, :], V("d_skip")[:, k:k + 1], ps[:, 4, k * T:(k + 1) * T],
                                               ALU.mult, ALU.add)
            link(dve, "dve", ins)
            dve.tensor_tensor(a3_y, a3_y, a3_conv[:, 0, :, :], ALU.mult).then_inc(sem("a3_y_ready"), 1)
            residual_vector(dve, 10, bank(6, D, T), (sem("a3_out_psum"), since("a3_out_psum", 1)))

        def a3_scalar(act):
            norm_scalar(act, 10)
            act.wait_ge(sem("a3_kvN_psum"), 1)
            act.copy(a3_kvN, ps[0:T, 1, 0:D]).then_inc(sem("a3_kvN_ready"), 1)

        def a3_pool(pool):
            norm_pool(pool, 10)
            pool.wait_ge(sem("norm_ready"), norm_no[10] + 1)
            pool.memset(a3_padded[:, :, :, 0:2], 0.0).then_inc(sem("a3_padding"), 1)
            bias_pool(pool, 10, "a3_out")

        STAGES[10] = (a3_tensor, a3_vector, a3_scalar, a3_pool)

        f3_s, f3_chosen = scratch(0, 16, T), scratch(16, 16, T)
        f3_sum = scratch(32, 1, T)
        f3_gates, f3_gatesT = scratch(36, NE, T), scratch(64, T, NE)
        f3_greater, f3_equal = cut(scratch(128, 256, T), 16, 16), cut(scratch(384, 256, T), 16, 16)
        f3_h = [cut(scratch(640 + 128 * i, 2 * T, FH), 2, T) for i in range(2)]

        def f3_tensor(pe):
            norm_tensor(pe, 11)
            normT_here(pe, 11)
            weights_here(pe, "f3_gate")
            w = W("f3_gate")
            for k in range(KT):
                ins = pe.matmul(ps[0:T, 0, 0:16], xnT[:, k, 0, :], w[:, 16 * k:16 * k + 16], start=k == 0, stop=k == KT - 1)
            ins.then_inc(sem("f3_logits_psum"), 1)

            def hidden(e):
                weights_here(pe, f"f3_experts{e // 2}")
                if e >= 2:
                    pe.wait_ge(sem("f3_hidden"), e - 1)
                for i in range(2):
                    for k in range(KT):
                        a = 864 * (e % 2) + FF * k + FH * i
                        ins = pe.matmul(ps[0:FH, 1 + e % 2, T * i:T * i + T], W(f"f3_experts{e // 2}")[:, a:a + FH], xnT[:, k, 0, :],
                                        start=k == 0, stop=k == KT - 1)
                ins.then_inc(sem("f3_hidden_psum"), 1)

            def output(e):
                pe.wait_ge(sem("f3_hidden"), e + 1)
                if e >= 2:
                    pe.wait_ge(sem("f3_added"), since("f3_added", e - 1))
                for i in range(2):
                    a = 864 * (e % 2) + 2 * FF + D * i
                    ins = pe.matmul(ps[0:T, 3 + e % 2, 0:D], f3_h[e % 2][:, i, :], W(f"f3_experts{e // 2}")[0:FH, a:a + D],
                                    start=i == 0, stop=i == 1)
                ins.then_inc(sem("f3_expert_psum"), 1)
                if e % 2:
                    pe.wait_ge(sem("f3_expert_psum"), since("f3_expert_psum", e + 1))
                    pe.sem_inc(weights_used, 1)

            hidden(0)
            hidden(1)
            pe.wait_ge(sem("f3_gates_ready"), 1)
            pe.transpose(ps[0:NE, 0, 32:32 + T], f3_gates, C("ident")[0:T, 0:T]).then_inc(sem("f3_gatesT_psum"), 1)
            pe.wait_ge(sem("f3_gatesT_ready"), since("f3_gatesT_ready", 1))
            pe.matmul(bank(6, D, T), f3_gatesT, w[0:NE, 32:288], start=True, stop=True).then_inc(sem("f3_bias_psum"), 1)
            pe.wait_ge(sem("f3_bias_psum"), since("f3_bias_psum", 1))
            pe.sem_inc(weights_used, 1)
            for e in range(NE):
                output(e)
                if e + 2 < NE:
                    hidden(e + 2)

        def f3_vector(dve):
            norm_vector(dve, 11)
            dve.memset(f3_gates[:, 16:NE], 1.0).then_inc(sem("f3_ones"), 1)
            dve.wait_ge(sem("f3_exp"), since("f3_exp", 1))
            link(dve, "dve", dve.tensor_scalar(f3_s, f3_s, 1.0, None, ALU.add))
            link(dve, "dve", dve.reciprocal(f3_s, f3_s))
            link(dve, "dve", dve.tensor_tensor(f3_s, f3_s, R("f3_bias"), ALU.add))
            rank_vector(dve, f3_s, 16, 4, C("earlier16"), f3_greater, f3_equal, f3_chosen)
            link(dve, "dve", dve.tensor_tensor(f3_s, f3_s, f3_chosen, ALU.mult))
            link(dve, "dve", dve.tensor_reduce(f3_sum, f3_s, AX, ALU.add))
            link(dve, "dve", dve.tensor_scalar(f3_sum, f3_sum, 1e-8, None, ALU.max))
            link(dve, "dve", dve.reciprocal(f3_sum, f3_sum))
            dve.wait_ge(sem("f3_ones"), 1)
            dve.tensor_scalar(f3_gates[:, 0:16], f3_s, f3_sum, None, ALU.mult).then_inc(sem("f3_gates_ready"), 1)
            dve.wait_ge(sem("f3_gates_ready"), 1)
            link(dve, "dve", dve.tensor_tensor(x[:, :], x[:, :], xn[:, :], ALU.add))
            residual_vector(dve, 11, bank(6, D, T), (sem("f3_bias_psum"), since("f3_bias_psum", 1)))
            for e in range(NE):
                dve.wait_ge(sem("f3_expert_psum"), since("f3_expert_psum", e + 1))
                dve.scalar_tensor_tensor(x[:, :], ps[0:T, 3 + e % 2, 0:D], f3_gates[:, e:e + 1], x[:, :], ALU.mult, ALU.add)\
                   .then_inc(sem("f3_added"), 1)
                dve.wait_ge(sem("f3_added"), since("f3_added", e + 1))

        def f3_scalar(act):
            norm_scalar(act, 11)
            act.wait_ge(sem("f3_logits_psum"), since("f3_logits_psum", 1))
            act.activation(f3_s, ps[0:T, 0, 0:16], ACT.Exp, scale=-1.0).then_inc(sem("f3_exp"), 1)

            def relu(e):
                act.wait_ge(sem("f3_hidden_psum"), since("f3_hidden_psum", e + 1))
                if e >= 2:
                    act.wait_ge(sem("f3_expert_psum"), since("f3_expert_psum", e - 1))
                for i in range(2):
                    ins = act.activation(f3_h[e % 2][:, i, :], ps[0:FH, 1 + e % 2, T * i:T * i + T], ACT.Relu,
                                         bias=V("f3_b1")[0:FH, 2 * e + i:2 * e + i + 1])
                ins.then_inc(sem("f3_hidden"), 1)

            relu(0)
            relu(1)
            act.wait_ge(sem("f3_gatesT_psum"), since("f3_gatesT_psum", 1))
            act.copy(f3_gatesT, ps[0:NE, 0, 32:32 + T]).then_inc(sem("f3_gatesT_ready"), 1)
            for e in range(2, NE):
                relu(e)

        STAGES[11] = (f3_tensor, f3_vector, f3_scalar, lambda pool: norm_pool(pool, 11))

        ds = bass.ds

        sw_ctxT = [cut(scratch(1024 * i, 1024), KT, CHUNK) for i in range(2)]
        sw_kT = cut(scratch(2048, 1024), KT, CHUNK)
        sw_features = [scratch(3072 + 1024 * i, 1024, TILE) for i in range(2)]
        sw_values = [cut(scratch(5120 + 264 * i, 264, TILE), PAIRS, 33) for i in range(2)]
        sw_key = scratch(5648, D, TILE)
        sw_absmax, sw_step, sw_inv = scratch(5904, 16, TILE), scratch(5920, 16, TILE), scratch(5936, 16, TILE)
        sw_key_both = sb("sw_key_out", [TILE, 2, D])
        sw_key_out = [sw_key_both[:, i, :] for i in range(2)]
        key_views = lambda: cut(sw_key, NH, HD)
        sw_value_absmax = scratch(5952, D)
        sw_value_part = sb("sw_value_part", [128, D])
        value_inv = scratch(5952, D, TILE)
        value_tmp = wide[:, :, :].rearrange("p a n -> p (a n)")
        vals_flat = vals[:, :, :].rearrange("p n d -> p (n d)")
        vals_int = cut(vals_flat[0:TILE, 0:NT * D // 2].bitcast(BF16), NT, D)
        back = vals_flat[:, NT * D // 2:]

        def sweep_first_load(sp, i):
            sp.dma_start(sw_ctxT[i], io["ctxT"][:, :, span(i)]).then_inc(sem(f"ctx_in{i}"), 16)

        def sweep_loads(sp):
            with sp.Fori(0, NC // 2 - 1) as i:
                for ph in range(2):
                    sp.wait_ge(sem("sw_proj_psum"), SUB * (i * 2 + ph + 1))
                    sp.dma_start(sw_ctxT[ph], io["ctxT"][:, :, ds((i * 2 + ph + 2) * CHUNK, CHUNK)]).then_inc(sem(f"ctx_in{ph}"), 16)
            sp.wait_ge(sem("sw_proj_psum"), SUB * (NC - 2))
            sp.dma_start(sw_ctxT[0][:, :, 0:width(NC - 1)], io["ctxT"][:, :, span(NC - 1)]).then_inc(sem("ctx_in0"), 16)

        def sweep_tensor(pe):
            weights_here(pe, "pre")
            weights_here(pe, "pre_features")
            w, wf = W("pre"), W("pre_features")
            sums = ps[:, 6, :]

            def add_sums(buf, start, stop):
                for j in range(PAIRS):
                    ins = pe.matmul(sums[:, 33 * j:33 * j + 33], sw_features[buf][:, 128 * j:128 * j + 128], sw_values[buf][:, j, :],
                                    start=start, stop=stop, skip_group_check=True)
                return ins

            def turn_keys(buf):
                for k in range(KT):
                    ins = pe.transpose(ps[:, 7, TILE * k:TILE * k + TILE], sw_key_out[buf][:, 128 * k:128 * k + 128],
                                       C("ident")[0:TILE, 0:TILE])
                ins.then_inc(sem("sw_keysT_psum"), 1)

            for free in ("sw_features_psum0", "sw_features_psum1", "sw_added", "sw_keysT_psum"):
                pe.sem_inc(sem(free), 1)
            pe.wait_ge(sem("sw_zeros"), 3)
            add_sums(1, True, False)
            pe.wait_ge(sem("constants_in"), 16)

            def chunk(it, ph, n, loaded):
                pe.wait_ge(sem(f"ctx_in{ph}"), loaded * 16)
                for o in range(KT):
                    pe.wait_ge(sem(f"sw_kT{o}"), it + 1)
                    for k in range(KT):
                        ins = pe.matmul(ps[:, o, 0:n * TILE], w[:, 256 * k + 128 * o:256 * k + 128 * o + 128], sw_ctxT[ph][:, k, 0:n * TILE],
                                        start=k == 0, stop=k == KT - 1)
                    ins.then_inc(sem(f"sw_kT_psum{o}"), 1)
                for s in range(n):
                    u = it * SUB + s
                    pe.wait_ge(sem("sw_proj_used"), u + 1)
                    for b, a, m in ((2, 0, 512), (3, 512, 256)):
                        for k in range(KT):
                            ins = pe.matmul(ps[0:TILE, b, 0:m], sw_ctxT[ph][:, k, TILE * s:TILE * s + TILE],
                                            w[:, 512 + 768 * k + a:512 + 768 * k + a + m], start=k == 0, stop=k == KT - 1)
                    ins.then_inc(sem("sw_proj_psum"), 1)
                    for g in range(KT):
                        if s == 0:
                            pe.wait_ge(sem(f"sw_kT{g}"), it + 2)
                        pe.wait_ge(sem(f"sw_features{g}"), u + 1)
                        pe.matmul(ps[0:TILE, 4 + g, :], sw_kT[:, g, TILE * s:TILE * s + TILE], wf, start=True, stop=True)\
                          .then_inc(sem(f"sw_features_psum{g}"), 1)
                    pe.wait_ge(sem("sw_values_ready"), u + 1)
                    add_sums((s + 1) % 2, False, False).then_inc(sem("sw_added"), 1)
                    pe.wait_ge(sem("sw_key_ready"), u + 1)
                    pe.wait_ge(sem("sw_keysT"), u + 1)
                    turn_keys((s + 1) % 2)
            with pe.Fori(0, NC // 2) as i:
                for ph in range(2):
                    chunk(i * 2 + ph, ph, SUB, i + 1)
            chunk(NC - 1, 0, subs(NC - 1), NC // 2 + 1)
            last = (subs(NC - 1) - 1) % 2
            for g in range(KT):
                pe.wait_ge(sem(f"sw_features{g}"), NT + 1)
            pe.wait_ge(sem("sw_values_ready"), NT + 1)
            add_sums(last, False, True).then_inc(sem("sw_added"), 1)
            pe.wait_ge(sem("sw_key_ready"), NT + 1)
            pe.wait_ge(sem("sw_keysT"), NT + 1)
            turn_keys(last)
            pe.wait_ge(sem("sw_features_psum1"), NT + 1)
            pe.sem_inc(weights_used, 2)
            pe.wait_ge(sem("sw_keysT"), NT + 2)

        def sweep_scalar(act):
            for free in ("sw_kT0", "sw_kT1", "sw_features0", "sw_features1", "sw_keysT"):
                act.sem_inc(sem(free), 1)

            def chunk(it, n):
                for o in range(KT):
                    act.wait_ge(sem(f"sw_kT_psum{o}"), it + 1)
                    act.wait_ge(sem(f"sw_features_psum{o}"), it * SUB + 1)
                    act.activation(sw_kT[:, o, 0:n * TILE], ps[:, o, 0:n * TILE], ACT.Identity, bias=V("bk0")[:, o:o + 1])\
                       .then_inc(sem(f"sw_kT{o}"), 1)
                for s in range(n):
                    u = it * SUB + s
                    act.wait_ge(sem("sw_added"), u + 1)
                    for g in range(KT):
                        act.wait_ge(sem(f"sw_features_psum{g}"), u + 2)
                        act.activation(sw_features[s % 2][:, 512 * g:512 * g + 512], ps[0:TILE, 4 + g, :], ACT.Relu)\
                           .then_inc(sem(f"sw_features{g}"), 1)
                    act.wait_ge(sem("sw_keysT_psum"), u + 2)
                    act.copy(keysT[:, :, ds(u * TILE, TILE)], cut(ps[:, 7, 0:KT * TILE], KT, TILE)).then_inc(sem("sw_keysT"), 1)
            with act.Fori(0, NC // 2) as i:
                for ph in range(2):
                    chunk(i * 2 + ph, SUB)
            chunk(NC - 1, subs(NC - 1))
            act.wait_ge(sem("sw_keysT_psum"), NT + 2)
            act.copy(keysT[:, :, NT * TILE:], cut(ps[:, 7, 0:KT * TILE], KT, TILE)).then_inc(sem("sw_keysT"), 1)

        def sweep_vector(dve):
            if runs(0):
                norm_vector(dve, 0)
            for free in ("sw_proj_used", "sw_values_ready", "sw_key_ready"):
                dve.sem_inc(sem(free), 1)
            dve.sem_inc(sem("sw_value_max"), 1)
            dve.wait_ge(sem("sw_zeros"), 4)
            dve.wait_ge(sem("mask_in"), 16)
            key = cut(sw_key, NH, HD)

            def chunk(it, n):
                dve.wait_ge(sem("sw_value_max"), it * 2 + 1)
                for s in range(n):
                    u = it * SUB + s
                    at = [0]

                    def step(ins):
                        at[0] += 1
                        ins.then_inc(sem("sw_step"), 1)
                        dve.wait_ge(sem("sw_step"), u * 5 + at[0])

                    m = mask_sb[:, ds(u, 1)]
                    dve.wait_ge(sem("sw_proj_psum"), u + 1)
                    dve.wait_ge(sem("sw_added"), u + 1)
                    dve.tensor_scalar(sw_values[s % 2][:, :, 0:32], cut(ps[0:TILE, 2, 0:D], PAIRS, 32), m, None, ALU.mult)\
                       .then_inc(sem("sw_part"), 1)
                    dve.tensor_copy(sw_values[s % 2][:, :, 32:33], m.unsqueeze(1).broadcast_to([TILE, PAIRS, 1]))\
                       .then_inc(sem("sw_values_ready"), 1)
                    dve.wait_ge(sem("sw_key_ready"), u + 1)
                    dve.tensor_tensor(sw_key, ps[0:TILE, 2, D:2 * D], R("kv1", TILE)[:, 0:D], ALU.add).then_inc(sem("sw_part"), 1)
                    dve.tensor_tensor(vals[0:TILE, ds(u, 1), :].rearrange("p a d -> p (a d)"), ps[0:TILE, 3, 0:D],
                                      R("kv1", TILE)[:, D:2 * D], ALU.add).then_inc(sem("sw_proj_used"), 1)
                    dve.wait_ge(sem("sw_proj_used"), u + 2)
                    step(dve.tensor_reduce(sw_absmax, key, AX, ALU.max, apply_absolute_value=True))
                    step(dve.tensor_scalar(sw_step, sw_absmax, 1.0 / 127.0, 1e-8, ALU.mult, ALU.max))
                    step(dve.reciprocal(sw_inv, sw_step))
                    step(dve.tensor_tensor(key, key, spread(sw_inv, 2, HD), ALU.mult))
                    step(dve.tensor_scalar(sw_key, sw_key, MAGIC, MAGIC, ALU.add, ALU.subtract))
                    dve.wait_ge(sem("sw_keysT_psum"), u + 1)
                    dve.tensor_tensor(cut(sw_key_out[s % 2], NH, HD), key, spread(sw_step, 2, HD), ALU.mult)\
                       .then_inc(sem("sw_key_ready"), 1)
                dve.tensor_reduce(sw_value_part[:, :], vals[:, ds(it * SUB, n), :].rearrange("p n d -> p d n"), AX, ALU.max,
                                  apply_absolute_value=True).then_inc(sem("sw_value_max"), 1)
                dve.wait_ge(sem("sw_value_max"), it * 2 + 2)
                dve.tensor_tensor(sw_value_absmax, sw_value_absmax, sw_value_part[:, :], ALU.max).then_inc(sem("sw_value_max"), 1)

            with dve.Fori(0, NC // 2) as i:
                for ph in range(2):
                    chunk(i * 2 + ph, SUB)
            chunk(NC - 1, subs(NC - 1))
            dve.wait_ge(sem("sw_key_ready"), NT + 1)
            dve.wait_ge(sem("sw_sums_zeros"), 1)
            dve.wait_ge(sem("sw_added"), NT + 2)
            total = cut(ps[:, 6, 0:33 * PAIRS], PAIRS, 33)
            for e in range(2):
                half = slice(T * e, T * e + T)
                dve.tensor_copy(sweep_sums[half, :, HD * e:HD * e + HD], total[half, :, HD * e:HD * e + HD]).then_inc(sem("sw_sums"), 1)
                dve.tensor_copy(sweep_sums[half, :, 32 + e:33 + e], total[half, :, 32:33]).then_inc(sem("sw_sums"), 1)

        def value_steps(dve):
            dve.wait_ge(sem("value_max"), 1)
            link(dve, "dve", dve.tensor_scalar(value_step[:, :], value_step[:, :], 1.0 / 127.0, 1e-8, ALU.mult, ALU.max))
            link(dve, "dve", dve.reciprocal(value_inv, value_step[0:TILE, :]))

        def quantise(dve, *parts):
            for part in parts:
                a, b = 6 * part, min(6 * part + 6, NT)
                tmp = value_tmp[0:TILE, 0:(b - a) * D]
                link(dve, "dve", dve.tensor_tensor(cut(tmp, b - a, D), vals[0:TILE, a:b, :], spread(value_inv, 1, b - a), ALU.mult))
                link(dve, "dve", dve.tensor_scalar(vals_int[:, a:b, :].rearrange("p n d -> p (n d)"), tmp, MAGIC, MAGIC,
                                                   ALU.add, ALU.subtract))

        def sweep_pool(pool):
            pool.memset(sw_features[1], 0.0).then_inc(sem("sw_zeros"), 1)
            pool.memset(sw_values[1], 0.0).then_inc(sem("sw_zeros"), 1)
            pool.memset(sw_key_out[1], 0.0).then_inc(sem("sw_zeros"), 1)
            pool.memset(sw_value_absmax, 0.0).then_inc(sem("sw_zeros"), 1)
            pool.memset(sweep_sums[:, :, :], 0.0).then_inc(sem("sw_sums_zeros"), 1)
            if runs(0):
                norm_pool(pool, 0)

        SWEEP = (sweep_tensor, sweep_vector, sweep_scalar, sweep_pool)
        SWEEP_LOADS = (sweep_first_load, sweep_loads)

        x0_qT = cut(scratch(0, KT * T), KT, T)
        x0_features = cut(scratch(128, PAIRS * T), PAIRS, T)
        x0_part = scratch(640, D, T).rearrange("p (j e d) -> p j e d", e=2, d=HD)
        x0_den = cut(scratch(896, NH, T), PAIRS, 2)

        def x0_tensor(pe):
            norm_tensor(pe, 0)
            normT_here(pe, 0)
            weights_here(pe, "x0")
            w = W("x0")
            for o in range(KT):
                for k in range(KT):
                    ins = pe.matmul(ps[:, 0, o * T:(o + 1) * T], w[:, 256 * k + 128 * o:256 * k + 128 * o + 128], xnT[:, k, 0, :],
                                    start=k == 0, stop=k == KT - 1)
            ins.then_inc(sem("x0_qT_psum"), 1)
            pe.wait_ge(sem("x0_qT"), 2)
            for j in range(PAIRS):
                ins = pe.matmul(ps[:, 1, j * T:(j + 1) * T], w[:, 512 + 128 * (j % 4):640 + 128 * (j % 4)], x0_qT[:, j // 4, :],
                                start=True, stop=True)
            ins.then_inc(sem("x0_features_psum"), 1)
            pe.wait_ge(sem("x0_features"), 1)
            pe.wait_ge(sem("sw_sums"), 4)
            for j in range(PAIRS):
                ins = pe.matmul(ps[0:T, 2, 34 * j:34 * j + 34], x0_features[:, j, :], sweep_sums[:, j, :], start=True, stop=True)
            ins.then_inc(sem("x0_sums_psum"), 1)
            out_tensor(pe, 0, attended, w[:, 1024:1536], "x0")

        def x0_vector(dve):
            value_steps(dve)
            quantise(dve, 0, 1)
            dve.wait_ge(sem("x0_sums_psum"), 1)
            sums = cut(ps[0:T, 2, 0:34 * PAIRS], PAIRS, 34)
            link(dve, "dve", dve.tensor_copy(x0_den, sums[:, :, 32:34]))
            link(dve, "dve", dve.tensor_tensor(x0_part, R("bv0").rearrange("p (j e d) -> p j e d", e=2, d=HD), spread(x0_den, 3, HD), ALU.mult))
            link(dve, "dve", dve.tensor_tensor(x0_part, x0_part, sums[:, :, 0:32].rearrange("p j (e d) -> p j e d", e=2), ALU.add))
            link(dve, "dve", dve.tensor_scalar(x0_den, x0_den, 1e-8, None, ALU.add))
            link(dve, "dve", dve.reciprocal(x0_den, x0_den))
            dve.tensor_tensor(attended[:, :].rearrange("p (j e d) -> p j e d", e=2, d=HD), x0_part, spread(x0_den, 3, HD), ALU.mult)\
               .then_inc(sem("attended"), 1)
            residual_vector(dve, 0, bank(6, D, T), (sem("projected"), outs.index(0) + 1))

        def x0_scalar(act):
            norm_scalar(act, 0)
            act.wait_ge(sem("x0_qT_psum"), since("x0_qT_psum", 1))
            for o in range(KT):
                act.activation(x0_qT[:, o, :], ps[:, 0, o * T:(o + 1) * T], ACT.Identity, bias=V("bq0")[:, o:o + 1])\
                   .then_inc(sem("x0_qT"), 1)
            act.wait_ge(sem("x0_features_psum"), 1)
            act.activation(x0_features, cut(bank(1), PAIRS, T), ACT.Relu).then_inc(sem("x0_features"), 1)
            out_scalar(act, 0)

        def x0_pool(pool):
            pool.wait_ge(sem("sw_value_max"), 2 * NC + 1)
            pool.partition_all_reduce(value_step[:, :], sw_value_absmax, 128, bass.bass_isa.ReduceOp.max).then_inc(sem("value_max"), 1)
            bias_pool(pool, 0, "bo0")

        STAGES[0] = (x0_tensor, x0_vector, x0_scalar, x0_pool)

        x1_q = back[0:T, 0:D]
        x1_absmax, x1_step, x1_inv = back[0:T, 256:272], back[0:T, 272:288], back[0:T, 288:304]
        x1_row_step = back[:, 304:312]
        x1_queries = back[:, 320:1344]
        x1_tile_q, x1_tile_step = back[:, 1344:1472], back[:, 1472:1473]
        x1_max, x1_top, x1_bias = back[:, 1480:1480 + NC], back[:, 1494:1495], back[:, 1495:1496]
        x1_sum, x1_total = back[:, 1500:1500 + NC], back[:, 1514:1515]
        x1_ident = back[:, 1520:1584].bitcast(BF16)
        x1_probs = [back[:, 1600 + 256 * i:1856 + 256 * i].bitcast(BF16) for i in range(2)]
        x1_probsT = [cut(back[0:TILE, 2112 + 256 * i:2368 + 256 * i].bitcast(BF16), SUB, 128) for i in range(2)]
        x1_out = back[:, 2624:2880]
        keys_flat = keysT[:, :, :].rearrange("p k n -> p (k n)")

        def x1_tensor(pe):
            norm_tensor(pe, 3)
            normT_here(pe, 3)
            weights_here(pe, "x1")
            w = W("x1")
            for k in range(KT):
                ins = pe.matmul(bank(0, D, T), xnT[:, k, 0, :], w[:, D * k:D * k + D], start=k == 0, stop=k == KT - 1)
            ins.then_inc(sem("x1_q_psum"), 1)
            pe.wait_ge(sem("x1_q_ready"), 1)
            for k in range(KT):
                ins = pe.transpose(ps[:, 1, k * T:(k + 1) * T], x1_q[:, 128 * k:128 * k + 128], C("ident")[0:T, 0:T])
            ins.then_inc(sem("x1_qT_psum"), 1)
            pe.wait_ge(sem("x1_ident_ready"), 1)

            def scores(j, c):
                if c == 0:
                    pe.wait_ge(sem("x1_tile_ready"), since("x1_tile_ready", j + 1))
                if c >= 2:
                    pe.wait_ge(sem("x1_scores"), since("x1_scores", j * NC + (c - 1)))
                pe.matmul(ps[:, c % 2, 0:width(c)], x1_tile_q, keys_flat[:, ds((j & 4) * ((TILE + SK) // 4) + (TILE + c * CHUNK), width(c))],
                          start=True, stop=True).then_inc(sem("x1_scores_psum"), 1)

            def turn(j, c):
                pe.wait_ge(sem("x1_probs_ready"), j * NC + (c + 1))
                if c >= 2:
                    pe.wait_ge(sem("x1_probsT_ready"), j * NC + (c - 1))
                out = ps[0:TILE, 2 + c % 2, 0:256].bitcast(BF16)
                for s in range(subs(c)):
                    ins = pe.transpose(out[:, 128 * s:128 * s + 128], x1_probs[c % 2][:, TILE * s:TILE * s + TILE], x1_ident)
                ins.then_inc(sem("x1_probsT_psum"), 1)

            def weigh(j, c):
                pe.wait_ge(sem("x1_probsT_ready"), j * NC + (c + 1))
                for s in range(subs(c)):
                    ins = pe.matmul(ps[:, 4, 0:32], x1_probsT[c % 2][:, s, :],
                                    vals_int[:, SUB * c + s, ds(j * 32, 32)], start=c == 0 and s == 0,
                                    stop=c == NC - 1 and s == subs(c) - 1)
                ins.then_inc(sem("x1_weighed"), 1)

            def step(scored, weighed, first=False):
                for c in range(NC + 1):
                    if scored is not None and c < NC:
                        scores(scored, c)
                    if weighed is not None:
                        if c < NC:
                            turn(weighed, c)
                        if c == 1 and not first:
                            pe.wait_ge(sem("x1_tile_done"), weighed)
                        if c >= 1:
                            weigh(weighed, c - 1)

            step(0, None)
            step(1, 0, first=True)
            with pe.Fori(1, PAIRS - 1) as j:
                j = pe.snap(j, max_val=PAIRS - 2)
                step(pe.snap(j + 1, max_val=PAIRS - 1), j)
            step(None, PAIRS - 1)
            out_tensor(pe, 3, attended, w[:, 512:1024], "x1")

        def x1_vector(dve):
            norm_vector(dve, 3)
            q = cut(x1_q, NH, HD)
            dve.wait_ge(sem("x1_q_psum"), since("x1_q_psum", 1))
            link(dve, "dve", dve.tensor_tensor(x1_q, bank(0, D, T), R("q1"), ALU.add))
            link(dve, "dve", dve.tensor_scalar(x1_q, x1_q, 0.25, None, ALU.mult))
            link(dve, "dve", dve.tensor_reduce(x1_absmax, q, AX, ALU.max, apply_absolute_value=True))
            link(dve, "dve", dve.tensor_scalar(x1_step, x1_absmax, 1.0 / 127.0, 1e-8, ALU.mult, ALU.max))
            link(dve, "dve", dve.reciprocal(x1_inv, x1_step))
            link(dve, "dve", dve.tensor_tensor(q, q, spread(x1_inv, 2, HD), ALU.mult))
            dve.tensor_scalar(x1_q, x1_q, MAGIC, MAGIC, ALU.add, ALU.subtract).then_inc(sem("x1_q_ready"), 1)
            by_pair = cut(x1_step, PAIRS, 2)
            for e in range(2):
                link(dve, "dve", dve.tensor_copy(x1_row_step[T * e:T * e + T, :], by_pair[:, :, e]))
            dve.wait_ge(sem("x1_qT_psum"), 1)
            link(dve, "dve", dve.tensor_tensor(x1_queries.rearrange("p (k h t) -> p k h t", k=KT, h=8),
                                               spread(cut(bank(1, KT * T), KT, T), 2, 8),
                                               spread(spread(C("heads16"), 1, KT), 3, T), ALU.mult))

            def score(j, c, weighed):
                dve.wait_ge(sem("x1_scores_psum"), since("x1_scores_psum", j * NC + (c + 1)))
                if weighed is not None:
                    dve.wait_ge(sem("x1_probs_ready"), weighed * NC + (c + 1))
                dve.tensor_scalar(S[:, span(c)], ps[:, c % 2, 0:width(c)], 1.0, NEG, ALU.mult, ALU.max,
                                  accum_out=x1_max[:, c:c + 1]).then_inc(sem("x1_scores"), 1)

            def exp_bias(j):
                dve.tensor_copy(x1_tile_step, x1_row_step[:, ds(j, 1)]).then_inc(sem("x1_step"), 1)
                dve.wait_ge(sem("x1_scores"), since("x1_scores", j * NC + NC))
                dve.tensor_reduce(x1_top, x1_max, AX, ALU.max).then_inc(sem("x1_step"), 1)
                dve.wait_ge(sem("x1_step"), j * 3 + 2)
                dve.tensor_tensor(x1_bias, x1_top, x1_tile_step, ALU.mult).then_inc(sem("x1_step"), 1)
                dve.wait_ge(sem("x1_step"), j * 3 + 3)
                dve.tensor_scalar(x1_bias, x1_bias, -1.0, LN255, ALU.mult, ALU.add).then_inc(sem("x1_bias_ready"), 1)

            def round_probs(j, c):
                dve.wait_ge(sem("x1_exp"), since("x1_exp", j * NC + (c + 1)))
                if c >= 2:
                    dve.wait_ge(sem("x1_probsT_psum"), since("x1_probsT_psum", j * NC + (c - 1)))
                dve.tensor_scalar(x1_probs[c % 2][:, 0:width(c)], S[:, span(c)], MAGIC, MAGIC, ALU.add, ALU.subtract)\
                   .then_inc(sem("x1_probs_ready"), 1)

            def inverse_sum(j):
                dve.tensor_reduce(x1_total, x1_sum, AX, ALU.add).then_inc(sem("x1_total"), 1)
                dve.wait_ge(sem("x1_total"), j * 2 + 1)
                dve.reciprocal(x1_total, x1_total).then_inc(sem("x1_total"), 1)

            def finish(j):
                dve.wait_ge(sem("x1_total"), j * 2 + 2)
                dve.wait_ge(sem("x1_weighed"), since("x1_weighed", j * NC + NC))
                dve.tensor_scalar(x1_out[:, ds(j * 32, 32)], ps[:, 4, 0:32], x1_total, None, ALU.mult).then_inc(sem("x1_tile_done"), 1)

            def step(scored, weighed):
                if scored is not None:
                    dve.tensor_copy(x1_tile_q, x1_queries[:, ds(scored * 128, 128)]).then_inc(sem("x1_tile_ready"), 1)
                for c in range(NC + 1):
                    if weighed is not None and c < NC:
                        round_probs(weighed, c)
                    if scored is not None and c >= 1:
                        score(scored, c - 1, weighed)
                if weighed is not None:
                    inverse_sum(weighed)
                if scored is not None:
                    exp_bias(scored)
                if weighed is not None:
                    finish(weighed)

            step(0, None)
            step(1, 0)
            with dve.Fori(1, PAIRS - 1) as j:
                j = dve.snap(j, max_val=PAIRS - 2)
                step(j + 1, j)
            step(None, PAIRS - 1)
            dve.wait_ge(sem("x1_tile_done"), PAIRS)
            out, step = cut(attended[:, :], PAIRS, 32), cut(value_step[:, :], PAIRS, 32)
            by_tile = cut(x1_out, PAIRS, 32)
            for e in range(2):
                rows_, cols_ = slice(T * e, T * e + T), slice(HD * e, HD * e + HD)
                ins = dve.tensor_tensor(out[:, :, cols_], by_tile[rows_, :, cols_], step[rows_, :, cols_], ALU.mult)
            ins.then_inc(sem("attended"), 1)
            residual_vector(dve, 3, bank(6, D, T), (sem("projected"), outs.index(3) + 1))

        def x1_scalar(act):
            norm_scalar(act, 3)
            act.wait_ge(sem("x1_q_psum"), since("x1_q_psum", 1))
            act.copy(x1_ident, C("ident")).then_inc(sem("x1_ident_ready"), 1)
            with act.Fori(0, PAIRS) as j:

                def exp(c):
                    chunk = S[:, span(c)]
                    act.activation(chunk, chunk, ACT.Exp, scale=x1_tile_step, bias=x1_bias, accum_out=x1_sum[:, c:c + 1])\
                       .then_inc(sem("x1_exp"), 1)

                def copy(c):
                    act.wait_ge(sem("x1_probsT_psum"), since("x1_probsT_psum", j * NC + (c + 1)))
                    if c >= 2:
                        act.wait_ge(sem("x1_weighed"), since("x1_weighed", j * NC + (c - 1)))
                    act.copy(x1_probsT[c % 2][:, 0:subs(c), :], cut(ps[0:TILE, 2 + c % 2, 0:64 * subs(c)].bitcast(BF16), subs(c), 128))\
                       .then_inc(sem("x1_probsT_ready"), 1)

                act.wait_ge(sem("x1_bias_ready"), since("x1_bias_ready", j + 1))
                for c in range(NC):
                    exp(c)
                    if c >= 2:
                        copy(c - 2)
                copy(NC - 2)
                copy(NC - 1)
            out_scalar(act, 3)

        def x1_pool(pool):
            norm_pool(pool, 3)
            bias_pool(pool, 3, "out1")

        STAGES[3] = (x1_tensor, x1_vector, x1_scalar, x1_pool)

        x2_cat = cut(row_biases[:, 0:2 * NQ * T], 2 * NQ, T)
        x2_queries = row_biases[:, 2048:3072]
        x2_wk = cut(row_biases[:, 3072:3328], KT, GD)
        x2_wv = cut(row_biases[:, 3328:3584], KT, GD)
        x2_keys = sb("x2_keys", [128, 2, CHUNK])
        x2_dev = wide
        x2_probsT = sb("x2_probsT", [TILE, 2, 512])
        x2_mix = sweep_sums[:, :, :].rearrange("p j d -> p (j d)")[:, 0:D]
        x2_mixT = cut(value_step[:, :], KT, 128)
        x2_q = sb("x2_q", [128, 128])
        x2_const, x2_tile_const = sb("x2_const", [128, GROUPS]), sb("x2_tile_const", [128, 1])
        x2_max, x2_sum, x2_small = sb("x2_max", [128, NC + 1]), sb("x2_sum", [128, NC + 1]), sb("x2_small", [128, 4])
        x2_eps = sb("x2_eps", [128, 1])
        SCALE2 = float(1 / np.sqrt(GD))
        x2_lnT = cut(scratch(5120, KT * T), KT, T)
        x2_in = scratch(5248, 512).rearrange("p (w k t) -> p w k t", w=4, k=KT)
        x2_inv_scale = scratch(5760, 8)
        x2_raw = scratch(0, 2560)
        x2_square = scratch(2560, 2560)
        x2_v = scratch(2560, 1024, T)
        x2_s, x2_stat = cut(scratch(3584, 512), GROUPS, T), scratch(5776, 16)
        x2_coreT = scratch(4096, 1024, T)
        x2_sq_cols = ((0, 1024, 0), (1024, 1536, 1), (1536, 2560, 2))
        x2_mean_w = scratch(5800, 16)
        x2_std = scratch(5816, 256, 10)
        x2_low = [sw_key_both[:, i, :].bitcast(BF16) for i in range(2)]
        x2_mean = sw_value_part[:, 0:64].bitcast(BF16)

        def high_half(c):
            return x2_dev[:, c % 3, 0:width(c)].bitcast(BF16).rearrange("p (n h) -> p n h", h=2)[:, :, 1]

        ctxT = keysT[:, :, TILE:]
        ctxN = vals[0:TILE, :, :]

        def x2_tensor(pe):
            norm_tensor(pe, 6.5, xr)
            pe.wait_ge(sem("x2_in_ready"), 1)

            blocks = [(name, which, b) for name, which in (("x2_q0", 0), ("x2_q1", 0), ("x2_k", 1), ("x2_qx0", 2), ("x2_qx1", 2))
                      for b in range(2)]

            def turn_block(j):
                pe.wait_ge(sem("x2_block"), j + 1)
                for h in range(4):
                    ins = pe.transpose(psf[:, 256 * j + T * h:256 * j + T * h + T], wide[0:T, j % 3, 128 * h:128 * h + 128], C("ident")[0:T, 0:T])
                    if h == 0 and j % 2:
                        ins.then_inc(weights_used, 1)
                ins.then_inc(sem("x2_block_turned"), 1)

            for j, (name, which, b) in enumerate(blocks):
                weights_here(pe, name)
                if j >= 2:
                    pe.wait_ge(sem("x2_block"), j - 1)
                for k in range(KT):
                    ins = pe.matmul(ps[0:T, 5 + j % 2, :], x2_in[:, which, k, :], W(name)[:, 1024 * k + 512 * b:1024 * k + 512 * b + 512],
                                    start=k == 0, stop=k == KT - 1)
                ins.then_inc(sem("x2_block_psum"), 1)
                if j >= 1:
                    turn_block(j - 1)
            turn_block(len(blocks) - 1)
            weights_here(pe, "x2_v")
            for c in range(2):
                for k in range(KT):
                    ins = pe.matmul(ps[0:T, 5 + c, :], x2_in[:, 3, k, :], W("x2_v")[:, 1024 * k + 512 * c:1024 * k + 512 * c + 512],
                                    start=k == 0, stop=k == KT - 1)
            ins.then_inc(sem("x2_heads_psum"), 1)
            for c, copied in enumerate((1, 1, 2, 3, 3)):
                pe.wait_ge(sem("x2_raw"), since("x2_raw", copied))
                pe.matmul(bank(c), C("centre128"), x2_raw[:, 512 * c:512 * c + 512], start=True, stop=True).then_inc(sem("x2_centre_psum"), 1)
            pe.wait_ge(sem("x2_heads_psum"), since("x2_heads_psum", 1))
            pe.sem_inc(weights_used, 1)
            for c in range(10):
                pe.wait_ge(sem("x2_square"), since("x2_square", c // 2 + 1))
                ins = pe.matmul(ps[0:10, 7, 0:256], C("mean_band")[:, 9 - c:19 - c], x2_square[:, 256 * c:256 * c + 256], start=c == 0, stop=c == 9)
            ins.then_inc(sem("x2_var_psum"), 1)
            pe.wait_ge(sem("x2_centred"), 5)
            pe.wait_ge(sem("x2_inv_std"), 1)
            for c in range(10):
                ins = pe.matmul(psf[:, 256 * c:256 * c + 256], C("ident")[0:10, c:c + 1].broadcast_to([10, 128]), x2_std, start=True, stop=True)
            ins.then_inc(sem("x2_inv_psum"), 1)
            pe.wait_ge(sem("x2_normed"), 1)
            for g in range(GROUPS):
                ins = pe.matmul(ps[:, 7, T * g:T * g + T], x2_raw[:, 128 * g:128 * g + 128], x2_raw[:, 1024 + T * g:1024 + T * g + T],
                                start=True, stop=True)
            ins.then_inc(sem("x2_core_psum"), 1)
            for g in range(GROUPS):
                ins = pe.matmul(ps[:, 4, g:g + 1], x2_raw[:, 1536 + 128 * g:1536 + 128 * g + 128], V("head_ln")[:, 7:8], start=True, stop=True)
            ins.then_inc(sem("x2_const_psum"), 1)
            pe.wait_ge(sem("x2_core_probs"), 1)
            for g in range(GROUPS):
                ins = pe.transpose(psf[0:T, 128 * g:128 * g + 128], x2_s[:, g, :], C("ident"))
            ins.then_inc(sem("x2_coreT_psum"), 1)
            pe.wait_ge(sem("x2_coreT"), since("x2_coreT", 1))
            for g in range(GROUPS):
                ins = pe.matmul(psf[:, 1024 + 128 * g:1024 + 128 * g + 128], x2_v[:, GD * g:GD * g + GD], x2_coreT[:, 128 * g:128 * g + 128],
                                start=True, stop=True)
            ins.then_inc(sem("x2_core_out_psum"), 1)
            pe.wait_ge(sem("x2_core_done"), since("x2_core_done", 1))
            pe.wait_ge(sem("ctx_reloaded"), 32)

            def keys(g, c):
                if c == 0:
                    pe.wait_ge(sem("x2_wk_ready"), g + 1)
                    if not (isinstance(g, int) and g == 0):
                        pe.wait_ge(sem("x2_keys_ready"), g * NC)
                if c >= 3:
                    pe.wait_ge(sem("x2_keys_ready"), g * NC + (c - 2))
                for k in range(KT):
                    ins = pe.matmul(ps[:, c % 3, 0:width(c)], x2_wk[:, k, :], ctxT[:, k, span(c)],
                                    start=k == 0, stop=k == KT - 1)
                ins.then_inc(sem("x2_keys_psum"), 1)

            def variance(g, c):
                pe.wait_ge(sem("x2_square_low"), g * NC + (c + 1))
                if c >= 1:
                    pe.wait_ge(sem("x2_refined"), (g * NC + c) * 3 - 2)
                pe.matmul(ps[:, 3, 0:width(c)], x2_mean, high_half(c), start=True, stop=False)
                pe.matmul(ps[:, 3, 0:width(c)], x2_mean, x2_low[c % 2][:, 0:width(c)], start=False, stop=True)\
                  .then_inc(sem("x2_keys_var"), 1)

            def scores(g, c):
                pe.wait_ge(sem("x2_keys_ready"), g * NC + (c + 1))
                if c == 0:
                    pe.wait_ge(sem("x2_tile_ready"), since("x2_tile_ready", g + 1))
                else:
                    pe.wait_ge(sem("x2_scores"), since("x2_scores", g * NC + c))
                pe.matmul(ps[:, 4, 0:width(c)], x2_q[:, :], x2_keys[:, c % 2, 0:width(c)], start=True, stop=True).then_inc(sem("x2_scores_psum"), 1)

            def turn(g, c):
                pe.wait_ge(sem("x2_exp"), since("x2_exp", g * NC + (c + 1)))
                if c >= 2:
                    pe.wait_ge(sem("x2_probsT_ready"), since("x2_probsT_ready", g * NC + (c - 1)))
                for s in range(subs(c)):
                    a = CHUNK * c + TILE * s
                    ins = pe.transpose(ps[0:TILE, 5 + 2 * (c % 2), 128 * s:128 * s + 128], S[:, a:a + TILE], C("ident"))
                ins.then_inc(sem("x2_probsT_psum"), 1)

            def weigh(g, c):
                pe.wait_ge(sem("x2_probsT_ready"), since("x2_probsT_ready", g * NC + (c + 1)))
                for s in range(subs(c)):
                    ins = pe.matmul(bank(6, D), x2_probsT[:, c % 2, 128 * s:128 * s + 128], ctxN[:, SUB * c + s, :],
                                    start=c == 0 and s == 0, stop=c == NC - 1 and s == subs(c) - 1)
                ins.then_inc(sem("x2_weighed"), 1)

            def turn_mix(g):
                pe.wait_ge(sem("x2_mix"), g + 1)
                for k in range(KT):
                    ins = pe.transpose(ps[:, 6, D + 128 * k:D + 128 * k + 128], x2_mix[:, 128 * k:128 * k + 128], C("ident"))
                ins.then_inc(sem("x2_mixT_psum"), 1)

            def values(g):
                pe.wait_ge(sem("x2_mixT"), g + 1)
                pe.wait_ge(sem("x2_wv_ready"), g + 1)
                for k in range(KT):
                    ins = pe.matmul(ps[:, 6, D:D + 128], x2_wv[:, k, :], x2_mixT[:, k, :], start=k == 0, stop=k == KT - 1)
                ins.then_inc(sem("x2_cross_psum"), 1)

            def step(scored, weighed, done, ahead):
                for c in range(NC + 3):
                    if scored is not None:
                        if (c >= 2 or weighed is None) and c < NC:
                            keys(scored, c)
                        if 1 <= c <= NC:
                            variance(scored, c - 1)
                        if c >= 3:
                            scores(scored, c - 3)
                    if done is not None and c == 1:
                        values(done)
                    if weighed is not None and c < NC:
                        turn(weighed, c)
                    if done is not None and c == 0:
                        turn_mix(done)
                    if weighed is not None and 2 <= c < NC + 2:
                        if done is not None and c == 2:
                            pe.wait_ge(sem("x2_cross_done"), done + 1)
                        weigh(weighed, c - 2)
                if ahead is not None:
                    keys(ahead, 0)
                    keys(ahead, 1)

            pe.wait_ge(sem("x2_mean_ready"), 1)
            step(0, None, None, 1)
            step(1, 0, None, 2)
            with pe.Fori(1, GROUPS - 2) as g:
                step(g + 1, g, g - 1, g + 2)
            step(GROUPS - 1, GROUPS - 2, GROUPS - 3, None)
            step(None, GROUPS - 1, GROUPS - 2, None)
            turn_mix(GROUPS - 1)
            values(GROUPS - 1)
            pe.wait_ge(sem("x2_cross_done"), GROUPS)
            pe.sem_inc(weights_used, 2)
            pe.wait_ge(sem("x2_cat_ready"), 1)
            for n in range(2 * NQ):
                name = f"x2_proj{n // 8}"
                if n % 8 == 0:
                    weights_here(pe, name)
                ins = pe.matmul(bank(0, D, T), x2_cat[:, n, :], W(name)[:, D * (n % 8):D * (n % 8) + D], start=n == 0, stop=n == 2 * NQ - 1)
                if n % 8 == 7 and n < 2 * NQ - 1:
                    ins.then_inc(weights_used, 1)
            ins.then_inc(sem("x2_out_psum"), 1)
            pe.wait_ge(sem("x2_out_psum"), since("x2_out_psum", 1))
            pe.sem_inc(weights_used, 1)

        def x2_vector(dve):
            norm_vector(dve, 6)
            norm_vector(dve, 6.5, xn, xr)
            link(dve, "dve", dve.memset(x2_eps[:, :], LN_EPS))
            link(dve, "dve", dve.reciprocal(x2_inv_scale, V("in_scale")))
            normT_here(dve, 6.5)
            by_use = lambda v: cut(v, 4, KT)
            flat_in = scratch(5248, 512)
            y = spread(x2_lnT, 1, 4)
            wide = scratch(0, 512).rearrange("p (w k t) -> p w k t", w=4, k=KT)
            link(dve, "dve", dve.tensor_tensor(wide, y, spread(by_use(x2_inv_scale), 3, T), ALU.mult))
            round_vector(dve, 512, 0, flat_in)
            dve.tensor_tensor(x2_in, x2_in, spread(by_use(V("in_scale")), 3, T), ALU.mult).then_inc(sem("x2_in_ready"), 1)
            for c in range(5):
                dve.wait_ge(sem("x2_centre_psum"), since("x2_centre_psum", c + 1))
                dve.tensor_copy(x2_raw[:, 512 * c:512 * c + 512], bank(c)).then_inc(sem("x2_centred"), 1)
            weights_here(dve, "x2_kx")
            wk = cut(W("x2_kx"), KT * GROUPS, GD)
            link(dve, "dve", dve.tensor_reduce(x2_mean_w, wk, AX, ALU.add))
            link(dve, "dve", dve.tensor_scalar(x2_mean_w, x2_mean_w, 1.0 / GD, None, ALU.mult))
            link(dve, "dve", dve.tensor_tensor(wk, wk, spread(x2_mean_w, 2, GD), ALU.subtract))
            dve.wait_ge(sem("x2_std"), since("x2_std", 1))
            dve.reciprocal(x2_std, x2_std).then_inc(sem("x2_inv_std"), 1)
            dve.wait_ge(sem("x2_inv_psum"), since("x2_inv_psum", 1))
            link(dve, "dve", dve.tensor_tensor(x2_raw, x2_raw, psf[:, 0:2560], ALU.mult))
            for a, b, i in x2_sq_cols:
                ins = dve.tensor_scalar(x2_raw[:, a:b], x2_raw[:, a:b], V("head_ln")[:, 2 * i:2 * i + 1], V("head_ln")[:, 2 * i + 1:2 * i + 2],
                                        ALU.mult, ALU.add)
            ins.then_inc(sem("x2_normed"), 1)
            dve.wait_ge(sem("x2_normed"), 1)
            link(dve, "dve", dve.tensor_scalar(x2_queries, x2_raw[:, 1536:2560], V("head_ln")[:, 6:7], None, ALU.mult))
            dve.wait_ge(sem("x2_const_psum"), since("x2_const_psum", 1))
            link(dve, "dve", dve.tensor_copy(x2_const[:, :], ps[:, 4, 0:GROUPS]))
            dve.wait_ge(sem("x2_core_psum"), since("x2_core_psum", 1))
            raw = cut(bank(7), GROUPS, T)
            link(dve, "dve", dve.tensor_reduce(x2_stat[:, 0:8], raw, AX, ALU.max))
            dve.tensor_tensor(x2_s, raw, spread(x2_stat[:, 0:8], 2, T), ALU.subtract).then_inc(sem("x2_core_shifted"), 1)
            dve.wait_ge(sem("x2_core_exp"), since("x2_core_exp", 1))
            link(dve, "dve", dve.tensor_reduce(x2_stat[:, 8:16], x2_s, AX, ALU.add))
            link(dve, "dve", dve.reciprocal(x2_stat[:, 8:16], x2_stat[:, 8:16]))
            dve.tensor_tensor(x2_s, x2_s, spread(x2_stat[:, 8:16], 2, T), ALU.mult).then_inc(sem("x2_core_probs"), 1)
            weights_here(dve, "x2_vx")
            dve.wait_ge(sem("x2_core_done"), since("x2_core_done", 1))
            wks, wvs = cut(W("x2_kx"), KT, 1024), cut(W("x2_vx"), KT, 1024)

            def key_weights(g):
                dve.tensor_copy(x2_wk, wks[:, :, ds(g * GD, GD)]).then_inc(sem("x2_wk_ready"), 1)

            def tile(g):
                dve.tensor_copy(x2_tile_const[:, :], x2_const[:, ds(g, 1)]).then_inc(sem("x2_tile_const_ready"), 1)
                dve.tensor_copy(x2_q[:, :], x2_queries[:, ds(g * 128, 128)]).then_inc(sem("x2_tile_ready"), 1)

            def low_half(g, c):
                dve.wait_ge(sem("x2_squared"), g * NC + (c + 1))
                if c >= 2:
                    dve.wait_ge(sem("x2_keys_var"), g * NC + (c - 1))
                dve.tensor_tensor(x2_low[c % 2][:, 0:width(c)], x2_dev[:, c % 3, 0:width(c)], high_half(c), ALU.subtract)\
                   .then_inc(sem("x2_square_low"), 1)

            def normalise(g, c):
                y, out = x2_dev[:, c % 3, 0:width(c)], x2_keys[:, c % 2, 0:width(c)]
                at = (g * NC + c) * 3

                def refined(n, ins):
                    ins.then_inc(sem("x2_refined"), 1)
                    dve.wait_ge(sem("x2_refined"), at + n)

                dve.wait_ge(sem("x2_inverse"), g * NC + (c + 1))
                if c >= 2:
                    dve.wait_ge(sem("x2_scores_psum"), since("x2_scores_psum", g * NC + (c - 1)))
                refined(1, dve.scalar_tensor_tensor(out, ps[:, 3, 0:width(c)], LN_EPS, y, ALU.add, ALU.mult))
                refined(2, dve.scalar_tensor_tensor(out, out, -0.5, y, ALU.mult, ALU.mult))
                refined(3, dve.scalar_tensor_tensor(out, out, 1.5, y, ALU.add, ALU.mult))
                dve.tensor_tensor(out, ps[:, c % 3, 0:width(c)], out, ALU.mult).then_inc(sem("x2_keys_ready"), 1)

            def score(g, c, weighed):
                dve.wait_ge(sem("x2_scores_psum"), since("x2_scores_psum", g * NC + (c + 1)))
                if c == 0:
                    dve.wait_ge(sem("x2_tile_ready"), since("x2_tile_ready", g + 1))
                if weighed is not None:
                    dve.wait_ge(sem("x2_probsT_psum"), since("x2_probsT_psum", weighed * NC + (c + 1)))
                dve.tensor_scalar(S[:, span(c)], ps[:, 4, 0:width(c)], x2_tile_const[:, 0:1], NEG, ALU.add, ALU.max,
                                  accum_out=x2_max[:, c:c + 1]).then_inc(sem("x2_scores"), 1)

            def exp_bias(g):
                dve.wait_ge(sem("x2_scores"), since("x2_scores", g * NC + NC))
                dve.tensor_reduce(x2_small[:, 0:1], x2_max[:, 0:NC], AX, ALU.max).then_inc(sem("x2_max"), 1)
                dve.wait_ge(sem("x2_max"), g + 1)
                dve.tensor_scalar(x2_small[:, 1:2], x2_small[:, 0:1], -SCALE2, None, ALU.mult).then_inc(sem("x2_bias_ready"), 1)

            def inverse_sum(g):
                dve.wait_ge(sem("x2_exp"), since("x2_exp", g * NC + NC))
                dve.tensor_reduce(x2_small[:, 2:3], x2_sum[:, 0:NC], AX, ALU.add).then_inc(sem("x2_sum"), 1)
                dve.wait_ge(sem("x2_sum"), g * 2 + 1)
                dve.reciprocal(x2_small[:, 3:4], x2_small[:, 2:3]).then_inc(sem("x2_sum"), 1)

            def mix(g):
                dve.wait_ge(sem("x2_sum"), g * 2 + 2)
                dve.wait_ge(sem("x2_weighed"), since("x2_weighed", g * NC + NC))
                dve.tensor_scalar(x2_mix, bank(6, D), x2_small[:, 3:4], None, ALU.mult).then_inc(sem("x2_mix"), 1)
                dve.tensor_copy(x2_wv, wvs[:, :, ds(g * GD, GD)]).then_inc(sem("x2_wv_ready"), 1)

            def step(scored, weighed, done, ahead):
                if scored is not None:
                    tile(scored)
                if done is not None:
                    mix(done)
                for c in range(NC + 3):
                    if scored is not None:
                        if c < NC:
                            low_half(scored, c)
                        if c >= 3:
                            score(scored, c - 3, weighed)
                        if 1 <= c <= NC:
                            normalise(scored, c - 1)
                    if ahead is not None and c == NC:
                        key_weights(ahead)
                    if weighed is not None and c == NC:
                        inverse_sum(weighed)
                if scored is not None:
                    exp_bias(scored)

            key_weights(0)
            step(0, None, None, 1)
            step(1, 0, None, 2)
            with dve.Fori(1, GROUPS - 2) as g:
                g = dve.snap(g, max_val=GROUPS - 3)
                step(g + 1, g, g - 1, g + 2)
            step(GROUPS - 1, GROUPS - 2, GROUPS - 3, None)
            step(None, GROUPS - 1, GROUPS - 2, None)
            mix(GROUPS - 1)
            dve.wait_ge(sem("x2_cross_done"), GROUPS)
            link(dve, "dve", dve.reciprocal(scratch(0, 32), V("smooth")))
            wide = cut(scratch(64, 2048), 32, T)
            link(dve, "dve", dve.tensor_tensor(wide, x2_cat, spread(scratch(0, 32), 2, T), ALU.mult))
            last = round_vector(dve, 2048, 64, row_biases[:, 0:2048], wait=False)
            last.then_inc(sem("x2_cat_ready"), 1)
            link(dve, "dve", dve.tensor_tensor(x2_small[0:T, 0:1], V("scales")[0:T, 4:5], V("scales")[0:T, 5:6], ALU.mult))
            dve.wait_ge(sem("x2_out_psum"), since("x2_out_psum", 1))
            link(dve, "dve", dve.scalar_tensor_tensor(x[:, :], bank(0, D, T), x2_small[0:T, 0:1], x[:, :], ALU.mult, ALU.add))

        def round_vector(dve, n, at, out, wait=True):
            wide, narrow = scratch(at, n), scratch(at + n, n // 2).bitcast(BF16)
            power = scratch(at + n + n // 2, n // 2).bitcast(BF16)
            u16 = mybir.dt.uint16
            link(dve, "dve", dve.tensor_scalar(narrow, wide, 448.0, -448.0, ALU.min, ALU.max))
            link(dve, "dve", dve.tensor_scalar(power.bitcast(u16), narrow.bitcast(u16), 0x7F80, None, ALU.bitwise_and))
            link(dve, "dve", dve.tensor_scalar(wide, power, 2.0 ** -6, 1.5 * 2.0 ** 20, ALU.max, ALU.mult))
            link(dve, "dve", dve.tensor_tensor(out, narrow, wide, ALU.add))
            last = dve.tensor_tensor(out, out, wide, ALU.subtract)
            if wait:
                link(dve, "dve", last)
            return last

        def x2_scalar(act):
            act.wait_ge(sem("normT_psum"), transposed_no[6.5] + 1)
            src = cut(bank(7, KT * T), KT, T)
            for k in range(KT):
                ins = act.activation(x2_lnT[:, k, :], src[:, k, :], ACT.Identity, scale=V("ln_w")[:, k:k + 1], bias=V("ln_b")[:, k:k + 1])
            ins.then_inc(sem("normT_ready"), 1)
            for j in range(10):
                act.wait_ge(sem("x2_block_psum"), j + 1)
                if j >= 3:
                    act.wait_ge(sem("x2_block_turned"), j - 2)
                act.copy(wide[0:T, j % 3, :], ps[0:T, 5 + j % 2, :]).then_inc(sem("x2_block"), 1)
            for (a, b, i), turned in zip(x2_sq_cols, (4, 6, 10)):
                act.wait_ge(sem("x2_block_turned"), turned)
                act.activation(x2_raw[:, a:b], psf[:, a:b], ACT.Copy, scale=V("scales")[:, i:i + 1]).then_inc(sem("x2_raw"), 1)
            for c in range(5):
                act.wait_ge(sem("x2_centred"), c + 1)
                act.activation(x2_square[:, 512 * c:512 * c + 512], x2_raw[:, 512 * c:512 * c + 512], ACT.Square).then_inc(sem("x2_square"), 1)
            act.preload_act_table_set("sqrt_and_others")
            act.wait_ge(sem("x2_var_psum"), since("x2_var_psum", 1))
            act.activation(x2_std, ps[0:10, 7, 0:256], ACT.Sqrt, bias=x2_eps[0:10, 0:1]).then_inc(sem("x2_std"), 1)
            act.preload_act_table_set("natural_log_exp_and_others")
            act.wait_ge(sem("x2_heads_psum"), since("x2_heads_psum", 1))
            act.wait_ge(sem("x2_normed"), 1)
            act.activation(x2_v, psf[0:T, 2560:3584], ACT.Copy, scale=V("scales")[0:T, 3:4]).then_inc(sem("x2_v_ready"), 1)
            act.wait_ge(sem("x2_core_shifted"), 1)
            act.activation(x2_s, x2_s, ACT.Exp, scale=SCALE2).then_inc(sem("x2_core_exp"), 1)
            act.wait_ge(sem("x2_coreT_psum"), since("x2_coreT_psum", 1))
            act.wait_ge(sem("x2_v_ready"), since("x2_v_ready", 1))
            act.copy(x2_coreT, psf[0:T, 0:1024]).then_inc(sem("x2_coreT"), 1)
            act.wait_ge(sem("x2_core_out_psum"), since("x2_core_out_psum", 1))
            act.copy(x2_cat[:, 0:NQ, :], cut(psf[:, 1024:2048], NQ, T)).then_inc(sem("x2_core_done"), 1)

            def square(g, c):
                act.wait_ge(sem("x2_keys_psum"), g * NC + (c + 1))
                if c >= 3:
                    act.wait_ge(sem("x2_keys_ready"), g * NC + (c - 2))
                act.activation(x2_dev[:, c % 3, 0:width(c)], ps[:, c % 3, 0:width(c)], ACT.Square).then_inc(sem("x2_squared"), 1)

            def deviation(g, c):
                act.wait_ge(sem("x2_keys_var"), g * NC + (c + 1))
                act.activation(x2_dev[:, c % 3, 0:width(c)], ps[:, 3, 0:width(c)], ACT.Ln, bias=x2_eps[:, 0:1]).then_inc(sem("x2_deviation"), 1)
                act.wait_ge(sem("x2_deviation"), g * NC + (c + 1))
                act.activation(x2_dev[:, c % 3, 0:width(c)], x2_dev[:, c % 3, 0:width(c)], ACT.Exp, scale=-0.5).then_inc(sem("x2_inverse"), 1)

            def exp(g, c):
                if c == 0:
                    act.wait_ge(sem("x2_bias_ready"), since("x2_bias_ready", g + 1))
                chunk = S[:, span(c)]
                act.activation(chunk, chunk, ACT.Exp, scale=SCALE2, bias=x2_small[:, 1:2], accum_out=x2_sum[:, c:c + 1])\
                   .then_inc(sem("x2_exp"), 1)

            def copy_probs(g, c):
                act.wait_ge(sem("x2_probsT_psum"), since("x2_probsT_psum", g * NC + (c + 1)))
                if c >= 2:
                    act.wait_ge(sem("x2_weighed"), since("x2_weighed", g * NC + (c - 1)))
                act.copy(x2_probsT[:, c % 2, 0:128 * subs(c)], ps[0:TILE, 5 + 2 * (c % 2), 0:128 * subs(c)]).then_inc(sem("x2_probsT_ready"), 1)

            def copy_mix(g):
                act.wait_ge(sem("x2_mixT_psum"), g + 1)
                act.copy(x2_mixT, cut(ps[:, 6, D:2 * D], KT, 128)).then_inc(sem("x2_mixT"), 1)

            def copy_cross(g):
                act.wait_ge(sem("x2_cross_psum"), g + 1)
                act.copy(x2_cat[:, ds(g * 2 + NQ, 2), :], cut(ps[:, 6, D:D + 128], 2, T)).then_inc(sem("x2_cross_done"), 1)

            act.copy(x2_mean, C("mean128")).then_inc(sem("x2_mean_ready"), 1)
            exps = {0: range(0, 2)} | {c: range(c + 1, c + 2) for c in range(1, NC - 1)}

            def step(scored, weighed, done):
                for c in range(NC + 3):
                    if scored is not None and c < NC:
                        square(scored, c)
                    if weighed is not None:
                        for e in exps.get(c, ()):
                            exp(weighed, e)
                    if done is not None and c == 1:
                        copy_cross(done)
                    if scored is not None and 1 <= c <= NC:
                        deviation(scored, c - 1)
                    if weighed is not None and c < NC:
                        copy_probs(weighed, c)
                    if done is not None and c == 0:
                        copy_mix(done)

            step(0, None, None)
            step(1, 0, None)
            with act.Fori(1, GROUPS - 2) as g:
                g = act.snap(g, max_val=GROUPS - 3)
                step(g + 1, g, g - 1)
            step(GROUPS - 1, GROUPS - 2, GROUPS - 3)
            step(None, GROUPS - 1, GROUPS - 2)
            copy_mix(GROUPS - 1)
            copy_cross(GROUPS - 1)

        def x2_pool(pool):
            norm_pool(pool, 6)
            norm_pool(pool, 6.5)

        STAGES[6] = (x2_tensor, x2_vector, x2_scalar, x2_pool)

        x3_qT, x3_kT = cut(x2_keys[:, 0, 0:128], KT, T), cut(x2_keys[:, 0, 128:256], KT, T)
        x3_v = x2_mix[0:T, :]
        x3_own, x3_ownT = x2_q[0:T, 0:T], x2_q[0:T, T:2 * T]
        x3_max, x3_sum, x3_small = x2_max[0:T, :], x2_sum[0:T, :], x2_small[0:T, :]
        x3_probsT = x2_probsT[:, :, 0:SUB * T]

        def x3_tensor(pe):
            norm_tensor(pe, 9)
            normT_here(pe, 9)
            weights_here(pe, "x3")
            w = W("x3")
            for i in range(2):
                for o in range(KT):
                    for k in range(KT):
                        a = 512 * i + 256 * k + 128 * o
                        pe.matmul(ps[:, 0, (2 * i + o) * T:(2 * i + o + 1) * T], w[:, a:a + 128], xnT[:, k, 0, :], start=k == 0, stop=k == KT - 1)
            for k in range(KT):
                ins = pe.matmul(bank(1, D, T), xnT[:, k, 0, :], w[:, 1024 + 256 * k:1280 + 256 * k], start=k == 0, stop=k == KT - 1)
            ins.then_inc(sem("x3_qkv_psum"), 1)
            pe.wait_ge(sem("x3_qkv"), 3)
            pe.wait_ge(sem("ctx_reloaded"), 32)
            for c in range(NC + 1):
                if c >= 2:
                    pe.wait_ge(sem("x3_scores"), since("x3_scores", c - 1))
                out = ps[0:T, 2 + c % 2, 0:width(c) if c < NC else T]
                for k in range(KT):
                    keys = ctxT[:, k, span(c)] if c < NC else x3_kT[:, k, :]
                    ins = pe.matmul(out, x3_qT[:, k, :], keys, start=k == 0, stop=k == KT - 1)
                ins.then_inc(sem("x3_scores_psum"), 1)

            def turn(c):
                pe.wait_ge(sem("x3_exp"), since("x3_exp", c + 1))
                if c >= 2:
                    pe.wait_ge(sem("x3_probsT"), since("x3_probsT", c - 1))
                if c == NC:
                    pe.transpose(ps[0:T, 4 + c % 2, 0:T], x3_own, C("ident")[0:T, 0:T]).then_inc(sem("x3_probsT_psum"), 1)
                    return
                for s in range(subs(c)):
                    a = CHUNK * c + TILE * s
                    ins = pe.transpose(ps[0:TILE, 4 + c % 2, T * s:T * s + T], S[0:T, a:a + TILE], C("ident")[0:T, 0:T])
                ins.then_inc(sem("x3_probsT_psum"), 1)

            def weigh(c):
                pe.wait_ge(sem("x3_probsT"), since("x3_probsT", c + 1))
                if c == NC:
                    ins = pe.matmul(bank(0, D, T), x3_ownT, x3_v, start=False, stop=True)
                else:
                    for s in range(subs(c)):
                        ins = pe.matmul(bank(0, D, T), x3_probsT[:, c % 2, T * s:T * s + T], ctxN[:, SUB * c + s, :],
                                        start=c == 0 and s == 0, stop=False)
                ins.then_inc(sem("x3_weighed"), 1)

            turn(0)
            for c in range(1, NC + 1):
                turn(c)
                weigh(c - 1)
            weigh(NC)
            out_tensor(pe, 9, attended, w[:, 1536:2048], "x3")

        def x3_vector(dve):
            norm_vector(dve, 9)
            for c in range(NC + 1):
                dve.wait_ge(sem("x3_scores_psum"), since("x3_scores_psum", c + 1))
                out = S[0:T, span(c)] if c < NC else x3_own
                dve.tensor_scalar(out, ps[0:T, 2 + c % 2, 0:width(c) if c < NC else T], 1.0, NEG, ALU.mult, ALU.max,
                                  accum_out=x3_max[:, c:c + 1]).then_inc(sem("x3_scores"), 1)
            dve.wait_ge(sem("x3_scores"), since("x3_scores", NC + 1))
            link(dve, "dve", dve.tensor_reduce(x3_small[:, 0:1], x3_max, AX, ALU.max))
            dve.tensor_scalar(x3_small[:, 1:2], x3_small[:, 0:1], -1.0 / 16, None, ALU.mult).then_inc(sem("x3_bias_ready"), 1)
            for c in range(NC + 1):
                dve.wait_ge(sem("x3_probsT_psum"), since("x3_probsT_psum", c + 1))
                if c >= 2:
                    dve.wait_ge(sem("x3_weighed"), since("x3_weighed", c - 1))
                if c < NC:
                    ins = dve.tensor_copy(x3_probsT[:, c % 2, 0:subs(c) * T], ps[0:TILE, 4 + c % 2, 0:subs(c) * T])
                else:
                    ins = dve.tensor_copy(x3_ownT, ps[0:T, 4 + c % 2, 0:T])
                ins.then_inc(sem("x3_probsT"), 1)
            link(dve, "dve", dve.tensor_reduce(x3_small[:, 2:3], x3_sum, AX, ALU.add))
            link(dve, "dve", dve.reciprocal(x3_small[:, 3:4], x3_small[:, 2:3]))
            dve.wait_ge(sem("x3_weighed"), since("x3_weighed", NC + 1))
            dve.tensor_scalar(attended[:, :], bank(0, D, T), x3_small[:, 3:4], None, ALU.mult).then_inc(sem("attended"), 1)
            residual_vector(dve, 9, bank(6, D, T), (sem("projected"), outs.index(9) + 1))

        def x3_scalar(act):
            norm_scalar(act, 9)
            act.wait_ge(sem("x3_qkv_psum"), since("x3_qkv_psum", 1))
            act.copy(x3_qT, cut(ps[:, 0, 0:KT * T], KT, T)).then_inc(sem("x3_qkv"), 1)
            act.copy(x3_kT, cut(ps[:, 0, KT * T:2 * KT * T], KT, T)).then_inc(sem("x3_qkv"), 1)
            act.copy(x3_v, bank(1, D, T)).then_inc(sem("x3_qkv"), 1)
            act.wait_ge(sem("x3_bias_ready"), since("x3_bias_ready", 1))
            for c in range(NC + 1):
                part = S[0:T, span(c)] if c < NC else x3_own
                act.activation(part, part, ACT.Exp, scale=1.0 / 16, bias=x3_small[:, 1:2], accum_out=x3_sum[:, c:c + 1])\
                   .then_inc(sem("x3_exp"), 1)
            out_scalar(act, 9)

        STAGES[9] = (x3_tensor, x3_vector, x3_scalar, lambda pool: norm_pool(pool, 9))

        def reload_scalar(act):
            if runs(3):
                act.wait_ge(sem("attended"), outs.index(3) + 1)
            act.dma_start(ctxT, io["ctxT"]).then_inc(sem("ctx_reloaded"), 16)
            act.dma_start(ctxN, io["ctxN"]).then_inc(sem("ctx_reloaded"), 16)

        block = stack.enter_context(nc.Block())

        @block.sync
        def _(sp):
            n_first = min(len(pieces), NSLOT)

            def load(n):
                _, name, w = pieces[n]
                a = piece_from[name]
                sp.dma_start(W(name), io["weights"][:, a:a + w]).then_inc(sem(f"weights_in{n % NSLOT}"), 16)

            sp.dma_start(x[:, :], io["x"]).then_inc(sem("x_in"), 16)
            if sweep:
                load(0)
                SWEEP_LOADS[0](sp, 0)
                load(1)
            kv1, kv1_end = row_bias_at["kv1"][0], sum(row_bias_at["kv1"])
            for a, b in ((kv1, kv1_end), (0, kv1), (kv1_end, n_row_biases)):
                sp.dma_start(row_biases[:, a:b], io["row_biases"][:, a:b]).then_inc(sem("kv1_in" if a == kv1 else "params_in"), 16)
                if a == kv1 and sweep:
                    SWEEP_LOADS[0](sp, 1)
            for n in range(2 if sweep else 0, n_first):
                load(n)
            sp.dma_start(filter_sb[:, :], io["filterT"]).then_inc(sem("params_in"), 16)
            if sweep:
                SWEEP_LOADS[1](sp)
            for n in range(n_first, len(pieces)):
                sp.wait_ge(weights_used, n - NSLOT + 1)
                load(n)
            sp.wait_ge(sem("latent_done"), 1)
            sp.dma_start(io["out"], x[:, :]).then_inc(sem("stored"), 16)
            sp.wait_ge(sem("stored"), 16)

        @block.tensor
        def _(pe):
            if sweep:
                SWEEP[0](pe)
            pe.wait_ge(sem("constants_in"), 16)
            pe.wait_ge(sem("params_in"), 48)
            for s in range(12):
                if runs(s):
                    STAGES[s][0](pe)

        @block.vector
        def _(dve):
            dve.wait_ge(sem("x_in"), 16)
            if sweep:
                dve.wait_ge(sem("kv1_in"), 16)
                SWEEP[1](dve)
            dve.wait_ge(sem("constants_in"), 16)
            dve.wait_ge(sem("columns_in"), 16)
            dve.wait_ge(sem("params_in"), 48)
            for s in range(12):
                if runs(s):
                    STAGES[s][1](dve)
            dve.sem_inc(sem("latent_done"), 1)

        @block.scalar
        def _(act):
            act.dma_start(consts[:, :], io["constants"]).then_inc(sem("constants_in"), 16)
            act.dma_start(cols[:, :], io["columns"]).then_inc(sem("columns_in"), 16)
            if sweep:
                act.dma_start(mask_sb[:, :], io["mask"]).then_inc(sem("mask_in"), 16)
            act.wait_ge(sem("columns_in"), 16)
            if sweep:
                SWEEP[2](act)
            act.wait_ge(sem("constants_in"), 16)
            act.wait_ge(sem("params_in"), 48)
            for s in range(12):
                if s == 4 and (runs(6) or runs(9)):
                    reload_scalar(act)
                if runs(s):
                    STAGES[s][2](act)

        @block.gpsimd
        def _(pool):
            if sweep:
                SWEEP[3](pool)
            pool.wait_ge(sem("constants_in"), 16)
            pool.wait_ge(sem("params_in"), 48)
            for s in range(12):
                if runs(s):
                    STAGES[s][3](pool)



def kernel(**inputs):
    import concourse.bacc as bacc
    from concourse.bass_utils import run_bass_kernel_spmd

    nc = bacc.Bacc("TRN2", target_bir_lowering=False, num_devices=1)
    arrays = laid_out({n: np.asarray(v) for n, v in inputs.items()})
    io = {n: nc.dram_tensor(n, v.shape, F32, kind="ExternalInput").ap() for n, v in arrays.items()}
    io["out"] = nc.dram_tensor("out", (T, D), F32, kind="ExternalOutput").ap()
    perceiver(nc, io)
    result = run_bass_kernel_spmd(nc, [arrays], core_ids=[0])
    return result.results[0]["out"].reshape(1, T, D)
```

```python
from contextlib import ExitStack

import numpy as np

import concourse.bass as bass
from concourse import mybir

ALU = mybir.AluOpType
ACT = mybir.ActivationFunctionType
AX = mybir.AxisListType.X
F32 = mybir.dt.float32
BF16 = mybir.dt.bfloat16
U32 = mybir.dt.uint32

T = 64
D = 256
KT = D // 128
SK = 6272
TILE = 128
NT = SK // TILE
SUB = 4
CHUNK = SUB * TILE
NC = -(-NT // SUB)
NH = 16
HD = 16
PAIRS = NH // 2
FD = 64
GROUPS = 8
GD = 128
NQ = 2 * GROUPS
NE = 18
FF = 176
FH = FF // 2
LN_EPS = 1e-5
RMS_EPS = 1e-6
NEG = -3.0e38
MAGIC = 12582912.0
LN255 = float(np.log(255.0))

SLOT = 2048
NSLOT = 4


def subs(c):
    return min(SUB, NT - SUB * c)


def width(c):
    return TILE * subs(c)


def span(c):
    return slice(CHUNK * c, CHUNK * c + width(c))



def k_major(m):
    k, n = m.shape
    return m.reshape(k // 128, 128, n).transpose(1, 0, 2).reshape(128, -1)


def rows(m):
    out = np.zeros((128, m.shape[1]), np.float32)
    out[:m.shape[0]] = m
    return out


def head_diagonal(w):
    d, f = w.shape
    out = np.zeros((128, 128 // d * f), np.float32)
    for h in range(128 // d):
        out[h * d:(h + 1) * d, h * f:(h + 1) * f] = w
    return out


def expert_columns(a):
    e, r, i = a.shape
    out = np.zeros((i, e, e, r), np.float32)
    for n in range(e):
        out[:, n, n, :] = a[n].T
    return out.reshape(i, -1)


def column(v):
    return v.reshape(-1, 128).T


def by_head(w):
    return w.reshape(-1, NH, 3, HD).transpose(0, 2, 1, 3).reshape(-1, 3 * D)


def for_query_groups(w):
    return np.repeat(w.reshape(8, 1, 8, -1), 4, axis=1).reshape(D, -1)


F3_EXPERTS = 2 * (KT * FF + 2 * D)
F3_GATE = KT * 16 + D

PIECES = (
    [(-1, "pre", 2048), (-1, "pre_features", 512)]
    + [(0, "x0", 1536), (1, "a0", 2048)]
    + [(2, "f0_gate", 2048), (2, "f0_up", 2048), (2, "f0_routed", 784), (2, "f0_down", 2048)]
    + [(3, "x1", 1024), (4, "a1", 2048)]
    + [(5, "f1_gate", 280), (5, "f1_lora", 1792)] + [(5, f"f1_experts{n}", 1536) for n in range(4)]
    + [(6, "x2_q0", 2048), (6, "x2_q1", 2048), (6, "x2_k", 2048), (6, "x2_qx0", 2048), (6, "x2_qx1", 2048),
       (6, "x2_v", 2048), (6, "x2_kx", 2048), (6, "x2_vx", 2048)]
    + [(6, f"x2_proj{n}", 2048) for n in range(4)]
    + [(7, "a2", 2048), (8, "f2_attn", 2048), (8, "f2_mod", 1056), (8, "f2_gate", 2048), (8, "f2_up", 2048),
       (8, "f2_down", 2048)]
    + [(9, "x3", 2048), (10, "a3", 2048)]
    + [(11, f"f3_experts{n}", F3_EXPERTS + (F3_GATE if n == 0 else 0)) for n in range(NE // 2)]
)


def pack_piece(name, a):
    tr = lambda n: k_major(np.ascontiguousarray(a[n].T))
    cat = lambda *p: np.concatenate(p, 1)
    last = int(name[-1]) if name[-1].isdigit() else 0
    half = lambda n, i: k_major(np.ascontiguousarray(a[n][1024 * i:1024 * (i + 1)].T))
    if name == "pre":
        return cat(tr("L0_xattn_Wk"), k_major(cat(a["L0_xattn_Wv"].T, a["L1_xattn_Wkv"])))
    if name == "pre_features":
        return head_diagonal(a["L0_xattn_Wkf"].T)
    if name == "x0":
        return cat(tr("L0_xattn_Wq"), head_diagonal(a["L0_xattn_Wqf"].T), tr("L0_xattn_Wo"))
    if name == "a0":
        return cat(k_major(a["L0_attn_Wqkv"]), k_major(a["L0_attn_Wo"]))
    if name == "f0_gate":
        return tr("L0_ffn_sh_gate")
    if name == "f0_up":
        return tr("L0_ffn_sh_up")
    if name == "f0_down":
        return tr("L0_ffn_sh_down")
    if name == "f0_routed":
        return cat(tr("L0_ffn_r_gate"), tr("L0_ffn_r_up"), tr("L0_ffn_r_down"), tr("L0_ffn_router_weight"))
    if name == "x1":
        return cat(k_major(a["L1_xattn_Wq"]), k_major(a["L1_xattn_Wp"]))
    if name == "a1":
        return cat(k_major(by_head(a["L1_attn_w_qkv"])), k_major(a["L1_attn_w_out"]))
    if name == "f1_gate":
        return cat(tr("L1_ffn_gate_weight"), rows(a["L1_ffn_gate_lora_A"]), rows(a["L1_ffn_gate_lora_B"].T))
    if name == "f1_lora":
        gup_b = a["L1_ffn_gup_lora_B"].transpose(0, 2, 1).reshape(128, D)
        down_b = a["L1_ffn_down_lora_B"].transpose(0, 2, 1).reshape(128, D)
        return cat(k_major(a["L1_ffn_gup_lora_A"].reshape(128, D).T), gup_b, down_b,
                   expert_columns(a["L1_ffn_down_lora_A"]))
    if name.startswith("f1_experts"):
        two = [cat(k_major(a["L1_ffn_gate_up_proj"][e]), a["L1_ffn_down_proj"][e]) for e in (2 * last, 2 * last + 1)]
        return cat(*two)
    if name in ("x2_q0", "x2_q1"):
        return half("L2_xattn_wq", last)
    if name in ("x2_qx0", "x2_qx1"):
        return half("L2_xattn_wqx", last)
    if name == "x2_k":
        return tr("L2_xattn_wk")
    if name == "x2_v":
        return tr("L2_xattn_wv")
    if name == "x2_kx":
        return half("L2_xattn_w_kv_x", 0)
    if name == "x2_vx":
        return half("L2_xattn_w_kv_x", 1)
    if name.startswith("x2_proj"):
        return k_major(np.ascontiguousarray(a["L2_xattn_wproj"].T[1024 * last:1024 * (last + 1)]))
    if name == "a2":
        w = cat(a["L2_attn_Wq"].T, for_query_groups(a["L2_attn_Wk"]).T, for_query_groups(a["L2_attn_Wv"]).T)
        return cat(k_major(w), tr("L2_attn_Wo"))
    if name == "f2_attn":
        return cat(k_major(cat(a["L2_ffn_Wq"].T, a["L2_ffn_Wk"].T, a["L2_ffn_Wv"].T)), tr("L2_ffn_Wo"))
    if name == "f2_mod":
        return cat(k_major(a["L2_ffn_A"]), rows(a["L2_ffn_B"]))
    if name == "f2_gate":
        return tr("L2_ffn_W_in_base")
    if name == "f2_up":
        return tr("L2_ffn_W_up_base")
    if name == "f2_down":
        return tr("L2_ffn_W_down")
    if name == "x3":
        return cat(*(tr(f"L3_xattn_{w}") for w in ("wq", "wk", "wv", "wo")))
    if name == "a3":
        return cat(*(tr(f"L3_attn_{w}") for w in ("Wq", "Wk", "Wv", "Wo")))
    w1 = np.concatenate([a["L3_ffn_routed_w1"], a["L3_ffn_shared_w1"]], 0)
    w2 = np.concatenate([a["L3_ffn_routed_w2"], a["L3_ffn_shared_w2"]], 0)
    two = [2 * last, 2 * last + 1]
    halves = [rows(w2[e].reshape(2, FH, D).transpose(1, 0, 2).reshape(FH, 2 * D)) for e in two]
    experts = cat(k_major(np.concatenate([w1[e] for e in two], 1)), *halves)
    if last > 0:
        return experts
    return cat(experts, tr("L3_ffn_centroids"), rows(np.concatenate([a["L3_ffn_routed_b2"], a["L3_ffn_shared_b2"]], 0)))


ROW_BIASES = (("bv0", D), ("bo0", D), ("a0_qkv", 3 * D), ("a0_out", D), ("kv1", 2 * D), ("q1", D), ("out1", D),
              ("a1_qkv", 3 * D), ("a1_out", D), ("a2_qkv", 3 * D), ("a2_out", D), ("a3_out", D), ("f3_bias", 16))


def pack_row_biases(a):
    r = {"bv0": a["L0_xattn_bv"], "bo0": a["L0_xattn_bo"], "a0_qkv": a["L0_attn_bqkv"], "a0_out": a["L0_attn_bo"],
         "kv1": a["L1_xattn_bkv"], "q1": a["L1_xattn_bq"], "out1": a["L1_xattn_bp"],
         "a1_qkv": by_head(a["L1_attn_b_qkv"][None])[0], "a1_out": a["L1_attn_b_out"],
         "a2_qkv": np.concatenate([a["L2_attn_bq"], for_query_groups(a["L2_attn_bk"]).ravel(),
                                   for_query_groups(a["L2_attn_bv"]).ravel()]),
         "a2_out": a["L2_attn_bo"], "a3_out": a["L3_attn_bo"], "f3_bias": a["L3_ffn_bias"]}
    row = np.concatenate([r[n] for n, _ in ROW_BIASES])
    return np.ascontiguousarray(np.broadcast_to(row, (128, row.size)))


COLUMNS = (("bk0", 2), ("bq0", 2), ("ln_w", 2), ("ln_b", 2), ("in_scale", 8), ("head_ln", 8), ("smooth", 32),
           ("scales", 6), ("ln1_w", 2), ("ln2_w", 2), ("a3_b", 6), ("conv_w", 12), ("conv_b", 4), ("d_skip", 2),
           ("f3_b1", 36))


def pack_columns(a):
    x2 = lambda n: a["L2_xattn_" + n]
    scalars = [x2(n) for n in ("wq_scale", "wk_scale", "wqx_scale", "wv_scale", "proj_in_scale", "proj_w_scale")]
    b1 = np.concatenate([a["L3_ffn_routed_b1"], a["L3_ffn_shared_b1"]], 0)
    c = {"bk0": column(a["L0_xattn_bk"]), "bq0": column(a["L0_xattn_bq"]),
         "ln_w": column(x2("ln_w")), "ln_b": column(x2("ln_b")),
         "in_scale": np.concatenate([column(x2(n + "_in_scale")) for n in ("q", "k", "qx", "v")], 1),
         "head_ln": np.stack([x2(n) for n in ("qln_w", "qln_b", "kln_w", "kln_b", "qxln_w", "qxln_b",
                                              "kxln_w", "kxln_b")], 1),
         "smooth": column(x2("proj_smooth")),
         "scales": np.broadcast_to(np.array([np.asarray(s).reshape(()) for s in scalars], np.float32), (128, 6)),
         "ln1_w": column(a["L2_ffn_ln1_w"]), "ln2_w": column(a["L2_ffn_ln2_w"]),
         "a3_b": np.concatenate([column(a["L3_attn_" + n]) for n in ("bq", "bk", "bv")], 1),
         "conv_w": np.concatenate([a[f"L3_attn_conv{n}_w"].reshape(2, 128, 3).transpose(1, 0, 2).reshape(128, 6)
                                   for n in "qk"], 1),
         "conv_b": np.concatenate([column(a[f"L3_attn_conv{n}_b"]) for n in "qk"], 1),
         "d_skip": column(a["L3_attn_D_skip"]),
         "f3_b1": rows(b1.reshape(18, 2, FH).transpose(2, 0, 1).reshape(FH, 36))}
    return np.ascontiguousarray(np.concatenate([c[n] for n, _ in COLUMNS], 1).astype(np.float32))


FREQ = T + 1
CONSTANTS = (("ident", 128), ("centre128", 128), ("mean128", 128), ("mean_band", 19), ("tri", T), ("tri_10000", T), ("tri_neg", T),
             ("heads16", 8), ("heads8", 16), ("neg_half", 1), ("earlier8", 64), ("earlier16", 256),
             ("rope1", 8), ("rope2", 16), ("dft", 2 * FREQ), ("idft", 2 * T))


def rope_table(angle):
    cos, sin = np.cos(angle), np.sin(angle)
    return np.concatenate([cos, cos, -sin, sin], 1)


def constants():
    p, t = np.arange(128), np.arange(T)
    lower = np.tile((t[None, :] <= t[:, None]).astype(np.float32), (2, 1))
    f32 = np.float32
    inv1 = f32(1.0) / f32(10000.0) ** (np.arange(0, 4, 2, dtype=f32) / f32(4))
    inv2 = f32(10000.0) ** (f32(-2.0) * np.arange(4, dtype=f32) / f32(8))
    angle = 2 * np.pi * np.outer(p, np.arange(FREQ)) / (2 * T)
    weight = np.where((np.arange(FREQ) % T) == 0, 1.0, 2.0)[:, None] / (2 * T)
    back = 2 * np.pi * np.outer(np.arange(FREQ), t) / (2 * T)
    c = {"ident": np.eye(128), "centre128": np.eye(128) - 1 / 128, "mean128": np.full((128, 128), 1 / 128),
         "mean_band": np.broadcast_to((np.arange(19) == 9) / 128, (128, 19)),
         "tri": lower, "tri_10000": -10000.0 * (1 - lower), "tri_neg": NEG * (1 - lower),
         "heads16": (p[:, None] // 16 == np.arange(8)), "heads8": (p[:, None] // 8 == np.arange(16)),
         "neg_half": np.full((128, 1), -0.5),
         "earlier8": np.tile((np.arange(8)[None, :] < np.arange(8)[:, None]).reshape(1, -1), (T, 1)),
         "earlier16": np.tile((np.arange(16)[None, :] < np.arange(16)[:, None]).reshape(1, -1), (T, 1)),
         "rope1": rope_table((t[:, None].astype(f32) * inv1[None]).astype(f32)),
         "rope2": rope_table(((t[:, None].astype(f32) + 1) * inv2[None]).astype(f32)),
         "dft": np.concatenate([np.cos(angle), -np.sin(angle)], 1),
         "idft": np.concatenate([weight * np.cos(back), -weight * np.sin(back)], 1)}
    return np.concatenate([rows(np.asarray(c[n], np.float32)) for n, _ in CONSTANTS], 1)


def offsets(table):
    at, out = 0, {}
    for n, w in table:
        out[n] = (at, w)
        at += w
    return out, at


def laid_out(a):
    ctx = a["ctx_2048"][0]
    out = {
        "x": a["x"][0],
        "ctxT": ctx.T.reshape(KT, 128, SK).transpose(1, 0, 2),
        "ctxN": ctx.reshape(NT, TILE, D).transpose(1, 0, 2),
        "mask": a["mask_BxS2_ff1"][0].reshape(NT, TILE).T,
        "row_biases": pack_row_biases(a),
        "columns": pack_columns(a),
        "constants": constants(),
        "filterT": a["L3_attn_ssm_kernel"][:, :2 * T].T,
        "weights": np.concatenate([pack_piece(n, a) for _, n, _ in PIECES], 1),
    }
    return {n: np.ascontiguousarray(v, np.float32) for n, v in out.items()}



def perceiver(nc, io, first=0, last=11):
    constant_at, n_constants = offsets(CONSTANTS)
    column_at, n_columns = offsets(COLUMNS)
    row_bias_at, n_row_biases = offsets(ROW_BIASES)
    runs = lambda s: first <= s <= last
    sweep = runs(0) or runs(3)
    pieces = [p for p in PIECES if runs(p[0]) or (p[0] == -1 and sweep)]
    piece_no = {n: k for k, (_, n, _) in enumerate(pieces)}
    piece_from, at = {}, 0
    for s, n, w in PIECES:
        piece_from[n] = at
        at += w

    with ExitStack() as stack:
        def sb(name, shape, dt=F32):
            return stack.enter_context(nc.sbuf_tensor(name, shape, dt))

        sems = {}

        shared = {
            "hiddenT_psum": (("f0_hT_psum", 2, 1), ("f1_hT_psum", 5, 4), ("f2_hiddenT_psum", 8, 1), ("f3_hT_psum", 11, NE // 2)),
            "hiddenT": (("f0_hT", 2, 1), ("f1_hT", 5, 4), ("f2_hiddenT", 8, 1), ("f3_relu", 11, NE // 2)),
            "low_ready": (("f1_low_ready", 5, 1), ("f2_mod_ready", 8, 1)),
            "rounded": (("x1_q_ready", 3, 1), ("x2_in_ready", 6, 2), ("x2_cat_ready", 6, 3)),
            "queries_psum": (("x0_qT_psum", 0, 1), ("x1_q_psum", 3, 1), ("x2_heads_psum", 6, 1),
                             ("x3_qkv_psum", 9, 1), ("a3_qkv_psum", 10, 1)),
            "scores_psum": (("x1_scores_psum", 3, PAIRS * NC), ("x2_scores_psum", 6, GROUPS * NC),
                            ("x3_scores_psum", 9, NC + 1)),
            "scores": (("x1_scores", 3, PAIRS * NC), ("x2_scores", 6, GROUPS * NC), ("x3_scores", 9, NC + 1)),
            "exp_bias_ready": (("x1_bias_ready", 3, PAIRS), ("x2_bias_ready", 6, GROUPS), ("x3_bias_ready", 9, 1)),
            "exp": (("x1_exp", 3, PAIRS * NC), ("x2_exp", 6, GROUPS * NC), ("x3_exp", 9, NC + 1)),
            "probsT_psum": (("x1_probsT_psum", 3, PAIRS * NC), ("x2_probsT_psum", 6, GROUPS * NC),
                            ("x3_probsT_psum", 9, NC + 1)),
            "probsT_ready": (("x2_probsT_ready", 6, GROUPS * NC), ("x3_probsT", 9, NC + 1)),
            "weighed": (("x1_weighed", 3, PAIRS * NC), ("x2_weighed", 6, GROUPS * NC), ("x3_weighed", 9, NC + 1)),
            "tile_ready": (("x1_tile_ready", 3, PAIRS), ("x2_tile_ready", 6, GROUPS)),
            "logits_psum": (("f0_logits_psum", 2, 1), ("f1_logits_psum", 5, 1), ("f3_logits_psum", 11, 1)),
            "logits_shifted": (("f0_shifted", 2, 1), ("f1_shifted", 5, 1)),
            "logits_exp": (("f0_router_exp", 2, 1), ("f1_router_exp", 5, 1), ("f3_exp", 11, 1)),
            "hidden_psum": (("f0_hidden_psum", 2, 1), ("f1_gates_psum", 5, 4), ("f2_hidden_psum", 8, 1),
                            ("f3_hidden_psum", 11, NE // 2)),
            "gates_tanh": (("f0_tanh", 2, 2), ("f1_tanh", 5, 4), ("f2_gate_tanh", 8, 1)),
            "hidden": (("f0_hidden", 2, 2), ("f1_hidden", 5, 4), ("f2_hidden", 8, 1), ("f3_copied", 11, NE // 2)),
            "expert_psum": (("f1_expert_psum", 5, 4), ("f3_expert_psum", 11, NE // 2)),
            "expert_added": (("f1_added", 5, 4), ("f3_added", 11, NE)),
            "out_psum": (("f0_out_psum", 2, 1), ("f1_lora_psum", 5, 1), ("x2_out_psum", 6, 1), ("f2_out_psum", 8, 1),
                         ("a3_out_psum", 10, 1), ("f3_bias_psum", 11, 1)),
            "low_psum": (("f1_low_psum", 5, 1), ("f2_low_psum", 8, 1)),
            "narrowT_psum": (("f1_down_lowT_psum", 5, 1), ("f2_modT_psum", 8, 1), ("f3_gatesT_psum", 11, 1)),
            "narrowT_ready": (("f1_down_lowT_ready", 5, 1), ("f2_modT_ready", 8, 1), ("f3_gatesT_ready", 11, 1)),
            "x2_head_sums_psum": (("x2_centre_psum", 6, 5), ("x2_var_psum", 6, 1), ("x2_inv_psum", 6, 2), ("x2_core_psum", 6, 1),
                                  ("x2_const_psum", 6, 1), ("x2_coreT_psum", 6, 1), ("x2_core_out_psum", 6, 1)),
            "x2_heads_step": (("x2_raw", 6, 3), ("x2_square", 6, 5), ("x2_std", 6, 1), ("x2_v_ready", 6, 1),
                              ("x2_core_exp", 6, 1), ("x2_coreT", 6, 1), ("x2_core_done", 6, 1)),
        }
        shared_by = {name: by for by, signals in shared.items() for name, _, _ in signals}

        def sem(name):
            name = shared_by.get(name, name)
            if name not in sems:
                sems[name] = stack.enter_context(nc.semaphore(name))
            return sems[name]

        def since(name, n):
            for other, s, times in shared[shared_by[name]]:
                if other == name:
                    return n
                if runs(s):
                    n = n + times

        consts = sb("consts", [128, n_constants])
        cols = sb("cols", [128, n_columns])
        row_biases = sb("row_biases_sb", [128, n_row_biases])
        filter_sb = sb("filter_sb", [128, D])
        ring = sb("ring", [128, NSLOT, SLOT])
        x = sb("x_sb", [T, D])
        xn = sb("xn", [T, D])
        xnT = sb("xnT", [128, KT, 2, T])
        stats = sb("stats", [T, 6])
        moments = sb("moments", [T, 2])
        var_eps = sb("var_eps", [T, 1])
        rstd = sb("rstd", [T, 1])
        keysT = sb("keysT", [128, KT, TILE + SK])
        vals = sb("vals", [128, NT, D])
        S = sb("S", [128, SK])
        mask_sb = sb("mask_sb", [TILE, NT])
        sweep_sums = sb("sweep_sums", [128, PAIRS, 34])
        value_step = sb("value_step", [128, D])
        wide = sb("wide", [128, 3, CHUNK])
        x2_keys = sb("x2_keys", [128, 2, CHUNK])
        ps = stack.enter_context(nc.psum_tensor("ps", [128, 8, 512], F32))
        psf = ps[:, :, :].rearrange("p b n -> p (b n)")

        def bank(b, n=512, p=128):
            return ps[0:p, b, 0:n]

        def C(name):
            a, w = constant_at[name]
            return consts[:, a:a + w]

        def V(name):
            a, w = column_at[name]
            return cols[:, a:a + w]

        def R(name, p=T):
            a, w = row_bias_at[name]
            return row_biases[0:p, a:a + w]

        def scratch(a, n, p=128):
            return S[0:p, a:a + n]

        def cut(ap, *dims):
            if len(dims) == 2:
                return ap.rearrange("p (a b) -> p a b", a=dims[0])
            return ap.rearrange("p (a b c) -> p a b c", a=dims[0], b=dims[1])

        def spread(ap, axis, n):
            shape = list(ap.shape)
            return ap.unsqueeze(axis).broadcast_to(shape[:axis] + [n] + shape[axis:])

        def W(name):
            n = piece_no[name]
            return ring[:, n % NSLOT, 0:pieces[n][2]]

        def weights_here(eng, name):
            n = piece_no[name]
            eng.wait_ge(sem(f"weights_in{n % NSLOT}"), 16 * (n // NSLOT + 1))

        weights_used = sem("weights_used")

        steps = {"dve": 0, "act": 0, "pool": 0}

        def link(eng, name, ins):
            steps[name] += 1
            ins.then_inc(sem(name + "_step"), 1)
            eng.wait_ge(sem(name + "_step"), steps[name])

        norms = [n for s in range(12) if runs(s) for n in ([s] if s not in (6, 8) else [s, s + 0.5])]
        norm_no = {n: k for k, n in enumerate(norms)}
        transposed = [n for n in norms if n not in (6, 8)]
        transposed_no = {n: k for k, n in enumerate(transposed)}

        def norm_vector(dve, n, src=x, out=xn, eps=LN_EPS, rms=False):
            k = norm_no[n]
            if rms:
                link(dve, "dve", dve.tensor_tensor_reduce(out[:, :], src[:, :], src[:, :], 1.0 / D, 0.0, ALU.mult,
                                                          ALU.add, moments[:, 1:2]))
            else:
                link(dve, "dve", dve.bn_stats(stats[:, :], src[:, :]))
                link(dve, "dve", dve.bn_aggr(moments[:, :], stats[:, :]))
            dve.tensor_scalar(var_eps[:, :], moments[:, 1:2], eps, None, ALU.add).then_inc(sem("var_ready"), 1)
            dve.wait_ge(sem("rstd_ready"), k + 1)
            if rms:
                ins = dve.tensor_scalar(out[:, :], src[:, :], rstd[:, 0:1], None, ALU.mult)
            else:
                ins = dve.tensor_scalar(out[:, :], src[:, :], moments[:, 0:1], rstd[:, 0:1], ALU.subtract, ALU.mult)
            ins.then_inc(sem("norm_ready"), 1)
            dve.wait_ge(sem("norm_ready"), k + 1)

        def norm_pool(pool, n):
            k = norm_no[n]
            if k == 0:
                pool.wait_ge(sem("constants_in"), 16)
            pool.wait_ge(sem("var_ready"), k + 1)
            pool.tensor_tensor(rstd[:, :], var_eps[:, :], C("neg_half")[0:T, :], ALU.pow).then_inc(sem("rstd_ready"), 1)

        def norm_tensor(pe, n, src=xn):
            if transposed_no[n] == 0:
                pe.wait_ge(sem("constants_in"), 16)
            pe.wait_ge(sem("norm_ready"), norm_no[n] + 1)
            for k in range(KT):
                ins = pe.transpose(ps[:, 7, k * T:(k + 1) * T], src[:, k * 128:(k + 1) * 128], C("ident")[0:T, 0:T])
            ins.then_inc(sem("normT_psum"), 1)

        def norm_scalar(act, n):
            act.wait_ge(sem("normT_psum"), transposed_no[n] + 1)
            act.copy(xnT[:, :, :, :], spread(cut(bank(7, KT * T), KT, T), 2, 2)).then_inc(sem("normT_ready"), 1)

        def normT_here(eng, n):
            eng.wait_ge(sem("normT_ready"), transposed_no[n] + 1)

        biased = [s for s in (0, 1, 3, 4, 7, 10) if runs(s)]

        def bias_pool(pool, s, name):
            pool.wait_ge(sem("norm_ready"), norm_no[s] + 1)
            pool.tensor_tensor(x[:, :], x[:, :], R(name), ALU.add).then_inc(sem("x_biased"), 1)

        def residual_vector(dve, s, product, ready):
            dve.wait_ge(*ready)
            if s in biased:
                dve.wait_ge(sem("x_biased"), biased.index(s) + 1)
            link(dve, "dve", dve.tensor_tensor(x[:, :], x[:, :], product, ALU.add))

        outs = [s for s in (0, 1, 3, 4, 7, 8, 9) if runs(s)]

        def out_tensor(pe, s, src, w, piece=None):
            k = outs.index(s)
            pe.wait_ge(sem("attended"), k + 1)
            for n in range(KT):
                ins = pe.transpose(ps[:, 7, n * T:(n + 1) * T], src[:, n * 128:(n + 1) * 128], C("ident")[0:T, 0:T])
            ins.then_inc(sem("attendedT_psum"), 1)
            pe.wait_ge(sem("attendedT_ready"), k + 1)
            for n in range(KT):
                ins = pe.matmul(bank(6, D, T), attendedT[:, n, :], w[:, n * D:(n + 1) * D], start=n == 0, stop=n == KT - 1)
            ins.then_inc(sem("projected"), 1)
            if piece:
                pe.wait_ge(sem("projected"), k + 1)
                pe.sem_inc(weights_used, 1)

        def out_scalar(act, s):
            k = outs.index(s)
            act.wait_ge(sem("attendedT_psum"), k + 1)
            act.copy(attendedT[:, :, :], cut(bank(7, KT * T), KT, T)).then_inc(sem("attendedT_ready"), 1)

        attendedT = sb("attendedT", [128, KT, T])
        attended = sb("attended", [T, D])

        MHA = {1: dict(piece="a0", bias="a0_qkv", heads=16, scale=0.25, rope=None, mask="tri_10000"),
               4: dict(piece="a1", bias="a1_qkv", heads=16, scale=1.0, rope=("rope1", 2), mask="tri_neg"),
               7: dict(piece="a2", bias="a2_qkv", heads=32, scale=float(1 / np.sqrt(8)), rope=("rope2", 4), mask="tri_neg"),
               8: dict(piece="f2_attn", bias=None, heads=16, scale=0.25, rope=None, mask="tri_neg")}
        mha_order = [s for s in MHA if runs(s)]
        m_qkv, m_tmp = scratch(0, 768), scratch(768, 512, T)
        m_qT = cut(scratch(4480, 4 * T), KT, 2 * T)
        m_qT_halves = cut(scratch(4480, 6 * T), KT, 3 * T)[:, :, 0:T]
        m_v = scratch(5504, 256)
        m_max, m_den, m_inv = scratch(5760, 16), scratch(5776, 16), scratch(5792, 32, T)

        def mha_views(s):
            h = MHA[s]["heads"]
            d = D // h
            g = h // KT
            keys = S[:, 1408:1408 + h * T].rearrange("p (k h t) -> p k h t", k=KT, h=g)
            scores = cut(scratch(3456, g * T), g, T)
            probsT = cut(scratch(1408, g * T), g // 2, 2 * T)
            values = cut(m_v, h // 2, 2 * d)
            return h, d, g, keys, scores, probsT, values

        def mha_part(g, c):
            return slice(g // 2 * c, g // 2 * (c + 1))

        m_scores_bank, m_probsT_bank = (3, 6), (0, 7)

        def mha_tensor(pe, s, n, meanwhile=None):
            u = mha_order.index(s)
            h, d, g, keys, scores, probsT, values = mha_views(s)
            w = W(MHA[s]["piece"])
            weights_here(pe, MHA[s]["piece"])
            normT_here(pe, n)
            for a, b in ((0, 512), (512, 768)):
                for k in range(KT):
                    ins = pe.matmul(psf[:, a:b], xnT[:, k, :, :].rearrange("p a t -> p (a t)"),
                                    w[:, 768 * k + a:768 * k + b], start=k == 0, stop=k == KT - 1)
            ins.then_inc(sem("mha_qkv_psum"), 1)
            pe.wait_ge(sem("mha_qk_ready"), u + 1)
            for k in range(2 * KT):
                ins = pe.transpose(ps[:, 2, k * T:(k + 1) * T], m_qkv[0:T, k * 128:(k + 1) * 128], C("ident")[0:T, 0:T])
            ins.then_inc(sem("mha_qkT_psum"), 1)
            for c in range(2):
                pe.wait_ge(sem("mha_keys_ready"), 2 * u + c + 1)
                for k in range(KT):
                    part = keys[:, k, mha_part(g, c), :].rearrange("p h t -> p (h t)")
                    ins = pe.matmul(bank(m_scores_bank[c], g // 2 * T), m_qT[:, k, :], part, start=k == 0, stop=k == KT - 1)
                ins.then_inc(sem("mha_scores_psum"), 1)
            if meanwhile:
                meanwhile()
            for c in range(2):
                pe.wait_ge(sem("mha_exp_ready"), 2 * u + c + 1)
                for j in range(g // 4):
                    a = g // 2 * c + 2 * j
                    ins = pe.transpose(ps[:, m_probsT_bank[c], 128 * j:128 * j + 128], scores[:, a:a + 2, :].rearrange("p h t -> p (h t)"), C("ident"))
                ins.then_inc(sem("mha_probsT_psum"), 1)
            pe.wait_ge(sem("mha_values_ready"), u + 1)
            for c in range(2):
                pe.wait_ge(sem("mha_probsT_ready"), 2 * u + c + 1)
                for half in range(2):
                    for pair in range(g // 4 * c, g // 4 * (c + 1)):
                        j = g // 2 * half + pair
                        ins = pe.matmul(ps[0:T, 2, 2 * d * j:2 * d * (j + 1)], probsT[:, pair, T * half:T * half + T], values[:, j, :],
                                        start=True, stop=True)
            ins.then_inc(sem("mha_out_psum"), 1)
            out_tensor(pe, s, attended, w[:, 1536:2048], MHA[s]["piece"])

        def mha_vector(dve, s):
            u = mha_order.index(s)
            m = MHA[s]
            h, d, g, keys, scores, probsT, values = mha_views(s)
            dve.wait_ge(sem("mha_qkv_psum"), u + 1)
            if m["bias"]:
                ins = dve.tensor_tensor(m_qkv, psf[:, 0:768], R(m["bias"], 128), ALU.add)
            else:
                ins = dve.tensor_copy(m_qkv, psf[:, 0:768])
            if m["rope"]:
                link(dve, "dve", ins)
                table, half = C(m["rope"][0])[0:T, :], m["rope"][1]
                r, n = 2 * half, 512 // d
                qk, tmp = cut(m_qkv[0:T, 0:512], n, d), cut(m_tmp[:, 0:n * r], n, r)
                cos, sin = spread(table[:, 0:r], 1, n), spread(table[:, r:2 * r], 1, n)
                link(dve, "dve", dve.tensor_tensor(tmp[:, :, 0:half], qk[:, :, half:r], sin[:, :, 0:half], ALU.mult))
                link(dve, "dve", dve.tensor_tensor(tmp[:, :, half:r], qk[:, :, 0:half], sin[:, :, half:r], ALU.mult))
                link(dve, "dve", dve.tensor_tensor(qk[:, :, 0:r], qk[:, :, 0:r], cos, ALU.mult))
                ins = dve.tensor_tensor(qk[:, :, 0:r], qk[:, :, 0:r], tmp, ALU.add)
            ins.then_inc(sem("mha_qk_ready"), 1)
            dve.wait_ge(sem("mha_qk_ready"), u + 1)
            dve.wait_ge(sem("mha_zeros"), 2 * u + 2)
            v = m_qkv[:, 512:768].rearrange("p (j e d) -> p j e d", e=2, d=d)
            dve.tensor_copy(values[0:T, :, 0:d], v[0:T, :, 0, :]).then_inc(sem("mha_half"), 1)
            dve.tensor_copy(values[T:128, :, d:2 * d], v[T:128, :, 1, :]).then_inc(sem("mha_values_ready"), 1)
            dve.wait_ge(sem("mha_qkT_psum"), u + 1)
            dve.tensor_scalar(m_qT_halves, cut(bank(2, KT * T), KT, T), m["scale"], None, ALU.mult).then_inc(sem("mha_half"), 1)
            kT = cut(ps[:, 2, KT * T:2 * KT * T], KT, T)
            for c in range(2):
                dve.tensor_tensor(keys[:, :, mha_part(g, c), :], spread(kT, 2, g // 2),
                                  spread(spread(C("heads%d" % d)[:, mha_part(g, c)], 1, KT), 3, T), ALU.mult).then_inc(sem("mha_keys_ready"), 1)
            for c in range(2):
                dve.wait_ge(sem("mha_scores_psum"), 2 * u + c + 1)
                part, top = scores[:, mha_part(g, c), :], m_max[:, mha_part(g, c)]
                raw = cut(bank(m_scores_bank[c], g // 2 * T), g // 2, T)
                if m["mask"] == "tri_10000":
                    link(dve, "dve", dve.tensor_tensor(part, raw, spread(C("tri"), 1, g // 2), ALU.mult))
                    raw = part
                link(dve, "dve", dve.tensor_tensor(part, raw, spread(C(m["mask"]), 1, g // 2), ALU.add))
                link(dve, "dve", dve.tensor_reduce(top, part, AX, ALU.max))
                dve.tensor_tensor(part, part, spread(top, 2, T), ALU.subtract).then_inc(sem("mha_shifted"), 1)
            dve.wait_ge(sem("mha_exp_ready"), 2 * u + 2)
            link(dve, "dve", dve.tensor_reduce(m_den[:, 0:g], scores, AX, ALU.add))
            for half in range(2):
                link(dve, "dve", dve.reciprocal(m_inv[:, g * half:g * half + g], m_den[T * half:T * half + T, 0:g]))
            dve.wait_ge(sem("mha_out_psum"), u + 1)
            dve.tensor_tensor(cut(attended[:, :], h, d), cut(bank(2, D, T), h, d), spread(m_inv[:, 0:h], 2, d), ALU.mult)\
               .then_inc(sem("attended"), 1)

        def mha_scalar(act, s):
            u = mha_order.index(s)
            h, d, g, keys, scores, probsT, values = mha_views(s)
            for c in range(2):
                act.wait_ge(sem("mha_shifted"), 2 * u + c + 1)
                part = scores[:, mha_part(g, c), :]
                act.activation(part, part, ACT.Exp).then_inc(sem("mha_exp_ready"), 1)
            for c in range(2):
                act.wait_ge(sem("mha_probsT_psum"), 2 * u + c + 1)
                act.copy(probsT[:, g // 4 * c:g // 4 * (c + 1), :], cut(bank(m_probsT_bank[c], g // 4 * 128), g // 4, 2 * T))\
                   .then_inc(sem("mha_probsT_ready"), 1)
            out_scalar(act, s)

        def mha_pool(pool, s):
            pool.wait_ge(sem("norm_ready"), norm_no[s if s != 8 else 8] + 1)
            pool.memset(m_v, 0.0).then_inc(sem("mha_zeros"), 1)
            pool.memset(m_qT, 0.0).then_inc(sem("mha_zeros"), 1)

        def self_attention(s, bias):
            def pe_(pe):
                norm_tensor(pe, s)
                mha_tensor(pe, s, s)

            def dve_(dve):
                norm_vector(dve, s)
                if s == 1:
                    quantise(dve, 3, 4)
                mha_vector(dve, s)
                if s == 1:
                    quantise(dve, 5)
                residual_vector(dve, s, bank(6, D, T), (sem("projected"), outs.index(s) + 1))

            def act_(act):
                norm_scalar(act, s)
                mha_scalar(act, s)

            def pool_(pool):
                norm_pool(pool, s)
                mha_pool(pool, s)
                bias_pool(pool, s, bias)
            return pe_, dve_, act_, pool_

        STAGES = {1: self_attention(1, "a0_out"), 4: self_attention(4, "a1_out"), 7: self_attention(7, "a2_out")}

        def rank_vector(dve, s, n, top, earlier, greater, equal, chosen):
            other, own = spread(s, 1, n), spread(s, 2, n)
            link(dve, "dve", dve.tensor_tensor(greater, other, own, ALU.is_gt))
            link(dve, "dve", dve.tensor_tensor(equal, other, own, ALU.is_equal))
            link(dve, "dve", dve.tensor_tensor(equal, equal, cut(earlier[0:T, :], n, n), ALU.mult))
            link(dve, "dve", dve.tensor_tensor(greater, greater, equal, ALU.add))
            link(dve, "dve", dve.tensor_reduce(chosen, greater, AX, ALU.add))
            link(dve, "dve", dve.tensor_scalar(chosen, chosen, top - 0.5, None, ALU.is_lt))

        f0_act = scratch(0, 1152, T)
        f0_h = cut(scratch(1152, 9 * T), 9, T)
        f0_l = scratch(1728, 8, T)
        f0_max, f0_sum, f0_weight = scratch(1736, 1, T), scratch(1737, 1, T), scratch(1738, 1, T)
        f0_exp, f0_chosen = scratch(1744, 8, T), scratch(1752, 8, T)
        f0_greater, f0_equal = cut(scratch(1760, 64, T), 8, 8), cut(scratch(1824, 64, T), 8, 8)
        f0_parts = ((f0_act[:, 0:1024], psf[0:T, 0:1024], psf[0:T, 1024:2048]), (f0_act[:, 1024:1152], ps[0:T, 4, 0:128], ps[0:T, 4, 128:256]))

        def f0_tensor(pe):
            norm_tensor(pe, 2)
            normT_here(pe, 2)
            for name, at in (("f0_gate", 0), ("f0_up", 1024)):
                weights_here(pe, name)
                for c in range(2):
                    for k in range(KT):
                        ins = pe.matmul(psf[0:T, at + 512 * c:at + 512 * c + 512], xnT[:, k, 0, :], W(name)[:, k * 1024 + 512 * c:k * 1024 + 512 * c + 512],
                                        start=k == 0, stop=k == KT - 1)
                ins.then_inc(sem("f0_part_psum"), 1)
            weights_here(pe, "f0_routed")
            w = W("f0_routed")
            for i in range(2):
                for k in range(KT):
                    ins = pe.matmul(ps[0:T, 4, 128 * i:128 * i + 128], xnT[:, k, 0, :], w[:, 256 * i + 128 * k:256 * i + 128 * k + 128],
                                    start=k == 0, stop=k == KT - 1)
            ins.then_inc(sem("f0_hidden_psum"), 1)
            for k in range(KT):
                ins = pe.matmul(ps[0:T, 7, 256:264], xnT[:, k, 0, :], w[:, 768 + 8 * k:776 + 8 * k], start=k == 0, stop=k == KT - 1)
            ins.then_inc(sem("f0_logits_psum"), 1)
            pe.wait_ge(sem("f0_logits_psum"), since("f0_logits_psum", 1))
            pe.sem_inc(weights_used, 2)
            for m in range(9):
                if m in (0, 8):
                    pe.wait_ge(sem("f0_hidden"), since("f0_hidden", m // 8 + 1))
                ins = pe.transpose(psf[:, T * m:T * m + T], f0_act[:, 128 * m:128 * m + 128], C("ident")[0:T, 0:T])
            ins.then_inc(sem("f0_hT_psum"), 1)
            pe.wait_ge(sem("f0_hT"), since("f0_hT", 1))
            pe.matmul(bank(5, D, T), f0_h[:, 8, :], w[:, 512:768], start=True, stop=True).then_inc(weights_used, 1)
            weights_here(pe, "f0_down")
            for m in range(8):
                ins = pe.matmul(bank(6, D, T), f0_h[:, m, :], W("f0_down")[:, m * D:(m + 1) * D], start=m == 0, stop=m == 7)
            ins.then_inc(sem("f0_out_psum"), 1)
            pe.wait_ge(sem("f0_out_psum"), since("f0_out_psum", 1))
            pe.sem_inc(weights_used, 1)

        def silu_vector(dve, act, g, u, done):
            link(dve, "dve", dve.scalar_tensor_tensor(act, act, 1.0, g, ALU.add, ALU.mult))
            dve.scalar_tensor_tensor(act, act, 0.5, u, ALU.mult, ALU.mult).then_inc(done, 1)

        def f0_vector(dve):
            norm_vector(dve, 2)
            quantise(dve, 6, 7, 8)
            for part, (hidden, g, u) in enumerate(f0_parts):
                dve.wait_ge(sem("f0_tanh"), since("f0_tanh", part + 1))
                if part == 0:
                    dve.wait_ge(sem("f0_part_psum"), 2)
                silu_vector(dve, hidden, g, u, sem("f0_hidden"))
            dve.wait_ge(sem("f0_logits_psum"), since("f0_logits_psum", 1))
            link(dve, "dve", dve.tensor_copy(f0_l, ps[0:T, 7, 256:264]))
            link(dve, "dve", dve.tensor_reduce(f0_max, f0_l, AX, ALU.max))
            dve.tensor_scalar(f0_exp, f0_l, f0_max, None, ALU.subtract).then_inc(sem("f0_shifted"), 1)
            rank_vector(dve, f0_l, 8, 2, C("earlier8"), f0_greater, f0_equal, f0_chosen)
            dve.wait_ge(sem("f0_router_exp"), since("f0_router_exp", 1))
            link(dve, "dve", dve.tensor_tensor(f0_exp, f0_exp, f0_chosen, ALU.mult))
            link(dve, "dve", dve.tensor_reduce(f0_sum, f0_exp, AX, ALU.add))
            link(dve, "dve", dve.reciprocal(f0_sum, f0_sum))
            link(dve, "dve", dve.tensor_scalar(f0_exp, f0_exp, f0_sum, None, ALU.mult))
            link(dve, "dve", dve.tensor_reduce(f0_weight, f0_exp, AX, ALU.add))
            dve.wait_ge(sem("f0_out_psum"), since("f0_out_psum", 1))
            link(dve, "dve", dve.tensor_tensor(x[:, :], x[:, :], bank(6, D, T), ALU.add))
            link(dve, "dve", dve.scalar_tensor_tensor(x[:, :], bank(5, D, T), f0_weight, x[:, :], ALU.mult, ALU.add))

        def f0_scalar(act):
            norm_scalar(act, 2)
            act.wait_ge(sem("f0_part_psum"), 1)
            act.activation(f0_act[:, 0:1024], psf[0:T, 0:1024], ACT.Tanh, scale=0.5).then_inc(sem("f0_tanh"), 1)
            act.wait_ge(sem("f0_hidden_psum"), since("f0_hidden_psum", 1))
            act.activation(f0_act[:, 1024:1152], ps[0:T, 4, 0:128], ACT.Tanh, scale=0.5).then_inc(sem("f0_tanh"), 1)
            act.wait_ge(sem("f0_hT_psum"), since("f0_hT_psum", 1))
            act.copy(f0_h, cut(psf[:, 0:9 * T], 9, T)).then_inc(sem("f0_hT"), 1)
            act.wait_ge(sem("f0_shifted"), since("f0_shifted", 1))
            act.activation(f0_exp, f0_exp, ACT.Exp).then_inc(sem("f0_router_exp"), 1)

        STAGES[2] = (f0_tensor, f0_vector, f0_scalar, lambda pool: norm_pool(pool, 2))

        f1_low_weights = wide[:, :, :].rearrange("p a n -> p (a n)")[:, 0:768]
        f1_up_a, f1_up_b, f1_down_b = f1_low_weights[:, 0:256], f1_low_weights[:, 256:512], f1_low_weights[:, 512:768]
        f1_down_a = x2_keys[:, :, :].rearrange("p a n -> p (a n)")
        f1_low = cut(scratch(1792, 8 * T), 8, T)
        f1_act = [cut(scratch(3500 + 256 * i, 256, T), 2, 128) for i in range(2)]
        f1_h = cut(scratch(2560, 8 * T), 8, T)
        f1_router = cut(scratch(3072, 16), KT, 8)
        f1_p, f1_chosen = scratch(3088, 8, T), scratch(3096, 8, T)
        f1_max, f1_sum = scratch(3104, 1, T), scratch(3105, 1, T)
        f1_greater, f1_equal = cut(scratch(3112, 64, T), 8, 8), cut(scratch(3176, 64, T), 8, 8)
        f1_down_low = scratch(3240, 128, T)
        f1_down_lowT = scratch(3368, T)

        def f1_tensor(pe):
            weights_here(pe, "f1_gate")
            gate = W("f1_gate")
            for k in range(KT):
                ins = pe.matmul(ps[:, 0, 8 * k:8 * k + 8], gate[0:16, 16 + 128 * k:144 + 128 * k], gate[0:16, 272:280],
                                start=True, stop=True)
            ins.then_inc(sem("f1_delta_psum"), 1)
            norm_tensor(pe, 5)
            normT_here(pe, 5)
            pe.wait_ge(sem("f1_router_ready"), 1)
            pe.sem_inc(weights_used, 1)
            for k in range(KT):
                ins = pe.matmul(ps[0:T, 0, 32:40], xnT[:, k, 0, :], f1_router[:, k, :], start=k == 0, stop=k == KT - 1)
            ins.then_inc(sem("f1_logits_psum"), 1)
            pe.wait_ge(sem("f1_lora_copied"), 2)
            pe.sem_inc(weights_used, 1)
            for k in range(KT):
                ins = pe.matmul(ps[:, 1, 0:T], f1_up_a[:, 128 * k:128 * k + 128], xnT[:, k, 0, :], start=k == 0, stop=k == KT - 1)
            ins.then_inc(sem("f1_low_psum"), 1)
            pe.wait_ge(sem("f1_low_ready"), since("f1_low_ready", 1))

            def up(n):
                weights_here(pe, f"f1_experts{n}")
                if n >= 2:
                    pe.wait_ge(sem("f1_hidden"), since("f1_hidden", n - 1))
                for i in range(2):
                    out = ps[0:T, 2 + n % 2, 256 * i:256 * i + 256]
                    for k in range(KT):
                        a = 768 * i + 256 * k
                        pe.matmul(out, xnT[:, k, 0, :], W(f"f1_experts{n}")[:, a:a + 256], start=k == 0, stop=False)
                    ins = pe.matmul(out, f1_low[:, 2 * n + i, :], f1_up_b, start=False, stop=True)
                ins.then_inc(sem("f1_gates_psum"), 1)

            def turn(n):
                pe.wait_ge(sem("f1_hidden"), since("f1_hidden", n + 1))
                if n >= 2:
                    pe.wait_ge(sem("f1_hT"), since("f1_hT", n - 1))
                for i in range(2):
                    ins = pe.transpose(ps[:, 6 + n % 2, T * i:T * i + T], f1_act[n % 2][:, i, :], C("ident")[0:T, 0:T])
                ins.then_inc(sem("f1_hT_psum"), 1)

            def down(n):
                pe.wait_ge(sem("f1_hT"), since("f1_hT", n + 1))
                for i in range(2):
                    e = 2 * n + i
                    pe.matmul(ps[0:T, 1, 128:256], f1_h[:, e, :], f1_down_a[:, 128 * e:128 * e + 128], start=e == 0, stop=e == 7,
                              skip_group_check=True)
                if n >= 2:
                    pe.wait_ge(sem("f1_added"), since("f1_added", n - 1))
                for i in range(2):
                    a = 768 * i + 512
                    ins = pe.matmul(ps[0:T, 4 + n % 2, D * i:D * i + D], f1_h[:, 2 * n + i, :], W(f"f1_experts{n}")[:, a:a + D],
                                    start=True, stop=True)
                ins.then_inc(sem("f1_expert_psum"), 1)
                pe.wait_ge(sem("f1_expert_psum"), since("f1_expert_psum", n + 1))
                pe.sem_inc(weights_used, 1)

            up(0)
            for n in range(1, 4):
                up(n)
                turn(n - 1)
                if n >= 2:
                    down(n - 2)
            turn(3)
            down(2)
            down(3)
            pe.wait_ge(sem("f1_down_low_ready"), 1)
            pe.transpose(ps[:, 0, 64:64 + T], f1_down_low, C("ident")[0:T, 0:T]).then_inc(sem("f1_down_lowT_psum"), 1)
            pe.wait_ge(sem("f1_down_lowT_ready"), since("f1_down_lowT_ready", 1))
            pe.matmul(bank(6, D, T), f1_down_lowT, f1_down_b, start=True, stop=True).then_inc(sem("f1_lora_psum"), 1)

        def f1_vector(dve):
            weights_here(dve, "f1_gate")
            dve.wait_ge(sem("f1_delta_psum"), 1)
            dve.scalar_tensor_tensor(f1_router, cut(ps[:, 0, 0:16], KT, 8), 2.0, cut(W("f1_gate")[:, 0:16], KT, 8),
                                     ALU.mult, ALU.add).then_inc(sem("f1_router_ready"), 1)
            norm_vector(dve, 5)
            dve.wait_ge(sem("f1_low_psum"), since("f1_low_psum", 1))
            dve.scalar_tensor_tensor(f1_low, spread(ps[:, 1, 0:T], 1, 8), 2.0, spread(C("heads16"), 2, T), ALU.mult, ALU.mult)\
               .then_inc(sem("f1_low_ready"), 1)
            dve.wait_ge(sem("f1_logits_psum"), since("f1_logits_psum", 1))
            link(dve, "dve", dve.tensor_reduce(f1_max, ps[0:T, 0, 32:40], AX, ALU.max))
            dve.tensor_scalar(f1_p, ps[0:T, 0, 32:40], f1_max, None, ALU.subtract).then_inc(sem("f1_shifted"), 1)
            dve.wait_ge(sem("f1_router_exp"), since("f1_router_exp", 1))
            link(dve, "dve", dve.tensor_reduce(f1_sum, f1_p, AX, ALU.add))
            link(dve, "dve", dve.reciprocal(f1_sum, f1_sum))
            link(dve, "dve", dve.tensor_scalar(f1_p, f1_p, f1_sum, None, ALU.mult))
            rank_vector(dve, f1_p, 8, 2, C("earlier8"), f1_greater, f1_equal, f1_chosen)
            link(dve, "dve", dve.tensor_tensor(f1_p, f1_p, f1_chosen, ALU.mult))
            link(dve, "dve", dve.tensor_reduce(f1_sum, f1_p, AX, ALU.add))
            link(dve, "dve", dve.reciprocal(f1_sum, f1_sum))
            link(dve, "dve", dve.tensor_scalar(f1_p, f1_p, f1_sum, None, ALU.mult))

            def add(n):
                dve.wait_ge(sem("f1_expert_psum"), since("f1_expert_psum", n + 1))
                for i in range(2):
                    ins = dve.scalar_tensor_tensor(x[:, :], ps[0:T, 4 + n % 2, D * i:D * i + D], f1_p[:, 2 * n + i:2 * n + i + 1],
                                                   x[:, :], ALU.mult, ALU.add)
                    if i == 0:
                        link(dve, "dve", ins)
                ins.then_inc(sem("f1_added"), 1)
                dve.wait_ge(sem("f1_added"), since("f1_added", n + 1))

            for n in range(4):
                dve.wait_ge(sem("f1_tanh"), since("f1_tanh", n + 1))
                b = cut(ps[0:T, 2 + n % 2, :], 2, 256)
                silu_vector(dve, f1_act[n % 2], b[:, :, 0:128], b[:, :, 128:256], sem("f1_hidden"))
                if n >= 2:
                    add(n - 2)
            add(2)
            dve.wait_ge(sem("f1_expert_psum"), since("f1_expert_psum", 4))
            dve.scalar_tensor_tensor(cut(f1_down_low, 8, 16), cut(ps[0:T, 1, 128:256], 8, 16), 2.0, spread(f1_p, 2, 16),
                                     ALU.mult, ALU.mult).then_inc(sem("f1_down_low_ready"), 1)
            add(3)
            residual_vector(dve, 5, bank(6, D, T), (sem("f1_lora_psum"), since("f1_lora_psum", 1)))

        def f1_scalar(act):
            norm_scalar(act, 5)
            act.wait_ge(sem("f1_shifted"), since("f1_shifted", 1))
            act.activation(f1_p, f1_p, ACT.Exp).then_inc(sem("f1_router_exp"), 1)

            def tanh(n):
                act.wait_ge(sem("f1_gates_psum"), since("f1_gates_psum", n + 1))
                if n >= 2:
                    act.wait_ge(sem("f1_hT_psum"), since("f1_hT_psum", n - 1))
                act.activation(f1_act[n % 2], cut(ps[0:T, 2 + n % 2, :], 2, 256)[:, :, 0:128], ACT.Tanh, scale=0.5)\
                   .then_inc(sem("f1_tanh"), 1)

            def copy(n):
                act.wait_ge(sem("f1_hT_psum"), since("f1_hT_psum", n + 1))
                act.copy(f1_h[:, 2 * n:2 * n + 2, :], cut(ps[:, 6 + n % 2, 0:2 * T], 2, T)).then_inc(sem("f1_hT"), 1)

            tanh(0)
            for n in range(1, 4):
                tanh(n)
                copy(n - 1)
            copy(3)
            act.wait_ge(sem("f1_down_lowT_psum"), since("f1_down_lowT_psum", 1))
            act.copy(f1_down_lowT, ps[:, 0, 64:64 + T]).then_inc(sem("f1_down_lowT_ready"), 1)

        def f1_pool(pool):
            weights_here(pool, "f1_lora")
            pool.tensor_copy(f1_low_weights, W("f1_lora")[:, 0:768]).then_inc(sem("f1_lora_copied"), 1)
            pool.tensor_copy(f1_down_a, W("f1_lora")[:, 768:1792]).then_inc(sem("f1_lora_copied"), 1)
            norm_pool(pool, 5)

        STAGES[5] = (f1_tensor, f1_vector, f1_scalar, f1_pool)

        xr = sb("xr", [T, D])
        f2_attn = scratch(0, D, T)
        f2_attnT = cut(scratch(256, KT * T), KT, T)
        f2_hT = cut(scratch(6016, KT * T), KT, T)
        f2_mod, f2_modT = scratch(384, 16, T), scratch(400, T, 16)
        f2_act, f2_h = scratch(512, 1024, T), cut(scratch(1536, 512), 8, T)
        f2_g, f2_u = psf[0:T, 2048:3072], ps[0:T, 1:4:2, :]

        def f2_tensor(pe):
            norm_tensor(pe, 8.5, xr)

            def hidden(name, c, out, stop):
                weights_here(pe, name)
                for k in range(KT):
                    ins = pe.matmul(bank(out, 512, T), f2_hT[:, k, :], W(name)[:, 1024 * k + 512 * c:1024 * k + 512 * c + 512],
                                    start=k == 0, stop=stop and k == KT - 1)
                return ins

            def meanwhile():
                hidden("f2_gate", 0, 4, False)
                hidden("f2_gate", 1, 5, False)
                hidden("f2_up", 0, 1, True)

            mha_tensor(pe, 8, 8.5, meanwhile)
            hidden("f2_up", 1, 3, True).then_inc(sem("f2_ups_psum"), 1)
            pe.wait_ge(sem("f2_attn_ready"), 1)
            for n in range(KT):
                ins = pe.transpose(ps[:, 7, n * T:(n + 1) * T], f2_attn[:, n * 128:(n + 1) * 128], C("ident")[0:T, 0:T])
            ins.then_inc(sem("f2_attnT_psum"), 1)
            weights_here(pe, "f2_mod")
            w = W("f2_mod")
            pe.wait_ge(sem("f2_attnT_ready"), 1)
            for at, src in ((0, f2_attnT), (16, f2_hT)):
                for k in range(KT):
                    ins = pe.matmul(ps[0:T, 0, at:at + 16], src[:, k, :], w[:, 16 * k:16 * k + 16], start=k == 0, stop=k == KT - 1)
            ins.then_inc(sem("f2_low_psum"), 1)
            pe.wait_ge(sem("f2_mod_ready"), since("f2_mod_ready", 1))
            pe.transpose(ps[0:16, 2, 0:T], f2_mod, C("ident")[0:T, 0:T]).then_inc(sem("f2_modT_psum"), 1)
            pe.wait_ge(sem("f2_modT_ready"), since("f2_modT_ready", 1))
            for c in range(2):
                ins = pe.matmul(bank(4 + c, 512, T), f2_modT, w[0:16, 32 + 512 * c:544 + 512 * c], start=False, stop=True)
            ins.then_inc(sem("f2_hidden_psum"), 1)
            pe.wait_ge(sem("f2_hidden_psum"), since("f2_hidden_psum", 1))
            pe.sem_inc(weights_used, 3)
            pe.wait_ge(sem("f2_hidden"), since("f2_hidden", 1))
            for m in range(8):
                ins = pe.transpose(ps[:, 0, T * m:T * m + T], f2_act[:, 128 * m:128 * m + 128], C("ident")[0:T, 0:T])
            ins.then_inc(sem("f2_hiddenT_psum"), 1)
            pe.wait_ge(sem("f2_hiddenT"), since("f2_hiddenT", 1))
            weights_here(pe, "f2_down")
            for m in range(8):
                ins = pe.matmul(bank(6, D, T), f2_h[:, m, :], W("f2_down")[:, m * D:(m + 1) * D], start=m == 0, stop=m == 7)
            ins.then_inc(sem("f2_out_psum"), 1)
            pe.wait_ge(sem("f2_out_psum"), since("f2_out_psum", 1))
            pe.sem_inc(weights_used, 1)

        def f2_vector(dve):
            norm_vector(dve, 8)
            norm_vector(dve, 8.5, xn, xr, RMS_EPS, rms=True)
            mha_vector(dve, 8)
            dve.wait_ge(sem("projected"), outs.index(8) + 1)
            dve.tensor_copy(f2_attn, bank(6, D, T)).then_inc(sem("f2_attn_ready"), 1)
            dve.wait_ge(sem("f2_tanh"), 1)
            dve.scalar_tensor_tensor(f2_mod, f2_mod, 0.1, ps[0:T, 0, 16:32], ALU.mult, ALU.mult).then_inc(sem("f2_mod_ready"), 1)
            dve.wait_ge(sem("f2_gate_tanh"), since("f2_gate_tanh", 1))
            dve.wait_ge(sem("f2_ups_psum"), 1)
            halves = cut(f2_act, 2, 512)
            silu_vector(dve, halves, cut(f2_g, 2, 512), f2_u, sem("f2_hidden"))
            link(dve, "dve", dve.tensor_tensor(x[:, :], x[:, :], xn[:, :], ALU.add))
            residual_vector(dve, 8, bank(6, D, T), (sem("f2_out_psum"), since("f2_out_psum", 1)))

        def f2_scalar(act):
            act.wait_ge(sem("normT_psum"), transposed_no[8.5] + 1)
            src = cut(bank(7, KT * T), KT, T)
            for k in range(KT):
                act.activation(f2_hT[:, k, :], src[:, k, :], ACT.Copy, scale=V("ln2_w")[:, k:k + 1]).then_inc(sem("f2_hT_half"), 1)
            for k in range(KT):
                ins = act.activation(xnT[:, k, :, :], spread(src[:, k, :], 1, 2), ACT.Copy, scale=V("ln1_w")[:, k:k + 1])
            ins.then_inc(sem("normT_ready"), 1)
            mha_scalar(act, 8)
            act.wait_ge(sem("f2_attnT_psum"), 1)
            act.copy(f2_attnT, src).then_inc(sem("f2_attnT_ready"), 1)
            act.wait_ge(sem("f2_low_psum"), since("f2_low_psum", 1))
            act.activation(f2_mod, ps[0:T, 0, 0:16], ACT.Tanh).then_inc(sem("f2_tanh"), 1)
            act.wait_ge(sem("f2_modT_psum"), since("f2_modT_psum", 1))
            act.copy(f2_modT, ps[0:16, 2, 0:T]).then_inc(sem("f2_modT_ready"), 1)
            act.wait_ge(sem("f2_hidden_psum"), since("f2_hidden_psum", 1))
            act.activation(f2_act, f2_g, ACT.Tanh, scale=0.5).then_inc(sem("f2_gate_tanh"), 1)
            act.wait_ge(sem("f2_hiddenT_psum"), since("f2_hiddenT_psum", 1))
            act.copy(f2_h, cut(bank(0), 8, T)).then_inc(sem("f2_hiddenT"), 1)

        def f2_pool(pool):
            norm_pool(pool, 8)
            norm_pool(pool, 8.5)
            mha_pool(pool, 8)

        STAGES[8] = (f2_tensor, f2_vector, f2_scalar, f2_pool)

        a3_padded = scratch(0, 4 * (T + 2)).rearrange("p (w k t) -> p w k t", w=2, k=KT)
        a3_v = cut(scratch(264, KT * T), KT, T)
        a3_conv = scratch(392, 4 * T).rearrange("p (w k t) -> p w k t", w=2, k=KT)
        a3_kv, a3_y = cut(scratch(648, KT * T), KT, T), cut(scratch(776, KT * T), KT, T)
        a3_kvN = scratch(904, D, T)
        a3_filter = cut(scratch(1160, 2 * D, FREQ), 2, D)
        a3_left, a3_right = cut(scratch(1672, 2 * D, FREQ), 2, D), cut(scratch(2184, 2 * D, FREQ), 2, D)

        def a3_tensor(pe):
            for i in range(2):
                ins = pe.matmul(ps[0:FREQ, 2, D * i:D * i + D], C("dft")[:, FREQ * i:FREQ * i + FREQ], filter_sb[:, :], start=True, stop=True)
            ins.then_inc(sem("a3_filter_psum"), 1)
            norm_tensor(pe, 10)
            normT_here(pe, 10)
            weights_here(pe, "a3")
            w = W("a3")
            for i in range(3):
                for o in range(KT):
                    for k in range(KT):
                        a = 512 * i + 256 * k + 128 * o
                        ins = pe.matmul(ps[:, 0, (2 * i + o) * T:(2 * i + o + 1) * T], w[:, a:a + 128], xnT[:, k, 0, :],
                                        start=k == 0, stop=k == KT - 1)
            ins.then_inc(sem("a3_qkv_psum"), 1)
            pe.wait_ge(sem("a3_kv_ready"), 1)
            for k in range(KT):
                ins = pe.transpose(ps[0:T, 1, 128 * k:128 * k + 128], a3_kv[:, k, :], C("ident"))
            ins.then_inc(sem("a3_kvN_psum"), 1)
            pe.wait_ge(sem("a3_kvN_ready"), 1)
            for i in range(2):
                ins = pe.matmul(ps[0:FREQ, 3, D * i:D * i + D], C("dft")[0:T, FREQ * i:FREQ * i + FREQ], a3_kvN, start=True, stop=True)
            ins.then_inc(sem("a3_spectrum_psum"), 1)
            pe.wait_ge(sem("a3_product_ready"), 1)
            for o in range(KT):
                for i in range(2):
                    ins = pe.matmul(ps[:, 4, o * T:(o + 1) * T], a3_left[:, i, 128 * o:128 * o + 128],
                                    C("idft")[0:FREQ, T * i:T * i + T], start=i == 0, stop=i == 1)
            ins.then_inc(sem("a3_long_psum"), 1)
            pe.wait_ge(sem("a3_y_ready"), 1)
            for k in range(KT):
                ins = pe.matmul(bank(6, D, T), a3_y[:, k, :], w[:, 1536 + D * k:1536 + D * k + D], start=k == 0, stop=k == KT - 1)
            ins.then_inc(sem("a3_out_psum"), 1)
            pe.wait_ge(sem("a3_out_psum"), since("a3_out_psum", 1))
            pe.sem_inc(weights_used, 1)

        def a3_vector(dve):
            norm_vector(dve, 10)
            dve.wait_ge(sem("a3_filter_psum"), 1)
            link(dve, "dve", dve.tensor_copy(a3_filter, cut(ps[0:FREQ, 2, :], 2, D)))
            dve.wait_ge(sem("a3_padding"), 1)
            dve.wait_ge(sem("a3_qkv_psum"), since("a3_qkv_psum", 1))
            for i in (1, 2, 0):
                for k in range(KT):
                    out = a3_padded[:, i, k, 2:] if i < 2 else a3_v[:, k, :]
                    ins = dve.tensor_scalar(out, ps[:, 0, (2 * i + k) * T:(2 * i + k + 1) * T], V("a3_b")[:, 2 * i + k:2 * i + k + 1],
                                            None, ALU.add)
            link(dve, "dve", ins)
            for i in (1, 0):
                for tap in range(3):
                    for k in range(KT):
                        src, out = a3_padded[:, i, k, tap:tap + T], a3_conv[:, i, k, :]
                        weight = V("conv_w")[:, 6 * i + 3 * k + tap:6 * i + 3 * k + tap + 1]
                        if tap == 0:
                            ins = dve.tensor_scalar(out, src, weight, V("conv_b")[:, 2 * i + k:2 * i + k + 1], ALU.mult, ALU.add)
                        else:
                            ins = dve.scalar_tensor_tensor(out, src, weight, out, ALU.mult, ALU.add)
                    link(dve, "dve", ins)
                if i == 1:
                    dve.tensor_tensor(a3_kv, a3_conv[:, 1, :, :], a3_v, ALU.mult).then_inc(sem("a3_kv_ready"), 1)
            dve.wait_ge(sem("a3_spectrum_psum"), 1)
            spectrum = cut(ps[0:FREQ, 3, :], 2, D)
            dve.tensor_tensor(a3_left, spectrum, spread(a3_filter[:, 0, :], 1, 2), ALU.mult).then_inc(sem("a3_part"), 1)
            dve.tensor_tensor(a3_right[:, 0, :], spectrum[:, 1, :], a3_filter[:, 1, :], ALU.mult).then_inc(sem("a3_part"), 1)
            dve.tensor_tensor(a3_right[:, 1, :], spectrum[:, 0, :], a3_filter[:, 1, :], ALU.mult).then_inc(sem("a3_part"), 1)
            dve.wait_ge(sem("a3_part"), 3)
            link(dve, "dve", dve.tensor_tensor(a3_left[:, 0, :], a3_left[:, 0, :], a3_right[:, 0, :], ALU.subtract))
            dve.tensor_tensor(a3_left[:, 1, :], a3_left[:, 1, :], a3_right[:, 1, :], ALU.add).then_inc(sem("a3_product_ready"), 1)
            dve.wait_ge(sem("a3_kv_ready"), 1)
            dve.wait_ge(sem("a3_long_psum"), 1)
            for k in range(KT):
                ins = dve.scalar_tensor_tensor(a3_y[:, k, :], a3_kv[:, k, :], V("d_skip")[:, k:k + 1], ps[:, 4, k * T:(k + 1) * T],
                                               ALU.mult, ALU.add)
            link(dve, "dve", ins)
            dve.tensor_tensor(a3_y, a3_y, a3_conv[:, 0, :, :], ALU.mult).then_inc(sem("a3_y_ready"), 1)
            residual_vector(dve, 10, bank(6, D, T), (sem("a3_out_psum"), since("a3_out_psum", 1)))

        def a3_scalar(act):
            norm_scalar(act, 10)
            act.wait_ge(sem("a3_kvN_psum"), 1)
            act.copy(a3_kvN, ps[0:T, 1, 0:D]).then_inc(sem("a3_kvN_ready"), 1)

        def a3_pool(pool):
            norm_pool(pool, 10)
            pool.wait_ge(sem("norm_ready"), norm_no[10] + 1)
            pool.memset(a3_padded[:, :, :, 0:2], 0.0).then_inc(sem("a3_padding"), 1)
            bias_pool(pool, 10, "a3_out")

        STAGES[10] = (a3_tensor, a3_vector, a3_scalar, a3_pool)

        f3_s, f3_chosen = scratch(0, 16, T), scratch(16, 16, T)
        f3_sum = scratch(32, 1, T)
        f3_gates, f3_gatesT = scratch(36, NE, T), scratch(64, T, NE)
        f3_greater, f3_equal = cut(scratch(128, 256, T), 16, 16), cut(scratch(384, 256, T), 16, 16)
        f3_hidden = [scratch(640 + 2 * FF * i, 2 * FF, T) for i in range(2)]
        f3_h = [cut(scratch(640 + 4 * FF + 4 * T * i, 4 * T, FH), 4, T) for i in range(2)]
        f3_out = lambda n: ps[0:T, 5 + 2 * (n % 2), :]

        def f3_tensor(pe):
            norm_tensor(pe, 11)
            normT_here(pe, 11)
            weights_here(pe, "f3_experts0")
            w = W("f3_experts0")[:, F3_EXPERTS:]
            for k in range(KT):
                ins = pe.matmul(ps[0:T, 0, 0:16], xnT[:, k, 0, :], w[:, 16 * k:16 * k + 16], start=k == 0, stop=k == KT - 1)
            ins.then_inc(sem("f3_logits_psum"), 1)

            def hidden(n):
                weights_here(pe, f"f3_experts{n}")
                if n >= 2:
                    pe.wait_ge(sem("f3_copied"), since("f3_copied", n - 1))
                for k in range(KT):
                    ins = pe.matmul(ps[0:T, 1 + n % 2, 0:2 * FF], xnT[:, k, 0, :], W(f"f3_experts{n}")[:, 2 * FF * k:2 * FF * (k + 1)],
                                    start=k == 0, stop=k == KT - 1)
                ins.then_inc(sem("f3_hidden_psum"), 1)

            def turn(n):
                pe.wait_ge(sem("f3_copied"), since("f3_copied", n + 1))
                if n >= 2:
                    pe.wait_ge(sem("f3_relu"), since("f3_relu", n - 1))
                for i in range(4):
                    ins = pe.transpose(ps[0:FH, 3 + n % 2, T * i:T * i + T], f3_hidden[n % 2][:, FH * i:FH * i + FH], C("ident")[0:T, 0:T])
                ins.then_inc(sem("f3_hT_psum"), 1)

            def output(n):
                pe.wait_ge(sem("f3_relu"), since("f3_relu", n + 1))
                if n >= 2:
                    pe.wait_ge(sem("f3_added"), since("f3_added", 2 * n - 2))
                for i in range(4):
                    a = 4 * FF + D * i
                    ins = pe.matmul(f3_out(n)[:, D * (i // 2):D * (i // 2) + D], f3_h[n % 2][:, i, :], W(f"f3_experts{n}")[0:FH, a:a + D],
                                    start=i % 2 == 0, stop=i % 2 == 1)
                ins.then_inc(sem("f3_expert_psum"), 1)

            hidden(0)
            hidden(1)
            turn(0)
            for n in range(NE // 2):
                if n + 2 < NE // 2:
                    hidden(n + 2)
                if n + 1 < NE // 2:
                    turn(n + 1)
                output(n)
                if n == 0:
                    pe.wait_ge(sem("f3_gates_ready"), 1)
                    pe.transpose(ps[0:NE, 0, 32:32 + T], f3_gates, C("ident")[0:T, 0:T]).then_inc(sem("f3_gatesT_psum"), 1)
                    pe.wait_ge(sem("f3_gatesT_ready"), since("f3_gatesT_ready", 1))
                    pe.matmul(bank(6, D, T), f3_gatesT, w[0:NE, 32:288], start=True, stop=True).then_inc(sem("f3_bias_psum"), 1)
                    pe.wait_ge(sem("f3_bias_psum"), since("f3_bias_psum", 1))
                if n + NSLOT < NE // 2:
                    pe.wait_ge(sem("f3_expert_psum"), since("f3_expert_psum", n + 1))
                    pe.sem_inc(weights_used, 1)

        def f3_vector(dve):
            norm_vector(dve, 11)
            dve.memset(f3_gates[:, 16:NE], 1.0).then_inc(sem("f3_ones"), 1)

            def copy(n):
                dve.wait_ge(sem("f3_hidden_psum"), since("f3_hidden_psum", n + 1))
                if n >= 2:
                    dve.wait_ge(sem("f3_hT_psum"), since("f3_hT_psum", n - 1))
                dve.tensor_copy(f3_hidden[n % 2], ps[0:T, 1 + n % 2, 0:2 * FF]).then_inc(sem("f3_copied"), 1)

            copy(0)
            copy(1)
            dve.wait_ge(sem("f3_exp"), since("f3_exp", 1))
            link(dve, "dve", dve.tensor_scalar(f3_s, f3_s, 1.0, None, ALU.add))
            link(dve, "dve", dve.reciprocal(f3_s, f3_s))
            link(dve, "dve", dve.tensor_tensor(f3_s, f3_s, R("f3_bias"), ALU.add))
            rank_vector(dve, f3_s, 16, 4, C("earlier16"), f3_greater, f3_equal, f3_chosen)
            link(dve, "dve", dve.tensor_tensor(f3_s, f3_s, f3_chosen, ALU.mult))
            link(dve, "dve", dve.tensor_reduce(f3_sum, f3_s, AX, ALU.add))
            link(dve, "dve", dve.tensor_scalar(f3_sum, f3_sum, 1e-8, None, ALU.max))
            link(dve, "dve", dve.reciprocal(f3_sum, f3_sum))
            dve.wait_ge(sem("f3_ones"), 1)
            dve.tensor_scalar(f3_gates[:, 0:16], f3_s, f3_sum, None, ALU.mult).then_inc(sem("f3_gates_ready"), 1)
            dve.wait_ge(sem("f3_gates_ready"), 1)
            link(dve, "dve", dve.tensor_tensor(x[:, :], x[:, :], xn[:, :], ALU.add))
            residual_vector(dve, 11, bank(6, D, T), (sem("f3_bias_psum"), since("f3_bias_psum", 1)))
            for n in range(NE // 2):
                if n + 2 < NE // 2:
                    copy(n + 2)
                dve.wait_ge(sem("f3_expert_psum"), since("f3_expert_psum", n + 1))
                for e in (2 * n, 2 * n + 1):
                    dve.scalar_tensor_tensor(x[:, :], f3_out(n)[:, D * (e % 2):D * (e % 2) + D], f3_gates[:, e:e + 1], x[:, :], ALU.mult, ALU.add)\
                       .then_inc(sem("f3_added"), 1)
                    dve.wait_ge(sem("f3_added"), since("f3_added", e + 1))

        def f3_scalar(act):
            norm_scalar(act, 11)
            act.wait_ge(sem("f3_logits_psum"), since("f3_logits_psum", 1))
            act.activation(f3_s, ps[0:T, 0, 0:16], ACT.Exp, scale=-1.0).then_inc(sem("f3_exp"), 1)

            def relu(n):
                act.wait_ge(sem("f3_hT_psum"), since("f3_hT_psum", n + 1))
                if n >= 2:
                    act.wait_ge(sem("f3_expert_psum"), since("f3_expert_psum", n - 1))
                for i in range(4):
                    ins = act.activation(f3_h[n % 2][:, i, :], ps[0:FH, 3 + n % 2, T * i:T * i + T], ACT.Relu,
                                         bias=V("f3_b1")[0:FH, 4 * n + i:4 * n + i + 1])
                ins.then_inc(sem("f3_relu"), 1)

            relu(0)
            relu(1)
            act.wait_ge(sem("f3_gatesT_psum"), since("f3_gatesT_psum", 1))
            act.copy(f3_gatesT, ps[0:NE, 0, 32:32 + T]).then_inc(sem("f3_gatesT_ready"), 1)
            for n in range(2, NE // 2):
                relu(n)

        STAGES[11] = (f3_tensor, f3_vector, f3_scalar, lambda pool: norm_pool(pool, 11))

        ds = bass.ds

        sw_ctxT = [cut(scratch(1024 * i, 1024), KT, CHUNK) for i in range(2)]
        sw_kT = cut(scratch(2048, 1024), KT, CHUNK)
        sw_features = [scratch(3072 + 1024 * i, 1024, TILE) for i in range(2)]
        sw_values = [cut(scratch(5120 + 264 * i, 264, TILE), PAIRS, 33) for i in range(2)]
        sw_key = scratch(5648, D, TILE)
        sw_absmax, sw_step, sw_inv = scratch(5904, 16, TILE), scratch(5920, 16, TILE), scratch(5936, 16, TILE)
        sw_key_both = sb("sw_key_out", [TILE, 2, D])
        sw_key_out = [sw_key_both[:, i, :] for i in range(2)]
        sw_value_absmax = scratch(5952, D)
        sw_value_part = sb("sw_value_part", [128, D])
        value_inv = scratch(5952, D, TILE)
        value_tmp = wide[:, :, :].rearrange("p a n -> p (a n)")
        vals_flat = vals[:, :, :].rearrange("p n d -> p (n d)")
        vals_int = cut(vals_flat[0:TILE, 0:NT * D // 2].bitcast(BF16), NT, D)
        back = vals_flat[:, NT * D // 2:]

        def sweep_first_load(sp, i):
            sp.dma_start(sw_ctxT[i], io["ctxT"][:, :, span(i)]).then_inc(sem(f"ctx_in{i}"), 16)

        def sweep_loads(sp):
            with sp.Fori(0, NC // 2 - 1) as i:
                for ph in range(2):
                    sp.wait_ge(sem("sw_proj_psum"), SUB * (i * 2 + ph + 1))
                    sp.dma_start(sw_ctxT[ph], io["ctxT"][:, :, ds((i * 2 + ph + 2) * CHUNK, CHUNK)]).then_inc(sem(f"ctx_in{ph}"), 16)
            sp.wait_ge(sem("sw_proj_psum"), SUB * (NC - 2))
            sp.dma_start(sw_ctxT[0][:, :, 0:width(NC - 1)], io["ctxT"][:, :, span(NC - 1)]).then_inc(sem("ctx_in0"), 16)

        def sweep_tensor(pe):
            w, wf = W("pre"), W("pre_features")
            sums = ps[:, 6, :]

            def add_sums(buf, start, stop):
                for j in range(PAIRS):
                    ins = pe.matmul(sums[:, 33 * j:33 * j + 33], sw_features[buf][:, 128 * j:128 * j + 128], sw_values[buf][:, j, :],
                                    start=start, stop=stop, skip_group_check=True)
                return ins

            def turn_keys(buf):
                for k in range(KT):
                    ins = pe.transpose(ps[:, 7, TILE * k:TILE * k + TILE], sw_key_out[buf][:, 128 * k:128 * k + 128],
                                       C("ident")[0:TILE, 0:TILE])
                ins.then_inc(sem("sw_keysT_psum"), 1)

            for free in ("sw_features_psum0", "sw_features_psum1", "sw_added", "sw_keysT_psum"):
                pe.sem_inc(sem(free), 1)
            pe.wait_ge(sem("sw_zeros"), 3)
            add_sums(1, True, False)
            pe.wait_ge(sem("key_weights_in"), 16)

            def chunk(it, ph, n, loaded):
                pe.wait_ge(sem(f"ctx_in{ph}"), loaded * 16)
                for o in range(KT):
                    pe.wait_ge(sem(f"sw_kT{o}"), it + 1)
                    for k in range(KT):
                        ins = pe.matmul(ps[:, o, 0:n * TILE], w[:, 256 * k + 128 * o:256 * k + 128 * o + 128], sw_ctxT[ph][:, k, 0:n * TILE],
                                        start=k == 0, stop=k == KT - 1)
                    ins.then_inc(sem(f"sw_kT_psum{o}"), 1)
                weights_here(pe, "pre")
                weights_here(pe, "pre_features")
                pe.wait_ge(sem("constants_in"), 16)
                for s in range(n):
                    u = it * SUB + s
                    pe.wait_ge(sem("sw_proj_used"), u + 1)
                    for b, a, m in ((2, 0, 512), (3, 512, 256)):
                        for k in range(KT):
                            ins = pe.matmul(ps[0:TILE, b, 0:m], sw_ctxT[ph][:, k, TILE * s:TILE * s + TILE],
                                            w[:, 512 + 768 * k + a:512 + 768 * k + a + m], start=k == 0, stop=k == KT - 1)
                    ins.then_inc(sem("sw_proj_psum"), 1)
                    for g in range(KT):
                        if s == 0:
                            pe.wait_ge(sem(f"sw_kT{g}"), it + 2)
                        pe.wait_ge(sem(f"sw_features{g}"), u + 1)
                        pe.matmul(ps[0:TILE, 4 + g, :], sw_kT[:, g, TILE * s:TILE * s + TILE], wf, start=True, stop=True)\
                          .then_inc(sem(f"sw_features_psum{g}"), 1)
                    pe.wait_ge(sem("sw_values_ready"), u + 1)
                    add_sums((s + 1) % 2, False, False).then_inc(sem("sw_added"), 1)
                    pe.wait_ge(sem("sw_key_ready"), u + 1)
                    pe.wait_ge(sem("sw_keysT"), u + 1)
                    turn_keys((s + 1) % 2)
            with pe.Fori(0, NC // 2) as i:
                for ph in range(2):
                    chunk(i * 2 + ph, ph, SUB, i + 1)
            chunk(NC - 1, 0, subs(NC - 1), NC // 2 + 1)
            last = (subs(NC - 1) - 1) % 2
            for g in range(KT):
                pe.wait_ge(sem(f"sw_features{g}"), NT + 1)
            pe.wait_ge(sem("sw_values_ready"), NT + 1)
            add_sums(last, False, True).then_inc(sem("sw_added"), 1)
            pe.wait_ge(sem("sw_key_ready"), NT + 1)
            pe.wait_ge(sem("sw_keysT"), NT + 1)
            turn_keys(last)
            pe.wait_ge(sem("sw_features_psum1"), NT + 1)
            pe.sem_inc(weights_used, 2)
            pe.wait_ge(sem("sw_keysT"), NT + 2)

        def sweep_scalar(act):
            for free in ("sw_kT0", "sw_kT1", "sw_features0", "sw_features1", "sw_keysT"):
                act.sem_inc(sem(free), 1)

            def chunk(it, n):
                for o in range(KT):
                    act.wait_ge(sem(f"sw_kT_psum{o}"), it + 1)
                    act.wait_ge(sem(f"sw_features_psum{o}"), it * SUB + 1)
                    act.activation(sw_kT[:, o, 0:n * TILE], ps[:, o, 0:n * TILE], ACT.Identity, bias=V("bk0")[:, o:o + 1])\
                       .then_inc(sem(f"sw_kT{o}"), 1)
                for s in range(n):
                    u = it * SUB + s
                    act.wait_ge(sem("sw_added"), u + 1)
                    for g in range(KT):
                        act.wait_ge(sem(f"sw_features_psum{g}"), u + 2)
                        act.activation(sw_features[s % 2][:, 512 * g:512 * g + 512], ps[0:TILE, 4 + g, :], ACT.Relu)\
                           .then_inc(sem(f"sw_features{g}"), 1)
                    act.wait_ge(sem("sw_keysT_psum"), u + 2)
                    act.copy(keysT[:, :, ds(u * TILE, TILE)], cut(ps[:, 7, 0:KT * TILE], KT, TILE)).then_inc(sem("sw_keysT"), 1)
            with act.Fori(0, NC // 2) as i:
                for ph in range(2):
                    chunk(i * 2 + ph, SUB)
            chunk(NC - 1, subs(NC - 1))
            act.wait_ge(sem("sw_keysT_psum"), NT + 2)
            act.copy(keysT[:, :, NT * TILE:], cut(ps[:, 7, 0:KT * TILE], KT, TILE)).then_inc(sem("sw_keysT"), 1)

        def sweep_vector(dve):
            if runs(0):
                norm_vector(dve, 0)
            for free in ("sw_proj_used", "sw_values_ready", "sw_key_ready"):
                dve.sem_inc(sem(free), 1)
            dve.sem_inc(sem("sw_value_max"), 1)
            dve.wait_ge(sem("sw_zeros"), 4)
            dve.wait_ge(sem("mask_in"), 16)
            key = cut(sw_key, NH, HD)

            def chunk(it, n):
                dve.wait_ge(sem("sw_value_max"), it * 2 + 1)
                for s in range(n):
                    u = it * SUB + s
                    at = [0]

                    def step(ins):
                        at[0] += 1
                        ins.then_inc(sem("sw_step"), 1)
                        dve.wait_ge(sem("sw_step"), u * 5 + at[0])

                    m = mask_sb[:, ds(u, 1)]
                    dve.wait_ge(sem("sw_proj_psum"), u + 1)
                    dve.wait_ge(sem("sw_added"), u + 1)
                    dve.tensor_scalar(sw_values[s % 2][:, :, 0:32], cut(ps[0:TILE, 2, 0:D], PAIRS, 32), m, None, ALU.mult)\
                       .then_inc(sem("sw_part"), 1)
                    dve.tensor_copy(sw_values[s % 2][:, :, 32:33], m.unsqueeze(1).broadcast_to([TILE, PAIRS, 1]))\
                       .then_inc(sem("sw_values_ready"), 1)
                    dve.wait_ge(sem("sw_key_ready"), u + 1)
                    dve.tensor_tensor(sw_key, ps[0:TILE, 2, D:2 * D], R("kv1", TILE)[:, 0:D], ALU.add).then_inc(sem("sw_part"), 1)
                    dve.tensor_tensor(vals[0:TILE, ds(u, 1), :].rearrange("p a d -> p (a d)"), ps[0:TILE, 3, 0:D],
                                      R("kv1", TILE)[:, D:2 * D], ALU.add).then_inc(sem("sw_proj_used"), 1)
                    dve.wait_ge(sem("sw_proj_used"), u + 2)
                    step(dve.tensor_reduce(sw_absmax, key, AX, ALU.max, apply_absolute_value=True))
                    step(dve.tensor_scalar(sw_step, sw_absmax, 1.0 / 127.0, 1e-8, ALU.mult, ALU.max))
                    step(dve.reciprocal(sw_inv, sw_step))
                    step(dve.tensor_tensor(key, key, spread(sw_inv, 2, HD), ALU.mult))
                    step(dve.tensor_scalar(sw_key, sw_key, MAGIC, MAGIC, ALU.add, ALU.subtract))
                    dve.wait_ge(sem("sw_keysT_psum"), u + 1)
                    dve.tensor_tensor(cut(sw_key_out[s % 2], NH, HD), key, spread(sw_step, 2, HD), ALU.mult)\
                       .then_inc(sem("sw_key_ready"), 1)
                dve.tensor_reduce(sw_value_part[:, :], vals[:, ds(it * SUB, n), :].rearrange("p n d -> p d n"), AX, ALU.max,
                                  apply_absolute_value=True).then_inc(sem("sw_value_max"), 1)
                dve.wait_ge(sem("sw_value_max"), it * 2 + 2)
                dve.tensor_tensor(sw_value_absmax, sw_value_absmax, sw_value_part[:, :], ALU.max).then_inc(sem("sw_value_max"), 1)

            with dve.Fori(0, NC // 2) as i:
                for ph in range(2):
                    chunk(i * 2 + ph, SUB)
            chunk(NC - 1, subs(NC - 1))
            dve.wait_ge(sem("sw_key_ready"), NT + 1)
            dve.wait_ge(sem("sw_sums_zeros"), 1)
            dve.wait_ge(sem("sw_added"), NT + 2)
            total = cut(ps[:, 6, 0:33 * PAIRS], PAIRS, 33)
            for e in range(2):
                half = slice(T * e, T * e + T)
                dve.tensor_copy(sweep_sums[half, :, HD * e:HD * e + HD], total[half, :, HD * e:HD * e + HD]).then_inc(sem("sw_sums"), 1)
                dve.tensor_copy(sweep_sums[half, :, 32 + e:33 + e], total[half, :, 32:33]).then_inc(sem("sw_sums"), 1)

        def value_steps(dve):
            dve.wait_ge(sem("value_max"), 1)
            link(dve, "dve", dve.tensor_scalar(value_step[:, :], value_step[:, :], 1.0 / 127.0, 1e-8, ALU.mult, ALU.max))
            link(dve, "dve", dve.reciprocal(value_inv, value_step[0:TILE, :]))

        def quantise(dve, *parts):
            for part in parts:
                a, b = 6 * part, min(6 * part + 6, NT)
                tmp = value_tmp[0:TILE, 0:(b - a) * D]
                link(dve, "dve", dve.tensor_tensor(cut(tmp, b - a, D), vals[0:TILE, a:b, :], spread(value_inv, 1, b - a), ALU.mult))
                link(dve, "dve", dve.tensor_scalar(vals_int[:, a:b, :].rearrange("p n d -> p (n d)"), tmp, MAGIC, MAGIC,
                                                   ALU.add, ALU.subtract))

        def sweep_pool(pool):
            pool.memset(sw_features[1], 0.0).then_inc(sem("sw_zeros"), 1)
            pool.memset(sw_values[1], 0.0).then_inc(sem("sw_zeros"), 1)
            pool.memset(sw_key_out[1], 0.0).then_inc(sem("sw_zeros"), 1)
            pool.memset(sw_value_absmax, 0.0).then_inc(sem("sw_zeros"), 1)
            pool.memset(sweep_sums[:, :, :], 0.0).then_inc(sem("sw_sums_zeros"), 1)
            if runs(0):
                norm_pool(pool, 0)

        SWEEP = (sweep_tensor, sweep_vector, sweep_scalar, sweep_pool)
        SWEEP_LOADS = (sweep_first_load, sweep_loads)

        x0_qT = cut(scratch(0, KT * T), KT, T)
        x0_features = cut(scratch(128, PAIRS * T), PAIRS, T)
        x0_part = scratch(640, D, T).rearrange("p (j e d) -> p j e d", e=2, d=HD)
        x0_den = cut(scratch(896, NH, T), PAIRS, 2)

        def x0_tensor(pe):
            norm_tensor(pe, 0)
            normT_here(pe, 0)
            weights_here(pe, "x0")
            w = W("x0")
            for o in range(KT):
                for k in range(KT):
                    ins = pe.matmul(ps[:, 0, o * T:(o + 1) * T], w[:, 256 * k + 128 * o:256 * k + 128 * o + 128], xnT[:, k, 0, :],
                                    start=k == 0, stop=k == KT - 1)
            ins.then_inc(sem("x0_qT_psum"), 1)
            pe.wait_ge(sem("x0_qT"), 2)
            for j in range(PAIRS):
                ins = pe.matmul(ps[:, 1, j * T:(j + 1) * T], w[:, 512 + 128 * (j % 4):640 + 128 * (j % 4)], x0_qT[:, j // 4, :],
                                start=True, stop=True)
            ins.then_inc(sem("x0_features_psum"), 1)
            pe.wait_ge(sem("x0_features"), 1)
            pe.wait_ge(sem("sw_sums"), 4)
            for j in range(PAIRS):
                ins = pe.matmul(ps[0:T, 2, 34 * j:34 * j + 34], x0_features[:, j, :], sweep_sums[:, j, :], start=True, stop=True)
            ins.then_inc(sem("x0_sums_psum"), 1)
            out_tensor(pe, 0, attended, w[:, 1024:1536], "x0")

        def x0_vector(dve):
            value_steps(dve)
            quantise(dve, 0, 1)
            dve.wait_ge(sem("x0_sums_psum"), 1)
            sums = cut(ps[0:T, 2, 0:34 * PAIRS], PAIRS, 34)
            link(dve, "dve", dve.tensor_copy(x0_den, sums[:, :, 32:34]))
            link(dve, "dve", dve.tensor_tensor(x0_part, R("bv0").rearrange("p (j e d) -> p j e d", e=2, d=HD), spread(x0_den, 3, HD), ALU.mult))
            link(dve, "dve", dve.tensor_tensor(x0_part, x0_part, sums[:, :, 0:32].rearrange("p j (e d) -> p j e d", e=2), ALU.add))
            link(dve, "dve", dve.tensor_scalar(x0_den, x0_den, 1e-8, None, ALU.add))
            link(dve, "dve", dve.reciprocal(x0_den, x0_den))
            dve.tensor_tensor(attended[:, :].rearrange("p (j e d) -> p j e d", e=2, d=HD), x0_part, spread(x0_den, 3, HD), ALU.mult)\
               .then_inc(sem("attended"), 1)
            quantise(dve, 2)
            residual_vector(dve, 0, bank(6, D, T), (sem("projected"), outs.index(0) + 1))

        def x0_scalar(act):
            norm_scalar(act, 0)
            act.wait_ge(sem("x0_qT_psum"), since("x0_qT_psum", 1))
            for o in range(KT):
                act.activation(x0_qT[:, o, :], ps[:, 0, o * T:(o + 1) * T], ACT.Identity, bias=V("bq0")[:, o:o + 1])\
                   .then_inc(sem("x0_qT"), 1)
            act.wait_ge(sem("x0_features_psum"), 1)
            act.activation(x0_features, cut(bank(1), PAIRS, T), ACT.Relu).then_inc(sem("x0_features"), 1)
            out_scalar(act, 0)

        def x0_pool(pool):
            pool.wait_ge(sem("sw_value_max"), 2 * NC + 1)
            pool.partition_all_reduce(value_step[:, :], sw_value_absmax, 128, bass.bass_isa.ReduceOp.max).then_inc(sem("value_max"), 1)
            bias_pool(pool, 0, "bo0")

        STAGES[0] = (x0_tensor, x0_vector, x0_scalar, x0_pool)

        x1_q = back[0:T, 0:D]
        x1_absmax, x1_step, x1_inv = back[0:T, 256:272], back[0:T, 272:288], back[0:T, 288:304]
        x1_row_step = back[:, 304:312]
        x1_queries = back[:, 320:1344]
        x1_tile_q = back[:, 1344:1472]
        x1_max, x1_top, x1_total = back[:, 1480:1480 + NC], back[:, 1494:1495], back[:, 1495:1496]
        x1_tile_step = [back[:, 1472 + p:1473 + p] for p in range(2)]
        x1_bias = [back[:, 1474 + p:1475 + p] for p in range(2)]
        x1_sum = [back[:, 4160 + 16 * p:4160 + 16 * p + NC] for p in range(2)]
        x1_ident = back[:, 1520:1584].bitcast(BF16)
        x1_probs = [back[:, 1600 + 256 * i:1856 + 256 * i].bitcast(BF16) for i in range(2)]
        x1_probsT = [cut(back[0:TILE, 2112 + 256 * i:2368 + 256 * i].bitcast(BF16), SUB, 128) for i in range(2)]
        x1_out = back[:, 2624:2880]
        keys_flat = keysT[:, :, :].rearrange("p k n -> p (k n)")

        def x1_chunk(p, c):
            if c < LAST2:
                return S[:, span(c)]
            a = 2880 + 640 * p + CHUNK * (c - LAST2)
            return back[:, a:a + width(c)]

        LAST2 = NC - 2
        x1_order = [LAST2, LAST2 + 1] + list(range(LAST2))

        def x1_copied(c):
            return sem(f"x1_probsT_ready{c % 2}")

        def x1_copies(j, c):
            return j * len(range(c % 2, NC, 2)) + (c // 2 + 1)

        def x1_copy(eng, copy, j, c, first):
            eng.wait_ge(sem("x1_probsT_psum"), since("x1_probsT_psum", j * NC + (c + 1)))
            if c >= 2 or not first:
                eng.wait_ge(sem("x1_weighed"), since("x1_weighed", j * NC + (c - 1 if c else 0)))
            copy(x1_probsT[c % 2][:, 0:subs(c), :], cut(ps[0:TILE, 2 + c % 2, 0:64 * subs(c)].bitcast(BF16), subs(c), 128))\
                .then_inc(x1_copied(c), 1)

        def x1_tensor(pe):
            norm_tensor(pe, 3)
            normT_here(pe, 3)
            weights_here(pe, "x1")
            w = W("x1")
            for k in range(KT):
                ins = pe.matmul(bank(0, D, T), xnT[:, k, 0, :], w[:, D * k:D * k + D], start=k == 0, stop=k == KT - 1)
            ins.then_inc(sem("x1_q_psum"), 1)
            pe.wait_ge(sem("x1_q_ready"), since("x1_q_ready", 1))
            for k in range(KT):
                ins = pe.transpose(ps[:, 1, k * T:(k + 1) * T], x1_q[:, 128 * k:128 * k + 128], C("ident")[0:T, 0:T])
            ins.then_inc(sem("x1_qT_psum"), 1)
            pe.wait_ge(sem("x1_ident_ready"), 1)

            def scores(j, c):
                k = x1_order.index(c)
                if k == 0:
                    pe.wait_ge(sem("x1_tile_ready"), since("x1_tile_ready", j + 1))
                if k >= 2:
                    pe.wait_ge(sem("x1_scores"), since("x1_scores", j * NC + (k - 1)))
                pe.matmul(ps[:, k % 2, 0:width(c)], x1_tile_q, keys_flat[:, ds((j & 4) * ((TILE + SK) // 4) + (TILE + c * CHUNK), width(c))],
                          start=True, stop=True).then_inc(sem("x1_scores_psum"), 1)

            def turn(j, c, first):
                pe.wait_ge(sem("x1_probs_ready"), j * NC + (c + 1))
                if c >= 2 or not first:
                    pe.wait_ge(x1_copied(c), x1_copies(j, c - 2))
                out = ps[0:TILE, 2 + c % 2, 0:256].bitcast(BF16)
                for s in range(subs(c)):
                    ins = pe.transpose(out[:, 128 * s:128 * s + 128], x1_probs[c % 2][:, TILE * s:TILE * s + TILE], x1_ident)
                ins.then_inc(sem("x1_probsT_psum"), 1)

            def weigh(j, c):
                pe.wait_ge(x1_copied(c), x1_copies(j, c))
                for s in range(subs(c)):
                    ins = pe.matmul(ps[:, 4, 0:32], x1_probsT[c % 2][:, s, :],
                                    vals_int[:, SUB * c + s, ds(j * 32, 32)], start=c == 0 and s == 0,
                                    stop=c == NC - 1 and s == subs(c) - 1)
                ins.then_inc(sem("x1_weighed"), 1)

            def step(j, first=False, scored=True, ahead=True):
                if scored:
                    scores(pe.snap(j + 1, max_val=PAIRS - 1), 0)
                for c in range(NC):
                    turn(j, c, first)
                    if c + 1 < LAST2 and scored:
                        scores(pe.snap(j + 1, max_val=PAIRS - 1), c + 1)
                    elif c >= LAST2 and ahead:
                        scores(pe.snap(j + 2, max_val=PAIRS - 1), c)
                    if c >= 1:
                        if c == 1 and not first:
                            pe.wait_ge(sem("x1_tile_done"), j)
                        weigh(j, c - 1)
                    elif not first:
                        weigh(j - 1, NC - 1)

            for c in x1_order:
                scores(0, c)
            for c in x1_order[:2]:
                scores(1, c)
            step(0, first=True)
            with pe.Fori(0, PAIRS // 2 - 2) as i:
                for p in range(2):
                    step(pe.snap(i * 2 + (1 + p), max_val=PAIRS - 4))
            step(PAIRS - 3)
            step(PAIRS - 2, ahead=False)
            step(PAIRS - 1, scored=False, ahead=False)
            weigh(PAIRS - 1, NC - 1)
            out_tensor(pe, 3, attended, w[:, 512:1024], "x1")

        def x1_vector(dve):
            norm_vector(dve, 3)
            q = cut(x1_q, NH, HD)
            dve.wait_ge(sem("x1_q_psum"), since("x1_q_psum", 1))
            link(dve, "dve", dve.tensor_tensor(x1_q, bank(0, D, T), R("q1"), ALU.add))
            link(dve, "dve", dve.tensor_scalar(x1_q, x1_q, 0.25, None, ALU.mult))
            link(dve, "dve", dve.tensor_reduce(x1_absmax, q, AX, ALU.max, apply_absolute_value=True))
            link(dve, "dve", dve.tensor_scalar(x1_step, x1_absmax, 1.0 / 127.0, 1e-8, ALU.mult, ALU.max))
            link(dve, "dve", dve.reciprocal(x1_inv, x1_step))
            link(dve, "dve", dve.tensor_tensor(q, q, spread(x1_inv, 2, HD), ALU.mult))
            dve.tensor_scalar(x1_q, x1_q, MAGIC, MAGIC, ALU.add, ALU.subtract).then_inc(sem("x1_q_ready"), 1)
            by_pair = cut(x1_step, PAIRS, 2)
            for e in range(2):
                link(dve, "dve", dve.tensor_copy(x1_row_step[T * e:T * e + T, :], by_pair[:, :, e]))
            dve.wait_ge(sem("x1_qT_psum"), 1)
            link(dve, "dve", dve.tensor_tensor(x1_queries.rearrange("p (k h t) -> p k h t", k=KT, h=8),
                                               spread(cut(bank(1, KT * T), KT, T), 2, 8),
                                               spread(spread(C("heads16"), 1, KT), 3, T), ALU.mult))

            def tile(j):
                dve.tensor_copy(x1_tile_q, x1_queries[:, ds(j * 128, 128)]).then_inc(sem("x1_tile_ready"), 1)

            def score(j, p, c, weighed):
                k = x1_order.index(c)
                dve.wait_ge(sem("x1_scores_psum"), since("x1_scores_psum", j * NC + (k + 1)))
                if weighed is not None and c < LAST2:
                    dve.wait_ge(sem("x1_probs_ready"), weighed * NC + (c + 1))
                dve.tensor_scalar(x1_chunk(p, c), ps[:, k % 2, 0:width(c)], 1.0, NEG, ALU.mult, ALU.max,
                                  accum_out=x1_max[:, c:c + 1]).then_inc(sem("x1_scores"), 1)

            def exp_bias(j, p):
                dve.tensor_copy(x1_tile_step[p], x1_row_step[:, ds(j, 1)]).then_inc(sem("x1_step"), 1)
                dve.wait_ge(sem("x1_scores"), since("x1_scores", j * NC + NC))
                dve.tensor_reduce(x1_top, x1_max, AX, ALU.max).then_inc(sem("x1_step"), 1)
                dve.wait_ge(sem("x1_step"), j * 3 + 2)
                dve.tensor_tensor(x1_bias[p], x1_top, x1_tile_step[p], ALU.mult).then_inc(sem("x1_step"), 1)
                dve.wait_ge(sem("x1_step"), j * 3 + 3)
                dve.tensor_scalar(x1_bias[p], x1_bias[p], -1.0, LN255, ALU.mult, ALU.add).then_inc(sem("x1_bias_ready"), 1)

            def round_probs(j, p, c, first):
                dve.wait_ge(sem("x1_exp"), since("x1_exp", j * NC + (c + 1)))
                if c >= 2 or (c == 0 and not first):
                    dve.wait_ge(sem("x1_probsT_psum"), since("x1_probsT_psum", j * NC + max(c - 1, 0)))
                dve.tensor_scalar(x1_probs[c % 2][:, 0:width(c)], x1_chunk(p, c), MAGIC, MAGIC, ALU.add, ALU.subtract)\
                   .then_inc(sem("x1_probs_ready"), 1)

            def inverse_sum(j, p):
                dve.tensor_reduce(x1_total, x1_sum[p], AX, ALU.add).then_inc(sem("x1_total"), 1)
                dve.wait_ge(sem("x1_total"), j * 2 + 1)
                dve.reciprocal(x1_total, x1_total).then_inc(sem("x1_total"), 1)

            def finish(j):
                dve.wait_ge(sem("x1_total"), j * 2 + 2)
                dve.wait_ge(sem("x1_weighed"), since("x1_weighed", j * NC + NC))
                dve.tensor_scalar(x1_out[:, ds(j * 32, 32)], ps[:, 4, 0:32], x1_total, None, ALU.mult).then_inc(sem("x1_tile_done"), 1)

            def step(j, p, first=False, scored=True, ahead=True):
                for c in range(NC):
                    round_probs(j, p, c, first)
                    if c % 2 == 0 and c >= 2:
                        x1_copy(dve, dve.tensor_copy, j, c - 1, first)
                    if c == 1 and not first:
                        finish(j - 1)
                    if scored and c < LAST2:
                        score(j + 1, 1 - p, c, j)
                    if scored and c == LAST2 - 1:
                        if ahead:
                            tile(j + 2)
                        exp_bias(j + 1, 1 - p)
                inverse_sum(j, p)
                if ahead:
                    for c in x1_order[:2]:
                        score(j + 2, p, c, None)

            tile(0)
            for c in x1_order:
                score(0, 0, c, None)
            tile(1)
            exp_bias(0, 0)
            for c in x1_order[:2]:
                score(1, 1, c, None)
            step(0, 0, first=True)
            with dve.Fori(0, PAIRS // 2 - 2) as i:
                for p in range(2):
                    step(dve.snap(i * 2 + (1 + p), max_val=PAIRS - 4), 1 - p)
            step(PAIRS - 3, 1)
            step(PAIRS - 2, 0, ahead=False)
            step(PAIRS - 1, 1, scored=False, ahead=False)
            finish(PAIRS - 1)
            dve.wait_ge(sem("x1_tile_done"), PAIRS)
            out, step = cut(attended[:, :], PAIRS, 32), cut(value_step[:, :], PAIRS, 32)
            by_tile = cut(x1_out, PAIRS, 32)
            for e in range(2):
                rows_, cols_ = slice(T * e, T * e + T), slice(HD * e, HD * e + HD)
                ins = dve.tensor_tensor(out[:, :, cols_], by_tile[rows_, :, cols_], step[rows_, :, cols_], ALU.mult)
            ins.then_inc(sem("attended"), 1)
            residual_vector(dve, 3, bank(6, D, T), (sem("projected"), outs.index(3) + 1))

        def x1_scalar(act):
            norm_scalar(act, 3)
            act.wait_ge(sem("x1_q_psum"), since("x1_q_psum", 1))
            act.copy(x1_ident, C("ident")).then_inc(sem("x1_ident_ready"), 1)

            def exp(j, p, c):
                if c == 0:
                    act.wait_ge(sem("x1_bias_ready"), since("x1_bias_ready", j + 1))
                chunk = x1_chunk(p, c)
                act.activation(chunk, chunk, ACT.Exp, scale=x1_tile_step[p], bias=x1_bias[p], accum_out=x1_sum[p][:, c:c + 1])\
                   .then_inc(sem("x1_exp"), 1)

            def step(j, p, first=False):
                for c in range(NC):
                    exp(j, p, c)
                    if c >= 2 and c % 2 == 0:
                        x1_copy(act, act.copy, j, c - 2, first)
                    if c == 0 and not first:
                        x1_copy(act, act.copy, j - 1, NC - 1, False)

            step(0, 0, first=True)
            with act.Fori(0, PAIRS // 2 - 1) as i:
                for p in range(2):
                    step(act.snap(i * 2 + (1 + p), max_val=PAIRS - 2), 1 - p)
            step(PAIRS - 1, 1)
            x1_copy(act, act.copy, PAIRS - 1, NC - 1, False)
            out_scalar(act, 3)

        def x1_pool(pool):
            norm_pool(pool, 3)
            bias_pool(pool, 3, "out1")

        STAGES[3] = (x1_tensor, x1_vector, x1_scalar, x1_pool)

        x2_cat = cut(row_biases[:, 0:2 * NQ * T], 2 * NQ, T)
        x2_queries = row_biases[:, 2048:3072]
        x2_wk = cut(row_biases[:, 3072:3328], KT, GD)
        x2_wv = cut(row_biases[:, 3328:3584], KT, GD)
        x2_dev = wide
        x2_probsT = sb("x2_probsT", [TILE, 2, 512])
        x2_mix = sweep_sums[:, :, :].rearrange("p j d -> p (j d)")[:, 0:D]
        x2_mixT = cut(value_step[:, :], KT, 128)
        x2_q = sb("x2_q", [128, 128])
        x2_const, x2_tile_const = sb("x2_const", [128, GROUPS]), sb("x2_tile_const", [128, 1])
        x2_max, x2_sum, x2_small = sb("x2_max", [128, NC + 1]), sb("x2_sum", [128, NC + 1]), sb("x2_small", [128, 4])
        x2_eps = sb("x2_eps", [128, 1])
        SCALE2 = float(1 / np.sqrt(GD))
        x2_lnT = cut(scratch(5120, KT * T), KT, T)
        x2_in = scratch(5248, 512).rearrange("p (w k t) -> p w k t", w=4, k=KT)
        x2_inv_scale = scratch(5760, 8)
        x2_raw = scratch(0, 2560)
        x2_square = scratch(2560, 2560)
        x2_v = scratch(2560, 1024, T)
        x2_s, x2_stat = cut(scratch(3584, 512), GROUPS, T), scratch(5776, 16)
        x2_coreT = scratch(4096, 1024, T)
        x2_sq_cols = ((0, 1024, 0), (1024, 1536, 1), (1536, 2560, 2))
        x2_mean_w = scratch(5800, 16)
        x2_std = scratch(5816, 256, 10)
        x2_low = [sw_key_both[:, i, :].bitcast(BF16) for i in range(2)]
        x2_dev_flat = x2_dev[:, :, :].rearrange("p a n -> p (a n)")
        x2_inv_smooth = x2_dev_flat[:, 1024:1024 + 2 * NQ]
        x2_narrow, x2_power = x2_keys[:, 0, :].bitcast(BF16), x2_keys[:, 1, :].bitcast(BF16)
        x2_rounded = (0, NQ, 2 * NQ - 2)
        x2_mean = sw_value_part[:, 0:64].bitcast(BF16)

        def high_half(c):
            return x2_dev[:, c % 3, 0:width(c)].bitcast(BF16).rearrange("p (n h) -> p n h", h=2)[:, :, 1]

        FOLD = 3
        x2_upper = sw_key_both[0:64, :, :].rearrange("p a n -> p (a n)")

        def x2_folded(g, c):
            return c >= FOLD and not (isinstance(g, int) and g == 0)

        ctxT = keysT[:, :, TILE:]
        ctxN = vals[0:TILE, :, :]

        def x2_tensor(pe):
            norm_tensor(pe, 6.5, xr)
            pe.wait_ge(sem("x2_in_ready"), since("x2_in_ready", 1))

            blocks = [(name, which, b) for name, which in (("x2_q0", 0), ("x2_q1", 0), ("x2_k", 1), ("x2_qx0", 2), ("x2_qx1", 2))
                      for b in range(2)]

            def turn_block(j):
                pe.wait_ge(sem("x2_block"), j + 1)
                for h in range(4):
                    ins = pe.transpose(psf[:, 256 * j + T * h:256 * j + T * h + T], wide[0:T, j % 3, 128 * h:128 * h + 128], C("ident")[0:T, 0:T])
                    if h == 0 and j % 2:
                        ins.then_inc(weights_used, 1)
                ins.then_inc(sem("x2_block_turned"), 1)

            for j, (name, which, b) in enumerate(blocks):
                weights_here(pe, name)
                if which == 1 and b == 0:
                    pe.wait_ge(sem("x2_in_ready"), since("x2_in_ready", 2))
                if j >= 2:
                    pe.wait_ge(sem("x2_block"), j - 1)
                for k in range(KT):
                    ins = pe.matmul(ps[0:T, 5 + j % 2, :], x2_in[:, which, k, :], W(name)[:, 1024 * k + 512 * b:1024 * k + 512 * b + 512],
                                    start=k == 0, stop=k == KT - 1)
                ins.then_inc(sem("x2_block_psum"), 1)
                if j >= 1:
                    turn_block(j - 1)
            turn_block(len(blocks) - 1)
            weights_here(pe, "x2_v")
            for c in range(2):
                for k in range(KT):
                    ins = pe.matmul(ps[0:T, 5 + c, :], x2_in[:, 3, k, :], W("x2_v")[:, 1024 * k + 512 * c:1024 * k + 512 * c + 512],
                                    start=k == 0, stop=k == KT - 1)
            ins.then_inc(sem("x2_heads_psum"), 1)
            for c, copied in enumerate((1, 1, 2, 3, 3)):
                pe.wait_ge(sem("x2_raw"), since("x2_raw", copied))
                pe.matmul(bank(c), C("centre128"), x2_raw[:, 512 * c:512 * c + 512], start=True, stop=True).then_inc(sem("x2_centre_psum"), 1)
            pe.wait_ge(sem("x2_heads_psum"), since("x2_heads_psum", 1))
            pe.sem_inc(weights_used, 1)
            for c in range(10):
                pe.wait_ge(sem("x2_square"), since("x2_square", c // 2 + 1))
                ins = pe.matmul(ps[0:10, 7, 0:256], C("mean_band")[:, 9 - c:19 - c], x2_square[:, 256 * c:256 * c + 256], start=c == 0, stop=c == 9)
            ins.then_inc(sem("x2_var_psum"), 1)
            pe.wait_ge(sem("x2_centred"), 5)
            pe.wait_ge(sem("x2_inv_std"), 1)
            for c in range(10):
                ins = pe.matmul(psf[:, 256 * c:256 * c + 256], C("ident")[0:10, c:c + 1].broadcast_to([10, 128]), x2_std, start=True, stop=True)
                if c in (5, 9):
                    ins.then_inc(sem("x2_inv_psum"), 1)
            def keys(g, c):
                if c == 0:
                    pe.wait_ge(sem("x2_wk_ready"), g + 1)
                    if not (isinstance(g, int) and g == 0):
                        pe.wait_ge(sem("x2_keys_ready"), g * NC)
                if c >= 3:
                    pe.wait_ge(sem("x2_keys_ready"), g * NC + (c - 2))
                for k in range(KT):
                    ins = pe.matmul(ps[:, c % 3, 0:width(c)], x2_wk[:, k, :], ctxT[:, k, span(c)],
                                    start=k == 0, stop=k == KT - 1)
                ins.then_inc(sem("x2_keys_psum"), 1)

            def variance(g, c):
                pe.wait_ge(sem("x2_square_low"), g * NC + (c + 1))
                if c >= 1:
                    pe.wait_ge(sem("x2_refined"), (g * NC + c) * 2 - 1)
                folded = x2_folded(g, c)
                ins = pe.matmul(ps[:, 3, 0:width(c)], x2_mean, high_half(c), start=True, stop=folded)
                if not folded:
                    ins = pe.matmul(ps[:, 3, 0:width(c)], x2_mean, x2_low[c % 2][:, 0:width(c)], start=False, stop=True)
                ins.then_inc(sem("x2_keys_var"), 1)

            def scores(g, c):
                pe.wait_ge(sem("x2_keys_ready"), g * NC + (c + 1))
                if c == 0:
                    pe.wait_ge(sem("x2_tile_ready"), since("x2_tile_ready", g + 1))
                else:
                    pe.wait_ge(sem("x2_scores"), since("x2_scores", g * NC + c))
                pe.matmul(ps[:, 4, 0:width(c)], x2_q[:, :], x2_keys[:, c % 2, 0:width(c)], start=True, stop=True).then_inc(sem("x2_scores_psum"), 1)

            def turn(g, c):
                pe.wait_ge(sem("x2_exp"), since("x2_exp", g * NC + (c + 1)))
                if c >= 2:
                    pe.wait_ge(sem("x2_probsT_ready"), since("x2_probsT_ready", g * NC + (c - 1)))
                for s in range(subs(c)):
                    a = CHUNK * c + TILE * s
                    ins = pe.transpose(ps[0:TILE, 5 + 2 * (c % 2), 128 * s:128 * s + 128], S[:, a:a + TILE], C("ident"))
                ins.then_inc(sem("x2_probsT_psum"), 1)

            def weigh(g, c):
                pe.wait_ge(sem("x2_probsT_ready"), since("x2_probsT_ready", g * NC + (c + 1)))
                for s in range(subs(c)):
                    ins = pe.matmul(bank(6, D), x2_probsT[:, c % 2, 128 * s:128 * s + 128], ctxN[:, SUB * c + s, :],
                                    start=c == 0 and s == 0, stop=c == NC - 1 and s == subs(c) - 1)
                ins.then_inc(sem("x2_weighed"), 1)

            def turn_mix(g):
                pe.wait_ge(sem("x2_mix"), g + 1)
                for k in range(KT):
                    ins = pe.transpose(ps[:, 6, D + 128 * k:D + 128 * k + 128], x2_mix[:, 128 * k:128 * k + 128], C("ident"))
                ins.then_inc(sem("x2_mixT_psum"), 1)

            def values(g):
                pe.wait_ge(sem("x2_mixT"), g + 1)
                pe.wait_ge(sem("x2_wv_ready"), g + 1)
                for k in range(KT):
                    ins = pe.matmul(ps[:, 6, D:D + 128], x2_wv[:, k, :], x2_mixT[:, k, :], start=k == 0, stop=k == KT - 1)
                ins.then_inc(sem("x2_cross_psum"), 1)

            def project(a, b):
                for n in range(a, b):
                    name = f"x2_proj{n // 8}"
                    if n % 8 == 0:
                        weights_here(pe, name)
                    if n in x2_rounded:
                        pe.wait_ge(sem("x2_cat_ready"), since("x2_cat_ready", x2_rounded.index(n) + 1))
                    ins = pe.matmul(bank(0, D, T), x2_cat[:, n, :], W(name)[:, D * (n % 8):D * (n % 8) + D], start=n == 0, stop=n == 2 * NQ - 1)
                    if n % 8 == 7 and n < 2 * NQ - 1:
                        ins.then_inc(weights_used, 1)
                return ins

            def change(weighed, ahead):
                last = ahead is None and weighed == GROUPS - 1
                if ahead is not None:
                    keys(ahead, 0)
                if weighed is not None:
                    if last:
                        project(0, 2)
                    turn_mix(weighed)
                if ahead is not None:
                    keys(ahead, 1)
                if last:
                    project(2, 4)
                if weighed is not None:
                    values(weighed)
                if ahead is not None:
                    variance(ahead, 0)

            def step(scored, weighed, ahead):
                for c in range(NC + 1):
                    if scored is not None and c + 2 < NC:
                        keys(scored, c + 2)
                    if weighed is not None:
                        if c == 0:
                            turn(weighed, 0)
                            turn(weighed, 1)
                        elif 2 <= c < NC:
                            turn(weighed, c)
                    if scored is not None and c + 1 < NC:
                        variance(scored, c + 1)
                    if scored is not None and c >= 1:
                        scores(scored, c - 1)
                    if weighed is not None:
                        if c == 0:
                            if not (isinstance(weighed, int) and weighed == 0):
                                pe.wait_ge(sem("x2_cross_done"), weighed)
                            weigh(weighed, 0)
                        elif c >= 2:
                            weigh(weighed, c - 1)
                change(weighed, ahead)

            pe.wait_ge(sem("x2_normed"), 1)
            for g in range(GROUPS):
                ins = pe.matmul(ps[:, 7, T * g:T * g + T], x2_raw[:, 128 * g:128 * g + 128], x2_raw[:, 1024 + T * g:1024 + T * g + T],
                                start=True, stop=True)
            ins.then_inc(sem("x2_core_psum"), 1)
            pe.wait_ge(sem("x2_normed"), 2)
            pe.wait_ge(sem("ctxT_in"), 16)
            keys(0, 0)
            keys(0, 1)
            for g in range(GROUPS):
                ins = pe.matmul(ps[:, 4, g:g + 1], x2_raw[:, 1536 + 128 * g:1536 + 128 * g + 128], V("head_ln")[:, 7:8], start=True, stop=True)
            ins.then_inc(sem("x2_const_psum"), 1)
            pe.wait_ge(sem("x2_core_probs"), 1)
            for g in range(GROUPS):
                ins = pe.transpose(psf[0:T, 2560 + 128 * g:2560 + 128 * g + 128], x2_s[:, g, :], C("ident"))
            ins.then_inc(sem("x2_coreT_psum"), 1)
            pe.wait_ge(sem("x2_mean_ready"), 1)
            variance(0, 0)
            pe.wait_ge(sem("x2_coreT"), since("x2_coreT", 1))
            for g in range(GROUPS):
                ins = pe.matmul(psf[:, 2560 + 128 * g:2560 + 128 * g + 128], x2_v[:, GD * g:GD * g + GD], x2_coreT[:, 128 * g:128 * g + 128],
                                start=True, stop=True)
            ins.then_inc(sem("x2_core_out_psum"), 1)
            step(0, None, 1)
            pe.wait_ge(sem("ctxN_in"), 16)
            step(1, 0, 2)
            with pe.Fori(1, GROUPS - 2) as g:
                step(g + 1, g, g + 2)
            step(GROUPS - 1, GROUPS - 2, None)
            step(None, GROUPS - 1, None)
            project(4, 2 * NQ).then_inc(sem("x2_out_psum"), 1)
            pe.wait_ge(sem("x2_out_psum"), since("x2_out_psum", 1))
            pe.sem_inc(weights_used, 1)

        def x2_vector(dve):
            norm_vector(dve, 6)
            norm_vector(dve, 6.5, xn, xr)
            link(dve, "dve", dve.memset(x2_eps[:, :], LN_EPS))
            link(dve, "dve", dve.reciprocal(x2_inv_scale, V("in_scale")))
            normT_here(dve, 6.5)
            by_use = lambda v: cut(v, 4, KT)
            for a, b in ((0, 1), (1, 4)):
                n = (b - a) * KT * T
                scaled, narrow, power = scratch(0, n), scratch(512, n // 2).bitcast(BF16), scratch(768, n // 2).bitcast(BF16)
                link(dve, "dve", dve.tensor_tensor(scaled.rearrange("p (w k t) -> p w k t", w=b - a, k=KT), spread(x2_lnT, 1, b - a),
                                                   spread(by_use(x2_inv_scale)[:, a:b, :], 3, T), ALU.mult))
                link(dve, "dve", round_vector(dve, scaled, narrow, power, scratch(5248 + KT * T * a, n)))
                ins = dve.tensor_tensor(x2_in[:, a:b], x2_in[:, a:b], spread(by_use(V("in_scale"))[:, a:b, :], 3, T), ALU.mult)
                ins.then_inc(sem("x2_in_ready"), 1)
            for c in range(5):
                dve.wait_ge(sem("x2_centre_psum"), since("x2_centre_psum", c + 1))
                dve.tensor_copy(x2_raw[:, 512 * c:512 * c + 512], bank(c)).then_inc(sem("x2_centred"), 1)
            weights_here(dve, "x2_kx")
            wk = cut(W("x2_kx"), KT * GROUPS, GD)
            link(dve, "dve", dve.tensor_reduce(x2_mean_w, wk, AX, ALU.add))
            link(dve, "dve", dve.tensor_scalar(x2_mean_w, x2_mean_w, 1.0 / GD, None, ALU.mult))
            dve.wait_ge(sem("x2_std"), since("x2_std", 1))
            dve.reciprocal(x2_std, x2_std).then_inc(sem("x2_inv_std"), 1)
            link(dve, "dve", dve.tensor_tensor(wk, wk, spread(x2_mean_w, 2, GD), ALU.subtract))

            def normed(a, b, i):
                return dve.tensor_scalar(x2_raw[:, a:b], x2_raw[:, a:b], V("head_ln")[:, 2 * i:2 * i + 1], V("head_ln")[:, 2 * i + 1:2 * i + 2],
                                         ALU.mult, ALU.add)

            for n, parts in enumerate((x2_sq_cols[0:2], x2_sq_cols[2:3])):
                a, b = parts[0][0], parts[-1][1]
                dve.wait_ge(sem("x2_inv_psum"), since("x2_inv_psum", n + 1))
                link(dve, "dve", dve.tensor_tensor(x2_raw[:, a:b], x2_raw[:, a:b], psf[:, a:b], ALU.mult))
                for part in parts:
                    ins = normed(*part)
                ins.then_inc(sem("x2_normed"), 1)
            dve.wait_ge(sem("x2_normed"), 2)
            link(dve, "dve", dve.tensor_scalar(x2_queries, x2_raw[:, 1536:2560], V("head_ln")[:, 6:7], -0.5, ALU.mult, ALU.mult))
            wks, wvs = cut(W("x2_kx"), KT, 1024), cut(W("x2_vx"), KT, 1024)

            def key_weights(g):
                dve.tensor_copy(x2_wk, wks[:, :, ds(g * GD, GD)]).then_inc(sem("x2_wk_ready"), 1)

            def tile(g):
                dve.tensor_copy(x2_tile_const[:, :], x2_const[:, ds(g, 1)]).then_inc(sem("x2_tile_const_ready"), 1)
                dve.tensor_copy(x2_q[:, :], x2_queries[:, ds(g * 128, 128)]).then_inc(sem("x2_tile_ready"), 1)

            def low_half(g, c):
                dve.wait_ge(sem("x2_squared"), g * NC + (c + 1))
                if x2_folded(g, c):
                    sums = x2_dev[0:64, c % 3, 0:width(c)]
                    dve.tensor_tensor(sums, sums, x2_upper[:, 0:width(c)], ALU.add).then_inc(sem("x2_square_sum"), 1)
                    dve.wait_ge(sem("x2_square_sum"), g * (NC - FOLD) + (c + 1 - NC))
                    dve.tensor_tensor(high_half(c)[64:128], sums, high_half(c)[0:64], ALU.subtract).then_inc(sem("x2_square_low"), 1)
                    return
                if c >= 2:
                    dve.wait_ge(sem("x2_keys_var"), g * NC + (c - 1))
                dve.tensor_tensor(x2_low[c % 2][:, 0:width(c)], x2_dev[:, c % 3, 0:width(c)], high_half(c), ALU.subtract)\
                   .then_inc(sem("x2_square_low"), 1)

            def normalise(g, c):
                y, out = x2_dev[:, c % 3, 0:width(c)], x2_keys[:, c % 2, 0:width(c)]
                at = (g * NC + c) * 2

                def refined(n, ins):
                    ins.then_inc(sem("x2_refined"), 1)
                    dve.wait_ge(sem("x2_refined"), at + n)

                dve.wait_ge(sem("x2_inverse"), g * NC + (c + 1))
                refined(1, dve.scalar_tensor_tensor(out, ps[:, 3, 0:width(c)], LN_EPS, out, ALU.add, ALU.mult))
                refined(2, dve.scalar_tensor_tensor(out, out, -3.0, y, ALU.add, ALU.mult))
                dve.tensor_tensor(out, ps[:, c % 3, 0:width(c)], out, ALU.mult).then_inc(sem("x2_keys_ready"), 1)

            def score(g, c, weighed):
                dve.wait_ge(sem("x2_scores_psum"), since("x2_scores_psum", g * NC + (c + 1)))
                if c == 0:
                    dve.wait_ge(sem("x2_tile_ready"), since("x2_tile_ready", g + 1))
                if weighed is not None:
                    dve.wait_ge(sem("x2_probsT_psum"), since("x2_probsT_psum", weighed * NC + (c + 1)))
                dve.tensor_scalar(S[:, span(c)], ps[:, 4, 0:width(c)], x2_tile_const[:, 0:1], NEG, ALU.add, ALU.max,
                                  accum_out=x2_max[:, c:c + 1]).then_inc(sem("x2_scores"), 1)

            def exp_bias(g):
                dve.wait_ge(sem("x2_scores"), since("x2_scores", g * NC + NC))
                dve.tensor_reduce(x2_small[:, 0:1], x2_max[:, 0:NC], AX, ALU.max).then_inc(sem("x2_max"), 1)
                dve.wait_ge(sem("x2_max"), g + 1)
                dve.tensor_scalar(x2_small[:, 1:2], x2_small[:, 0:1], -SCALE2, None, ALU.mult).then_inc(sem("x2_bias_ready"), 1)

            def inverse_sum(g):
                dve.wait_ge(sem("x2_exp"), since("x2_exp", g * NC + NC))
                dve.tensor_reduce(x2_small[:, 2:3], x2_sum[:, 0:NC], AX, ALU.add).then_inc(sem("x2_sum"), 1)
                dve.wait_ge(sem("x2_sum"), g * 2 + 1)
                dve.reciprocal(x2_small[:, 3:4], x2_small[:, 2:3]).then_inc(sem("x2_sum"), 1)

            def mix(g):
                dve.wait_ge(sem("x2_sum"), g * 2 + 2)
                dve.wait_ge(sem("x2_weighed"), since("x2_weighed", g * NC + NC))
                dve.tensor_scalar(x2_mix, bank(6, D), x2_small[:, 3:4], None, ALU.mult).then_inc(sem("x2_mix"), 1)

            def value_weights(g):
                if not (isinstance(g, int) and g == 0):
                    dve.wait_ge(sem("x2_cross_done"), g)
                dve.tensor_copy(x2_wv, wvs[:, :, ds(g * GD, GD)]).then_inc(sem("x2_wv_ready"), 1)

            def step(scored, weighed, ahead):
                if scored is not None:
                    tile(scored)
                for c in range(NC + 1):
                    if scored is not None:
                        if c + 2 < NC:
                            low_half(scored, c + 2)
                        if c >= 1:
                            score(scored, c - 1, weighed)
                        if c == NC:
                            exp_bias(scored)
                        if c + 1 < NC:
                            normalise(scored, c + 1)
                    if c == 1 and weighed is not None and scored is not None:
                        value_weights(weighed)
                    if c == NC - 1:
                        if ahead is not None:
                            key_weights(ahead)
                        if weighed is not None:
                            inverse_sum(weighed)
                if weighed is not None:
                    mix(weighed)
                if ahead is not None:
                    lead(ahead)

            def lead(g):
                low_half(g, 0)
                low_half(g, 1)
                normalise(g, 0)

            key_weights(0)
            dve.wait_ge(sem("x2_core_psum"), since("x2_core_psum", 1))
            raw = cut(bank(7), GROUPS, T)
            link(dve, "dve", dve.tensor_reduce(x2_stat[:, 0:8], raw, AX, ALU.max))
            dve.tensor_tensor(x2_s, raw, spread(x2_stat[:, 0:8], 2, T), ALU.subtract).then_inc(sem("x2_core_shifted"), 1)
            dve.wait_ge(sem("x2_core_exp"), since("x2_core_exp", 1))
            link(dve, "dve", dve.tensor_reduce(x2_stat[:, 8:16], x2_s, AX, ALU.add))
            link(dve, "dve", dve.reciprocal(x2_stat[:, 8:16], x2_stat[:, 8:16]))
            dve.tensor_tensor(x2_s, x2_s, spread(x2_stat[:, 8:16], 2, T), ALU.mult).then_inc(sem("x2_core_probs"), 1)
            dve.wait_ge(sem("x2_const_psum"), since("x2_const_psum", 1))
            link(dve, "dve", dve.tensor_copy(x2_const[:, :], ps[:, 4, 0:GROUPS]))
            lead(0)
            weights_here(dve, "x2_vx")
            dve.wait_ge(sem("x2_core_done"), since("x2_core_done", 1))
            step(0, None, 1)
            step(1, 0, 2)
            with dve.Fori(1, GROUPS - 2) as g:
                g = dve.snap(g, max_val=GROUPS - 3)
                step(g + 1, g, g + 2)
            step(GROUPS - 1, GROUPS - 2, None)
            value_weights(GROUPS - 1)
            dve.wait_ge(sem("x2_wv_ready"), GROUPS)
            dve.sem_inc(weights_used, 2)
            link(dve, "dve", dve.reciprocal(x2_inv_smooth, V("smooth")))
            link(dve, "dve", dve.tensor_tensor(x2_small[0:T, 0:1], V("scales")[0:T, 4:5], V("scales")[0:T, 5:6], ALU.mult))

            def round_heads(a, b):
                n = (b - a) * T
                smoothed = x2_dev_flat[:, 0:n]
                link(dve, "dve", dve.tensor_tensor(cut(smoothed, b - a, T), x2_cat[:, a:b, :], spread(x2_inv_smooth[:, a:b], 2, T), ALU.mult))
                round_vector(dve, smoothed, x2_narrow[:, 0:n], x2_power[:, 0:n], row_biases[:, T * a:T * b]).then_inc(sem("x2_cat_ready"), 1)

            round_heads(0, NQ)
            dve.wait_ge(sem("x2_cat_ready"), since("x2_cat_ready", 1))
            round_heads(NQ, 2 * NQ - 2)
            dve.wait_ge(sem("x2_cat_ready"), since("x2_cat_ready", 2))
            step(None, GROUPS - 1, None)
            dve.wait_ge(sem("x2_cross_done"), GROUPS)
            round_heads(2 * NQ - 2, 2 * NQ)
            dve.wait_ge(sem("x2_out_psum"), since("x2_out_psum", 1))
            link(dve, "dve", dve.scalar_tensor_tensor(x[:, :], bank(0, D, T), x2_small[0:T, 0:1], x[:, :], ALU.mult, ALU.add))

        def round_vector(dve, wide, narrow, power, out):
            u16 = mybir.dt.uint16
            link(dve, "dve", dve.tensor_scalar(narrow, wide, 448.0, -448.0, ALU.min, ALU.max))
            link(dve, "dve", dve.tensor_scalar(power.bitcast(u16), narrow.bitcast(u16), 0x7F80, None, ALU.bitwise_and))
            link(dve, "dve", dve.tensor_scalar(wide, power, 2.0 ** -6, 1.5 * 2.0 ** 20, ALU.max, ALU.mult))
            link(dve, "dve", dve.tensor_tensor(out, narrow, wide, ALU.add))
            return dve.tensor_tensor(out, out, wide, ALU.subtract)

        def x2_scalar(act):
            act.wait_ge(sem("normT_psum"), transposed_no[6.5] + 1)
            src = cut(bank(7, KT * T), KT, T)
            for k in range(KT):
                ins = act.activation(x2_lnT[:, k, :], src[:, k, :], ACT.Identity, scale=V("ln_w")[:, k:k + 1], bias=V("ln_b")[:, k:k + 1])
            ins.then_inc(sem("normT_ready"), 1)
            for j in range(10):
                act.wait_ge(sem("x2_block_psum"), j + 1)
                if j >= 3:
                    act.wait_ge(sem("x2_block_turned"), j - 2)
                act.copy(wide[0:T, j % 3, :], ps[0:T, 5 + j % 2, :]).then_inc(sem("x2_block"), 1)
            for (a, b, i), turned in zip(x2_sq_cols, (4, 6, 10)):
                act.wait_ge(sem("x2_block_turned"), turned)
                act.activation(x2_raw[:, a:b], psf[:, a:b], ACT.Copy, scale=V("scales")[:, i:i + 1]).then_inc(sem("x2_raw"), 1)
            for c in range(5):
                act.wait_ge(sem("x2_centred"), c + 1)
                act.activation(x2_square[:, 512 * c:512 * c + 512], x2_raw[:, 512 * c:512 * c + 512], ACT.Square).then_inc(sem("x2_square"), 1)
            act.preload_act_table_set("sqrt_and_others")
            act.wait_ge(sem("x2_var_psum"), since("x2_var_psum", 1))
            act.activation(x2_std, ps[0:10, 7, 0:256], ACT.Sqrt, bias=x2_eps[0:10, 0:1]).then_inc(sem("x2_std"), 1)
            act.preload_act_table_set("natural_log_exp_and_others")
            act.wait_ge(sem("x2_heads_psum"), since("x2_heads_psum", 1))
            act.wait_ge(sem("x2_normed"), 1)
            act.activation(x2_v, psf[0:T, 2560:3584], ACT.Copy, scale=V("scales")[0:T, 3:4]).then_inc(sem("x2_v_ready"), 1)
            act.wait_ge(sem("x2_core_shifted"), 1)
            act.activation(x2_s, x2_s, ACT.Exp, scale=SCALE2).then_inc(sem("x2_core_exp"), 1)
            def square(g, c):
                act.wait_ge(sem("x2_keys_psum"), g * NC + (c + 1))
                if c >= 3:
                    act.wait_ge(sem("x2_keys_ready"), g * NC + (c - 2))
                if x2_folded(g, c):
                    act.activation(x2_dev[0:64, c % 3, 0:width(c)], ps[0:64, c % 3, 0:width(c)], ACT.Square)
                    if c == FOLD:
                        act.wait_ge(sem("x2_keys_var"), g * NC + c)
                    else:
                        act.wait_ge(sem("x2_square_low"), g * NC + c)
                    ins = act.activation(x2_upper[:, 0:width(c)], ps[64:128, c % 3, 0:width(c)], ACT.Square)
                else:
                    ins = act.activation(x2_dev[:, c % 3, 0:width(c)], ps[:, c % 3, 0:width(c)], ACT.Square)
                ins.then_inc(sem("x2_squared"), 1)

            def deviation(g, c):
                act.wait_ge(sem("x2_keys_var"), g * NC + (c + 1))
                act.activation(x2_dev[:, c % 3, 0:width(c)], ps[:, 3, 0:width(c)], ACT.Ln, bias=x2_eps[:, 0:1]).then_inc(sem("x2_deviation"), 1)
                act.wait_ge(sem("x2_deviation"), (g * NC + c) * 2 + 1)
                inverse = x2_dev[:, c % 3, 0:width(c)]
                act.activation(inverse, inverse, ACT.Exp, scale=-0.5).then_inc(sem("x2_deviation"), 1)
                act.wait_ge(sem("x2_deviation"), (g * NC + c) * 2 + 2)
                if c >= 2:
                    act.wait_ge(sem("x2_scores_psum"), since("x2_scores_psum", g * NC + (c - 1)))
                act.activation(x2_keys[:, c % 2, 0:width(c)], inverse, ACT.Square).then_inc(sem("x2_inverse"), 1)

            def exp(g, c):
                if c == 0:
                    act.wait_ge(sem("x2_bias_ready"), since("x2_bias_ready", g + 1))
                chunk = S[:, span(c)]
                act.activation(chunk, chunk, ACT.Exp, scale=SCALE2, bias=x2_small[:, 1:2], accum_out=x2_sum[:, c:c + 1])\
                   .then_inc(sem("x2_exp"), 1)

            def copy_probs(g, c):
                act.wait_ge(sem("x2_probsT_psum"), since("x2_probsT_psum", g * NC + (c + 1)))
                if c >= 2:
                    act.wait_ge(sem("x2_weighed"), since("x2_weighed", g * NC + (c - 1)))
                act.copy(x2_probsT[:, c % 2, 0:128 * subs(c)], ps[0:TILE, 5 + 2 * (c % 2), 0:128 * subs(c)]).then_inc(sem("x2_probsT_ready"), 1)

            def copy_mix(g):
                act.wait_ge(sem("x2_mixT_psum"), g + 1)
                act.copy(x2_mixT, cut(ps[:, 6, D:2 * D], KT, 128)).then_inc(sem("x2_mixT"), 1)

            def copy_cross(g):
                act.wait_ge(sem("x2_cross_psum"), g + 1)
                act.copy(x2_cat[:, ds(g * 2 + NQ, 2), :], cut(ps[:, 6, D:D + 128], 2, T)).then_inc(sem("x2_cross_done"), 1)

            act.copy(x2_mean, C("mean128")).then_inc(sem("x2_mean_ready"), 1)

            def change(weighed, ahead):
                if weighed is not None:
                    copy_mix(weighed)
                if ahead is not None:
                    square(ahead, 0)
                if weighed is not None:
                    copy_cross(weighed)
                if ahead is not None:
                    square(ahead, 1)
                    deviation(ahead, 0)

            def step(scored, weighed, ahead):
                for c in range(NC):
                    if scored is not None and c + 2 < NC:
                        square(scored, c + 2)
                    if weighed is not None and 1 <= c and c + 1 < NC:
                        exp(weighed, c + 1)
                    if weighed is not None and c == 0:
                        copy_probs(weighed, 0)
                    if scored is not None and c + 1 < NC:
                        deviation(scored, c + 1)
                    if weighed is not None and c >= 1:
                        copy_probs(weighed, c)
                if scored is not None:
                    exp(scored, 0)
                    exp(scored, 1)
                change(weighed, ahead)

            square(0, 0)
            square(0, 1)
            act.wait_ge(sem("x2_coreT_psum"), since("x2_coreT_psum", 1))
            act.wait_ge(sem("x2_v_ready"), since("x2_v_ready", 1))
            act.copy(x2_coreT, psf[0:T, 2560:3584]).then_inc(sem("x2_coreT"), 1)
            deviation(0, 0)
            act.wait_ge(sem("x2_core_out_psum"), since("x2_core_out_psum", 1))
            act.copy(x2_cat[:, 0:NQ, :], cut(psf[:, 2560:3584], NQ, T)).then_inc(sem("x2_core_done"), 1)
            step(0, None, 1)
            step(1, 0, 2)
            with act.Fori(1, GROUPS - 2) as g:
                g = act.snap(g, max_val=GROUPS - 3)
                step(g + 1, g, g + 2)
            step(GROUPS - 1, GROUPS - 2, None)
            step(None, GROUPS - 1, None)
            act.preload_act_table_set("exp_and_others")

        def x2_pool(pool):
            norm_pool(pool, 6)
            norm_pool(pool, 6.5)

        STAGES[6] = (x2_tensor, x2_vector, x2_scalar, x2_pool)

        x3_qT, x3_kT = cut(x2_keys[:, 0, 0:128], KT, T), cut(x2_keys[:, 0, 128:256], KT, T)
        x3_v = x2_mix[0:T, :]
        x3_own, x3_ownT = x2_q[0:T, 0:T], x2_q[0:T, T:2 * T]
        x3_max, x3_sum, x3_small = x2_max[0:T, :], x2_sum[0:T, :], x2_small[0:T, :]
        x3_probsT = x2_probsT[:, :, 0:SUB * T]

        def x3_tensor(pe):
            norm_tensor(pe, 9)
            normT_here(pe, 9)
            weights_here(pe, "x3")
            w = W("x3")
            for i in range(2):
                for o in range(KT):
                    for k in range(KT):
                        a = 512 * i + 256 * k + 128 * o
                        pe.matmul(ps[:, 0, (2 * i + o) * T:(2 * i + o + 1) * T], w[:, a:a + 128], xnT[:, k, 0, :], start=k == 0, stop=k == KT - 1)
            for k in range(KT):
                ins = pe.matmul(bank(1, D, T), xnT[:, k, 0, :], w[:, 1024 + 256 * k:1280 + 256 * k], start=k == 0, stop=k == KT - 1)
            ins.then_inc(sem("x3_qkv_psum"), 1)
            pe.wait_ge(sem("x3_qkv"), 3)
            pe.wait_ge(sem("ctxT_in"), 16)
            pe.wait_ge(sem("ctxN_in"), 16)
            for c in range(NC + 1):
                if c >= 2:
                    pe.wait_ge(sem("x3_scores"), since("x3_scores", c - 1))
                out = ps[0:T, 2 + c % 2, 0:width(c) if c < NC else T]
                for k in range(KT):
                    keys = ctxT[:, k, span(c)] if c < NC else x3_kT[:, k, :]
                    ins = pe.matmul(out, x3_qT[:, k, :], keys, start=k == 0, stop=k == KT - 1)
                ins.then_inc(sem("x3_scores_psum"), 1)

            def turn(c):
                pe.wait_ge(sem("x3_exp"), since("x3_exp", c + 1))
                if c >= 2:
                    pe.wait_ge(sem("x3_probsT"), since("x3_probsT", c - 1))
                if c == NC:
                    pe.transpose(ps[0:T, 4 + c % 2, 0:T], x3_own, C("ident")[0:T, 0:T]).then_inc(sem("x3_probsT_psum"), 1)
                    return
                for s in range(subs(c)):
                    a = CHUNK * c + TILE * s
                    ins = pe.transpose(ps[0:TILE, 4 + c % 2, T * s:T * s + T], S[0:T, a:a + TILE], C("ident")[0:T, 0:T])
                ins.then_inc(sem("x3_probsT_psum"), 1)

            def weigh(c):
                pe.wait_ge(sem("x3_probsT"), since("x3_probsT", c + 1))
                if c == NC:
                    ins = pe.matmul(bank(0, D, T), x3_ownT, x3_v, start=False, stop=True)
                else:
                    for s in range(subs(c)):
                        ins = pe.matmul(bank(0, D, T), x3_probsT[:, c % 2, T * s:T * s + T], ctxN[:, SUB * c + s, :],
                                        start=c == 0 and s == 0, stop=False)
                ins.then_inc(sem("x3_weighed"), 1)

            turn(0)
            for c in range(1, NC + 1):
                turn(c)
                weigh(c - 1)
            weigh(NC)
            out_tensor(pe, 9, attended, w[:, 1536:2048], "x3")

        def x3_vector(dve):
            norm_vector(dve, 9)
            for c in range(NC + 1):
                dve.wait_ge(sem("x3_scores_psum"), since("x3_scores_psum", c + 1))
                out = S[0:T, span(c)] if c < NC else x3_own
                dve.tensor_scalar(out, ps[0:T, 2 + c % 2, 0:width(c) if c < NC else T], 1.0, NEG, ALU.mult, ALU.max,
                                  accum_out=x3_max[:, c:c + 1]).then_inc(sem("x3_scores"), 1)
            dve.wait_ge(sem("x3_scores"), since("x3_scores", NC + 1))
            link(dve, "dve", dve.tensor_reduce(x3_small[:, 0:1], x3_max, AX, ALU.max))
            dve.tensor_scalar(x3_small[:, 1:2], x3_small[:, 0:1], -1.0 / 16, None, ALU.mult).then_inc(sem("x3_bias_ready"), 1)
            for c in range(NC + 1):
                dve.wait_ge(sem("x3_probsT_psum"), since("x3_probsT_psum", c + 1))
                if c >= 2:
                    dve.wait_ge(sem("x3_weighed"), since("x3_weighed", c - 1))
                if c < NC:
                    ins = dve.tensor_copy(x3_probsT[:, c % 2, 0:subs(c) * T], ps[0:TILE, 4 + c % 2, 0:subs(c) * T])
                else:
                    ins = dve.tensor_copy(x3_ownT, ps[0:T, 4 + c % 2, 0:T])
                ins.then_inc(sem("x3_probsT"), 1)
            link(dve, "dve", dve.tensor_reduce(x3_small[:, 2:3], x3_sum, AX, ALU.add))
            link(dve, "dve", dve.reciprocal(x3_small[:, 3:4], x3_small[:, 2:3]))
            dve.wait_ge(sem("x3_weighed"), since("x3_weighed", NC + 1))
            dve.tensor_scalar(attended[:, :], bank(0, D, T), x3_small[:, 3:4], None, ALU.mult).then_inc(sem("attended"), 1)
            residual_vector(dve, 9, bank(6, D, T), (sem("projected"), outs.index(9) + 1))

        def x3_scalar(act):
            norm_scalar(act, 9)
            act.wait_ge(sem("x3_qkv_psum"), since("x3_qkv_psum", 1))
            act.copy(x3_qT, cut(ps[:, 0, 0:KT * T], KT, T)).then_inc(sem("x3_qkv"), 1)
            act.copy(x3_kT, cut(ps[:, 0, KT * T:2 * KT * T], KT, T)).then_inc(sem("x3_qkv"), 1)
            act.copy(x3_v, bank(1, D, T)).then_inc(sem("x3_qkv"), 1)
            act.wait_ge(sem("x3_bias_ready"), since("x3_bias_ready", 1))
            for c in range(NC + 1):
                part = S[0:T, span(c)] if c < NC else x3_own
                act.activation(part, part, ACT.Exp, scale=1.0 / 16, bias=x3_small[:, 1:2], accum_out=x3_sum[:, c:c + 1])\
                   .then_inc(sem("x3_exp"), 1)
            out_scalar(act, 9)

        STAGES[9] = (x3_tensor, x3_vector, x3_scalar, lambda pool: norm_pool(pool, 9))

        def reload_ctx(sp, kept, source):
            if runs(3):
                sp.wait_ge(sem("attended"), outs.index(3) + 1)
            sp.dma_start(kept, io[source]).then_inc(sem(f"{source}_in"), 16)

        block = stack.enter_context(nc.Block())

        @block.sync
        def _(sp):
            n_first = min(len(pieces), NSLOT)

            def load(n):
                _, name, w = pieces[n]
                a = piece_from[name]
                sp.dma_start(W(name), io["weights"][:, a:a + w]).then_inc(sem(f"weights_in{n % NSLOT}"), 16)
                if name == "f1_experts0":
                    reload_ctx(sp, ctxT, "ctxT")
                if name == "f1_experts3":
                    reload_ctx(sp, ctxN, "ctxN")

            if sweep:
                a, n_keys = piece_from["pre"], KT * D
                sp.dma_start(W("pre")[:, 0:n_keys], io["weights"][:, a:a + n_keys]).then_inc(sem("key_weights_in"), 16)
                SWEEP_LOADS[0](sp, 0)
                sp.dma_start(W("pre")[:, n_keys:], io["weights"][:, a + n_keys:a + pieces[0][2]]).then_inc(sem("weights_in0"), 16)
            sp.dma_start(x[:, :], io["x"]).then_inc(sem("x_in"), 16)
            if sweep:
                load(1)
            kv1, kv1_end = row_bias_at["kv1"][0], sum(row_bias_at["kv1"])
            for a, b in ((kv1, kv1_end), (0, kv1), (kv1_end, n_row_biases)):
                sp.dma_start(row_biases[:, a:b], io["row_biases"][:, a:b]).then_inc(sem("kv1_in" if a == kv1 else "params_in"), 16)
                if a == kv1 and sweep:
                    SWEEP_LOADS[0](sp, 1)
            if not runs(5) and (runs(6) or runs(9)):
                reload_ctx(sp, ctxT, "ctxT")
                reload_ctx(sp, ctxN, "ctxN")
            for n in range(2 if sweep else 0, n_first):
                load(n)
            sp.dma_start(filter_sb[:, :], io["filterT"]).then_inc(sem("params_in"), 16)
            if sweep:
                SWEEP_LOADS[1](sp)
            for n in range(n_first, len(pieces)):
                sp.wait_ge(weights_used, n - NSLOT + 1)
                load(n)
            sp.wait_ge(sem("latent_done"), 1)
            sp.dma_start(io["out"], x[:, :]).then_inc(sem("stored"), 16)
            sp.wait_ge(sem("stored"), 16)

        @block.tensor
        def _(pe):
            if sweep:
                SWEEP[0](pe)
            pe.wait_ge(sem("constants_in"), 16)
            pe.wait_ge(sem("params_in"), 48)
            for s in range(12):
                if runs(s):
                    STAGES[s][0](pe)

        @block.vector
        def _(dve):
            dve.wait_ge(sem("x_in"), 16)
            if sweep:
                dve.wait_ge(sem("kv1_in"), 16)
                SWEEP[1](dve)
            dve.wait_ge(sem("constants_in"), 16)
            dve.wait_ge(sem("columns_in"), 16)
            dve.wait_ge(sem("params_in"), 48)
            for s in range(12):
                if runs(s):
                    STAGES[s][1](dve)
            dve.sem_inc(sem("latent_done"), 1)

        @block.scalar
        def _(act):
            act.dma_start(cols[:, :], io["columns"]).then_inc(sem("columns_in"), 16)
            if sweep:
                act.dma_start(mask_sb[:, :], io["mask"]).then_inc(sem("mask_in"), 16)
            act.dma_start(consts[:, :], io["constants"]).then_inc(sem("constants_in"), 16)
            act.preload_act_table_set("exp_and_others")
            act.wait_ge(sem("columns_in"), 16)
            if sweep:
                SWEEP[2](act)
            act.wait_ge(sem("constants_in"), 16)
            act.wait_ge(sem("params_in"), 48)
            for s in range(12):
                if runs(s):
                    STAGES[s][2](act)

        @block.gpsimd
        def _(pool):
            if sweep:
                SWEEP[3](pool)
            pool.wait_ge(sem("constants_in"), 16)
            pool.wait_ge(sem("params_in"), 48)
            for s in range(12):
                if runs(s):
                    STAGES[s][3](pool)



def kernel(**inputs):
    import concourse.bacc as bacc
    from concourse.bass_utils import run_bass_kernel_spmd

    nc = bacc.Bacc("TRN2", target_bir_lowering=False, num_devices=1)
    arrays = laid_out({n: np.asarray(v) for n, v in inputs.items()})
    io = {n: nc.dram_tensor(n, v.shape, F32, kind="ExternalInput").ap() for n, v in arrays.items()}
    io["out"] = nc.dram_tensor("out", (T, D), F32, kind="ExternalOutput").ap()
    perceiver(nc, io)
    result = run_bass_kernel_spmd(nc, [arrays], core_ids=[0])
    return result.results[0]["out"].reshape(1, T, D)
```
